# Optimizing a Trainium2 kernel written in Bass

```python
import numpy as np
import jax
import jax.numpy as jnp

def _softmax(x, axis=-1):
    return jax.nn.softmax(x, axis=axis)

def _gelu(x):
    return jax.nn.gelu(x, approximate=True)

def _silu(x):
    return jax.nn.silu(x)

def _sigmoid(x):
    return jax.nn.sigmoid(x)

def _layernorm(x, axis=-1, eps=1e-05):
    m = jnp.mean(x, axis=axis, keepdims=True)
    v = jnp.var(x, axis=axis, keepdims=True)
    return (x - m) / jnp.sqrt(v + eps)

def _scatter_add(tgt, idx, src, axis=0):
    return tgt.at[idx].add(src)

def _segment_sum(src, seg, n):
    return jax.ops.segment_sum(src, seg, n)
kernel_name = 'mk_perceiver_d4_seqx_r4_52ba4f'

def setup_inputs(seed: int=0):
    np.random.seed(seed)
    _w = jnp.asarray

    def _rec_inputs():
        import jax
        import jax.numpy as jnp
        _rk = jax.random.key(seed)
        x = -0.0002928 + 1 * jax.random.normal(jax.random.fold_in(_rk, 1), (16, 64, 256), jnp.float32)
        _lenS = 64 - jax.random.randint(jax.random.fold_in(_rk, 7), (16,), 0, max(1, 64 // 4) + 1, jnp.int32)
        _lenS2 = 1601 - jax.random.randint(jax.random.fold_in(_rk, 8), (16,), 0, max(1, 1601 // 4) + 1, jnp.int32)
        _ctx_1024P = jax.random.normal(jax.random.fold_in(_rk, 11), (16, 16, 256), jnp.float32)
        _ctx_1024c = jax.random.dirichlet(jax.random.fold_in(_rk, 511), 0.3 * jnp.ones((16,), jnp.float32), (16, 1601))
        _ctx_1024t = jnp.einsum('bsk,bkd->bsd', _ctx_1024c, _ctx_1024P)
        _ctx_1024t = _ctx_1024t * jax.lax.rsqrt(jnp.mean(jnp.square(_ctx_1024t)) + 1e-12) * 0.953939
        ctx_1024 = -1.39393e-06 + 0.999914 * (_ctx_1024t + 0.3 * jax.random.normal(jax.random.fold_in(_rk, 611), (16, 1601, 256), jnp.float32))
        _validS = jnp.arange(64)[None, :] < _lenS[:, None]
        _validS2 = jnp.arange(1601)[None, :] < _lenS2[:, None]
        _causal = jnp.tril(jnp.ones((64, 64), dtype=bool))
        mask_BxSxS2_bk1 = jnp.broadcast_to(_validS2[:, None, :], (16, 64, 1601))
        mask_1xSxS2_ff0 = jnp.where(jnp.ones((1, 64, 1601), dtype=bool), 0.0, -1000000000.0).astype(jnp.float32)
        return (x, ctx_1024, mask_BxSxS2_bk1, mask_1xSxS2_ff0)
    x, ctx_1024, mask_BxSxS2_bk1, mask_1xSxS2_ff0 = _rec_inputs()

    def _L0_xattn_setup():
        import jax, jax.numpy as jnp
        import numpy as np
        HEADS = 16
        B, S, D = (2, 512, 256)
        key = jax.random.key(seed)
        kq, kk, kv, km = jax.random.split(key, 4)
        q = jax.random.normal(kq, (B, S, D), dtype=jnp.float32)
        k = jax.random.normal(kk, (B, S, D), dtype=jnp.float32)
        v = jax.random.normal(kv, (B, S, D), dtype=jnp.float32)
        mask = jax.random.randint(km, (B, S, S), 0, 2).astype(bool)
        return {'q': q, 'k': k, 'v': v, 'mask': mask}
    _L0_xattn_all = _L0_xattn_setup()
    _L0_xattn_in = {k: v for k, v in _L0_xattn_all.items() if k in ()}
    del _L0_xattn_all

    def _L0_attn_setup():
        import jax, jax.numpy as jnp
        import numpy as np
        import math
        B, S, E = (2, 512, 256)
        H, DC, DR = (16, 64, 128)
        HD = E // H

        def _linear_params(key, din, dout):
            k1, k2 = jax.random.split(key)
            bound = 1.0 / math.sqrt(din)
            w = jax.random.uniform(k1, (din, dout), minval=-bound, maxval=bound, dtype=jnp.float32)
            b = jax.random.uniform(k2, (dout,), minval=-bound, maxval=bound, dtype=jnp.float32)
            return (w, b)

        def _gelu(x):
            return jax.nn.gelu(x, approximate=False)

        def _rope_cos_sin(seq_len, d_rope):
            inv_freq = 1.0 / 10000.0 ** (jnp.arange(0, d_rope, 2, dtype=jnp.float32) / d_rope)
            t = jnp.arange(seq_len, dtype=jnp.float32)
            freqs = t[:, None] * inv_freq[None, :]
            emb = jnp.concatenate([freqs, freqs], axis=-1)
            return (jnp.cos(emb), jnp.sin(emb))

        def _apply_rope(x, cos, sin):
            d = x.shape[-1]
            x1, x2 = (x[..., :d // 2], x[..., d // 2:])
            rot = jnp.concatenate([-x2, x1], axis=-1)
            return x * cos + rot * sin
        key = jax.random.key(seed)
        ks = jax.random.split(key, 10)
        x = jax.random.normal(ks[0], (B, S, E), dtype=jnp.float32)
        wq, bq = _linear_params(ks[1], E, DC)
        wqc, bqc = _linear_params(ks[2], DC, E - DR)
        wqr, bqr = _linear_params(ks[3], E, DR)
        wkv, bkv = _linear_params(ks[4], E, DC)
        wkr, bkr = _linear_params(ks[5], E, DR)
        wkc, bkc = _linear_params(ks[6], DC, E - DR)
        wv, bv = _linear_params(ks[7], DC, E)
        wo, bo = _linear_params(ks[8], E, E)
        return dict(x=x, wq=wq, bq=bq, wqc=wqc, bqc=bqc, wqr=wqr, bqr=bqr, wkv=wkv, bkv=bkv, wkr=wkr, bkr=bkr, wkc=wkc, bkc=bkc, wv=wv, bv=bv, wo=wo, bo=bo)
    _L0_attn_all = _L0_attn_setup()
    _L0_attn_in = {k: v for k, v in _L0_attn_all.items() if k in ('wq', 'bq', 'wqc', 'bqc', 'wqr', 'bqr', 'wkv', 'bkv', 'wkr', 'bkr', 'wkc', 'bkc', 'wv', 'bv', 'wo', 'bo')}
    del _L0_attn_all

    def _L0_ffn_setup():
        import jax, jax.numpy as jnp
        import numpy as np
        EMB_DIM = 256
        HIDDEN = int(2 / 3 * 4 * EMB_DIM)
        NUM_EXPERTS = 8
        TOP_K = 2
        B, S = (4, 256)
        key = jax.random.key(seed)
        ks = jax.random.split(key, 5)
        sc = 1.0 / np.sqrt(EMB_DIM)
        sh = 1.0 / np.sqrt(HIDDEN)
        return {'x': jax.random.normal(ks[0], (B, S, EMB_DIM), dtype=jnp.float32), 'Wg': jax.random.normal(ks[1], (NUM_EXPERTS, EMB_DIM), dtype=jnp.float32) * sc, 'W1': jax.random.normal(ks[2], (NUM_EXPERTS, HIDDEN, EMB_DIM), dtype=jnp.float32) * sc, 'W2': jax.random.normal(ks[3], (NUM_EXPERTS, HIDDEN, EMB_DIM), dtype=jnp.float32) * sc, 'W3': jax.random.normal(ks[4], (NUM_EXPERTS, EMB_DIM, HIDDEN), dtype=jnp.float32) * sh}
    _L0_ffn_all = _L0_ffn_setup()
    _L0_ffn_in = {k: v for k, v in _L0_ffn_all.items() if k in ('Wg', 'W1', 'W2', 'W3')}
    del _L0_ffn_all

    def _L1_xattn_setup():
        import jax, jax.numpy as jnp
        import numpy as np
        DIM = 256
        NUM_HEADS = 8
        HEAD_DIM = 64
        INNER = NUM_HEADS * HEAD_DIM
        key = jax.random.key(seed)
        ks = jax.random.split(key, 7)
        B, N, M = (8, 128, 1024)
        x = jax.random.normal(ks[0], (B, N, DIM), dtype=jnp.float32)
        context = jax.random.normal(ks[1], (B, M, DIM), dtype=jnp.float32)
        s_in = 1.0 / np.sqrt(DIM)
        s_inner = 1.0 / np.sqrt(INNER)
        Wq = jax.random.normal(ks[2], (DIM, INNER), dtype=jnp.float32) * s_in
        Wk = jax.random.normal(ks[3], (DIM, INNER), dtype=jnp.float32) * s_in
        Wv = jax.random.normal(ks[4], (DIM, INNER), dtype=jnp.float32) * s_in
        Wo = jax.random.normal(ks[5], (INNER, DIM), dtype=jnp.float32) * s_inner
        bo = jax.random.normal(ks[6], (DIM,), dtype=jnp.float32) * 0.01
        return {'x': x, 'context': context, 'Wq': Wq, 'Wk': Wk, 'Wv': Wv, 'Wo': Wo, 'bo': bo}
    _L1_xattn_all = _L1_xattn_setup()
    _L1_xattn_in = {k: v for k, v in _L1_xattn_all.items() if k in ('Wq', 'Wk', 'Wv', 'Wo', 'bo')}
    del _L1_xattn_all

    def _L1_attn_setup():
        import jax, jax.numpy as jnp
        import numpy as np
        B, T, C, H = (2, 256, 256, 16)
        D = C // H
        EPS = 1e-06
        key = jax.random.key(seed)
        k1, k2, k3, k4, k5 = jax.random.split(key, 5)
        s = 0.02
        return {'x': jax.random.normal(k1, (B, T, C), dtype=jnp.float32), 'w_qkv': jax.random.normal(k2, (3 * C, C), dtype=jnp.float32) * s, 'b_qkv': jax.random.normal(k3, (3 * C,), dtype=jnp.float32) * s, 'w_out': jax.random.normal(k4, (C, C), dtype=jnp.float32) * s, 'b_out': jax.random.normal(k5, (C,), dtype=jnp.float32) * s}
    _L1_attn_all = _L1_attn_setup()
    _L1_attn_in = {k: v for k, v in _L1_attn_all.items() if k in ('w_qkv', 'b_qkv', 'w_out', 'b_out')}
    del _L1_attn_all

    def _L1_ffn_setup():
        import jax, jax.numpy as jnp
        import numpy as np
        B, S, D_MODEL, D_HIDDEN = (4, 512, 256, 1024)

        def act_quant(x):
            scale = 127.0 / jnp.clip(jnp.max(jnp.abs(x), axis=-1, keepdims=True), 1e-05)
            return jnp.clip(jnp.round(x * scale), -128, 127) / scale

        def weight_quant(w):
            scale = 1.0 / jnp.clip(jnp.mean(jnp.abs(w)), 1e-05)
            return jnp.clip(jnp.round(w * scale), -1, 1) / scale

        def bit_linear(x, w):
            xq = x + jax.lax.stop_gradient(act_quant(x) - x)
            wq = w + jax.lax.stop_gradient(weight_quant(w) - w)
            return jnp.einsum('bsd,hd->bsh', xq, wq)

        def depthwise_conv1d(x_bcl, w, b):
            y = jax.lax.conv_general_dilated(x_bcl, w, window_strides=(1,), padding=[(1, 1)], dimension_numbers=('NCH', 'OIH', 'NCH'), feature_group_count=x_bcl.shape[1])
            return y + b[None, :, None]
        key = jax.random.key(seed)
        ks = jax.random.split(key, 5)
        lim1 = 1.0 / np.sqrt(D_MODEL)
        lim2 = 1.0 / np.sqrt(D_HIDDEN)
        limc = 1.0 / np.sqrt(3.0)
        return {'x': jax.random.normal(ks[0], (B, S, D_MODEL), dtype=jnp.float32), 'w1': jax.random.uniform(ks[1], (D_HIDDEN, D_MODEL), jnp.float32, -lim1, lim1), 'conv_w': jax.random.uniform(ks[2], (D_HIDDEN, 1, 3), jnp.float32, -limc, limc), 'conv_b': jax.random.uniform(ks[3], (D_HIDDEN,), jnp.float32, -limc, limc), 'w2': jax.random.uniform(ks[4], (D_MODEL, D_HIDDEN), jnp.float32, -lim2, lim2)}
    _L1_ffn_all = _L1_ffn_setup()
    _L1_ffn_in = {k: v for k, v in _L1_ffn_all.items() if k in ('w1', 'conv_w', 'conv_b', 'w2')}
    del _L1_ffn_all

    def _L2_xattn_setup():
        import jax, jax.numpy as jnp
        import numpy as np
        B, S, D_IN, D_MODEL = (4, 512, 256, 256)
        key = jax.random.key(seed)
        ks = jax.random.split(key, 8)
        glorot = np.sqrt(6.0 / (D_IN + D_MODEL))
        inp = {'q': jax.random.normal(ks[0], (B, S, D_IN), dtype=jnp.float32), 'k': jax.random.normal(ks[1], (B, S, D_IN), dtype=jnp.float32), 'v': jax.random.normal(ks[2], (B, S, D_IN), dtype=jnp.float32), 'mask': jnp.zeros((1, S, S), dtype=jnp.float32), 'kernel_q': jax.random.uniform(ks[3], (1, 1, D_IN, D_MODEL), jnp.float32, -glorot, glorot), 'kernel_k': jax.random.uniform(ks[4], (1, 1, D_IN, D_MODEL), jnp.float32, -glorot, glorot), 'kernel_v': jax.random.uniform(ks[5], (1, 1, D_IN, D_MODEL), jnp.float32, -glorot, glorot), 'bias_q': 0.05 * jax.random.normal(ks[6], (D_MODEL,), dtype=jnp.float32), 'bias_k': 0.05 * jax.random.normal(ks[7], (D_MODEL,), dtype=jnp.float32), 'bias_v': 0.05 * jax.random.normal(jax.random.fold_in(key, 7), (D_MODEL,), dtype=jnp.float32)}
        return inp
    _L2_xattn_all = _L2_xattn_setup()
    _L2_xattn_in = {k: v for k, v in _L2_xattn_all.items() if k in ('kernel_q', 'kernel_k', 'kernel_v', 'bias_q', 'bias_k', 'bias_v')}
    del _L2_xattn_all

    def _L2_attn_setup():
        import jax, jax.numpy as jnp
        import numpy as np
        DIM_Q = 256
        DIM_K = 256
        DIM_V = 256
        OUT_DIM = 256
        B, N = (4, 512)

        def _layer_norm(h, gamma, beta, eps=1e-05):
            mu = jnp.mean(h, axis=-1, keepdims=True)
            var = jnp.mean(jnp.square(h - mu), axis=-1, keepdims=True)
            return (h - mu) * jax.lax.rsqrt(var + eps) * gamma + beta
        key = jax.random.key(seed)
        ks = jax.random.split(key, 8)
        s_in = 1.0 / np.sqrt(DIM_Q)
        s_v = 1.0 / np.sqrt(DIM_V)
        return {'x': jax.random.normal(ks[0], (B, N, DIM_Q), dtype=jnp.float32), 'Wq': jax.random.normal(ks[1], (DIM_Q, DIM_K), dtype=jnp.float32) * s_in, 'Wk': jax.random.normal(ks[2], (DIM_Q, DIM_K), dtype=jnp.float32) * s_in, 'Wv': jax.random.normal(ks[3], (DIM_Q, DIM_V), dtype=jnp.float32) * s_in, 'Wfc': jax.random.normal(ks[4], (DIM_V, OUT_DIM), dtype=jnp.float32) * s_v, 'bfc': jax.random.normal(ks[5], (OUT_DIM,), dtype=jnp.float32) * 0.02, 'gamma': jnp.ones((DIM_V,), dtype=jnp.float32), 'beta': jnp.zeros((DIM_V,), dtype=jnp.float32)}
    _L2_attn_all = _L2_attn_setup()
    _L2_attn_in = {k: v for k, v in _L2_attn_all.items() if k in ('Wq', 'Wk', 'Wv', 'Wfc', 'bfc', 'gamma', 'beta')}
    del _L2_attn_all

    def _L2_ffn_setup():
        import jax, jax.numpy as jnp
        import numpy as np
        NUM_EXPERTS = 8
        IN_FEATURES = 256
        HIDDEN_FEATURES = 1024
        GATE_DIM = 16
        EPS = 0.0001
        key = jax.random.key(seed)
        ks = jax.random.split(key, 7)
        hidden_states = jax.random.normal(ks[0], (1, 512, IN_FEATURES), dtype=jnp.float32)
        wg_red = jax.random.normal(ks[1], (GATE_DIM, IN_FEATURES), dtype=jnp.float32) * 0.02
        wg = jax.random.normal(ks[2], (NUM_EXPERTS, GATE_DIM), dtype=jnp.float32)
        w1 = jax.random.uniform(ks[3], (NUM_EXPERTS, IN_FEATURES, HIDDEN_FEATURES), dtype=jnp.float32)
        b1 = jax.random.uniform(ks[4], (NUM_EXPERTS, HIDDEN_FEATURES), dtype=jnp.float32)
        w2 = jax.random.uniform(ks[5], (NUM_EXPERTS, HIDDEN_FEATURES, IN_FEATURES), dtype=jnp.float32)
        b2 = jax.random.uniform(ks[6], (NUM_EXPERTS, IN_FEATURES), dtype=jnp.float32)
        return {'hidden_states': hidden_states, 'wg_red': wg_red, 'wg': wg, 'w1': w1, 'b1': b1, 'w2': w2, 'b2': b2}
    _L2_ffn_all = _L2_ffn_setup()
    _L2_ffn_in = {k: v for k, v in _L2_ffn_all.items() if k in ('wg_red', 'wg', 'w1', 'b1', 'w2', 'b2')}
    del _L2_ffn_all

    def _L3_xattn_setup():
        import jax, jax.numpy as jnp
        import numpy as np
        NUM_HEADS = 16

        def _split_heads(x, h):
            b, s, d = x.shape
            return x.reshape(b, s, h, d // h).transpose(0, 2, 1, 3)
        key = jax.random.key(seed)
        kv, kk, kq = jax.random.split(key, 3)
        shape = (2, 512, 256)
        return {'v': jax.random.normal(kv, shape, dtype=jnp.float32), 'k': jax.random.normal(kk, shape, dtype=jnp.float32), 'q': jax.random.normal(kq, shape, dtype=jnp.float32)}
    _L3_xattn_all = _L3_xattn_setup()
    _L3_xattn_in = {k: v for k, v in _L3_xattn_all.items() if k in ()}
    del _L3_xattn_all

    def _L3_attn_setup():
        import jax, jax.numpy as jnp
        import numpy as np
        B, L, C, H = (8, 512, 256, 16)
        HID = 4 * C

        def _rope(x):
            b, n, c = x.shape
            k_max = c // 2
            theta = 1.0 / 10000.0 ** (jnp.arange(k_max, dtype=jnp.float32) / k_max)
            cos_t, sin_t = (jnp.cos(theta), jnp.sin(theta))
            xr = x.reshape(b, n, k_max, 2)
            re = xr[..., 0] * cos_t - xr[..., 1] * sin_t
            im = xr[..., 0] * sin_t + xr[..., 1] * cos_t
            return jnp.stack((re, im), axis=-1).reshape(b, n, c)

        def _dwconv(x_bcl, w, bias):
            y = jax.lax.conv_general_dilated(x_bcl, w, (1,), [(1, 1)], dimension_numbers=('NCH', 'OIH', 'NCH'), feature_group_count=x_bcl.shape[1])
            return y + bias[None, :, None]

        def _ln(x, g, b, eps=1e-05):
            mu = x.mean(-1, keepdims=True)
            var = ((x - mu) ** 2).mean(-1, keepdims=True)
            return (x - mu) * jax.lax.rsqrt(var + eps) * g + b

        def _mlla_forward(x, cpe1_w, cpe1_b, norm1_g, norm1_b, in_w, in_b, actp_w, actp_b, dwc_w, dwc_b, qk_w, qk_b, lepe_w, lepe_b, out_w, out_b, cpe2_w, cpe2_b, norm2_g, norm2_b, fc1_w, fc1_b, fc2_w, fc2_b):
            b, n, c = x.shape
            h, d = (H, c // H)
            x = x + _dwconv(x.transpose(0, 2, 1), cpe1_w, cpe1_b).transpose(0, 2, 1)
            shortcut = x
            xn = _ln(x, norm1_g, norm1_b)
            act_res = jax.nn.silu(xn @ actp_w + actp_b)
            xi = xn @ in_w + in_b
            xi = jax.nn.silu(_dwconv(xi.transpose(0, 2, 1), dwc_w, dwc_b)).transpose(0, 2, 1)
            qk = xi @ qk_w + qk_b
            q = jax.nn.elu(qk[..., :c]) + 1.0
            k = jax.nn.elu(qk[..., c:]) + 1.0
            q_rope = _rope(q).reshape(b, n, h, d).transpose(0, 2, 1, 3)
            k_rope = _rope(k).reshape(b, n, h, d).transpose(0, 2, 1, 3)
            qh = q.reshape(b, n, h, d).transpose(0, 2, 1, 3)
            kh = k.reshape(b, n, h, d).transpose(0, 2, 1, 3)
            vh = xi.reshape(b, n, h, d).transpose(0, 2, 1, 3)
            k_mean = kh.mean(axis=2, keepdims=True)
            z = 1.0 / (jnp.einsum('bhnd,bhmd->bhnm', qh, k_mean) + 1e-06)
            kv = jnp.einsum('bhnd,bhne->bhde', k_rope, vh) * (1.0 / n)
            attn = jnp.einsum('bhnd,bhde->bhne', q_rope, kv) * z
            attn = attn.transpose(0, 2, 1, 3).reshape(b, n, c)
            v_bcl = vh.transpose(0, 2, 1, 3).reshape(b, n, c).transpose(0, 2, 1)
            attn = attn + _dwconv(v_bcl, lepe_w, lepe_b).transpose(0, 2, 1)
            x = shortcut + attn * act_res @ out_w + out_b
            x = x + _dwconv(x.transpose(0, 2, 1), cpe2_w, cpe2_b).transpose(0, 2, 1)
            xn2 = _ln(x, norm2_g, norm2_b)
            mlp = jax.nn.gelu(xn2 @ fc1_w + fc1_b, approximate=False) @ fc2_w + fc2_b
            return x + mlp
        key = jax.random.key(seed)
        ks = jax.random.split(key, 12)

        def nrm(k, shape, scale=0.02):
            return jax.random.normal(k, shape, jnp.float32) * scale
        return {'x': jax.random.normal(ks[0], (B, L, C), jnp.float32), 'cpe1_w': nrm(ks[1], (C, 1, 3), 0.1), 'cpe1_b': jnp.zeros((C,), jnp.float32), 'norm1_g': jnp.ones((C,), jnp.float32), 'norm1_b': jnp.zeros((C,), jnp.float32), 'in_w': nrm(ks[2], (C, C)), 'in_b': jnp.zeros((C,), jnp.float32), 'actp_w': nrm(ks[3], (C, C)), 'actp_b': jnp.zeros((C,), jnp.float32), 'dwc_w': nrm(ks[4], (C, 1, 3), 0.1), 'dwc_b': jnp.zeros((C,), jnp.float32), 'qk_w': nrm(ks[5], (C, 2 * C)), 'qk_b': jnp.zeros((2 * C,), jnp.float32), 'lepe_w': nrm(ks[6], (C, 1, 3), 0.1), 'lepe_b': jnp.zeros((C,), jnp.float32), 'out_w': nrm(ks[7], (C, C)), 'out_b': jnp.zeros((C,), jnp.float32), 'cpe2_w': nrm(ks[8], (C, 1, 3), 0.1), 'cpe2_b': jnp.zeros((C,), jnp.float32), 'norm2_g': jnp.ones((C,), jnp.float32), 'norm2_b': jnp.zeros((C,), jnp.float32), 'fc1_w': nrm(ks[9], (C, HID)), 'fc1_b': jnp.zeros((HID,), jnp.float32), 'fc2_w': nrm(ks[10], (HID, C)), 'fc2_b': jnp.zeros((C,), jnp.float32)}
    _L3_attn_all = _L3_attn_setup()
    _L3_attn_in = {k: v for k, v in _L3_attn_all.items() if k in ('cpe1_w', 'cpe1_b', 'norm1_g', 'norm1_b', 'in_w', 'in_b', 'actp_w', 'actp_b', 'dwc_w', 'dwc_b', 'qk_w', 'qk_b', 'lepe_w', 'lepe_b', 'out_w', 'out_b', 'cpe2_w', 'cpe2_b', 'norm2_g', 'norm2_b', 'fc1_w', 'fc1_b', 'fc2_w', 'fc2_b')}
    del _L3_attn_all

    def _L3_ffn_setup():
        import jax, jax.numpy as jnp
        import numpy as np
        HID, FFN, E, K = (256, 1024, 8, 2)
        CAP_FACTOR = 1.25
        key = jax.random.key(seed)
        k1, k2, k3, k4 = jax.random.split(key, 4)
        B, T = (4, 512)
        x = jax.random.normal(k1, (B, T, HID), dtype=jnp.float32)
        router_w = jax.random.normal(k2, (E, HID), dtype=jnp.float32) * 0.02
        w1 = jax.random.normal(k3, (E, HID, FFN), dtype=jnp.float32) * 0.02
        w2 = jax.random.normal(k4, (E, FFN, HID), dtype=jnp.float32) * 0.02
        return {'x': x, 'router_w': router_w, 'w1': w1, 'w2': w2}
    _L3_ffn_all = _L3_ffn_setup()
    _L3_ffn_in = {k: v for k, v in _L3_ffn_all.items() if k in ('router_w', 'w1', 'w2')}
    del _L3_ffn_all
    return {'x': x, 'ctx_1024': ctx_1024, 'mask_BxSxS2_bk1': mask_BxSxS2_bk1, 'mask_1xSxS2_ff0': mask_1xSxS2_ff0, 'L0_attn_wq': _L0_attn_in['wq'], 'L0_attn_bq': _L0_attn_in['bq'], 'L0_attn_wqc': _L0_attn_in['wqc'], 'L0_attn_bqc': _L0_attn_in['bqc'], 'L0_attn_wqr': _L0_attn_in['wqr'], 'L0_attn_bqr': _L0_attn_in['bqr'], 'L0_attn_wkv': _L0_attn_in['wkv'], 'L0_attn_bkv': _L0_attn_in['bkv'], 'L0_attn_wkr': _L0_attn_in['wkr'], 'L0_attn_bkr': _L0_attn_in['bkr'], 'L0_attn_wkc': _L0_attn_in['wkc'], 'L0_attn_bkc': _L0_attn_in['bkc'], 'L0_attn_wv': _L0_attn_in['wv'], 'L0_attn_bv': _L0_attn_in['bv'], 'L0_attn_wo': _L0_attn_in['wo'], 'L0_attn_bo': _L0_attn_in['bo'], 'L0_ffn_Wg': _L0_ffn_in['Wg'], 'L0_ffn_W1': _L0_ffn_in['W1'], 'L0_ffn_W2': _L0_ffn_in['W2'], 'L0_ffn_W3': _L0_ffn_in['W3'], 'L1_xattn_Wq': _L1_xattn_in['Wq'], 'L1_xattn_Wk': _L1_xattn_in['Wk'], 'L1_xattn_Wv': _L1_xattn_in['Wv'], 'L1_xattn_Wo': _L1_xattn_in['Wo'], 'L1_xattn_bo': _L1_xattn_in['bo'], 'L1_attn_w_qkv': _L1_attn_in['w_qkv'], 'L1_attn_b_qkv': _L1_attn_in['b_qkv'], 'L1_attn_w_out': _L1_attn_in['w_out'], 'L1_attn_b_out': _L1_attn_in['b_out'], 'L1_ffn_w1': _L1_ffn_in['w1'], 'L1_ffn_conv_w': _L1_ffn_in['conv_w'], 'L1_ffn_conv_b': _L1_ffn_in['conv_b'], 'L1_ffn_w2': _L1_ffn_in['w2'], 'L2_xattn_kernel_q': _L2_xattn_in['kernel_q'], 'L2_xattn_kernel_k': _L2_xattn_in['kernel_k'], 'L2_xattn_kernel_v': _L2_xattn_in['kernel_v'], 'L2_xattn_bias_q': _L2_xattn_in['bias_q'], 'L2_xattn_bias_k': _L2_xattn_in['bias_k'], 'L2_xattn_bias_v': _L2_xattn_in['bias_v'], 'L2_attn_Wq': _L2_attn_in['Wq'], 'L2_attn_Wk': _L2_attn_in['Wk'], 'L2_attn_Wv': _L2_attn_in['Wv'], 'L2_attn_Wfc': _L2_attn_in['Wfc'], 'L2_attn_bfc': _L2_attn_in['bfc'], 'L2_attn_gamma': _L2_attn_in['gamma'], 'L2_attn_beta': _L2_attn_in['beta'], 'L2_ffn_wg_red': _L2_ffn_in['wg_red'], 'L2_ffn_wg': _L2_ffn_in['wg'], 'L2_ffn_w1': _L2_ffn_in['w1'], 'L2_ffn_b1': _L2_ffn_in['b1'], 'L2_ffn_w2': _L2_ffn_in['w2'], 'L2_ffn_b2': _L2_ffn_in['b2'], 'L3_attn_cpe1_w': _L3_attn_in['cpe1_w'], 'L3_attn_cpe1_b': _L3_attn_in['cpe1_b'], 'L3_attn_norm1_g': _L3_attn_in['norm1_g'], 'L3_attn_norm1_b': _L3_attn_in['norm1_b'], 'L3_attn_in_w': _L3_attn_in['in_w'], 'L3_attn_in_b': _L3_attn_in['in_b'], 'L3_attn_actp_w': _L3_attn_in['actp_w'], 'L3_attn_actp_b': _L3_attn_in['actp_b'], 'L3_attn_dwc_w': _L3_attn_in['dwc_w'], 'L3_attn_dwc_b': _L3_attn_in['dwc_b'], 'L3_attn_qk_w': _L3_attn_in['qk_w'], 'L3_attn_qk_b': _L3_attn_in['qk_b'], 'L3_attn_lepe_w': _L3_attn_in['lepe_w'], 'L3_attn_lepe_b': _L3_attn_in['lepe_b'], 'L3_attn_out_w': _L3_attn_in['out_w'], 'L3_attn_out_b': _L3_attn_in['out_b'], 'L3_attn_cpe2_w': _L3_attn_in['cpe2_w'], 'L3_attn_cpe2_b': _L3_attn_in['cpe2_b'], 'L3_attn_norm2_g': _L3_attn_in['norm2_g'], 'L3_attn_norm2_b': _L3_attn_in['norm2_b'], 'L3_attn_fc1_w': _L3_attn_in['fc1_w'], 'L3_attn_fc1_b': _L3_attn_in['fc1_b'], 'L3_attn_fc2_w': _L3_attn_in['fc2_w'], 'L3_attn_fc2_b': _L3_attn_in['fc2_b'], 'L3_ffn_router_w': _L3_ffn_in['router_w'], 'L3_ffn_w1': _L3_ffn_in['w1'], 'L3_ffn_w2': _L3_ffn_in['w2']}

def reference(x, ctx_1024, mask_BxSxS2_bk1, mask_1xSxS2_ff0, L0_attn_wq, L0_attn_bq, L0_attn_wqc, L0_attn_bqc, L0_attn_wqr, L0_attn_bqr, L0_attn_wkv, L0_attn_bkv, L0_attn_wkr, L0_attn_bkr, L0_attn_wkc, L0_attn_bkc, L0_attn_wv, L0_attn_bv, L0_attn_wo, L0_attn_bo, L0_ffn_Wg, L0_ffn_W1, L0_ffn_W2, L0_ffn_W3, L1_xattn_Wq, L1_xattn_Wk, L1_xattn_Wv, L1_xattn_Wo, L1_xattn_bo, L1_attn_w_qkv, L1_attn_b_qkv, L1_attn_w_out, L1_attn_b_out, L1_ffn_w1, L1_ffn_conv_w, L1_ffn_conv_b, L1_ffn_w2, L2_xattn_kernel_q, L2_xattn_kernel_k, L2_xattn_kernel_v, L2_xattn_bias_q, L2_xattn_bias_k, L2_xattn_bias_v, L2_attn_Wq, L2_attn_Wk, L2_attn_Wv, L2_attn_Wfc, L2_attn_bfc, L2_attn_gamma, L2_attn_beta, L2_ffn_wg_red, L2_ffn_wg, L2_ffn_w1, L2_ffn_b1, L2_ffn_w2, L2_ffn_b2, L3_attn_cpe1_w, L3_attn_cpe1_b, L3_attn_norm1_g, L3_attn_norm1_b, L3_attn_in_w, L3_attn_in_b, L3_attn_actp_w, L3_attn_actp_b, L3_attn_dwc_w, L3_attn_dwc_b, L3_attn_qk_w, L3_attn_qk_b, L3_attn_lepe_w, L3_attn_lepe_b, L3_attn_out_w, L3_attn_out_b, L3_attn_cpe2_w, L3_attn_cpe2_b, L3_attn_norm2_g, L3_attn_norm2_b, L3_attn_fc1_w, L3_attn_fc1_b, L3_attn_fc2_w, L3_attn_fc2_b, L3_ffn_router_w, L3_ffn_w1, L3_ffn_w2):
    import jax
    import jax.numpy as jnp

    def _L0_xattn_ref(q, k, v, mask):
        import jax, jax.numpy as jnp
        import numpy as np
        HEADS = 16
        B, S, D = (2, 512, 256)
        hd = q.shape[-1] // HEADS

        def split_heads(x):
            return x.reshape(x.shape[:-1] + (HEADS, hd)).swapaxes(-3, -2)
        qh, kh, vh = (split_heads(q), split_heads(k), split_heads(v))
        scores = jnp.einsum('bhqd,bhkd->bhqk', qh, kh) / jnp.sqrt(jnp.float32(hd))
        scores = scores + mask[:, None, :, :].astype(scores.dtype) * jnp.float32(-10000.0)
        attn = jax.nn.softmax(scores, axis=-1)
        out = jnp.einsum('bhqk,bhkd->bhqd', attn, vh)
        return out.swapaxes(-3, -2).reshape(q.shape[:-2] + (q.shape[-2], HEADS * hd))

    def _L0_attn_ref(x, wq, bq, wqc, bqc, wqr, bqr, wkv, bkv, wkr, bkr, wkc, bkc, wv, bv, wo, bo):
        import jax, jax.numpy as jnp
        import numpy as np
        import math
        B, S, E = (2, 512, 256)
        H, DC, DR = (16, 64, 128)
        HD = E // H

        def _linear_params(key, din, dout):
            k1, k2 = jax.random.split(key)
            bound = 1.0 / math.sqrt(din)
            w = jax.random.uniform(k1, (din, dout), minval=-bound, maxval=bound, dtype=jnp.float32)
            b = jax.random.uniform(k2, (dout,), minval=-bound, maxval=bound, dtype=jnp.float32)
            return (w, b)

        def _gelu(x):
            return jax.nn.gelu(x, approximate=False)

        def _rope_cos_sin(seq_len, d_rope):
            inv_freq = 1.0 / 10000.0 ** (jnp.arange(0, d_rope, 2, dtype=jnp.float32) / d_rope)
            t = jnp.arange(seq_len, dtype=jnp.float32)
            freqs = t[:, None] * inv_freq[None, :]
            emb = jnp.concatenate([freqs, freqs], axis=-1)
            return (jnp.cos(emb), jnp.sin(emb))

        def _apply_rope(x, cos, sin):
            d = x.shape[-1]
            x1, x2 = (x[..., :d // 2], x[..., d // 2:])
            rot = jnp.concatenate([-x2, x1], axis=-1)
            return x * cos + rot * sin
        b, s, _ = x.shape
        cq = _gelu(x @ wq + bq)
        q_c = cq @ wqc + bqc
        q_r = x @ wqr + bqr
        ckv = _gelu(x @ wkv + bkv)
        k_r = x @ wkr + bkr
        k_c = ckv @ wkc + bkc
        v = (ckv @ wv + bv).reshape(b, s, H, HD).transpose(0, 2, 1, 3)
        cos, sin = _rope_cos_sin(s, DR)
        q_r = _apply_rope(q_r, cos, sin)
        k_r = _apply_rope(k_r, cos, sin)
        q = _gelu(jnp.concatenate([q_c, q_r], axis=-1)).reshape(b, s, H, HD).transpose(0, 2, 1, 3)
        k = _gelu(jnp.concatenate([k_c, k_r], axis=-1)).reshape(b, s, H, HD).transpose(0, 2, 1, 3)
        scale = 1.0 / math.sqrt(HD)
        scores = jnp.einsum('bhqd,bhkd->bhqk', q, k) * scale
        causal = jnp.triu(jnp.ones((s, s), dtype=bool), k=1)
        scores = jnp.where(causal[None, None], -jnp.inf, scores)
        attn = jax.nn.softmax(scores, axis=-1)
        out = jnp.einsum('bhqk,bhkd->bhqd', attn, v)
        out = out.transpose(0, 2, 1, 3).reshape(b, s, E)
        return out @ wo + bo

    def _L0_ffn_ref(x, Wg, W1, W2, W3):
        import jax, jax.numpy as jnp
        import numpy as np
        EMB_DIM = 256
        HIDDEN = int(2 / 3 * 4 * EMB_DIM)
        NUM_EXPERTS = 8
        TOP_K = 2
        B, S = (4, 256)
        gate_logits = jnp.einsum('bsd,ed->bse', x, Wg)
        top_v, top_i = jax.lax.top_k(gate_logits, TOP_K)
        mask = jnp.any(top_i[..., :, None] == jnp.arange(NUM_EXPERTS), axis=-2)
        sparse_logits = jnp.where(mask, gate_logits, -jnp.inf)
        gating = jax.nn.softmax(sparse_logits, axis=-1)
        h1 = jnp.einsum('bsd,ehd->bseh', x, W1)
        h2 = jnp.einsum('bsd,ehd->bseh', x, W2)
        hidden = jax.nn.silu(h1) * h2
        expert_out = jnp.einsum('bseh,edh->bsed', hidden, W3)
        return jnp.einsum('bsed,bse->bsd', expert_out, gating)

    def _L1_xattn_ref(x, context, Wq, Wk, Wv, Wo, bo):
        import jax, jax.numpy as jnp
        import numpy as np
        DIM = 256
        NUM_HEADS = 8
        HEAD_DIM = 64
        INNER = NUM_HEADS * HEAD_DIM
        B, N, _ = x.shape
        M = context.shape[1]
        scale = HEAD_DIM ** (-0.5)
        q = (x @ Wq).reshape(B, N, NUM_HEADS, HEAD_DIM).transpose(0, 2, 1, 3)
        k = (context @ Wk).reshape(B, M, NUM_HEADS, HEAD_DIM).transpose(0, 2, 1, 3)
        v = (context @ Wv).reshape(B, M, NUM_HEADS, HEAD_DIM).transpose(0, 2, 1, 3)
        attn = jax.nn.softmax(jnp.einsum('bhnd,bhmd->bhnm', q, k) * scale, axis=-1)
        out = jnp.einsum('bhnm,bhmd->bhnd', attn, v)
        out = out.transpose(0, 2, 1, 3).reshape(B, N, INNER)
        return out @ Wo + bo

    def _L1_attn_ref(x, w_qkv, b_qkv, w_out, b_out):
        import jax, jax.numpy as jnp
        import numpy as np
        B, T, C, H = (2, 256, 256, 16)
        D = C // H
        EPS = 1e-06
        b, t, c = x.shape
        qkv = x @ w_qkv.T + b_qkv
        q, k, v = jnp.split(qkv, 3, axis=-1)

        def to_heads(u):
            return u.reshape(b, t, H, D).transpose(0, 2, 1, 3).astype(jnp.float32)
        q, k, v = (to_heads(q), to_heads(k), to_heads(v))
        q_prime = jax.nn.elu(q) + 1.0
        k_prime = jax.nn.elu(k) + 1.0
        kv_cumsum = jnp.cumsum(jnp.einsum('bhtd,bhte->bhtde', k_prime, v), axis=2)
        context = jnp.einsum('bhtd,bhtde->bhte', q_prime, kv_cumsum)
        norm = jnp.einsum('bhtd,bhtd->bht', q_prime, jnp.cumsum(k_prime, axis=2))
        out = context / (norm[..., None] + EPS)
        out = out.astype(x.dtype).transpose(0, 2, 1, 3).reshape(b, t, c)
        return out @ w_out.T + b_out

    def _L1_ffn_ref(x, w1, conv_w, conv_b, w2):
        import jax, jax.numpy as jnp
        import numpy as np
        B, S, D_MODEL, D_HIDDEN = (4, 512, 256, 1024)

        def act_quant(x):
            scale = 127.0 / jnp.clip(jnp.max(jnp.abs(x), axis=-1, keepdims=True), 1e-05)
            return jnp.clip(jnp.round(x * scale), -128, 127) / scale

        def weight_quant(w):
            scale = 1.0 / jnp.clip(jnp.mean(jnp.abs(w)), 1e-05)
            return jnp.clip(jnp.round(w * scale), -1, 1) / scale

        def bit_linear(x, w):
            xq = x + jax.lax.stop_gradient(act_quant(x) - x)
            wq = w + jax.lax.stop_gradient(weight_quant(w) - w)
            return jnp.einsum('bsd,hd->bsh', xq, wq)

        def depthwise_conv1d(x_bcl, w, b):
            y = jax.lax.conv_general_dilated(x_bcl, w, window_strides=(1,), padding=[(1, 1)], dimension_numbers=('NCH', 'OIH', 'NCH'), feature_group_count=x_bcl.shape[1])
            return y + b[None, :, None]
        h = bit_linear(x, w1)
        h = depthwise_conv1d(h.transpose(0, 2, 1), conv_w, conv_b)
        h = h.transpose(0, 2, 1)
        h = jax.nn.silu(h)
        return bit_linear(h, w2)

    def _L2_xattn_ref(q, k, v, mask, kernel_q, kernel_k, kernel_v, bias_q, bias_k, bias_v):
        import jax, jax.numpy as jnp
        import numpy as np
        B, S, D_IN, D_MODEL = (4, 512, 256, 256)
        Wq, Wk, Wv = (kernel_q[0, 0], kernel_k[0, 0], kernel_v[0, 0])
        qp = jax.nn.relu(jnp.einsum('bsd,de->bse', q, Wq) + bias_q)
        kp = jax.nn.relu(jnp.einsum('bsd,de->bse', k, Wk) + bias_k)
        vp = jax.nn.relu(jnp.einsum('bsd,de->bse', v, Wv) + bias_v)
        scores = jax.nn.relu(jnp.einsum('bqe,bke->bqk', qp, kp))
        dk = jnp.asarray(kp.shape[-1], dtype=scores.dtype)
        logits = scores / jnp.sqrt(dk) + mask
        out = jax.nn.relu(jnp.einsum('bqk,bke->bqe', logits, vp))
        return out

    def _L2_attn_ref(x, Wq, Wk, Wv, Wfc, bfc, gamma, beta):
        import jax, jax.numpy as jnp
        import numpy as np
        DIM_Q = 256
        DIM_K = 256
        DIM_V = 256
        OUT_DIM = 256
        B, N = (4, 512)

        def _layer_norm(h, gamma, beta, eps=1e-05):
            mu = jnp.mean(h, axis=-1, keepdims=True)
            var = jnp.mean(jnp.square(h - mu), axis=-1, keepdims=True)
            return (h - mu) * jax.lax.rsqrt(var + eps) * gamma + beta
        q = jnp.einsum('bnd,dk->bnk', x, Wq)
        k = jnp.einsum('bnd,dk->bnk', x, Wk)
        v = jnp.einsum('bnd,dv->bnv', x, Wv)
        scale = 1.0 / np.sqrt(DIM_K)
        scores = jnp.einsum('bnk,bmk->bnm', q, k) * scale
        n = x.shape[1]
        causal = jnp.tril(jnp.ones((n, n), dtype=bool))
        scores = jnp.where(causal, scores, -jnp.inf)
        att = jax.nn.softmax(scores, axis=-1)
        out = jnp.einsum('bnm,bmv->bnv', att, v)
        out = _layer_norm(out + v, gamma, beta)
        return jnp.einsum('bnv,vo->bno', out, Wfc) + bfc

    def _L2_ffn_ref(hidden_states, wg_red, wg, w1, b1, w2, b2):
        import jax, jax.numpy as jnp
        import numpy as np
        NUM_EXPERTS = 8
        IN_FEATURES = 256
        HIDDEN_FEATURES = 1024
        GATE_DIM = 16
        EPS = 0.0001
        b, t, c = hidden_states.shape
        x = hidden_states.reshape(-1, c)
        xr = x @ wg_red.T
        wg_unit = wg / jnp.maximum(jnp.linalg.norm(wg, axis=1, keepdims=True), EPS)
        logits = xr @ wg_unit.T
        gates = jax.nn.softmax(logits, axis=1)
        indices_s = jnp.argmax(gates, axis=1)
        scores = jnp.max(gates, axis=1)
        E = wg.shape[0]
        out = jnp.zeros_like(x)
        for e in range(E):
            mask = (indices_s == e).astype(x.dtype)[:, None]
            h = jax.nn.gelu(x @ w1[e] + b1[e], approximate=False)
            out = out + mask * (h @ w2[e] + b2[e])
        out = out * scores[:, None]
        return out.reshape(b, t, c)

    def _L3_xattn_ref(v, k, q):
        import jax, jax.numpy as jnp
        import numpy as np
        NUM_HEADS = 16

        def _split_heads(x, h):
            b, s, d = x.shape
            return x.reshape(b, s, h, d // h).transpose(0, 2, 1, 3)
        b = q.shape[0]
        qh = _split_heads(q, NUM_HEADS)
        kh = _split_heads(k, NUM_HEADS)
        vh = _split_heads(v, NUM_HEADS)
        scores = jnp.einsum('bhqd,bhkd->bhqk', qh, kh)
        av = jnp.einsum('bhqk,bhkd->bhqd', jax.nn.silu(scores), vh)
        return av.transpose(0, 2, 1, 3).reshape(b, av.shape[2], -1)

    def _L3_attn_ref(x, cpe1_w, cpe1_b, norm1_g, norm1_b, in_w, in_b, actp_w, actp_b, dwc_w, dwc_b, qk_w, qk_b, lepe_w, lepe_b, out_w, out_b, cpe2_w, cpe2_b, norm2_g, norm2_b, fc1_w, fc1_b, fc2_w, fc2_b):
        import jax, jax.numpy as jnp
        import numpy as np
        B, L, C, H = (8, 512, 256, 16)
        HID = 4 * C

        def _rope(x):
            b, n, c = x.shape
            k_max = c // 2
            theta = 1.0 / 10000.0 ** (jnp.arange(k_max, dtype=jnp.float32) / k_max)
            cos_t, sin_t = (jnp.cos(theta), jnp.sin(theta))
            xr = x.reshape(b, n, k_max, 2)
            re = xr[..., 0] * cos_t - xr[..., 1] * sin_t
            im = xr[..., 0] * sin_t + xr[..., 1] * cos_t
            return jnp.stack((re, im), axis=-1).reshape(b, n, c)

        def _dwconv(x_bcl, w, bias):
            y = jax.lax.conv_general_dilated(x_bcl, w, (1,), [(1, 1)], dimension_numbers=('NCH', 'OIH', 'NCH'), feature_group_count=x_bcl.shape[1])
            return y + bias[None, :, None]

        def _ln(x, g, b, eps=1e-05):
            mu = x.mean(-1, keepdims=True)
            var = ((x - mu) ** 2).mean(-1, keepdims=True)
            return (x - mu) * jax.lax.rsqrt(var + eps) * g + b

        def _mlla_forward(x, cpe1_w, cpe1_b, norm1_g, norm1_b, in_w, in_b, actp_w, actp_b, dwc_w, dwc_b, qk_w, qk_b, lepe_w, lepe_b, out_w, out_b, cpe2_w, cpe2_b, norm2_g, norm2_b, fc1_w, fc1_b, fc2_w, fc2_b):
            b, n, c = x.shape
            h, d = (H, c // H)
            x = x + _dwconv(x.transpose(0, 2, 1), cpe1_w, cpe1_b).transpose(0, 2, 1)
            shortcut = x
            xn = _ln(x, norm1_g, norm1_b)
            act_res = jax.nn.silu(xn @ actp_w + actp_b)
            xi = xn @ in_w + in_b
            xi = jax.nn.silu(_dwconv(xi.transpose(0, 2, 1), dwc_w, dwc_b)).transpose(0, 2, 1)
            qk = xi @ qk_w + qk_b
            q = jax.nn.elu(qk[..., :c]) + 1.0
            k = jax.nn.elu(qk[..., c:]) + 1.0
            q_rope = _rope(q).reshape(b, n, h, d).transpose(0, 2, 1, 3)
            k_rope = _rope(k).reshape(b, n, h, d).transpose(0, 2, 1, 3)
            qh = q.reshape(b, n, h, d).transpose(0, 2, 1, 3)
            kh = k.reshape(b, n, h, d).transpose(0, 2, 1, 3)
            vh = xi.reshape(b, n, h, d).transpose(0, 2, 1, 3)
            k_mean = kh.mean(axis=2, keepdims=True)
            z = 1.0 / (jnp.einsum('bhnd,bhmd->bhnm', qh, k_mean) + 1e-06)
            kv = jnp.einsum('bhnd,bhne->bhde', k_rope, vh) * (1.0 / n)
            attn = jnp.einsum('bhnd,bhde->bhne', q_rope, kv) * z
            attn = attn.transpose(0, 2, 1, 3).reshape(b, n, c)
            v_bcl = vh.transpose(0, 2, 1, 3).reshape(b, n, c).transpose(0, 2, 1)
            attn = attn + _dwconv(v_bcl, lepe_w, lepe_b).transpose(0, 2, 1)
            x = shortcut + attn * act_res @ out_w + out_b
            x = x + _dwconv(x.transpose(0, 2, 1), cpe2_w, cpe2_b).transpose(0, 2, 1)
            xn2 = _ln(x, norm2_g, norm2_b)
            mlp = jax.nn.gelu(xn2 @ fc1_w + fc1_b, approximate=False) @ fc2_w + fc2_b
            return x + mlp
        return _mlla_forward(x, cpe1_w, cpe1_b, norm1_g, norm1_b, in_w, in_b, actp_w, actp_b, dwc_w, dwc_b, qk_w, qk_b, lepe_w, lepe_b, out_w, out_b, cpe2_w, cpe2_b, norm2_g, norm2_b, fc1_w, fc1_b, fc2_w, fc2_b)

    def _L3_ffn_ref(x, router_w, w1, w2):
        import jax, jax.numpy as jnp
        import numpy as np
        HID, FFN, E, K = (256, 1024, 8, 2)
        CAP_FACTOR = 1.25
        B, T, H = x.shape
        N = B * T
        x_flat = x.reshape(N, H)
        C = max(1, int(CAP_FACTOR * N / E * K))
        logits = x_flat @ router_w.T
        probs = jax.nn.softmax(logits, axis=-1)
        top_v, top_i = jax.lax.top_k(probs, K)
        top_v = top_v / jnp.sum(top_v, axis=-1, keepdims=True)
        out = jnp.zeros_like(x_flat)
        for k in range(K):
            eid = top_i[:, k]
            gate = top_v[:, k]
            onehot = jax.nn.one_hot(eid, E, dtype=jnp.int32)
            pos = jnp.take_along_axis(jnp.cumsum(onehot, axis=0), eid[:, None], axis=1)[:, 0] - 1
            keep = pos < C
            slot = jnp.where(keep, eid * C + pos, E * C)
            buf = jnp.zeros((E * C + 1, H), dtype=x.dtype).at[slot].add(x_flat * keep[:, None].astype(x.dtype))
            expert_in = buf[:E * C].reshape(E, C, H)
            h = jax.nn.gelu(jnp.einsum('ech,ehf->ecf', expert_in, w1), approximate=False)
            y = jnp.einsum('ecf,efh->ech', h, w2)
            tok = y.reshape(E * C, H)[jnp.minimum(slot, E * C - 1)]
            out = out + tok * (gate * keep.astype(x.dtype))[:, None]
        return out.reshape(B, T, H)
    x = x + _L0_xattn_ref(_layernorm(x, axis=-1), ctx_1024, ctx_1024, mask_BxSxS2_bk1)
    x = x + _L0_attn_ref(_layernorm(x, axis=-1), L0_attn_wq, L0_attn_bq, L0_attn_wqc, L0_attn_bqc, L0_attn_wqr, L0_attn_bqr, L0_attn_wkv, L0_attn_bkv, L0_attn_wkr, L0_attn_bkr, L0_attn_wkc, L0_attn_bkc, L0_attn_wv, L0_attn_bv, L0_attn_wo, L0_attn_bo)
    x = x + _L0_ffn_ref(_layernorm(x, axis=-1), L0_ffn_Wg, L0_ffn_W1, L0_ffn_W2, L0_ffn_W3)
    x = x + _L1_xattn_ref(_layernorm(x, axis=-1), ctx_1024, L1_xattn_Wq, L1_xattn_Wk, L1_xattn_Wv, L1_xattn_Wo, L1_xattn_bo)
    x = x + _L1_attn_ref(_layernorm(x, axis=-1), L1_attn_w_qkv, L1_attn_b_qkv, L1_attn_w_out, L1_attn_b_out)
    x = x + _L1_ffn_ref(_layernorm(x, axis=-1), L1_ffn_w1, L1_ffn_conv_w, L1_ffn_conv_b, L1_ffn_w2)
    x = x + _L2_xattn_ref(_layernorm(x, axis=-1), ctx_1024, ctx_1024, mask_1xSxS2_ff0, L2_xattn_kernel_q, L2_xattn_kernel_k, L2_xattn_kernel_v, L2_xattn_bias_q, L2_xattn_bias_k, L2_xattn_bias_v)
    x = x + _L2_attn_ref(_layernorm(x, axis=-1), L2_attn_Wq, L2_attn_Wk, L2_attn_Wv, L2_attn_Wfc, L2_attn_bfc, L2_attn_gamma, L2_attn_beta)
    x = x + _L2_ffn_ref(_layernorm(x, axis=-1), L2_ffn_wg_red, L2_ffn_wg, L2_ffn_w1, L2_ffn_b1, L2_ffn_w2, L2_ffn_b2)
    x = x + _L3_xattn_ref(ctx_1024, ctx_1024, _layernorm(x, axis=-1))
    x = x + _L3_attn_ref(_layernorm(x, axis=-1), L3_attn_cpe1_w, L3_attn_cpe1_b, L3_attn_norm1_g, L3_attn_norm1_b, L3_attn_in_w, L3_attn_in_b, L3_attn_actp_w, L3_attn_actp_b, L3_attn_dwc_w, L3_attn_dwc_b, L3_attn_qk_w, L3_attn_qk_b, L3_attn_lepe_w, L3_attn_lepe_b, L3_attn_out_w, L3_attn_out_b, L3_attn_cpe2_w, L3_attn_cpe2_b, L3_attn_norm2_g, L3_attn_norm2_b, L3_attn_fc1_w, L3_attn_fc1_b, L3_attn_fc2_w, L3_attn_fc2_b)
    x = x + _L3_ffn_ref(_layernorm(x, axis=-1), L3_ffn_router_w, L3_ffn_w1, L3_ffn_w2)
    return x

_drawn_inputs = setup_inputs


def setup_inputs(seed=0):
    import zlib

    import numpy as np

    out = dict(_drawn_inputs(seed))
    spreads = {'L2_attn_gamma': (1.0, 0.6),
     'L2_attn_beta': (0.0, 0.8),
     'L3_attn_cpe1_b': (0.0, 0.8),
     'L3_attn_norm1_g': (1.0, 0.6),
     'L3_attn_norm1_b': (0.0, 0.8),
     'L3_attn_in_b': (0.0, 0.8),
     'L3_attn_actp_b': (0.0, 0.8),
     'L3_attn_dwc_b': (0.0, 0.8),
     'L3_attn_qk_b': (0.0, 0.1),
     'L3_attn_lepe_b': (0.0, 0.8),
     'L3_attn_out_b': (0.0, 0.8),
     'L3_attn_cpe2_b': (0.0, 0.8),
     'L3_attn_norm2_g': (1.0, 0.6),
     'L3_attn_norm2_b': (0.0, 0.8),
     'L3_attn_fc1_b': (0.0, 0.8),
     'L3_attn_fc2_b': (0.0, 0.8)}
    factors = {'L0_attn_wq': 8.0,
     'L0_attn_bq': 8.0,
     'L0_attn_wqc': 8.0,
     'L0_attn_bqc': 8.0,
     'L0_attn_wqr': 8.0,
     'L0_attn_bqr': 8.0,
     'L0_attn_wkv': 8.0,
     'L0_attn_bkv': 8.0,
     'L0_attn_wkr': 8.0,
     'L0_attn_bkr': 8.0,
     'L0_attn_wkc': 8.0,
     'L0_attn_bkc': 8.0,
     'L0_attn_wv': 8.0,
     'L0_attn_bv': 8.0,
     'L0_attn_wo': 8.0,
     'L0_attn_bo': 8.0,
     'L1_xattn_Wq': 4.703,
     'L1_xattn_Wk': 4.382,
     'L1_xattn_bo': 8.0,
     'L1_attn_w_qkv': 8.0,
     'L1_attn_b_qkv': 8.0,
     'L1_attn_w_out': 8.0,
     'L1_attn_b_out': 8.0,
     'L1_ffn_w1': 8.0,
     'L1_ffn_conv_w': 8.0,
     'L1_ffn_conv_b': 8.0,
     'L1_ffn_w2': 8.0,
     'L2_xattn_bias_q': 8.0,
     'L2_xattn_bias_k': 8.0,
     'L2_attn_Wq': 8.0,
     'L2_attn_Wk': 8.0,
     'L2_attn_Wv': 8.0,
     'L2_attn_Wfc': 8.0,
     'L2_attn_bfc': 8.0,
     'L2_ffn_wg_red': 4.705,
     'L2_ffn_wg': 5.973,
     'L2_ffn_w1': 8.0,
     'L2_ffn_b1': 8.0,
     'L2_ffn_w2': 8.0,
     'L2_ffn_b2': 8.0,
     'L3_attn_cpe1_w': 8.0,
     'L3_attn_in_w': 8.0,
     'L3_attn_actp_w': 8.0,
     'L3_attn_dwc_w': 8.0,
     'L3_attn_lepe_w': 8.0,
     'L3_attn_out_w': 8.0,
     'L3_attn_cpe2_w': 8.0,
     'L3_attn_fc1_w': 8.0,
     'L3_attn_fc2_w': 8.0,
     'L3_ffn_router_w': 8.0,
     'L3_ffn_w1': 8.0,
     'L3_ffn_w2': 8.0}
    for name, (base, spread) in spreads.items():
        noise = np.random.default_rng([zlib.crc32(name.encode()), seed]).standard_normal(out[name].shape)
        drawn = base * np.exp(spread * noise) if base else spread * noise
        out[name] = jnp.asarray(drawn.astype(out[name].dtype))
    for name, factor in factors.items():
        out[name] = (out[name] * factor).astype(out[name].dtype)
    return out
```

```python
from contextlib import ExitStack

import numpy as np

import concourse.bass as bass
from concourse import mybir

F32 = mybir.dt.float32
U32 = mybir.dt.uint32
U8 = mybir.dt.uint8
BF16 = mybir.dt.bfloat16
ALU = mybir.AluOpType
ACT = mybir.ActivationFunctionType
AX = mybir.AxisListType

P = 128
B, S, D = 16, 64, 256
M = 1601
TOK = B * S
NT = TOK // P
DC = D // P
KT = (M + P - 1) // P
KFULL = M // P
KREST = M - KFULL * P
BANK = 512
NHALF = TOK // BANK
H16 = 16
HD = D // H16
E8 = 8
PAIRS = H16 // 2
PAIR_F = 2 * HD
NEG = -1.0e30
START = 64

CHUNKS = [(c, min(BANK, M - c)) for c in range(0, M, BANK)]
NCH = len(CHUNKS)
ZERO_PARTS = 3


def key_rows(t):
    return P if t < KFULL else KREST


COLS = [
    ("L0_bq", 1), ("L0_bkv", 1), ("L0_bqc", 1), ("L0_bkc", 1), ("L0_bqr", 1), ("L0_bkr", 1),
    ("L0_bqr_sw", 1), ("L0_bkr_sw", 1), ("L1a_bqk", 4), ("L1f_cw", 24), ("L1f_cb", 8),
    ("L2x_bq", 2), ("L2x_bk", 2), ("L2a_gamma", 2), ("L2a_beta", 2),
    ("L3_cpe1_w", 6), ("L3_cpe1_b", 2), ("L3_n1g", 2), ("L3_n1b", 2), ("L3_in_b", 2), ("L3_actp_b", 2),
    ("L3_dwc_w", 6), ("L3_dwc_b", 2), ("L3_qk_b", 4), ("L3_lepe_w", 6), ("L3_lepe_b", 2),
    ("L3_out_b", 2), ("L3_cpe2_w", 6), ("L3_cpe2_b", 2), ("L3_n2g", 2), ("L3_n2b", 2), ("L3_fc1_b", 8),
]
ROWS = ["L0_bv", "L0_bo", "L1x_bo", "L1a_bv", "L1a_bo", "L2x_bv", "L2a_bfc", "L3_fc2_b"]
COL_AT, _n = {}, 0
for _name, _w in COLS:
    COL_AT[_name] = (_n, _w)
    _n += _w
NCOLS = _n


class Signal:

    def __init__(self, nc, ctx, name, credit=0):
        self.sem = ctx.enter_context(nc.semaphore(name))
        self.credit = credit

    def at(self, count):
        return count + self.credit


class Kit:
    pass


def give_credits(nc, signals):
    with nc.Block() as block:

        @block.sync
        def _(sp):
            for s in signals:
                if s.credit:
                    sp.sem_inc(s.sem, s.credit)


class Job:

    def __init__(self, groups, by, drain):
        self.groups, self.by, self.drain = groups, by, drain


def matmul_pass(nc, k, jobs, loaded=()):
    base_f, base_a, base_v = k.n_filled, k.n_act, k.n_dve
    nth = []
    na = nv = 0
    for job in jobs:
        if job.by == "act":
            na += 1
            nth.append((k.act_drained, base_a + na))
        else:
            nv += 1
            nth.append((k.dve_drained, base_v + nv))
    with nc.Block() as block:

        @block.tensor
        def _(pe):
            for sem, value in loaded:
                pe.wait_ge(sem, value)
            for j, job in enumerate(jobs):
                bank = k.ps[:, j % 8, :]
                if j >= 8:
                    pe.wait_ge(*nth[j - 8])
                for where, products in job.groups:
                    out = where(bank)
                    for n, (lhsT, rhs) in enumerate(products):
                        if rhs is None:
                            rows = lhsT.shape[0]
                            last = pe.transpose(out, lhsT, k.ident[0:rows, 0:rows])
                        else:
                            last = pe.matmul(out, lhsT, rhs, start=(n == 0), stop=(n == len(products) - 1))
                last.then_inc(k.filled, 1)

        @block.scalar
        def _(act):
            for j, job in enumerate(jobs):
                if job.by == "act":
                    act.wait_ge(k.filled, base_f + j + 1)
                    job.drain(act, k.ps[:, j % 8, :]).then_inc(k.act_drained, 1)

        @block.vector
        def _(dve):
            for j, job in enumerate(jobs):
                if job.by == "dve":
                    dve.wait_ge(k.filled, base_f + j + 1)
                    job.drain(dve, k.ps[:, j % 8, :]).then_inc(k.dve_drained, 1)

    k.n_filled += len(jobs)
    k.n_act += na
    k.n_dve += nv


def full(bank):
    return bank


def load_block(nc, k, copies):
    with nc.Block() as block:

        @block.sync
        def _(sp):
            for dst, src in copies:
                sp.dma_start(dst, src).then_inc(k.weights, 16)

    k.n_weights += 16 * len(copies)
    return (k.weights, k.n_weights)


def wk(w):
    return w.rearrange("(c p) n -> p c n", p=P)


def layer_norm(nc, k, src, out, eps):
    with nc.Block() as block:
        base = k.n_ln

        @block.vector
        def _(dve):
            for t in range(NT):
                dve.bn_stats(k.stats[:, t, :], src[:, t, :]).then_inc(k.ln_step, 1)
            for t in range(NT):
                dve.wait_ge(k.ln_step, base + t + 1)
                dve.bn_aggr(k.mv[:, t, :], k.stats[:, t, :]).then_inc(k.ln_step, 1)
            dve.wait_ge(k.ln_step, base + 2 * NT)
            dve.tensor_scalar(k.rstd[:, 0, :], k.mv[:, :, 1], eps, None, ALU.add).then_inc(k.ln_step, 1)
            dve.wait_ge(k.ln_root, k.n_root + 1)
            dve.reciprocal(k.rstd[:, 2, :], k.rstd[:, 1, :]).then_inc(k.ln_step, 1)
            dve.wait_ge(k.ln_step, base + 2 * NT + 2)
            for t in range(NT):
                dve.tensor_scalar(out[:, t, :], src[:, t, :], k.mv[:, t, 0:1], k.rstd[:, 2, t:t + 1],
                                  ALU.subtract, ALU.mult).then_inc(k.ln_step, 1)

        @block.scalar
        def _(act):
            act.wait_ge(k.ln_step, base + 2 * NT + 1)
            act.activation(k.rstd[:, 1, :], k.rstd[:, 0, :], ACT.Sqrt).then_inc(k.ln_root, 1)

    k.n_ln += 3 * NT + 2
    k.n_root += 1


def to_features(nc, k, src, dst, chunks=DC, scale=None, bias=None):
    jobs = []
    for c in range(chunks):
        for n in range(NHALF):
            groups = [(lambda bank, t=t: bank[:, t * P:(t + 1) * P],
                       [(src[:, n * 4 + t, c * P:(c + 1) * P], None)]) for t in range(4)]
            out = dst[:, c, n * BANK:(n + 1) * BANK]
            if scale is not None:
                jobs.append(Job(groups, "dve", lambda e, bank, out=out, c=c: e.tensor_scalar(
                    out, bank, scale[:, c:c + 1], bias[:, c:c + 1], ALU.mult, ALU.add)))
            elif (c + n) % 2:
                jobs.append(Job(groups, "dve", lambda e, bank, out=out: e.tensor_copy(out, bank)))
            else:
                jobs.append(Job(groups, "act", lambda e, bank, out=out: e.activation(out, bank, ACT.Copy)))
    matmul_pass(nc, k, jobs)


def add_transposed(nc, k, srcT, dst, add=True):
    jobs = []
    for t in range(NT):
        groups = [(lambda bank, c=c: bank[:, c * P:(c + 1) * P], [(srcT[:, c, t * P:(t + 1) * P], None)])
                  for c in range(DC)]
        if add:
            jobs.append(Job(groups, "dve", lambda e, bank, t=t: e.tensor_tensor(
                dst[:, t, :], dst[:, t, :], bank[:, 0:D], ALU.add)))
        else:
            jobs.append(Job(groups, "act", lambda e, bank, t=t: e.activation(
                dst[:, t, :], bank[:, 0:D], ACT.Copy)))
    matmul_pass(nc, k, jobs)


def linear_jobs(wt, xT, kchunks, width, drain, by="act", krows=P):
    jobs = []
    for m0 in range(0, width, P):
        mw = min(P, width - m0)
        for n in range(NHALF):
            products = [(wt[0:krows, c, m0:m0 + mw], xT[0:krows, c, n * BANK:(n + 1) * BANK])
                        for c in range(kchunks)]
            jobs.append(Job([(lambda bank, mw=mw: bank[0:mw, :], products)], by,
                            lambda e, bank, m=m0 // P, n=n, mw=mw: drain(e, bank[0:mw, :], m, n)))
    return jobs


def residual_linear(nc, k, xT, w, kchunks, bias_row, dst, loaded=(), add=True):
    jobs = []
    for t in range(NT):
        products = [(xT[:, c, t * P:(t + 1) * P], w[:, c, :]) for c in range(kchunks)]
        if bias_row is not None:
            products.append((k.ones_row[0:1, :], k.row(bias_row)))
        if add:
            jobs.append(Job([(lambda bank: bank[:, 0:D], products)], "dve", lambda e, bank, t=t: e.tensor_tensor(
                dst[:, t, :], dst[:, t, :], bank[:, 0:D], ALU.add)))
        else:
            jobs.append(Job([(lambda bank: bank[:, 0:D], products)], "act", lambda e, bank, t=t: e.activation(
                dst[:, t, :], bank[:, 0:D], ACT.Copy)))
    matmul_pass(nc, k, jobs, loaded)


def softmax_cross_attention(nc, k, name, ins, heads16, q_all):
    TPB = PAIRS if heads16 else 4
    U = 2 * TPB
    with ExitStack() as ctx:
        def sb(n, shape, dt=F32):
            return ctx.enter_context(nc.sbuf_tensor(f"{name}_{n}", shape, dt))

        def signal(n, credit=0):
            return Signal(nc, ctx, f"{name}_{n}", credit)

        rows_sb = sb("rows", [P, 2, KT, D])
        keysT = sb("keysT", [P, 2, DC, M])
        prob = sb("prob", [P, 2, M])
        probT = sb("probT", [P, 2, KT * P])
        mx = sb("mx", [P, 2, NCH])
        nmx = sb("nmx", [P, 2, 1])
        sums = sb("sums", [P, U])
        rinv = sb("rinv", [P, U])
        if heads16:
            mask8 = sb("mask8", [P, 2, M], U8)
            maskf = sb("maskf", [P, 2, M])
            q_sb = sb("q", [P, 2, H16, S])
            att = sb("att", [P, D])
        else:
            q_sb = sb("q", [P, 2, DC, BANK])

        loaded = [signal(f"loaded{j}") for j in range(2)]
        mask_ready = signal("mask_ready", 2)
        q_ready = signal("q_ready")
        s_filled = signal("s_filled")
        s_taken = signal("s_taken", (U + 1) * NCH)
        max_ready = signal("max_ready")
        exp_done = signal("exp_done", 1)
        t_filled = signal("t_filled", 8)
        t_act = signal("t_act", 1)
        t_dve = signal("t_dve", 1)
        av_done = signal("av_done", U + 2)
        r_ready = signal("r_ready")
        o_drained = signal("o_drained", 2)
        x_step = signal("x_step", 1)
        give_credits(nc, [mask_ready, s_taken, exp_done, t_filled, t_act, t_dve, av_done, o_drained, x_step])
        S_BANK, T_BANK, O_BANK = 0, 4, 6
        n_loads = 5 if heads16 else 3
        sflat = k.ps[:, S_BANK:S_BANK + NCH, :].rearrange("p a b -> p (a b)")

        with nc.Block() as block:

            @block.sync
            def _(sp):
                with sp.Fori(0, B // 2) as i:
                    for j in range(2):
                        b = i * 2 + j
                        sp.wait_ge(av_done.sem, i * U + av_done.at(-U + (j + 1) * TPB))
                        sp.dma_start(keysT[:, j, :, :], ins["ctxT"][b].rearrange("c p n -> p c n")
                                     ).then_inc(loaded[j].sem, 16)
                        sp.dma_start(rows_sb[:, j, 0:KFULL, :],
                                     ins["ctx"][b, 0:KFULL * P, :].rearrange("(t p) d -> p t d", p=P)
                                     ).then_inc(loaded[j].sem, 16)
                        sp.dma_start(rows_sb[0:KREST, j, KFULL, :], ins["ctx"][b, KFULL * P:M, :]
                                     ).then_inc(loaded[j].sem, 16)
                        if heads16:
                            sp.wait_ge(mask_ready.sem, i * 2 + mask_ready.at(j - 1))
                            sp.sem_inc(k.tick, 1)
                            for h in range(2):
                                sp.dma_start(mask8[h * S:(h + 1) * S, j, :], ins["mask"][b]
                                             ).then_inc(loaded[j].sem, 16)

            @block.gpsimd
            def _(pool):
                with pool.Fori(0, B // 2) as i:
                    for j in range(2):
                        if heads16:
                            pool.wait_ge(loaded[j].sem, i * 16 * n_loads + 16 * n_loads)
                            pool.wait_ge(s_taken.sem, i * (U * NCH) + s_taken.at(((j + 1) * TPB - U) * NCH))
                            pool.sem_inc(k.tick, 1)
                            pool.tensor_scalar(maskf[:, j, :], mask8[:, j, :], -10000.0, None, ALU.mult
                                               ).then_inc(mask_ready.sem, 1)
                        else:
                            pool.wait_ge(av_done.sem, i * U + av_done.at(-U + (j + 1) * TPB))
                            pool.tensor_copy(q_sb[:, j, :, :], q_all[:, i * 2 + j, :, :]).then_inc(q_ready.sem, 1)

            @block.tensor
            def _(pe):
                with pe.Fori(0, B // 2) as i:
                    def scores(u):
                        j, t = u // TPB, u % TPB
                        if t == 0:
                            pe.wait_ge(loaded[j].sem, i * 16 * n_loads + 16 * n_loads)
                            pe.wait_ge(q_ready.sem, i * 2 + (j + 1))
                        for c, (at, w) in enumerate(CHUNKS):
                            if heads16:
                                pe.wait_ge(s_taken.sem, i * (U * NCH) + s_taken.at(NCH * (u - 1) + c + 1))
                                last = pe.matmul(k.ps[:, S_BANK + c, 0:w], q_sb[:, j, 2 * t:2 * t + 2, :],
                                                 keysT[:, j, t // 4, at:at + w], start=True, stop=True)
                            else:
                                if c == 0:
                                    pe.wait_ge(exp_done.sem, i * U + exp_done.at(u))
                                for f in range(DC):
                                    last = pe.matmul(k.ps[:, S_BANK + c, 0:w], q_sb[:, j, f, t * P:(t + 1) * P],
                                                     keysT[:, j, f, at:at + w], start=(f == 0), stop=(f == DC - 1))
                            last.then_inc(s_filled.sem, 1)

                    def transposes(u, groups):
                        if groups[0] == 0:
                            pe.wait_ge(exp_done.sem, i * U + exp_done.at(u + 1))
                        for g in groups:
                            free = (t_act, t_dve)[g % 2]
                            pe.wait_ge(free.sem, i * (2 * U) + free.at(2 * u + g // 2))
                            for kt in range(4 * g, min(4 * g + 4, KT)):
                                rows = key_rows(kt)
                                last = pe.transpose(k.ps[0:rows, T_BANK + g % 2, (kt % 4) * P:(kt % 4 + 1) * P],
                                                    prob[:, u % 2, kt * P:kt * P + rows], k.ident[:])
                            last.then_inc(t_filled.sem, 1)

                    def values(u, kts):
                        j, t = u // TPB, u % TPB
                        if kts[0] == 0:
                            pe.wait_ge(t_act.sem, i * (2 * U) + t_act.at(2 * u + 2))
                            pe.wait_ge(t_dve.sem, i * (2 * U) + t_dve.at(2 * u + 2))
                            if not heads16:
                                pe.wait_ge(o_drained.sem, i * U + o_drained.at(u - 1))
                            elif t == 0:
                                pe.wait_ge(o_drained.sem, i * 2 + o_drained.at(j - 1))
                        for kt in kts:
                            rows = key_rows(kt)
                            if heads16:
                                out = k.ps[:, O_BANK + j, t * PAIR_F:(t + 1) * PAIR_F]
                                rhs = rows_sb[0:rows, j, kt, t * PAIR_F:(t + 1) * PAIR_F]
                            else:
                                out = k.ps[:, O_BANK + u % 2, 0:D]
                                rhs = rows_sb[0:rows, j, kt, :]
                            last = pe.matmul(out, probT[0:rows, u % 2, kt * P:(kt + 1) * P], rhs,
                                             start=(kt == 0), stop=(kt == KT - 1))
                        if kts[-1] == KT - 1:
                            last.then_inc(av_done.sem, 1)

                    scores(0)
                    for u in range(U):
                        if u + 1 < U:
                            scores(u + 1)
                        transposes(u, (0, 1))
                        if u > 0:
                            values(u - 1, range(0, KT // 2))
                        transposes(u, (2, 3))
                        if u > 0:
                            values(u - 1, range(KT // 2, KT))
                    values(U - 1, range(KT))

            def take_transposes(eng, i, u, free, groups, copy):
                eng.wait_ge(av_done.sem, i * U + av_done.at(u - 1))
                for g in groups:
                    eng.wait_ge(t_filled.sem, i * (4 * U) + t_filled.at(4 * u + g + 1))
                    n = min(4, KT - 4 * g)
                    rows = key_rows(4 * g)
                    copy(probT[0:rows, u % 2, 4 * g * P:(4 * g + n) * P],
                         k.ps[0:rows, T_BANK + g % 2, 0:n * P]).then_inc(free.sem, 1)

            @block.scalar
            def _(act):
                with act.Fori(0, B // 2) as i:
                    def exps(u):
                        act.wait_ge(max_ready.sem, i * U + (u + 1))
                        act.wait_ge(t_filled.sem, i * (4 * U) + t_filled.at(4 * (u - 1)))
                        src = prob[:, u % 2, :] if heads16 else sflat[:, 0:M]
                        act.activation(prob[:, u % 2, :], src, ACT.Exp, bias=nmx[:, u % 2, :],
                                       accum_out=sums[:, u:u + 1]).then_inc(exp_done.sem, 1)

                    def weighted_rows(u):
                        act.wait_ge(av_done.sem, i * U + av_done.at(u + 1))
                        act.wait_ge(r_ready.sem, i * U + (u + 1))
                        act.activation(q_all.rearrange("p b f n -> p b (f n)")[
                                           :, i * 2 + u // TPB, (u % TPB) * D:(u % TPB + 1) * D],
                                       k.ps[:, O_BANK + u % 2, 0:D], ACT.Copy, scale=rinv[:, u:u + 1]
                                       ).then_inc(o_drained.sem, 1)

                    exps(0)
                    for u in range(U):
                        take_transposes(act, i, u, t_act, (0, 2),
                                        lambda o, s: act.activation(o, s, ACT.Copy))
                        if u + 1 < U:
                            exps(u + 1)
                        if not heads16 and u > 0:
                            weighted_rows(u - 1)
                    if not heads16:
                        weighted_rows(U - 1)

            @block.vector
            def _(dve):
                with dve.Fori(0, B // 2) as i:
                    def maxima(u):
                        j, t = u // TPB, u % TPB
                        if heads16 and t == 0:
                            dve.wait_ge(mask_ready.sem, i * 2 + mask_ready.at(j + 1))
                        dve.wait_ge(t_filled.sem, i * (4 * U) + t_filled.at(4 * (u - 1)))
                        for c, (at, w) in enumerate(CHUNKS):
                            dve.wait_ge(s_filled.sem, i * (U * NCH) + (u * NCH + c + 1))
                            if heads16:
                                dve.sem_inc(k.tick, 1)
                                ins_ = dve.tensor_tensor_reduce(
                                    out=prob[:, u % 2, at:at + w], in0=k.ps[:, S_BANK + c, 0:w],
                                    in1=maskf[:, j, at:at + w], scale=1.0, scalar=-3.0e38, op0=ALU.add,
                                    op1=ALU.max, accum_out=mx[:, u % 2, c:c + 1])
                            else:
                                ins_ = dve.tensor_reduce(mx[:, u % 2, c:c + 1], k.ps[:, S_BANK + c, 0:w], AX.X, ALU.max)
                            ins_.then_inc(s_taken.sem, 1)
                        dve.wait_ge(s_taken.sem, i * (U * NCH) + s_taken.at((u + 1) * NCH))
                        dve.tensor_reduce(nmx[:, u % 2, :], mx[:, u % 2, :], AX.X, ALU.max, negate=True
                                          ).then_inc(max_ready.sem, 1)

                    if heads16:
                        for j in range(2):
                            block_queries(dve, k, q_sb[:, j, :, :], q_all, i * P + j * S, HD ** -0.5
                                          ).then_inc(q_ready.sem, 1)
                    def batch_out(j):
                        dve.wait_ge(exp_done.sem, i * U + exp_done.at((j + 1) * TPB))
                        dve.reciprocal(rinv[:, j * TPB:(j + 1) * TPB], sums[:, j * TPB:(j + 1) * TPB]
                                       ).then_inc(r_ready.sem, 1)
                        dve.wait_ge(r_ready.sem, i * 2 + (j + 1))
                        dve.wait_ge(av_done.sem, i * U + av_done.at((j + 1) * TPB))
                        if j == 0:
                            dve.wait_ge(x_step.sem, i * 3 + x_step.at(0))
                        a4 = att[j * S:(j + 1) * S, :].rearrange("p (t h f) -> p t h f", h=2, f=HD)
                        for h in range(2):
                            o3 = k.ps[h * S:(h + 1) * S, O_BANK + j, 0:TPB * PAIR_F].rearrange(
                                "p (t f) -> p t f", f=PAIR_F)[:, :, h * HD:(h + 1) * HD]
                            r3 = rinv[h * S:(h + 1) * S, j * TPB:(j + 1) * TPB].unsqueeze(2).broadcast_to((S, TPB, HD))
                            ins_ = dve.tensor_tensor(a4[:, :, h, :], o3, r3, ALU.mult)
                            if h == 0:
                                ins_.then_inc(x_step.sem, 1)
                            else:
                                ins_.then_inc(o_drained.sem, 1)

                    maxima(0)
                    for u in range(U):
                        j, t = u // TPB, u % TPB
                        if u + 1 < U:
                            maxima(u + 1)
                        if not heads16:
                            dve.wait_ge(exp_done.sem, i * U + exp_done.at(u + 1))
                            dve.wait_ge(o_drained.sem, i * U + o_drained.at(u - 1))
                            dve.reciprocal(rinv[:, u:u + 1], sums[:, u:u + 1]).then_inc(r_ready.sem, 1)
                        take_transposes(dve, i, u, t_dve, (1, 3), dve.tensor_copy)
                        if heads16 and u > 0 and t == 0:
                            batch_out(u // TPB - 1)
                    if heads16:
                        batch_out(1)
                    if heads16:
                        dve.wait_ge(x_step.sem, i * 3 + x_step.at(2))
                        dve.wait_ge(o_drained.sem, i * 2 + o_drained.at(2))
                        xt = k.x[:, i, :]
                        dve.tensor_tensor(xt, xt, att[:], ALU.add).then_inc(x_step.sem, 1)


def silu_cross_attention(nc, k, name, ins, attT):
    with ExitStack() as ctx:
        def sb(n, shape, dt=F32):
            return ctx.enter_context(nc.sbuf_tensor(f"{name}_{n}", shape, dt))

        def signal(n, credit=0):
            return Signal(nc, ctx, f"{name}_{n}", credit)

        RPB = (KT + 1) // 2
        NR = 2 * RPB
        rows_sb = sb("rows", [P, 2, KT, D])
        keysT = sb("keysT", [P, 2, DC, M])
        q_sb = sb("q", [P, 2, DC, 2, S])
        w_sb = sb("w", [P, 2, 2, DC, BANK])
        own = sb("own", [P, DC, H16 // DC, S])
        loaded = [signal(f"loaded{j}") for j in range(2)]
        q_ready = signal("q_ready")
        s_filled = signal("s_filled")
        s_taken = signal("s_taken")
        av_done = signal("av_done", NR)
        o_taken = signal("o_taken", 2)
        own_done = signal("own_done", 1)
        give_credits(nc, [av_done, o_taken, own_done])
        GROUPS = P // PAIR_F

        def tiles_of(r):
            t = 2 * (r % RPB)
            return list(range(t, min(t + 2, KT)))

        with nc.Block() as block:

            @block.sync
            def _(sp):
                with sp.Fori(0, B // 2) as i:
                    for j in range(2):
                        b = i * 2 + j
                        sp.wait_ge(av_done.sem, i * NR + av_done.at((j + 1) * RPB - NR))
                        sp.dma_start(keysT[:, j, :, :], ins["ctxT"][b].rearrange("c p n -> p c n")
                                     ).then_inc(loaded[j].sem, 16)
                        sp.dma_start(rows_sb[:, j, 0:KFULL, :],
                                     ins["ctx"][b, 0:KFULL * P, :].rearrange("(t p) d -> p t d", p=P)
                                     ).then_inc(loaded[j].sem, 16)
                        sp.dma_start(rows_sb[0:KREST, j, KFULL, :], ins["ctx"][b, KFULL * P:M, :]
                                     ).then_inc(loaded[j].sem, 16)

            taken_by = [sum(len(tiles_of(x)) for x in range(r)) for r in range(NR + 1)]
            NTK = taken_by[NR]

            @block.tensor
            def _(pe):
                with pe.Fori(0, B // 2) as i:
                    def scores(r):
                        j = r // RPB
                        if r % RPB == 0:
                            pe.wait_ge(loaded[j].sem, i * 48 + 48)
                            pe.wait_ge(q_ready.sem, i * 2 + (j + 1))
                        if r > 0:
                            pe.wait_ge(s_taken.sem, i * NTK + taken_by[r])
                        for x, t in enumerate(tiles_of(r)):
                            rows = key_rows(t)
                            for g in range(DC):
                                for group in range(GROUPS):
                                    a = PAIR_F * group
                                    last = pe.matmul(
                                        k.ps[0:rows, group, (2 * x + g) * P:(2 * x + g + 1) * P],
                                        keysT[a:a + PAIR_F, j, g, t * P:t * P + rows],
                                        q_sb[a:a + PAIR_F, j, g, :, :], start=True, stop=True)
                                    if t == tiles_of(r)[-1] and g == DC - 1:
                                        last.then_inc(s_filled.sem, 1)

                    def values(r):
                        j = r // RPB
                        pe.wait_ge(s_taken.sem, i * NTK + taken_by[r + 1])
                        if r % RPB == 0:
                            pe.wait_ge(o_taken.sem, i * 2 + o_taken.at(j - 1))
                        for x, t in enumerate(tiles_of(r)):
                            rows = key_rows(t)
                            for g in range(DC):
                                last = pe.matmul(k.ps[:, 4 + 2 * j + g, :], rows_sb[0:rows, j, t, g * P:(g + 1) * P],
                                                 w_sb[0:rows, r % 2, x, g, :], start=(t == 0), stop=(t == KT - 1))
                        last.then_inc(av_done.sem, 1)

                    scores(0)
                    for r in range(NR):
                        if r + 1 < NR:
                            scores(r + 1)
                        values(r)

            @block.scalar
            def _(act):
                with act.Fori(0, B // 2) as i:
                    for r in range(NR):
                        act.wait_ge(s_filled.sem, i * (4 * NR) + 4 * (r + 1))
                        act.wait_ge(av_done.sem, i * NR + av_done.at(r - 1))
                        for x, t in enumerate(tiles_of(r)):
                            rows = key_rows(t)
                            act.activation(w_sb[0:rows, r % 2, x, :, :].rearrange("p g (r n) -> p r g n", n=P),
                                           k.ps[0:rows, 0:4, x * D:(x + 1) * D].rearrange(
                                               "p r (g n) -> p r g n", n=P), ACT.Silu).then_inc(s_taken.sem, 1)

            @block.vector
            def _(dve):
                with dve.Fori(0, B // 2) as i:
                    for j in range(2):
                        dve.wait_ge(av_done.sem, i * NR + av_done.at((j + 1) * RPB - NR))
                        for h in range(2):
                            ins_ = dve.tensor_scalar(q_sb[:, j, :, h, :], k.xnT[:, :, bass.ds(i * P + j * S, S)],
                                                     k.parity[:, h:h + 1], None, ALU.mult)
                        ins_.then_inc(q_ready.sem, 1)
                    for j in range(2):
                        dve.wait_ge(av_done.sem, i * NR + av_done.at((j + 1) * RPB))
                        take_own_blocks(dve, k, k.ps[:, 4 + 2 * j:6 + 2 * j, :], own, o_taken, own_done,
                                        i * 2 + j, attT[:, :, bass.ds(i * P + j * S, S)])


def block_queries(dve, k, out, xT, at, scale):
    for g in range(DC):
        last = dve.scalar_tensor_tensor(out[:, g * 8:(g + 1) * 8, :],
                                        xT[:, g:g + 1, bass.ds(at, S)].broadcast_to((P, 8, S)), scale,
                                        k.blocks8[:].unsqueeze(2).broadcast_to((P, 8, S)), ALU.mult, ALU.mult)
    return last


def take_own_blocks(dve, k, products, own, taken, done, nth, out):
    dve.wait_ge(done.sem, nth * 1 + done.at(0))
    for g in range(DC):
        ins_ = dve.tensor_tensor(own[:, g, :, :], products[:, g, :].rearrange("p (h q) -> p h q", q=S),
                                 k.blocks8[:].unsqueeze(2).broadcast_to((P, H16 // DC, S)), ALU.mult)
    ins_.then_inc(taken.sem, 1)
    dve.wait_ge(taken.sem, nth + taken.at(1))
    dve.tensor_reduce(out, own[:].rearrange("p g h q -> p g q h"), AX.X, ALU.add).then_inc(done.sem, 1)


def relu_cross_attention(nc, k, name, ins, wk_sb, wv_sb, qT, maskT, loaded_weights):
    with ExitStack() as ctx:
        def sb(n, shape, dt=F32):
            return ctx.enter_context(nc.sbuf_tensor(f"{name}_{n}", shape, dt))

        def signal(n, credit=0):
            return Signal(nc, ctx, f"{name}_{n}", credit)

        ctxT = sb("ctxT", [P, 2, DC, M])
        kT = sb("kT", [P, DC, M])
        v = sb("v", [P, KT, D])
        q_sb = sb("q", [P, 2, DC, S])
        lg = sb("lg", [P, KT, S])
        att = sb("att", [P, D])
        bk = k.col("L2x_bk")
        loaded = [signal(f"loaded{j}") for j in range(2)]
        q_ready = signal("q_ready", 2)
        p_filled = signal("p_filled")
        p_taken = signal("p_taken", 8)
        l_filled = signal("l_filled")
        l_relu = signal("l_relu", 2)
        l_ready = signal("l_ready", 2)
        av_done = signal("av_done", 2)
        att_done = signal("att_done", 2)
        x_done = signal("x_done", 1)
        give_credits(nc, [q_ready, p_taken, l_relu, l_ready, av_done, att_done, x_done])
        kjobs = [(m, c) for m in range(DC) for c in range(NCH)]
        vjobs = [list(range(t, min(t + 2, KT))) for t in range(0, KT, 2)]
        NJ = len(kjobs) + len(vjobs)
        PB = 4

        with nc.Block() as block:

            @block.sync
            def _(sp):
                with sp.Fori(0, B // 2) as i:
                    for j in range(2):
                        sp.wait_ge(av_done.sem, i * 2 + av_done.at(j - 1))
                        sp.dma_start(ctxT[:, j, :, :], ins["ctxT"][i * 2 + j].rearrange("c p n -> p c n")
                                     ).then_inc(loaded[j].sem, 16)

            @block.gpsimd
            def _(pool):
                with pool.Fori(0, B // 2) as i:
                    for j in range(2):
                        pool.wait_ge(av_done.sem, i * 2 + av_done.at(j - 1))
                        pool.tensor_copy(q_sb[:, j, :, :], qT[:, :, bass.ds(i * P + j * S, S)]
                                         ).then_inc(q_ready.sem, 1)

            @block.tensor
            def _(pe):
                pe.wait_ge(*loaded_weights)
                with pe.Fori(0, B // 2) as i:
                    for j in range(2):
                        pe.wait_ge(loaded[j].sem, i * 16 + 16)
                        for n in range(NJ):
                            pe.wait_ge(p_taken.sem, i * (2 * NJ) + p_taken.at(max(j * NJ + n - PB + 1, 0)))
                            bank = k.ps[:, (j * NJ + n) % PB, :]
                            if n < len(kjobs):
                                m, c = kjobs[n]
                                at, w = CHUNKS[c]
                                for f in range(DC):
                                    last = pe.matmul(bank[:, 0:w], wk_sb[:, f, m * P:(m + 1) * P],
                                                     ctxT[:, j, f, at:at + w], start=(f == 0), stop=(f == DC - 1))
                            else:
                                for s, t in enumerate(vjobs[n - len(kjobs)]):
                                    rows = key_rows(t)
                                    for f in range(DC):
                                        pe.matmul(bank[0:rows, s * D:(s + 1) * D],
                                                  ctxT[:, j, f, t * P:t * P + rows], wv_sb[:, f, :],
                                                  start=(f == 0), stop=False)
                                    last = pe.matmul(bank[0:rows, s * D:(s + 1) * D], k.ones_row[0:1, 0:rows],
                                                     k.row("L2x_bv"), start=False, stop=True)
                            last.then_inc(p_filled.sem, 1)
                        pe.wait_ge(q_ready.sem, i * 2 + q_ready.at(j + 1))
                        pe.wait_ge(p_taken.sem, i * (2 * NJ) + p_taken.at((j + 1) * NJ))
                        for t in range(KT):
                            rows = key_rows(t)
                            if t == 0:
                                pe.wait_ge(l_relu.sem, i * 4 + l_relu.at(j * 2))
                            for f in range(DC):
                                last = pe.matmul(k.ps[0:rows, 4 + t // 8, (t % 8) * S:(t % 8 + 1) * S],
                                                 kT[:, f, t * P:t * P + rows], q_sb[:, j, f, :],
                                                 start=(f == 0), stop=(f == DC - 1))
                            if t == 7 or t == KT - 1:
                                last.then_inc(l_filled.sem, 1)
                        for t in range(KT):
                            rows = key_rows(t)
                            if t == 0:
                                pe.wait_ge(l_ready.sem, i * 6 + l_ready.at(j * 3 + 1))
                                pe.wait_ge(att_done.sem, i * 2 + att_done.at(j - 1))
                            if t == 8:
                                pe.wait_ge(l_ready.sem, i * 6 + l_ready.at(j * 3 + 3))
                            last = pe.matmul(k.ps[0:S, 6 + j, 0:D], lg[0:rows, t, :], v[0:rows, t, :],
                                             start=(t == 0), stop=(t == KT - 1))
                        last.then_inc(av_done.sem, 1)

            @block.scalar
            def _(act):
                with act.Fori(0, B // 2) as i:
                    for j in range(2):
                        act.wait_ge(av_done.sem, i * 2 + av_done.at(j))
                        for n in range(NJ):
                            act.wait_ge(p_filled.sem, i * (2 * NJ) + (j * NJ + n + 1))
                            bank = k.ps[:, (j * NJ + n) % PB, :]
                            if n < len(kjobs):
                                m, c = kjobs[n]
                                at, w = CHUNKS[c]
                                ins_ = act.activation(kT[:, m, at:at + w], bank[:, 0:w], ACT.Relu, bias=bk[:, m:m + 1])
                            else:
                                ts = vjobs[n - len(kjobs)]
                                rows = key_rows(ts[-1])
                                ins_ = act.activation(v[0:rows, ts[0]:ts[-1] + 1, :],
                                                      bank[0:rows, 0:len(ts) * D].rearrange("p (t d) -> p t d", d=D),
                                                      ACT.Relu)
                            ins_.then_inc(p_taken.sem, 1)

            @block.vector
            def _(dve):
                dve.wait_ge(*loaded_weights)
                with dve.Fori(0, B // 2) as i:
                    for j in range(2):
                        dve.wait_ge(av_done.sem, i * 2 + av_done.at(j))
                        spans = [(P, 0, 8), (P, 8, KFULL), (KREST, KFULL, KT)]
                        for n, (rows, t0, t1) in enumerate(spans):
                            dve.wait_ge(l_filled.sem, i * 4 + (2 * j + min(n, 1) + 1))
                            src = k.ps[0:rows, 4 + t0 // 8, (t0 % 8) * S:(t0 % 8 + t1 - t0) * S].rearrange(
                                "p (t q) -> p t q", q=S)
                            ins_ = dve.tensor_scalar(lg[0:rows, t0:t1, :], src, 0.0, D ** -0.5, ALU.max, ALU.mult)
                            if n != 1:
                                ins_.then_inc(l_relu.sem, 1)
                        dve.wait_ge(l_relu.sem, i * 4 + l_relu.at(2 * j + 2))
                        for rows, t0, t1 in spans:
                            dve.tensor_tensor(lg[0:rows, t0:t1, :], lg[0:rows, t0:t1, :], maskT[0:rows, t0:t1, :],
                                              ALU.add).then_inc(l_ready.sem, 1)
                        dve.wait_ge(av_done.sem, i * 2 + av_done.at(j + 1))
                        if j == 0:
                            dve.wait_ge(x_done.sem, i + x_done.at(0))
                        dve.tensor_scalar(att[j * S:(j + 1) * S, :], k.ps[0:S, 6 + j, 0:D], 0.0, None, ALU.max
                                          ).then_inc(att_done.sem, 1)
                    dve.wait_ge(att_done.sem, i * 2 + att_done.at(2))
                    xt = k.x[:, i, :]
                    dve.tensor_tensor(xt, xt, att[:], ALU.add).then_inc(x_done.sem, 1)


def self_attention(nc, k, name, qT, kT, v_all, attT, softmax, eps=0.0):
    with ExitStack() as ctx:
        def sb(n, shape, dt=F32):
            return ctx.enter_context(nc.sbuf_tensor(f"{name}_{n}", shape, dt))

        def signal(n, credit=0):
            return Signal(nc, ctx, f"{name}_{n}", credit)

        kb = sb("kb", [P, 2, DC, S])
        vb = sb("vb", [S, 2, D])
        qb = sb("qb", [P, 2, DC, 2, S])
        w = sb("w", [P, 2, PAIRS, S])
        wT = sb("wT", [S, 2, PAIRS * P])
        mxs = sb("mxs", [P, 2, PAIRS])
        own = sb("own", [P, DC, H16 // DC, S])
        own2 = sb("own2", [P, DC, H16 // DC, S])
        num = sb("num", [P, DC, S])
        den = sb("den", [P, DC, S])
        ready = signal("ready")
        q_ready = signal("q_ready")
        s_filled = signal("s_filled")
        shifted = signal("shifted")
        exp_done = signal("exp_done")
        w_ready = signal("w_ready")
        t_filled = signal("t_filled")
        wT_ready = signal("wT_ready", 1)
        av_done = signal("av_done", 2)
        taken = signal("taken", 1)
        done = signal("done", 1)
        step = signal("step")
        give_credits(nc, [wT_ready, av_done, taken, done])
        with nc.Block() as block:

            @block.gpsimd
            def _(pool):
                with pool.Fori(0, B // 2) as i:
                    for j in range(2):
                        pool.wait_ge(av_done.sem, i * 2 + av_done.at(j - 1))
                        pool.tensor_copy(kb[:, j, :, :], kT[:, :, bass.ds(i * P + j * S, S)]).then_inc(ready.sem, 1)
                        pool.tensor_copy(vb[:, j, :], v_all[:, i * 2 + j, :]).then_inc(ready.sem, 1)

            @block.tensor
            def _(pe):
                with pe.Fori(0, B // 2) as i:
                    for j in range(2):
                        pe.wait_ge(ready.sem, i * 4 + (2 * j + 2))
                        pe.wait_ge(q_ready.sem, i * 2 + (j + 1))
                        for pair in range(PAIRS):
                            g, r = pair // 4, 32 * (pair % 4)
                            if softmax:
                                last = pe.matmul(k.ps[:, pair % 4, (2 * j + g) * S:(2 * j + g + 1) * S], qb[r:r + 32, j, g, :, :],
                                                 kb[r:r + 32, j, g, :], start=True, stop=True)
                            else:
                                last = pe.matmul(k.ps[0:S, pair % 4, (2 * j + g) * P:(2 * j + g + 1) * P],
                                                 kb[r:r + 32, j, g, :], qb[r:r + 32, j, g, :, :], start=True, stop=True)
                            if g == DC - 1:
                                last.then_inc(s_filled.sem, 1)
                    if softmax:
                        for j in range(2):
                            pe.wait_ge(w_ready.sem, i * 2 + (j + 1))
                            pe.wait_ge(wT_ready.sem, i * 2 + wT_ready.at(j))
                            pe.sem_inc(k.tick, 1)
                            for pair in range(PAIRS):
                                g = pair // 4
                                last = pe.transpose(k.ps[0:S, 4 + g, (pair % 4) * P:(pair % 4 + 1) * P],
                                                    w[:, j, pair, :], k.ident[:])
                            last.then_inc(t_filled.sem, 1)
                    for j in range(2):
                        pe.wait_ge(wT_ready.sem, i * 2 + wT_ready.at(j + 1))
                        pe.wait_ge(taken.sem, i * 2 + taken.at(j))
                        for g in range(DC):
                            moving = wT[:, j, g * BANK:(g + 1) * BANK]
                            if not softmax:
                                pe.matmul(k.ps[:, 4 + g, :], k.ones64[0:S, :], moving, start=True, stop=True)
                            last = pe.matmul(k.ps[:, 6 + g, :], vb[:, j, g * P:(g + 1) * P], moving,
                                             start=True, stop=True)
                        last.then_inc(av_done.sem, 1)

            @block.scalar
            def _(act):
                if softmax:
                    with act.Fori(0, B // 2) as i:
                        for j in range(2):
                            act.wait_ge(shifted.sem, i * 2 + (j + 1))
                            act.activation(w[:, j, :, :], w[:, j, :, :], ACT.Exp).then_inc(exp_done.sem, 1)
                        for j in range(2):
                            act.wait_ge(t_filled.sem, i * 2 + (j + 1))
                            act.activation(wT[:, j, :], k.ps[0:S, 4:6, :].rearrange(
                                "p a b -> p (a b)"), ACT.Copy).then_inc(wT_ready.sem, 1)

            @block.vector
            def _(dve):
                with dve.Fori(0, B // 2) as i:
                    per_body = 8
                    count = [0]

                    def link(ins_):
                        count[0] += 1
                        ins_.then_inc(step.sem, 1)
                        dve.wait_ge(step.sem, i * per_body + count[0])

                    for j in range(2):
                        for h in range(2):
                            ins_ = dve.tensor_scalar(qb[:, j, :, h, :], qT[:, :, bass.ds(i * P + j * S, S)],
                                                     k.parity[:, h:h + 1], HD ** -0.5 if softmax else 1.0,
                                                     ALU.mult, ALU.mult)
                        ins_.then_inc(q_ready.sem, 1)
                    if softmax:
                        for j in range(2):
                            dve.wait_ge(s_filled.sem, i * 8 + 8)
                            link(dve.tensor_tensor(
                                w[:, j, :, :].rearrange("p (g r) s -> p r g s", g=DC),
                                k.ps[:, 0:4, 2 * j * S:(2 * j + 2) * S].rearrange("p r (g s) -> p r g s", s=S),
                                k.causal_rows[:].unsqueeze(1).unsqueeze(1).broadcast_to((P, 4, DC, S)), ALU.add))
                            link(dve.tensor_reduce(mxs[:, j, :], w[:, j, :, :], AX.X, ALU.max))
                            dve.tensor_tensor(w[:, j, :, :], w[:, j, :, :], mxs[:, j, :].unsqueeze(2).broadcast_to(
                                (P, PAIRS, S)), ALU.subtract).then_inc(shifted.sem, 1)
                        for j in range(2):
                            dve.wait_ge(exp_done.sem, i * 2 + (j + 1))
                            link(dve.tensor_reduce(mxs[:, j, :], w[:, j, :, :], AX.X, ALU.add))
                            link(dve.reciprocal(mxs[:, j, :], mxs[:, j, :]))
                            dve.tensor_tensor(w[:, j, :, :], w[:, j, :, :], mxs[:, j, :].unsqueeze(2).broadcast_to(
                                (P, PAIRS, S)), ALU.mult).then_inc(w_ready.sem, 1)
                    else:
                        for j in range(2):
                            dve.wait_ge(s_filled.sem, i * 8 + 8)
                            for g in range(DC):
                                ins_ = dve.tensor_tensor(
                                    wT[:, j, g * BANK:(g + 1) * BANK].rearrange("p (r h q) -> p r h q", h=2, q=S),
                                    k.ps[0:S, 0:4, (2 * j + g) * P:(2 * j + g + 1) * P].rearrange(
                                        "p r (h q) -> p r h q", q=S),
                                    k.causal_keys[0:S, :].unsqueeze(1).unsqueeze(1).broadcast_to((S, 4, 2, S)),
                                    ALU.mult)
                            ins_.then_inc(wT_ready.sem, 1)
                    for j in range(2):
                        out = attT[:, :, bass.ds(i * P + j * S, S)]
                        dve.wait_ge(av_done.sem, i * 2 + av_done.at(j + 1))
                        dve.wait_ge(done.sem, i * 2 + done.at(j))
                        if not softmax:
                            for g in range(DC):
                                ins_ = dve.tensor_tensor(own2[:, g, :, :], k.ps[:, 4 + g, :].rearrange(
                                    "p (h q) -> p h q", q=S), k.blocks8[:].unsqueeze(2).broadcast_to(
                                        (P, H16 // DC, S)), ALU.mult)
                            link(ins_)
                            link(dve.tensor_reduce(den[:], own2[:].rearrange("p g h q -> p g q h"), AX.X, ALU.add))
                        for g in range(DC):
                            ins_ = dve.tensor_tensor(own[:, g, :, :], k.ps[:, 6 + g, :].rearrange(
                                "p (h q) -> p h q", q=S), k.blocks8[:].unsqueeze(2).broadcast_to(
                                    (P, H16 // DC, S)), ALU.mult)
                        ins_.then_inc(taken.sem, 1)
                        dve.wait_ge(taken.sem, i * 2 + taken.at(j + 1))
                        summed = own[:].rearrange("p g h q -> p g q h")
                        if softmax:
                            dve.tensor_reduce(out, summed, AX.X, ALU.add).then_inc(done.sem, 1)
                        else:
                            dve.tensor_scalar(den[:], den[:], eps, None, ALU.add)
                            link(dve.tensor_reduce(num[:], summed, AX.X, ALU.add))
                            link(dve.reciprocal(den[:], den[:]))
                            dve.tensor_tensor(out, num[:], den[:], ALU.mult).then_inc(done.sem, 1)
                    assert count[0] == per_body


def expert_tiles(choices):
    return (TOK * choices + E8 * (P - 1)) // P


def place_tokens(nc, k, st, hot, choices, kept=None):
    W = choices * E8
    tiles = expert_tiles(choices)
    count = st.sb("count", [P, NT + 1, W])
    row, row_u = st.sb("row", [P, NT, choices]), st.sb("row_u", [P, NT, choices], U32)
    total, used = st.sb("total", [P, E8]), st.sb("used", [P, E8])
    pairwise, before = st.sb("pairwise", [P, E8, E8]), st.sb("before", [P, E8])
    shift = st.sb("shift", [P, W])
    past, owner = st.sb("past", [P, tiles, E8]), st.sb("owner", [P, tiles])
    owner_u = st.sb("owner_u", [P, tiles], U32)
    groups = []
    for t in range(NT + 1):
        products = [(k.ones64[:], hot[:, s, :]) for s in range(t)]
        if t < NT:
            products.append((k.upto[:], hot[:, t, :]))
        groups.append((lambda bank, t=t: bank[:, t * W:(t + 1) * W], products))
    matmul_pass(nc, k, [Job(groups, "dve", lambda e, bank: e.tensor_copy(
        count[:].rearrange("p t w -> p (t w)"), bank[:, 0:(NT + 1) * W]))])

    def over_e(ap, n):
        return ap.unsqueeze(2).broadcast_to((P, n, E8))

    def along(ap, n):
        return ap.unsqueeze(1).broadcast_to((P, n, E8))

    def steps(dve, link):
        link(dve.tensor_reduce(total[:], count[:, NT, :].rearrange("p (r e) -> p e r", e=E8), AX.X, ALU.add))
        link(dve.tensor_scalar(before[:], k.iota[:, 0:E8], float(P), None, ALU.mult))
        link(dve.tensor_tensor(pairwise[:], over_e(total[:], E8), along(before[:], E8), ALU.is_gt))
        link(dve.tensor_reduce(used[:], pairwise[:], AX.X, ALU.add))
        link(dve.tensor_tensor(pairwise[:], over_e(k.iota[:, 0:E8], E8), along(k.iota[:, 0:E8], E8), ALU.is_gt))
        link(dve.tensor_tensor(pairwise[:], pairwise[:], along(used[:], E8), ALU.mult))
        link(dve.tensor_reduce(before[:], pairwise[:], AX.X, ALU.add))
        link(dve.tensor_tensor(used[:], used[:], before[:], ALU.add))
        link(dve.tensor_tensor(past[:], along(used[:], tiles), over_e(k.iota[:, 0:tiles], tiles), ALU.is_le))
        link(dve.tensor_reduce(owner[:], past[:], AX.X, ALU.add))
        link(dve.tensor_scalar(owner[:], owner[:], float(E8 - 1), None, ALU.min))
        link(dve.tensor_copy(owner_u[:], owner[:]))
        for r in range(choices):
            link(dve.tensor_scalar(shift[:, r * E8:(r + 1) * E8], before[:], float(P), -1.0, ALU.mult, ALU.add))
        if choices > 1:
            link(dve.tensor_tensor(shift[:, E8:W], shift[:, E8:W], count[:, NT, 0:E8], ALU.add))
        if kept is not None:
            within = st.sb("within", [P, NT, W])
            link(dve.tensor_scalar(within[:], count[:, 0:NT, :], float(CAPACITY), None, ALU.is_le))
            link(dve.tensor_tensor(within[:], within[:], hot, ALU.mult))
            link(dve.tensor_reduce(kept, within[:].rearrange("p t (r e) -> p t r e", e=E8), AX.X, ALU.add))
        link(dve.tensor_tensor(count[:, 0:NT, :], count[:, 0:NT, :],
                               shift[:].unsqueeze(1).broadcast_to((P, NT, W)), ALU.add))
        link(dve.tensor_tensor(count[:, 0:NT, :], count[:, 0:NT, :], hot, ALU.mult))
        link(dve.tensor_reduce(row[:], count[:, 0:NT, :].rearrange("p t (r e) -> p t r e", e=E8), AX.X, ALU.add))
        link(dve.tensor_copy(row_u[:], row[:]))

    vector_block(nc, k, steps)
    return row_u, owner_u


def experts(nc, k, name, w_in, w_gate, w_out, hidden, rows, owner, gates, choices, b_in=None, b_out=None):
    gated = w_gate is not None
    MT = (hidden + P - 1) // P
    HW = [min(P, hidden - m * P) for m in range(MT)]
    full_w2 = hidden % P == 0
    tiles = expert_tiles(choices)
    whole = hidden // P
    sorted_out = nc.dram_tensor(f"{name}_sorted_out", (tiles * P, D), F32).ap()

    with ExitStack() as ctx:
        def sb(n, shape, dt=F32):
            return ctx.enter_context(nc.sbuf_tensor(f"{name}_{n}", shape, dt))

        def signal(n, credit=0):
            return Signal(nc, ctx, f"{name}_{n}", credit)

        w1 = sb("w1", [P, 2, DC, hidden])
        wg = sb("wg", [P, 2, DC, hidden]) if gated else None
        w2 = sb("w2", [P, 2, MT, D])
        b1 = sb("b1", [P, 2, MT]) if b_in is not None else None
        b2 = sb("b2", [1, 2, D]) if b_out is not None else None
        tokens = sb("tokens", [P, 2, D])
        tokT = sb("tokT", [P, 2, DC, P])
        sig = sb("sig", [P, 2, P]) if gated else None
        hid = sb("hid", [P, 2, MT, P])
        y = sb("y", [P, 2, D])
        n_loads = 2 + gated + (not full_w2) + (b_in is not None) + (b_out is not None)
        RING = 2 if gated else 4

        tok_loaded = [signal(f"tok_loaded{j}") for j in range(2)]
        w_loaded = [signal(f"w_loaded{j}") for j in range(2)]
        t_filled = signal("t_filled", 1)
        t_taken = signal("t_taken")
        h_filled = signal("h_filled")
        sig_done = signal("sig_done") if gated else None
        h_taken = signal("h_taken", RING)
        o_filled = signal("o_filled", 2)
        o_taken = signal("o_taken", 2)
        y_stored = signal("y_stored")
        y_free = signal("y_free", 2)
        scattered = signal("scattered")
        give_credits(nc, [t_filled, h_taken, o_filled, o_taken, y_free])

        with nc.Block() as block:

            @block.gpsimd
            def _(pool):
                pool.wait_ge(k.zeroed, 16 * ZERO_PARTS)
                for t in range(NT):
                    for r in range(choices):
                        pool.indirect_dma_start(k.sorted_in, bass.IndirectOffsetOnAxis(rows[:, t, r:r + 1], 0),
                                                k.xn[:, t, :], None).then_inc(scattered.sem, 16)
                pool.wait_ge(scattered.sem, 16 * NT * choices)

        def over_tiles(engine, body):
            with engine.Fori(0, tiles // 2) as i:
                for j in range(2):
                    body(i, j)
            if tiles % 2:
                body(tiles // 2, 0)

        with nc.Block() as block:

            @block.sync
            def _(sp):
                def body(i, j):
                    n = i * 2 + j
                    e = nc.values_load(owner[0:1, bass.ds(n, 1)], [mybir.EngineType.SP], min_val=0, max_val=E8 - 1,
                                       skip_runtime_bounds_check_because="place_tokens clamps it to 0..7")
                    sp.wait_ge(o_filled.sem, i * 2 + o_filled.at(j - 1))
                    sp.sem_inc(k.tick, 1)
                    sp.dma_start(tokens[:, j, :], k.sorted_in[bass.ds(n * P, P), :]
                                 ).then_inc(tok_loaded[j].sem, 16)
                    done = w_loaded[j].sem
                    sp.dma_start(w1[:, j, :, :], w_in[e].rearrange("(c p) n -> p c n", p=P)).then_inc(done, 16)
                    if gated:
                        sp.dma_start(wg[:, j, :, :], w_gate[e].rearrange("(c p) n -> p c n", p=P)).then_inc(done, 16)
                    if b_in is not None:
                        sp.dma_start(b1[:, j, :], b_in[e]).then_inc(done, 16)
                    if b_out is not None:
                        sp.dma_start(b2[:, j, :], b_out[e]).then_inc(done, 16)
                    sp.dma_start(w2[:, j, 0:whole, :],
                                 w_out[e][0:whole * P, :].rearrange("(c p) n -> p c n", p=P)).then_inc(done, 16)
                    if not full_w2:
                        sp.dma_start(w2[0:HW[-1], j, whole, :], w_out[e][whole * P:hidden, :]).then_inc(done, 16)

                over_tiles(sp, body)

            @block.tensor
            def _(pe):
                def transposes(i, j):
                    pe.wait_ge(tok_loaded[j].sem, i * 16 + 16)
                    pe.sem_inc(k.tick, 1)
                    for c in range(DC):
                        last = pe.transpose(k.ps[:, 4 + j, c * P:(c + 1) * P], tokens[:, j, c * P:(c + 1) * P],
                                            k.ident[:])
                    last.then_inc(t_filled.sem, 1)

                def body(i, j, more=True):
                    pe.wait_ge(t_taken.sem, i * 2 + (j + 1))
                    pe.wait_ge(w_loaded[j].sem, i * (16 * n_loads) + 16 * n_loads)
                    for m in range(MT):
                        job = j * MT + m
                        pe.wait_ge(h_taken.sem, i * (2 * MT) + h_taken.at(job - RING + 1))
                        for x, w in enumerate((w1, wg) if gated else (w1,)):
                            bank = (2 * (job % 2) + x) if gated else job % 4
                            for c in range(DC):
                                last = pe.matmul(k.ps[0:HW[m], bank, 0:P], w[:, j, c, m * P:m * P + HW[m]],
                                                 tokT[:, j, c, :], start=(c == 0), stop=(c == DC - 1))
                        last.then_inc(h_filled.sem, 1)
                    if more:
                        transposes(i + (j == 1), 1 - j)
                    pe.wait_ge(o_taken.sem, i * 2 + o_taken.at(j - 1))
                    for m in range(MT):
                        pe.wait_ge(h_taken.sem, i * (2 * MT) + h_taken.at(j * MT + m + 1))
                        last = pe.matmul(k.ps[:, 6 + j, 0:D], hid[0:HW[m], j, m, :], w2[0:HW[m], j, m, :],
                                         start=(m == 0), stop=(m == MT - 1 and b2 is None))
                    if b2 is not None:
                        last = pe.matmul(k.ps[:, 6 + j, 0:D], k.ones_row[0:1, :], b2[0:1, j, :],
                                         start=False, stop=True)
                    last.then_inc(o_filled.sem, 1)

                transposes(0, 0)
                with pe.Fori(0, tiles // 2) as i:
                    for j in range(2):
                        body(i, j)
                body(tiles // 2, 0, False)

            @block.scalar
            def _(act):
                def body(i, j):
                    act.wait_ge(o_filled.sem, i * 2 + o_filled.at(j - 1))
                    act.sem_inc(k.tick, 1)
                    for m in range(MT):
                        job = j * MT + m
                        act.wait_ge(h_filled.sem, i * (2 * MT) + (job + 1))
                        if gated:
                            act.wait_ge(h_taken.sem, i * (2 * MT) + h_taken.at(job - 1))
                            act.activation(sig[0:HW[m], job % 2, :], k.ps[0:HW[m], 2 * (job % 2), 0:P],
                                           ACT.Silu).then_inc(sig_done.sem, 1)
                        else:
                            bias = b1[:, j, m:m + 1] if b1 is not None else 0.0
                            act.activation(hid[:, j, m, :], k.ps[:, job % 4, 0:P], ACT.Gelu, bias=bias
                                           ).then_inc(h_taken.sem, 1)

                over_tiles(act, body)

            @block.vector
            def _(dve):
                def take_transposed(i, j):
                    dve.wait_ge(t_filled.sem, i * 2 + t_filled.at(j + 1))
                    dve.tensor_copy(tokT[:, j, :, :].rearrange("p c n -> p (c n)"), k.ps[:, 4 + j, 0:D]
                                    ).then_inc(t_taken.sem, 1)

                def body(i, j, more=True):
                    if gated:
                        dve.wait_ge(o_filled.sem, i * 2 + o_filled.at(j - 1))
                        dve.sem_inc(k.tick, 1)
                        for m in range(MT):
                            job = j * MT + m
                            dve.wait_ge(sig_done.sem, i * (2 * MT) + (job + 1))
                            dve.tensor_tensor(hid[0:HW[m], j, m, :], sig[0:HW[m], job % 2, :],
                                              k.ps[0:HW[m], 2 * (job % 2) + 1, 0:P], ALU.mult
                                              ).then_inc(h_taken.sem, 1)
                    if more:
                        take_transposed(i + (j == 1), 1 - j)
                    dve.wait_ge(y_free.sem, i * 2 + y_free.at(j - 1))
                    dve.wait_ge(o_filled.sem, i * 2 + o_filled.at(j + 1))
                    dve.tensor_copy(y[:, j, :], k.ps[:, 6 + j, 0:D]).then_inc(o_taken.sem, 1)

                take_transposed(0, 0)
                with dve.Fori(0, tiles // 2) as i:
                    for j in range(2):
                        body(i, j)
                body(tiles // 2, 0, False)

            @block.gpsimd
            def _(pool):
                def body(i, j):
                    pool.wait_ge(o_taken.sem, i * 2 + o_taken.at(j + 1))
                    pool.sem_inc(k.tick, 1)
                    pool.dma_start(sorted_out[bass.ds((i * 2 + j) * P, P), :], y[:, j, :]
                                   ).then_inc(y_stored.sem, 16)
                    pool.wait_ge(y_stored.sem, i * 32 + (16 * j + 16))
                    pool.sem_inc(y_free.sem, 1)

                over_tiles(pool, body)

    with ExitStack() as ctx:
        back = ctx.enter_context(nc.sbuf_tensor(f"{name}_back", [P, NT, choices, D], F32))
        fetched = Signal(nc, ctx, f"{name}_fetched")
        with nc.Block() as block:

            @block.gpsimd
            def _(pool):
                for t in range(NT):
                    for r in range(choices):
                        pool.indirect_dma_start(back[:, t, r, :], None, sorted_out,
                                                bass.IndirectOffsetOnAxis(rows[:, t, r:r + 1], 0)
                                                ).then_inc(fetched.sem, 16)

            @block.vector
            def _(dve):
                for r in range(choices):
                    for t in range(NT):
                        dve.wait_ge(fetched.sem, 16 * NT * choices)
                        if r:
                            dve.wait_ge(k.dve_link, k.n_dve_link + t + 1)
                        dve.scalar_tensor_tensor(k.x[:, t, :], back[:, t, r, :], gates[:, t, r:r + 1],
                                                 k.x[:, t, :], ALU.mult, ALU.add).then_inc(k.dve_link, 1)
        k.n_dve_link += NT * choices


def vector_block(nc, k, steps):
    with nc.Block() as block:

        @block.vector
        def _(dve):
            def link(ins_):
                k.n_dve_link += 1
                ins_.then_inc(k.dve_link, 1)
                dve.wait_ge(k.dve_link, k.n_dve_link)

            steps(dve, link)


def scalar_block(nc, k, steps):
    with nc.Block() as block:

        @block.scalar
        def _(act):
            def link(ins_):
                k.n_act_link += 1
                ins_.then_inc(k.act_link, 1)
                act.wait_ge(k.act_link, k.n_act_link)

            steps(act, link)


def add_bias(col, func):
    return lambda out: lambda e, bank, m, n: e.activation(
        out[0:bank.shape[0], m, n * BANK:(n + 1) * BANK], bank, func, bias=col[0:bank.shape[0], m:m + 1])


def top2_gates(nc, k, st, logits, top, kept=None):
    idx, idxf = st.sb("idx", [P, NT, 8], U32), st.sb("idxf", [P, NT, 8])
    hot = st.sb("hot", [P, NT, 2, E8])
    gap, g2 = st.sb("gap", [P, NT]), st.sb("g2", [P, NT, 2])

    def first(dve, link):
        for t in range(NT):
            link(dve.max(top[:, t, :], logits[:, t, :]))
            link(dve.max_index(idx[:, t, :], top[:, t, :], logits[:, t, :]))
        link(dve.tensor_copy(idxf[:], idx[:]))
        for r in range(2):
            link(dve.tensor_tensor(hot[:, :, r, :], k.iota8[:].unsqueeze(1).broadcast_to((P, NT, E8)),
                                   idxf[:, :, r:r + 1].broadcast_to((P, NT, E8)), ALU.is_equal))
        link(dve.tensor_tensor(gap[:], top[:, :, 1], top[:, :, 0], ALU.subtract))

    vector_block(nc, k, first)
    scalar_block(nc, k, lambda act, link: link(act.activation(g2[:, :, 1], gap[:], ACT.Exp)))
    rows, owner = place_tokens(nc, k, st, hot[:].rearrange("p t r e -> p t (r e)"), 2, kept)

    def second(dve, link):
        link(dve.tensor_scalar(gap[:], g2[:, :, 1], 1.0, None, ALU.add))
        link(dve.reciprocal(g2[:, :, 0], gap[:]))
        link(dve.tensor_tensor(g2[:, :, 1], g2[:, :, 1], g2[:, :, 0], ALU.mult))
        if kept is not None:
            link(dve.tensor_tensor(g2[:], g2[:], kept, ALU.mult))

    vector_block(nc, k, second)
    return rows, owner, g2


def router_logits(nc, k, wgT, logits, loaded):
    groups = [(lambda bank, t=t: bank[:, t * E8:(t + 1) * E8],
               [(k.xnT[:, c, t * P:(t + 1) * P], wgT[:, c, :]) for c in range(DC)]) for t in range(NT)]
    matmul_pass(nc, k, [Job(groups, "dve", lambda e, bank: e.tensor_copy(
        logits[:].rearrange("p t e -> p (t e)"), bank[:, 0:NT * E8]))], [loaded])


def conv3(dve, link, out, src, w, bias, batches=B):
    o = out.rearrange("p (b s) -> p b s", s=S)
    x = src.rearrange("p (b s) -> p b s", s=S)
    link(dve.tensor_scalar(o, x, w[:, 1:2], bias, ALU.mult, ALU.add))
    link(dve.scalar_tensor_tensor(o[:, :, 1:S], x[:, :, 0:S - 1], w[:, 0:1], o[:, :, 1:S], ALU.mult, ALU.add))
    link(dve.scalar_tensor_tensor(o[:, :, 0:S - 1], x[:, :, 1:S], w[:, 2:3], o[:, :, 0:S - 1], ALU.mult, ALU.add))


class Stage:
    def __init__(self, nc, name):
        self.nc, self.name, self.ctx = nc, name, ExitStack()

    def __enter__(self):
        self.ctx.__enter__()
        return self

    def __exit__(self, *a):
        return self.ctx.__exit__(*a)

    def sb(self, n, shape, dt=F32):
        return self.ctx.enter_context(self.nc.sbuf_tensor(f"{self.name}_{n}", shape, dt))


def normed(nc, k):
    layer_norm(nc, k, k.x, k.xn, 1e-5)
    to_features(nc, k, k.xn, k.xnT)


def stage_L0_cross(nc, k, ins):
    normed(nc, k)
    softmax_cross_attention(nc, k, "L0x", ins, True, k.xnT)


def stage_L0_attn(nc, k, ins):
    normed(nc, k)
    with Stage(nc, "L0a") as st:
        w = {}
        copies = []
        for n, dout in (("wq", 64), ("wkv", 64), ("wqr", 128), ("wqr_sw", 128), ("wkr", 128), ("wkr_sw", 128),
                        ("wo", 256)):
            w[n] = st.sb(n, [P, DC, dout])
            copies.append((w[n][:], wk(ins["L0_" + n])))
        for n, dout in (("wqc", 128), ("wkc", 128), ("wv", 256)):
            w[n] = st.sb(n, [64, 1, dout])
            copies.append((w[n][:, 0, :], ins["L0_" + n]))
        loaded = load_block(nc, k, copies)
        cT = {n: st.sb("c" + n, [64, 1, TOK]) for n in ("q", "kv")}
        rot = {n: st.sb("rot" + n, [P, 2, TOK]) for n in "qk"}
        heads = {n: st.sb("heads" + n, [P, DC, TOK]) for n in "qk"}
        v_all = st.sb("v", [S, B, D])
        attT = st.sb("attT", [P, DC, TOK])
        jobs = []
        for n, bias in (("q", "L0_bq"), ("kv", "L0_bkv")):
            jobs += linear_jobs(w["w" + n], k.xnT, DC, 64, add_bias(k.col(bias), ACT.Gelu)(cT[n]))
        for n in "qk":
            for x, (suffix, table) in enumerate((("", k.rope_cos), ("_sw", k.rope_sin))):
                def drain(e, bank, m, n_, n=n, x=x, suffix=suffix, table=table):
                    return e.scalar_tensor_tensor(
                        rot[n][:, x, n_ * BANK:(n_ + 1) * BANK].rearrange("p (b s) -> p b s", s=S),
                        bank.rearrange("p (b s) -> p b s", s=S), k.col(f"L0_b{n}r{suffix}"),
                        table[:].unsqueeze(1).broadcast_to((P, BANK // S, S)), ALU.add, ALU.mult)
                jobs += linear_jobs(w[f"w{n}r{suffix}"], k.xnT, DC, 128, drain, by="dve")
        matmul_pass(nc, k, jobs, [loaded])

        def rope(dve, link):
            for n in "qk":
                link(dve.tensor_tensor(rot[n][:, 0, :], rot[n][:, 0, :], rot[n][:, 1, :], ALU.add))

        vector_block(nc, k, rope)
        jobs = []
        for n, c in (("q", "q"), ("k", "kv")):
            jobs += linear_jobs(w[f"w{n}c"], cT[c], 1, 128, add_bias(k.col(f"L0_b{n}c"), ACT.Gelu)(heads[n]), krows=64)
        for pair in range(B // 2):
            groups = [(lambda bank, h=h: bank[0:S, h * D:(h + 1) * D],
                       [(cT["kv"][:, 0, (2 * pair + h) * S:(2 * pair + h + 1) * S], w["wv"][:, 0, :]),
                        (k.ones_row[0:1, 0:S], k.row("L0_bv"))]) for h in range(2)]
            jobs.append(Job(groups, "dve", lambda e, bank, pair=pair: e.tensor_copy(
                v_all[:, 2 * pair:2 * pair + 2, :].rearrange("p b d -> p (b d)"), bank[0:S, :])))
        matmul_pass(nc, k, jobs)

        def gelus(act, link):
            for n in "qk":
                link(act.activation(heads[n][:, 1, :], rot[n][:, 0, :], ACT.Gelu))

        scalar_block(nc, k, gelus)
        self_attention(nc, k, "L0s", heads["q"], heads["k"], v_all, attT, True)
        residual_linear(nc, k, attT, w["wo"], DC, "L0_bo", k.x)


def stage_L0_ffn(nc, k, ins):
    normed(nc, k)
    with Stage(nc, "L0f") as st:
        wgT = st.sb("wgT", [P, DC, E8])
        loaded = load_block(nc, k, [(wgT[:], wk(ins["L0_Wg"]))])
        logits, top = st.sb("logits", [P, NT, E8]), st.sb("top", [P, NT, E8])
        router_logits(nc, k, wgT, logits, loaded)
        rows, owner, gates = top2_gates(nc, k, st, logits, top)
        experts(nc, k, "L0e", ins["L0_W1"], ins["L0_W2"], ins["L0_W3"], 682, rows, owner, gates, 2)


def stage_L1_cross(nc, k, ins):
    normed(nc, k)
    with Stage(nc, "L1x") as st:
        INNER, HDIM = 512, 64
        IC = INNER // P
        q_ctx = st.sb("q_ctx", [P, B, 2, BANK])
        with Stage(nc, "L1q") as s2:
            wq, wkT = s2.sb("wq", [P, DC, INNER]), s2.sb("wkT", [P, IC, D])
            qT = s2.sb("qT", [P, IC, TOK])
            loaded = load_block(nc, k, [(wq[:], wk(ins["L1x_Wq"])), (wkT[:], wk(ins["L1x_WkT"]))])
            matmul_pass(nc, k, linear_jobs(wq, k.xnT, DC, INNER, lambda e, bank, m, n: e.activation(
                qT[:, m, n * BANK:(n + 1) * BANK], bank, ACT.Copy, scale=HDIM ** -0.5)), [loaded])
            jobs = []
            for h in range(8):
                r = HDIM * (h % 2)
                for f in range(DC):
                    for n in range(NHALF):
                        products = [(wkT[r:r + HDIM, h // 2, f * P:(f + 1) * P],
                                     qT[r:r + HDIM, h // 2, n * BANK:(n + 1) * BANK])]
                        out = q_ctx[:, n * 8:(n + 1) * 8, f, h * S:(h + 1) * S]
                        by = ("act", "dve")[n]
                        jobs.append(Job([(full, products)], by, lambda e, bank, out=out, by=by: (
                            e.activation(out, bank.rearrange("p (b s) -> p b s", s=S), ACT.Copy) if by == "act"
                            else e.tensor_copy(out, bank.rearrange("p (b s) -> p b s", s=S)))))
            matmul_pass(nc, k, jobs)
        softmax_cross_attention(nc, k, "L1c", ins, False, q_ctx)
        wv, wo = st.sb("wv", [P, DC, INNER]), st.sb("wo", [P, IC, D])
        loaded = load_block(nc, k, [(wv[:], wk(ins["L1x_Wv"])), (wo[:], wk(ins["L1x_Wo"]))])
        accT = st.sb("accT", [P, DC, 8, TOK])
        oT = st.sb("oT", [P, IC, TOK])
        rows = q_ctx[:].rearrange("p b f n -> p b (f n)")
        jobs = []
        for b in range(B):
            for f in range(DC):
                groups = [(lambda bank, t=t: bank[:, t * P:(t + 1) * P],
                           [(rows[:, b, t * D + f * P:t * D + (f + 1) * P], None)]) for t in range(4)]
                out = accT[:, f, :, b * S:(b + 1) * S]
                by = ("act", "dve")[f]
                jobs.append(Job(groups, by, lambda e, bank, out=out, by=by: (
                    e.activation(out, bank.rearrange("p (h s) -> p h s", s=S), ACT.Copy) if by == "act"
                    else e.tensor_copy(out, bank.rearrange("p (h s) -> p h s", s=S)))))
        matmul_pass(nc, k, jobs, [loaded])
        jobs = []
        for c in range(IC):
            for n in range(NHALF):
                groups = [(lambda bank, h=h: bank[h * HDIM:(h + 1) * HDIM, :],
                           [(wv[:, f, (2 * c + h) * HDIM:(2 * c + h + 1) * HDIM],
                             accT[:, f, 2 * c + h, n * BANK:(n + 1) * BANK]) for f in range(DC)]) for h in range(2)]
                jobs.append(Job(groups, "act", lambda e, bank, c=c, n=n: e.activation(
                    oT[:, c, n * BANK:(n + 1) * BANK], bank, ACT.Copy)))
        matmul_pass(nc, k, jobs)
        residual_linear(nc, k, oT, wo, IC, "L1x_bo", k.x)


def stage_L1_attn(nc, k, ins):
    normed(nc, k)
    with Stage(nc, "L1a") as st:
        wqkv, wo = st.sb("wqkv", [P, DC, 3 * D]), st.sb("wo", [P, DC, D])
        loaded = load_block(nc, k, [(wqkv[:], wk(ins["L1a_wqkv"])), (wo[:], wk(ins["L1a_wo"]))])
        qk = st.sb("qk", [P, 2 * DC, TOK])
        pos = st.sb("pos", [P, 2 * DC, TOK])
        v_all = st.sb("v", [S, B, D])
        attT = st.sb("attT", [P, DC, TOK])
        bias = k.col("L1a_bqk")
        jobs = linear_jobs(wqkv, k.xnT, DC, 2 * D, lambda e, bank, m, n: e.activation(
            pos[:, m, n * BANK:(n + 1) * BANK], bank, ACT.Identity, bias=bias[:, m:m + 1]))
        for pair in range(B // 2):
            groups = [(lambda bank, h=h: bank[0:S, h * D:(h + 1) * D],
                       [(k.xnT[:, c, (2 * pair + h) * S:(2 * pair + h + 1) * S], wqkv[:, c, 2 * D:3 * D])
                        for c in range(DC)] + [(k.ones_row[0:1, 0:S], k.row("L1a_bv"))]) for h in range(2)]
            jobs.append(Job(groups, "dve", lambda e, bank, pair=pair: e.tensor_copy(
                v_all[:, 2 * pair:2 * pair + 2, :].rearrange("p b d -> p (b d)"), bank[0:S, :])))
        matmul_pass(nc, k, jobs, [loaded])
        elu_plus_one(nc, k, qk, pos)
        self_attention(nc, k, "L1s", qk[:, 0:DC, :], qk[:, DC:2 * DC, :], v_all, attT, False, 1e-6)
        residual_linear(nc, k, attT, wo, DC, "L1a_bo", k.x)


def elu_plus_one(nc, k, out, src):
    vector_block(nc, k, lambda dve, link: link(dve.tensor_scalar(out[:], src[:], 0.0, None, ALU.min)))
    scalar_block(nc, k, lambda act, link: link(act.activation(out[:], out[:], ACT.Exp)))
    vector_block(nc, k, lambda dve, link: link(
        dve.scalar_tensor_tensor(out[:], src[:], 0.0, out[:], ALU.max, ALU.add)))


ROUND = 1.5 * 2.0 ** 23


def round_clip(dve, link, t, lo, hi):
    link(dve.tensor_scalar(t, t, ROUND, None, ALU.add))
    link(dve.tensor_scalar(t, t, ROUND, None, ALU.subtract))
    link(dve.tensor_scalar(t, t, lo, hi, ALU.max, ALU.min))


def quantise_rows(nc, k, st, name, src, width):
    amax, sc, inv = (st.sb(name + n, [P, NT]) for n in ("amax", "scale", "inv"))

    def steps(dve, link):
        link(dve.tensor_reduce(amax[:], src[:], AX.X, ALU.max, apply_absolute_value=True))
        link(dve.tensor_scalar(amax[:], amax[:], 1e-5, None, ALU.max))
        link(dve.reciprocal(inv[:], amax[:]))
        link(dve.tensor_scalar(sc[:], inv[:], 127.0, None, ALU.mult))
        link(dve.reciprocal(inv[:], sc[:]))
        link(dve.tensor_tensor(src[:], src[:], sc[:].unsqueeze(2).broadcast_to((P, NT, width)), ALU.mult))
        round_clip(dve, link, src[:], -128.0, 127.0)
        link(dve.tensor_tensor(src[:], src[:], inv[:].unsqueeze(2).broadcast_to((P, NT, width)), ALU.mult))

    vector_block(nc, k, steps)


def quantise_weight(nc, k, st, name, w, chunks, width):
    part, mean, sc = (st.sb(name + n, [P, 1]) for n in ("part", "mean", "scale"))
    vector_block(nc, k, lambda dve, link: link(
        dve.tensor_reduce(part[:], w[:].rearrange("p c n -> p (c n)"), AX.X, ALU.add, apply_absolute_value=True)))
    matmul_pass(nc, k, [Job([(lambda bank: bank[:, 0:1], [(k.ones64[:], part[:])])], "dve",
                            lambda e, bank: e.tensor_scalar(mean[:], bank[:, 0:1], 1.0 / (P * chunks * width), 1e-5,
                                                            ALU.mult, ALU.max))])

    def steps(dve, link):
        link(dve.reciprocal(sc[:], mean[:]))
        link(dve.tensor_scalar(w[:], w[:], sc[:, 0:1], None, ALU.mult))
        round_clip(dve, link, w[:], -1.0, 1.0)

    vector_block(nc, k, steps)
    return mean


def stage_L1_ffn(nc, k, ins):
    HID = 1024
    HC = HID // P
    layer_norm(nc, k, k.x, k.xn, 1e-5)
    with Stage(nc, "L1f") as st:
        w1, w2 = st.sb("w1", [P, DC, HID]), st.sb("w2", [P, HC, D])
        loaded = load_block(nc, k, [(w1[:], wk(ins["L1f_w1"])), (w2[:], wk(ins["L1f_w2"]))])
        vector_wait(nc, k, loaded)
        m1 = quantise_weight(nc, k, st, "q1", w1, DC, HID)
        m2 = quantise_weight(nc, k, st, "q2", w2, HC, D)
        quantise_rows(nc, k, st, "x", k.xn, D)
        to_features(nc, k, k.xn, k.xnT)
        hT = st.sb("hT", [P, HC, TOK])
        cT = st.sb("cT", [P, HC, TOK])
        h_tok = st.sb("h", [P, NT, HID])
        matmul_pass(nc, k, linear_jobs(w1, k.xnT, DC, HID, lambda e, bank, m, n: e.activation(
            hT[:, m, n * BANK:(n + 1) * BANK], bank, ACT.Copy, scale=m1[:, 0:1])))
        cw, cb = k.col("L1f_cw"), k.col("L1f_cb")

        def conv(dve, link):
            for c in range(HC):
                conv3(dve, link, cT[:, c, :], hT[:, c, :], cw[:, 3 * c:3 * c + 3], cb[:, c:c + 1])

        vector_block(nc, k, conv)
        scalar_block(nc, k, lambda act, link: link(act.activation(cT[:], cT[:], ACT.Silu)))
        jobs = []
        for t in range(NT):
            for half in range(2):
                groups = [(lambda bank, c=c: bank[:, c * P:(c + 1) * P],
                           [(cT[:, 4 * half + c, t * P:(t + 1) * P], None)]) for c in range(4)]
                out = h_tok[:, t, half * BANK:(half + 1) * BANK]
                jobs.append(Job(groups, "act", lambda e, bank, out=out: e.activation(out, bank, ACT.Copy)))
        matmul_pass(nc, k, jobs)
        quantise_rows(nc, k, st, "h", h_tok, HID)
        to_features(nc, k, h_tok, hT, chunks=HC)
        jobs = []
        for t in range(NT):
            products = [(hT[:, c, t * P:(t + 1) * P], w2[:, c, :]) for c in range(HC)]
            jobs.append(Job([(lambda bank: bank[:, 0:D], products)], "dve", lambda e, bank, t=t:
                            e.scalar_tensor_tensor(k.x[:, t, :], bank[:, 0:D], m2[:, 0:1], k.x[:, t, :],
                                                   ALU.mult, ALU.add)))
        matmul_pass(nc, k, jobs)


def vector_wait(nc, k, loaded):
    with nc.Block() as block:

        @block.vector
        def _(dve):
            dve.wait_ge(*loaded)


def stage_L2_cross(nc, k, ins):
    normed(nc, k)
    with Stage(nc, "L2x") as st:
        wq, wkk, wv = (st.sb(n, [P, DC, D]) for n in ("wq", "wk", "wv"))
        maskT = st.sb("maskT", [P, KT, S])
        qT = st.sb("qT", [P, DC, TOK])
        loaded = load_block(nc, k, [
            (wq[:], wk(ins["L2x_wq"])), (wkk[:], wk(ins["L2x_wk"])), (wv[:], wk(ins["L2x_wv"])),
            (maskT[:, 0:KFULL, :], ins["maskT"][0:KFULL * P, :].rearrange("(t p) q -> p t q", p=P)),
            (maskT[0:KREST, KFULL, :], ins["maskT"][KFULL * P:M, :])])
        matmul_pass(nc, k, linear_jobs(wq, k.xnT, DC, D, add_bias(k.col("L2x_bq"), ACT.Relu)(qT)), [loaded])
        relu_cross_attention(nc, k, "L2c", ins, wkk, wv, qT, maskT, loaded)


def stage_L2_attn(nc, k, ins):
    normed(nc, k)
    with Stage(nc, "L2a") as st:
        w = {n: st.sb(n, [P, DC, D]) for n in ("wq", "wk", "wv", "wfc")}
        loaded = load_block(nc, k, [(w[n][:], wk(ins["L2a_" + n])) for n in w])
        qT, kT = st.sb("qT", [P, DC, TOK]), st.sb("kT", [P, DC, TOK])
        v = st.sb("v", [P, NT, D])
        s, sT = st.sb("s", [P, NT, P]), st.sb("sT", [P, NT, P])
        mxs = st.sb("mxs", [P, NT])
        jobs = linear_jobs(w["wq"], k.xnT, DC, D, lambda e, bank, m, n: e.activation(
            qT[:, m, n * BANK:(n + 1) * BANK], bank, ACT.Copy, scale=D ** -0.5))
        jobs += linear_jobs(w["wk"], k.xnT, DC, D, lambda e, bank, m, n: e.activation(
            kT[:, m, n * BANK:(n + 1) * BANK], bank, ACT.Copy))
        matmul_pass(nc, k, jobs, [loaded])
        residual_linear(nc, k, k.xnT, w["wv"], DC, None, v, add=False)
        jobs = []
        for t in range(NT):
            products = [(qT[:, c, t * P:(t + 1) * P], kT[:, c, t * P:(t + 1) * P]) for c in range(DC)]
            jobs.append(Job([(lambda bank: bank[:, 0:P], products)], "dve", lambda e, bank, t=t: e.tensor_tensor(
                s[:, t, :], bank[:, 0:P], k.causal_tile[:], ALU.add)))
        matmul_pass(nc, k, jobs)

        def shift(dve, link):
            link(dve.tensor_reduce(mxs[:], s[:], AX.X, ALU.max))
            link(dve.tensor_tensor(s[:], s[:], mxs[:].unsqueeze(2).broadcast_to((P, NT, P)), ALU.subtract))

        vector_block(nc, k, shift)
        scalar_block(nc, k, lambda act, link: link(act.activation(s[:], s[:], ACT.Exp)))

        def divide(dve, link):
            link(dve.tensor_reduce(mxs[:], s[:], AX.X, ALU.add))
            link(dve.reciprocal(mxs[:], mxs[:]))
            link(dve.tensor_tensor(s[:], s[:], mxs[:].unsqueeze(2).broadcast_to((P, NT, P)), ALU.mult))

        vector_block(nc, k, divide)
        jobs = []
        for n in range(2):
            groups = [(lambda bank, t=t: bank[:, t * P:(t + 1) * P], [(s[:, 4 * n + t, :], None)]) for t in range(4)]
            jobs.append(Job(groups, "act", lambda e, bank, n=n: e.activation(
                sT[:, 4 * n:4 * n + 4, :].rearrange("p t q -> p (t q)"), bank, ACT.Copy)))
        matmul_pass(nc, k, jobs)
        jobs = []
        for t in range(NT):
            jobs.append(Job([(lambda bank: bank[:, 0:D], [(sT[:, t, :], v[:, t, :])])], "dve",
                            lambda e, bank, t=t: e.tensor_tensor(k.xn[:, t, :], bank[:, 0:D], v[:, t, :], ALU.add)))
        matmul_pass(nc, k, jobs)
        layer_norm(nc, k, k.xn, k.xn, 1e-5)
        to_features(nc, k, k.xn, k.xnT, scale=k.col("L2a_gamma"), bias=k.col("L2a_beta"))
        residual_linear(nc, k, k.xnT, w["wfc"], DC, "L2a_bfc", k.x)


def stage_L2_ffn(nc, k, ins):
    normed(nc, k)
    with Stage(nc, "L2f") as st:
        GD = 16
        redT, wg = st.sb("redT", [P, DC, GD]), st.sb("wg", [E8, GD])
        wgT = st.sb("wgT", [GD, E8])
        loaded = load_block(nc, k, [(redT[:], wk(ins["L2f_redT"])), (wg[:], ins["L2f_wg"])])
        sq, norm = st.sb("sq", [E8, GD]), st.sb("norm", [E8, 1])
        xr = st.sb("xr", [GD, TOK])
        logits, top = st.sb("logits", [P, NT, E8]), st.sb("top", [P, NT, 8])
        idx, idxf = st.sb("idx", [P, NT, 8], U32), st.sb("idxf", [P, NT, 8])
        ex, score = st.sb("ex", [P, NT, E8]), st.sb("score", [P, NT, 1])
        vector_wait(nc, k, loaded)

        def squares(dve, link):
            link(dve.tensor_tensor(sq[:], wg[:], wg[:], ALU.mult))
            link(dve.tensor_reduce(norm[:], sq[:], AX.X, ALU.add))

        vector_block(nc, k, squares)
        scalar_block(nc, k, lambda act, link: link(act.activation(norm[:], norm[:], ACT.Sqrt)))

        def unit(dve, link):
            link(dve.tensor_scalar(norm[:], norm[:], 1e-4, None, ALU.max))
            link(dve.reciprocal(norm[:], norm[:]))
            link(dve.tensor_scalar(wg[:], wg[:], norm[:, 0:1], None, ALU.mult))

        vector_block(nc, k, unit)
        jobs = [Job([(lambda bank: bank[0:GD, 0:E8], [(wg[:], None)])], "dve",
                    lambda e, bank: e.tensor_copy(wgT[:], bank[0:GD, 0:E8]))]
        for n in range(NHALF):
            jobs.append(Job([(lambda bank: bank[0:GD, :], [
                (redT[:, c, :], k.xnT[:, c, n * BANK:(n + 1) * BANK]) for c in range(DC)])], "act",
                lambda e, bank, n=n: e.activation(xr[:, n * BANK:(n + 1) * BANK], bank[0:GD, :], ACT.Copy)))
        matmul_pass(nc, k, jobs)
        groups = [(lambda bank, t=t: bank[:, t * E8:(t + 1) * E8], [(xr[:, t * P:(t + 1) * P], wgT[:])])
                  for t in range(NT)]
        matmul_pass(nc, k, [Job(groups, "dve", lambda e, bank: e.tensor_copy(
            logits[:].rearrange("p t e -> p (t e)"), bank[:, 0:NT * E8]))])

        def pick(dve, link):
            for t in range(NT):
                link(dve.max(top[:, t, :], logits[:, t, :]))
                link(dve.max_index(idx[:, t, :], top[:, t, :], logits[:, t, :]))
            link(dve.tensor_copy(idxf[:], idx[:]))
            link(dve.tensor_tensor(ex[:], logits[:], top[:, :, 0:1].broadcast_to((P, NT, E8)), ALU.subtract))

        vector_block(nc, k, pick)
        scalar_block(nc, k, lambda act, link: link(act.activation(ex[:], ex[:], ACT.Exp)))

        def score_gates(dve, link):
            link(dve.tensor_reduce(score[:, :, 0], ex[:], AX.X, ALU.add))
            link(dve.reciprocal(score[:, :, 0], score[:, :, 0]))
            link(dve.tensor_tensor(ex[:], k.iota8[:].unsqueeze(1).broadcast_to((P, NT, E8)),
                                   idxf[:, :, 0:1].broadcast_to((P, NT, E8)), ALU.is_equal))

        vector_block(nc, k, score_gates)
        rows, owner = place_tokens(nc, k, st, ex[:], 1)
        experts(nc, k, "L2e", ins["L2f_w1"], None, ins["L2f_w2"], 1024, rows, owner, score, 1,
                ins["L2f_b1"], ins["L2f_b2"])


def stage_L3_cross(nc, k, ins):
    normed(nc, k)
    with Stage(nc, "L3x") as st:
        attT = st.sb("attT", [P, DC, TOK])
        silu_cross_attention(nc, k, "L3c", ins, attT)
        add_transposed(nc, k, attT, k.x)


def stage_L3_attn(nc, k, ins):
    normed(nc, k)
    HID = 1024
    with Stage(nc, "L3a") as st:
        shapes = {"in_w": D, "actp_w": D, "qk_w": 2 * D, "out_w": D, "fc1_w": HID}
        w = {n: st.sb(n, [P, DC, dout]) for n, dout in shapes.items()}
        w["fc2_w"] = st.sb("fc2_w", [P, HID // P, D])
        loaded = load_block(nc, k, [(w[n][:], wk(ins["L3a_" + n])) for n in w])
        u = st.sb("u", [P, DC, TOK])
        u2 = st.sb("u2", [P, DC, TOK])
        gate = st.sb("gate", [P, DC, TOK])
        xi = st.sb("xi", [P, DC, TOK])
        qk = st.sb("qk", [P, 2 * DC, TOK])
        tok = st.sb("tok", [P, NT, D])

        def cpe1(dve, link):
            for c in range(DC):
                conv3(dve, link, u[:, c, :], k.xnT[:, c, :], k.col("L3_cpe1_w")[:, 3 * c:3 * c + 3],
                      k.col("L3_cpe1_b")[:, c:c + 1])
            link(dve.tensor_tensor(u[:], u[:], k.xnT[:], ALU.add))

        vector_block(nc, k, cpe1)
        add_transposed(nc, k, u, tok, add=False)
        layer_norm(nc, k, tok, tok, 1e-5)
        to_features(nc, k, tok, k.xnT, scale=k.col("L3_n1g"), bias=k.col("L3_n1b"))
        jobs = linear_jobs(w["actp_w"], k.xnT, DC, D, add_bias(k.col("L3_actp_b"), ACT.Silu)(gate))
        jobs += linear_jobs(w["in_w"], k.xnT, DC, D, lambda e, bank, m, n: e.tensor_scalar(
            u2[:, m, n * BANK:(n + 1) * BANK], bank, k.col("L3_in_b")[:, m:m + 1], None, ALU.add), by="dve")
        matmul_pass(nc, k, jobs, [loaded])

        def dwc(dve, link):
            for c in range(DC):
                conv3(dve, link, xi[:, c, :], u2[:, c, :], k.col("L3_dwc_w")[:, 3 * c:3 * c + 3],
                      k.col("L3_dwc_b")[:, c:c + 1])

        vector_block(nc, k, dwc)
        scalar_block(nc, k, lambda act, link: link(act.activation(xi[:], xi[:], ACT.Silu)))
        with Stage(nc, "L3q") as s2:
            pos = s2.sb("pos", [P, 2 * DC, TOK])
            rope = s2.sb("rope", [P, 2 * DC, TOK])
            k_tok, v_tok = s2.sb("k_tok", [S, B, D]), s2.sb("v_tok", [S, B, D])
            kmean = s2.sb("kmean", [P, DC, B])
            zd = s2.sb("zd", [P, DC, TOK])
            kv = s2.sb("kv", [P, B, DC, P])
            matmul_pass(nc, k, linear_jobs(w["qk_w"], xi, DC, 2 * D, lambda e, bank, m, n: e.activation(
                pos[:, m, n * BANK:(n + 1) * BANK], bank, ACT.Identity, bias=k.col("L3_qk_b")[:, m:m + 1])))
            elu_plus_one(nc, k, qk, pos)
            jobs = []
            for m in range(2 * DC):
                for n in range(NHALF):
                    jobs.append(Job([(full, [(k.rotation[:, m % DC, :], qk[:, m, n * BANK:(n + 1) * BANK])])], "act",
                                    lambda e, bank, m=m, n=n: e.activation(rope[:, m, n * BANK:(n + 1) * BANK],
                                                                           bank, ACT.Copy)))
            matmul_pass(nc, k, jobs)

            def means(dve, link):
                link(dve.tensor_reduce(kmean[:], qk[:, DC:2 * DC, :].rearrange("p c (b s) -> p c b s", s=S),
                                       AX.X, ALU.add))
                link(dve.tensor_scalar(kmean[:], kmean[:], 1.0 / S, None, ALU.mult))
                for c in range(DC):
                    link(dve.tensor_tensor(zd[:, c, :].rearrange("p (b s) -> p b s", s=S),
                                           qk[:, c, :].rearrange("p (b s) -> p b s", s=S),
                                           kmean[:, c, :].unsqueeze(2).broadcast_to((P, B, S)), ALU.mult))

            vector_block(nc, k, means)
            jobs = []
            for c in range(DC):
                for n in range(NHALF):
                    jobs.append(Job([(full, [(k.same_head[:], zd[:, c, n * BANK:(n + 1) * BANK])])], "dve",
                                    lambda e, bank, c=c, n=n: e.tensor_scalar(u2[:, c, n * BANK:(n + 1) * BANK],
                                                                              bank, 1e-6, None, ALU.add)))
            for src, dst in ((rope[:, DC:2 * DC, :], k_tok), (xi, v_tok)):
                for pair in range(B // 2):
                    groups = [(lambda bank, h=h, c=c: bank[0:S, h * D + c * P:h * D + (c + 1) * P],
                               [(src[:, c, (2 * pair + h) * S:(2 * pair + h + 1) * S], None)])
                              for h in range(2) for c in range(DC)]
                    out = dst[:, 2 * pair:2 * pair + 2, :].rearrange("p b d -> p (b d)")
                    jobs.append(Job(groups, "act", lambda e, bank, out=out: e.activation(out, bank[0:S, :], ACT.Copy)))
            matmul_pass(nc, k, jobs)
            vector_block(nc, k, lambda dve, link: link(dve.reciprocal(u2[:], u2[:])))
            jobs = []
            for pair in range(B // 2):
                groups = [(lambda bank, h=h, c=c: bank[:, (h * DC + c) * P:(h * DC + c + 1) * P],
                           [(k_tok[:, 2 * pair + h, c * P:(c + 1) * P], v_tok[:, 2 * pair + h, c * P:(c + 1) * P])])
                          for h in range(2) for c in range(DC)]
                out = kv[:, 2 * pair:2 * pair + 2, :, :].rearrange("p b c n -> p (b c) n")
                jobs.append(Job(groups, "dve", lambda e, bank, out=out: e.scalar_tensor_tensor(
                    out, bank.rearrange("p (a n) -> p a n", n=P), 1.0 / S,
                    k.same_head[:].unsqueeze(1).broadcast_to((P, 2 * DC, P)), ALU.mult, ALU.mult)))
            matmul_pass(nc, k, jobs)
            jobs = []
            for c in range(DC):
                for n in range(NHALF):
                    groups = [(lambda bank, b=b: bank[:, b * S:(b + 1) * S],
                               [(kv[:, 8 * n + b, c, :], rope[:, c, (8 * n + b) * S:(8 * n + b + 1) * S])])
                              for b in range(8)]
                    sl = slice(n * BANK, (n + 1) * BANK)
                    jobs.append(Job(groups, "dve", lambda e, bank, c=c, sl=sl: e.tensor_tensor(
                        zd[:, c, sl], bank, u2[:, c, sl], ALU.mult)))
            matmul_pass(nc, k, jobs)

            def lepe(dve, link):
                for c in range(DC):
                    conv3(dve, link, u2[:, c, :], xi[:, c, :], k.col("L3_lepe_w")[:, 3 * c:3 * c + 3],
                          k.col("L3_lepe_b")[:, c:c + 1])
                link(dve.tensor_tensor(zd[:], zd[:], u2[:], ALU.add))
                link(dve.tensor_tensor(xi[:], zd[:], gate[:], ALU.mult))

            vector_block(nc, k, lepe)
        jobs = linear_jobs(w["out_w"], xi, DC, D, lambda e, bank, m, n: e.scalar_tensor_tensor(
            u[:, m, n * BANK:(n + 1) * BANK], bank, k.col("L3_out_b")[:, m:m + 1],
            u[:, m, n * BANK:(n + 1) * BANK], ALU.add, ALU.add), by="dve")
        matmul_pass(nc, k, jobs)

        def cpe2(dve, link):
            for c in range(DC):
                conv3(dve, link, u2[:, c, :], u[:, c, :], k.col("L3_cpe2_w")[:, 3 * c:3 * c + 3],
                      k.col("L3_cpe2_b")[:, c:c + 1])
            link(dve.tensor_tensor(u[:], u[:], u2[:], ALU.add))

        vector_block(nc, k, cpe2)
        add_transposed(nc, k, u, tok, add=False)
        vector_block(nc, k, lambda dve, link: link(dve.tensor_tensor(k.x[:], k.x[:], tok[:], ALU.add)))
        layer_norm(nc, k, tok, tok, 1e-5)
        to_features(nc, k, tok, k.xnT, scale=k.col("L3_n2g"), bias=k.col("L3_n2b"))
        h1 = st.sb("h1", [P, HID // P, TOK])
        matmul_pass(nc, k, linear_jobs(w["fc1_w"], k.xnT, DC, HID, add_bias(k.col("L3_fc1_b"), ACT.Gelu)(h1)))
        residual_linear(nc, k, h1, w["fc2_w"], HID // P, "L3_fc2_b", k.x)


CAPACITY = int(1.25 * TOK / E8 * 2)


def stage_L3_ffn(nc, k, ins):
    normed(nc, k)
    with Stage(nc, "L3f") as st:
        wgT = st.sb("wgT", [P, DC, E8])
        loaded = load_block(nc, k, [(wgT[:], wk(ins["L3f_router"]))])
        logits, top = st.sb("logits", [P, NT, E8]), st.sb("top", [P, NT, E8])
        kept = st.sb("kept", [P, NT, 2])
        router_logits(nc, k, wgT, logits, loaded)
        rows, owner, gates = top2_gates(nc, k, st, logits, top, kept[:])
        experts(nc, k, "L3e", ins["L3f_w1"], None, ins["L3f_w2"], 1024, rows, owner, gates, 2)


STAGES = [stage_L0_cross, stage_L0_attn, stage_L0_ffn, stage_L1_cross, stage_L1_attn, stage_L1_ffn,
          stage_L2_cross, stage_L2_attn, stage_L2_ffn, stage_L3_cross, stage_L3_attn, stage_L3_ffn]

CONSTS = [("ident", P), ("ones64", P), ("parity", 2), ("blocks8", 8), ("same_head", P), ("causal_rows", S),
          ("causal_keys", S), ("causal_tile", P), ("upto", P), ("iota", 24),
          ("rope_cos", S), ("rope_sin", S), ("rotation", DC * P)]
N_CONST = sum(w for _, w in CONSTS)


def constants():
    p = np.arange(P)
    t = {}
    t["ident"] = np.eye(P)
    t["ones64"] = np.ones((P, P))
    t["parity"] = (p[:, None] // HD % 2 == np.arange(2)[None])
    t["blocks8"] = (p[:, None] // HD == np.arange(8)[None])
    t["same_head"] = (p[:, None] // HD == p[None] // HD)
    t["causal_rows"] = np.where(np.arange(S)[None] > p[:, None] % S, NEG, 0.0)
    t["causal_keys"] = (p[:, None] % S <= np.arange(S)[None])
    t["causal_tile"] = np.where((p[:, None] // S == p[None] // S) & (p[None] <= p[:, None]), 0.0, NEG)
    t["upto"] = (p[:, None] <= p[None])
    t["iota"] = np.broadcast_to(np.arange(24)[None], (P, 24))
    half = P // 2
    inv = (np.float32(1.0) / np.float32(10000.0) ** (np.arange(0, P, 2, dtype=np.float32) / np.float32(P)))
    ang = (np.arange(S, dtype=np.float32)[None] * inv[p % half][:, None]).astype(np.float32)
    t["rope_cos"] = np.cos(ang)
    t["rope_sin"] = np.where(p[:, None] < half, -1.0, 1.0) * np.sin(ang)
    kmax = D // 2
    theta = (np.float32(1.0) / np.float32(10000.0) ** (np.arange(kmax, dtype=np.float32) / np.float32(kmax)))
    rot = np.zeros((P, DC, P))
    for c in range(DC):
        for m in range(P // 2):
            cos, sin = np.cos(theta[c * half + m]), np.sin(theta[c * half + m])
            rot[2 * m, c, 2 * m], rot[2 * m + 1, c, 2 * m] = cos, -sin
            rot[2 * m, c, 2 * m + 1], rot[2 * m + 1, c, 2 * m + 1] = sin, cos
    t["rotation"] = rot.reshape(P, DC * P)
    return np.concatenate([np.asarray(t[n], np.float32).reshape(P, w) for n, w in CONSTS], axis=1)


def build(nc, ins, out, stages=STAGES):
    with ExitStack() as ctx:
        k = Kit()

        def sb(name, shape, dt=F32):
            return ctx.enter_context(nc.sbuf_tensor(name, shape, dt))

        def sem(name):
            return ctx.enter_context(nc.semaphore(name))

        k.ps = ctx.enter_context(nc.psum_tensor("ps", [P, 8, BANK], F32))
        k.x, k.xn, k.xnT = sb("x", [P, NT, D]), sb("xn", [P, NT, D]), sb("xnT", [P, DC, TOK])
        k.stats, k.mv, k.rstd = sb("stats", [P, NT, 6]), sb("mv", [P, NT, 2]), sb("rstd", [P, 3, NT])
        consts = sb("consts_sb", [P, N_CONST])

        def table(name):
            names = [n for n, _ in CONSTS]
            at = sum(w for _, w in CONSTS[:names.index(name)])
            return consts[:, at:at + CONSTS[names.index(name)][1]]

        k.ident, k.ones64, k.parity, k.blocks8 = table("ident"), table("ones64"), table("parity"), table("blocks8")
        k.same_head, k.upto, k.iota = table("same_head"), table("upto"), table("iota")
        k.iota8 = k.iota[:, 0:E8]
        k.causal_rows, k.causal_keys, k.causal_tile = table("causal_rows"), table("causal_keys"), table("causal_tile")
        k.rope_cos, k.rope_sin = table("rope_cos"), table("rope_sin")
        k.rotation = table("rotation").rearrange("p (c n) -> p c n", n=P)
        k.ones_row = k.ones64
        cols, rows = sb("cols_sb", [P, NCOLS]), sb("rows_sb", [1, len(ROWS), D])
        k.col = lambda n: cols[:, COL_AT[n][0]:COL_AT[n][0] + COL_AT[n][1]]
        k.row = lambda n: rows[0:1, ROWS.index(n), :]
        k.filled, k.act_drained, k.dve_drained = sem("filled"), sem("act_drained"), sem("dve_drained")
        k.weights, k.ln_step, k.ln_root = sem("weights"), sem("ln_step"), sem("ln_root")
        k.dve_link, k.act_link, k.start, k.stored = sem("dve_link"), sem("act_link"), sem("start"), sem("stored")
        k.tick = sem("tick")
        k.sorted_in = nc.dram_tensor("sorted_in", (expert_tiles(2) * P, D), F32).ap()
        k.zeroed, k.zeros_made = sem("zeroed"), sem("zeros_made")
        k.n_filled = k.n_act = k.n_dve = k.n_weights = k.n_ln = k.n_root = k.n_dve_link = k.n_act_link = 0

        with nc.Block() as block:

            @block.sync
            def _(sp):
                sp.dma_start(k.x[:], ins["x"].rearrange("(t p) d -> p t d", p=P)).then_inc(k.start, 16)
                sp.dma_start(consts[:], ins["consts"]).then_inc(k.start, 16)
                sp.dma_start(cols[:], ins["cols"]).then_inc(k.start, 16)
                sp.dma_start(rows[:], ins["rows"]).then_inc(k.start, 16)
                sp.wait_ge(k.zeros_made, 1)
                for part in range(ZERO_PARTS):
                    n = min(NT, expert_tiles(2) - part * NT)
                    sp.dma_start(k.sorted_in.rearrange("(t p) d -> p t d", p=P)[:, part * NT:part * NT + n, :],
                                 k.xn[:, 0:n, :]).then_inc(k.zeroed, 16)
                sp.wait_ge(k.start, START)
                sp.wait_ge(k.zeroed, 16 * ZERO_PARTS)

            @block.vector
            def _(dve):
                dve.memset(k.xn[:], 0.0).then_inc(k.zeros_made, 1)

        for stage in stages:
            stage(nc, k, ins)

        with nc.Block() as block:

            @block.sync
            def _(sp):
                sp.dma_start(out.rearrange("(t p) d -> p t d", p=P), k.x[:]).then_inc(k.stored, 16)
                sp.wait_ge(k.stored, 16)


def laid_out(v):
    a = {n: np.asarray(x) for n, x in v.items()}
    o = {"x": a["x"].reshape(TOK, D), "ctx": a["ctx_1024"],
         "ctxT": a["ctx_1024"].transpose(0, 2, 1).reshape(B, DC, P, M),
         "mask": a["mask_BxSxS2_bk1"], "maskT": a["mask_1xSxS2_ff0"][0].T}
    half = P // 2

    def swap(w):
        return np.concatenate([w[..., half:], w[..., :half]], axis=-1)

    for n in ("wq", "wqc", "wqr", "wkv", "wkr", "wkc", "wv", "wo"):
        o["L0_" + n] = a["L0_attn_" + n]
    o["L0_wqr_sw"], o["L0_wkr_sw"] = swap(a["L0_attn_wqr"]), swap(a["L0_attn_wkr"])
    o["L0_Wg"] = a["L0_ffn_Wg"].T
    o["L0_W1"], o["L0_W2"] = (a["L0_ffn_" + n].transpose(0, 2, 1) for n in ("W1", "W2"))
    o["L0_W3"] = a["L0_ffn_W3"].transpose(0, 2, 1)
    o["L1x_Wq"], o["L1x_WkT"] = a["L1_xattn_Wq"], a["L1_xattn_Wk"].T
    o["L1x_Wv"], o["L1x_Wo"] = a["L1_xattn_Wv"], a["L1_xattn_Wo"]
    o["L1a_wqkv"], o["L1a_wo"] = a["L1_attn_w_qkv"].T, a["L1_attn_w_out"].T
    o["L1f_w1"], o["L1f_w2"] = a["L1_ffn_w1"].T, a["L1_ffn_w2"].T
    for n in "qkv":
        o["L2x_w" + n] = a["L2_xattn_kernel_" + n][0, 0]
    for n, m in (("wq", "Wq"), ("wk", "Wk"), ("wv", "Wv"), ("wfc", "Wfc")):
        o["L2a_" + n] = a["L2_attn_" + m]
    o["L2f_redT"], o["L2f_wg"] = a["L2_ffn_wg_red"].T, a["L2_ffn_wg"]
    o["L2f_w1"], o["L2f_w2"] = a["L2_ffn_w1"], a["L2_ffn_w2"]
    o["L2f_b1"] = a["L2_ffn_b1"].reshape(E8, 8, P).transpose(0, 2, 1)
    o["L2f_b2"] = a["L2_ffn_b2"].reshape(E8, 1, D)
    for n in ("in_w", "actp_w", "qk_w", "out_w", "fc1_w", "fc2_w"):
        o["L3a_" + n] = a["L3_attn_" + n]
    o["L3f_router"] = a["L3_ffn_router_w"].T
    o["L3f_w1"], o["L3f_w2"] = a["L3_ffn_w1"], a["L3_ffn_w2"]

    def taps(w):
        return w[:, 0, :].reshape(-1, P, 3).transpose(1, 0, 2).reshape(P, -1)

    def col(b):
        if b.size < P:
            b = np.concatenate([b, np.zeros(P - b.size, np.float32)])
        return b.reshape(-1, P).T

    c = {"L0_bq": a["L0_attn_bq"], "L0_bkv": a["L0_attn_bkv"], "L0_bqc": a["L0_attn_bqc"],
         "L0_bkc": a["L0_attn_bkc"], "L0_bqr": a["L0_attn_bqr"], "L0_bkr": a["L0_attn_bkr"],
         "L0_bqr_sw": swap(a["L0_attn_bqr"]), "L0_bkr_sw": swap(a["L0_attn_bkr"]),
         "L1a_bqk": a["L1_attn_b_qkv"][:2 * D], "L1f_cb": a["L1_ffn_conv_b"],
         "L2x_bq": a["L2_xattn_bias_q"], "L2x_bk": a["L2_xattn_bias_k"],
         "L2a_gamma": a["L2_attn_gamma"], "L2a_beta": a["L2_attn_beta"]}
    for n, m in (("cpe1_b", "cpe1_b"), ("n1g", "norm1_g"), ("n1b", "norm1_b"), ("in_b", "in_b"),
                 ("actp_b", "actp_b"), ("dwc_b", "dwc_b"), ("qk_b", "qk_b"), ("lepe_b", "lepe_b"),
                 ("out_b", "out_b"), ("cpe2_b", "cpe2_b"), ("n2g", "norm2_g"), ("n2b", "norm2_b"),
                 ("fc1_b", "fc1_b")):
        c["L3_" + n] = a["L3_attn_" + m]
    c = {n: col(x) for n, x in c.items()}
    c["L1f_cw"] = taps(a["L1_ffn_conv_w"])
    for n in ("cpe1_w", "dwc_w", "lepe_w", "cpe2_w"):
        c["L3_" + n] = taps(a["L3_attn_" + n])
    o["cols"] = np.concatenate([c[n] for n, _ in COLS], axis=1)
    r = {"L0_bv": a["L0_attn_bv"], "L0_bo": a["L0_attn_bo"], "L1x_bo": a["L1_xattn_bo"],
         "L1a_bv": a["L1_attn_b_qkv"][2 * D:], "L1a_bo": a["L1_attn_b_out"], "L2x_bv": a["L2_xattn_bias_v"],
         "L2a_bfc": a["L2_attn_bfc"], "L3_fc2_b": a["L3_attn_fc2_b"]}
    o["rows"] = np.stack([r[n] for n in ROWS])[None]
    o["consts"] = constants()
    return {n: np.ascontiguousarray(x) for n, x in o.items()}


def kernel(**inputs):
    import concourse.bacc as _bacc
    from concourse.bass_utils import run_bass_kernel_spmd as _run

    arrays = {f"in_{n}": x for n, x in laid_out(inputs).items()}
    nc = _bacc.Bacc("TRN2", target_bir_lowering=False, num_devices=1)
    ins = {n[3:]: nc.dram_tensor(n, x.shape, mybir.dt.from_np(x.dtype), kind="ExternalInput").ap()
           for n, x in arrays.items()}
    out = nc.dram_tensor("out_x", (TOK, D), F32, kind="ExternalOutput").ap()
    build(nc, ins, out)
    r = _run(nc, [arrays], core_ids=[0])
    return r.results[0]["out_x"].reshape(B, S, D)
```

```python
from contextlib import ExitStack

import numpy as np

import concourse.bass as bass
from concourse import mybir

F32 = mybir.dt.float32
U32 = mybir.dt.uint32
U8 = mybir.dt.uint8
BF16 = mybir.dt.bfloat16
ALU = mybir.AluOpType
ACT = mybir.ActivationFunctionType
AX = mybir.AxisListType

P = 128
B, S, D = 16, 64, 256
M = 1601
TOK = B * S
NT = TOK // P
DC = D // P
KT = (M + P - 1) // P
KFULL = M // P
KREST = M - KFULL * P
BANK = 512
NHALF = TOK // BANK
H16 = 16
HD = D // H16
E8 = 8
PAIRS = H16 // 2
PAIR_F = 2 * HD
NEG = -1.0e30
START = 64

CHUNKS = [(c, min(BANK, M - c)) for c in range(0, M, BANK)]
NCH = len(CHUNKS)
ZERO_PARTS = 3
THIRD = 32


def key_rows(t):
    return P if t < KFULL else KREST


COLS = [
    ("L0_bq", 1), ("L0_bkv", 1), ("L0_bqc", 1), ("L0_bkc", 1), ("L0_bqr", 1), ("L0_bkr", 1),
    ("L0_bqr_sw", 1), ("L0_bkr_sw", 1), ("L1a_bqk", 4), ("L1f_cw", 24), ("L1f_cb", 8),
    ("L2x_bq", 2), ("L2x_bk", 2), ("L2a_gamma", 2), ("L2a_beta", 2),
    ("L3_cpe1_w", 6), ("L3_cpe1_b", 2), ("L3_n1g", 2), ("L3_n1b", 2), ("L3_in_b", 2), ("L3_actp_b", 2),
    ("L3_dwc_w", 6), ("L3_dwc_b", 2), ("L3_qk_b", 4), ("L3_lepe_w", 6), ("L3_lepe_b", 2),
    ("L3_out_b", 2), ("L3_cpe2_w", 6), ("L3_cpe2_b", 2), ("L3_n2g", 2), ("L3_n2b", 2), ("L3_fc1_b", 8),
]
ROWS = ["L0_bv", "L0_bo", "L1x_bo", "L1a_bv", "L1a_bo", "L2x_bv", "L2a_bfc", "L3_fc2_b"]
COL_AT, _n = {}, 0
for _name, _w in COLS:
    COL_AT[_name] = (_n, _w)
    _n += _w
NCOLS = _n


class Signal:

    def __init__(self, nc, ctx, name, credit=0):
        self.sem = ctx.enter_context(nc.semaphore(name))
        self.credit = credit

    def at(self, count):
        return count + self.credit


class Kit:
    pass


def give_credits(nc, signals):
    with nc.Block() as block:

        @block.sync
        def _(sp):
            for s in signals:
                if s.credit:
                    sp.sem_inc(s.sem, s.credit)


class Job:

    def __init__(self, groups, by, drain):
        self.groups, self.by, self.drain = groups, by, drain


def matmul_pass(nc, k, jobs, loaded=()):
    base_f, base_a, base_v = k.n_filled, k.n_act, k.n_dve
    nth = []
    na = nv = 0
    for job in jobs:
        if job.by == "act":
            na += 1
            nth.append((k.act_drained, base_a + na))
        else:
            nv += 1
            nth.append((k.dve_drained, base_v + nv))
    with nc.Block() as block:

        @block.tensor
        def _(pe):
            for sem, value in loaded:
                pe.wait_ge(sem, value)
            for j, job in enumerate(jobs):
                bank = k.ps[:, j % 8, :]
                if j >= 8:
                    pe.wait_ge(*nth[j - 8])
                for where, products in job.groups:
                    out = where(bank)
                    for n, (lhsT, rhs) in enumerate(products):
                        if rhs is None:
                            rows = lhsT.shape[0]
                            last = pe.transpose(out, lhsT, k.ident[0:rows, 0:rows])
                        else:
                            last = pe.matmul(out, lhsT, rhs, start=(n == 0), stop=(n == len(products) - 1))
                last.then_inc(k.filled, 1)

        @block.scalar
        def _(act):
            for j, job in enumerate(jobs):
                if job.by == "act":
                    act.wait_ge(k.filled, base_f + j + 1)
                    job.drain(act, k.ps[:, j % 8, :]).then_inc(k.act_drained, 1)

        @block.vector
        def _(dve):
            for j, job in enumerate(jobs):
                if job.by == "dve":
                    dve.wait_ge(k.filled, base_f + j + 1)
                    job.drain(dve, k.ps[:, j % 8, :]).then_inc(k.dve_drained, 1)

    k.n_filled += len(jobs)
    k.n_act += na
    k.n_dve += nv


def full(bank):
    return bank


def load_block(nc, k, copies):
    with nc.Block() as block:

        @block.sync
        def _(sp):
            for dst, src in copies:
                sp.dma_start(dst, src).then_inc(k.weights, 16)

    k.n_weights += 16 * len(copies)
    return (k.weights, k.n_weights)


def wk(w):
    return w.rearrange("(c p) n -> p c n", p=P)


def layer_norm(nc, k, src, out, eps):
    with nc.Block() as block:
        base = k.n_ln

        @block.vector
        def _(dve):
            for t in range(NT):
                dve.bn_stats(k.stats[:, t, :], src[:, t, :]).then_inc(k.ln_step, 1)
            for t in range(NT):
                dve.wait_ge(k.ln_step, base + t + 1)
                dve.bn_aggr(k.mv[:, t, :], k.stats[:, t, :]).then_inc(k.ln_step, 1)
            dve.wait_ge(k.ln_step, base + 2 * NT)
            dve.tensor_scalar(k.rstd[:, 0, :], k.mv[:, :, 1], eps, None, ALU.add).then_inc(k.ln_step, 1)
            dve.wait_ge(k.ln_root, k.n_root + 1)
            dve.reciprocal(k.rstd[:, 2, :], k.rstd[:, 1, :]).then_inc(k.ln_step, 1)
            dve.wait_ge(k.ln_step, base + 2 * NT + 2)
            for t in range(NT):
                dve.tensor_scalar(out[:, t, :], src[:, t, :], k.mv[:, t, 0:1], k.rstd[:, 2, t:t + 1],
                                  ALU.subtract, ALU.mult).then_inc(k.ln_step, 1)

        @block.scalar
        def _(act):
            act.wait_ge(k.ln_step, base + 2 * NT + 1)
            act.activation(k.rstd[:, 1, :], k.rstd[:, 0, :], ACT.Sqrt).then_inc(k.ln_root, 1)

    k.n_ln += 3 * NT + 2
    k.n_root += 1


def to_features(nc, k, src, dst, chunks=DC, scale=None, bias=None):
    jobs = []
    for c in range(chunks):
        for n in range(NHALF):
            groups = [(lambda bank, t=t: bank[:, t * P:(t + 1) * P],
                       [(src[:, n * 4 + t, c * P:(c + 1) * P], None)]) for t in range(4)]
            out = dst[:, c, n * BANK:(n + 1) * BANK]
            if scale is not None:
                jobs.append(Job(groups, "dve", lambda e, bank, out=out, c=c: e.tensor_scalar(
                    out, bank, scale[:, c:c + 1], bias[:, c:c + 1], ALU.mult, ALU.add)))
            elif (c + n) % 2:
                jobs.append(Job(groups, "dve", lambda e, bank, out=out: e.tensor_copy(out, bank)))
            else:
                jobs.append(Job(groups, "act", lambda e, bank, out=out: e.activation(out, bank, ACT.Copy)))
    matmul_pass(nc, k, jobs)


def add_transposed(nc, k, srcT, dst, add=True):
    jobs = []
    for t in range(NT):
        groups = [(lambda bank, c=c: bank[:, c * P:(c + 1) * P], [(srcT[:, c, t * P:(t + 1) * P], None)])
                  for c in range(DC)]
        if add:
            jobs.append(Job(groups, "dve", lambda e, bank, t=t: e.tensor_tensor(
                dst[:, t, :], dst[:, t, :], bank[:, 0:D], ALU.add)))
        else:
            jobs.append(Job(groups, "act", lambda e, bank, t=t: e.activation(
                dst[:, t, :], bank[:, 0:D], ACT.Copy)))
    matmul_pass(nc, k, jobs)


def linear_jobs(wt, xT, kchunks, width, drain, by="act", krows=P):
    jobs = []
    for m0 in range(0, width, P):
        mw = min(P, width - m0)
        for n in range(NHALF):
            products = [(wt[0:krows, c, m0:m0 + mw], xT[0:krows, c, n * BANK:(n + 1) * BANK])
                        for c in range(kchunks)]
            jobs.append(Job([(lambda bank, mw=mw: bank[0:mw, :], products)], by,
                            lambda e, bank, m=m0 // P, n=n, mw=mw: drain(e, bank[0:mw, :], m, n)))
    return jobs


def residual_linear(nc, k, xT, w, kchunks, bias_row, dst, loaded=(), add=True):
    jobs = []
    for t in range(NT):
        products = [(xT[:, c, t * P:(t + 1) * P], w[:, c, :]) for c in range(kchunks)]
        if bias_row is not None:
            products.append((k.ones3[:, :], k.row(bias_row)))
        if add:
            jobs.append(Job([(lambda bank: bank[:, 0:D], products)], "dve", lambda e, bank, t=t: e.tensor_tensor(
                dst[:, t, :], dst[:, t, :], bank[:, 0:D], ALU.add)))
        else:
            jobs.append(Job([(lambda bank: bank[:, 0:D], products)], "act", lambda e, bank, t=t: e.activation(
                dst[:, t, :], bank[:, 0:D], ACT.Copy)))
    matmul_pass(nc, k, jobs, loaded)


def softmax_cross_attention(nc, k, name, ins, heads16, q_all):
    TPB = PAIRS if heads16 else 4
    U = 2 * TPB
    with ExitStack() as ctx:
        def sb(n, shape, dt=F32):
            return ctx.enter_context(nc.sbuf_tensor(f"{name}_{n}", shape, dt))

        def signal(n, credit=0):
            return Signal(nc, ctx, f"{name}_{n}", credit)

        rows_sb = sb("rows", [P, 2, KT, D])
        keysT = sb("keysT", [P, 2, DC, M])
        prob = sb("prob", [P, 2, M])
        probT = sb("probT", [P, 2, KT * P])
        mx = sb("mx", [P, 2, NCH])
        nmx = sb("nmx", [P, 2, 1])
        sums = sb("sums", [P, U])
        rinv = sb("rinv", [P, U])
        if heads16:
            mask8 = sb("mask8", [P, 2, M], U8)
            maskf = sb("maskf", [P, 2, M])
            q_sb = sb("q", [P, 2, H16, S])
            att = sb("att", [P, D])
        else:
            q_sb = sb("q", [P, 2, DC, BANK])

        loaded = [signal(f"loaded{j}") for j in range(2)]
        mask_ready = signal("mask_ready", 2)
        q_ready = signal("q_ready")
        s_filled = signal("s_filled")
        s_taken = signal("s_taken", (U + 1) * NCH)
        max_ready = signal("max_ready")
        exp_done = signal("exp_done", 1)
        t_filled = signal("t_filled", 8)
        t_act = signal("t_act", 1)
        t_dve = signal("t_dve", 1)
        av_done = signal("av_done", U + 2)
        r_ready = signal("r_ready")
        o_drained = signal("o_drained", 2)
        x_step = signal("x_step", 1)
        give_credits(nc, [mask_ready, s_taken, exp_done, t_filled, t_act, t_dve, av_done, o_drained, x_step])
        S_BANK, T_BANK, O_BANK = 0, 4, 6
        n_loads = 5 if heads16 else 3
        sflat = k.ps[:, S_BANK:S_BANK + NCH, :].rearrange("p a b -> p (a b)")

        with nc.Block() as block:

            @block.sync
            def _(sp):
                with sp.Fori(0, B // 2) as i:
                    for j in range(2):
                        b = i * 2 + j
                        sp.wait_ge(av_done.sem, i * U + av_done.at(-U + (j + 1) * TPB))
                        sp.dma_start(keysT[:, j, :, :], ins["ctxT"][b].rearrange("c p n -> p c n")
                                     ).then_inc(loaded[j].sem, 16)
                        sp.dma_start(rows_sb[:, j, 0:KFULL, :],
                                     ins["ctx"][b, 0:KFULL * P, :].rearrange("(t p) d -> p t d", p=P)
                                     ).then_inc(loaded[j].sem, 16)
                        sp.dma_start(rows_sb[0:KREST, j, KFULL, :], ins["ctx"][b, KFULL * P:M, :]
                                     ).then_inc(loaded[j].sem, 16)
                        if heads16:
                            sp.wait_ge(mask_ready.sem, i * 2 + mask_ready.at(j - 1))
                            sp.sem_inc(k.tick, 1)
                            for h in range(2):
                                sp.dma_start(mask8[h * S:(h + 1) * S, j, :], ins["mask"][b]
                                             ).then_inc(loaded[j].sem, 16)

            @block.gpsimd
            def _(pool):
                with pool.Fori(0, B // 2) as i:
                    for j in range(2):
                        if heads16:
                            pool.wait_ge(loaded[j].sem, i * 16 * n_loads + 16 * n_loads)
                            pool.wait_ge(s_taken.sem, i * (U * NCH) + s_taken.at(((j + 1) * TPB - U) * NCH))
                            pool.sem_inc(k.tick, 1)
                            pool.tensor_scalar(maskf[:, j, :], mask8[:, j, :], -10000.0, None, ALU.mult
                                               ).then_inc(mask_ready.sem, 1)
                        else:
                            pool.wait_ge(av_done.sem, i * U + av_done.at(-U + (j + 1) * TPB))
                            pool.tensor_copy(q_sb[:, j, :, :], q_all[:, i * 2 + j, :, :]).then_inc(q_ready.sem, 1)

            @block.tensor
            def _(pe):
                with pe.Fori(0, B // 2) as i:
                    def scores(u):
                        j, t = u // TPB, u % TPB
                        if t == 0:
                            pe.wait_ge(loaded[j].sem, i * 16 * n_loads + 16 * n_loads)
                            pe.wait_ge(q_ready.sem, i * 2 + (j + 1))
                        for c, (at, w) in enumerate(CHUNKS):
                            if heads16:
                                pe.wait_ge(s_taken.sem, i * (U * NCH) + s_taken.at(NCH * (u - 1) + c + 1))
                                last = pe.matmul(k.ps[:, S_BANK + c, 0:w], q_sb[:, j, 2 * t:2 * t + 2, :],
                                                 keysT[:, j, t // 4, at:at + w], start=True, stop=True)
                            else:
                                if c == 0:
                                    pe.wait_ge(exp_done.sem, i * U + exp_done.at(u))
                                for f in range(DC):
                                    last = pe.matmul(k.ps[:, S_BANK + c, 0:w], q_sb[:, j, f, t * P:(t + 1) * P],
                                                     keysT[:, j, f, at:at + w], start=(f == 0), stop=(f == DC - 1))
                            last.then_inc(s_filled.sem, 1)

                    def transposes(u, groups):
                        if groups[0] == 0:
                            pe.wait_ge(exp_done.sem, i * U + exp_done.at(u + 1))
                        for g in groups:
                            free = (t_act, t_dve)[g % 2]
                            pe.wait_ge(free.sem, i * (2 * U) + free.at(2 * u + g // 2))
                            for kt in range(4 * g, min(4 * g + 4, KT)):
                                rows = key_rows(kt)
                                last = pe.transpose(k.ps[0:rows, T_BANK + g % 2, (kt % 4) * P:(kt % 4 + 1) * P],
                                                    prob[:, u % 2, kt * P:kt * P + rows], k.ident[:])
                            last.then_inc(t_filled.sem, 1)

                    def values(u, kts):
                        j, t = u // TPB, u % TPB
                        if kts[0] == 0:
                            pe.wait_ge(t_act.sem, i * (2 * U) + t_act.at(2 * u + 2))
                            pe.wait_ge(t_dve.sem, i * (2 * U) + t_dve.at(2 * u + 2))
                            if not heads16:
                                pe.wait_ge(o_drained.sem, i * U + o_drained.at(u - 1))
                            elif t == 0:
                                pe.wait_ge(o_drained.sem, i * 2 + o_drained.at(j - 1))
                        for kt in kts:
                            rows = key_rows(kt)
                            if heads16:
                                out = k.ps[:, O_BANK + j, t * PAIR_F:(t + 1) * PAIR_F]
                                rhs = rows_sb[0:rows, j, kt, t * PAIR_F:(t + 1) * PAIR_F]
                            else:
                                out = k.ps[:, O_BANK + u % 2, 0:D]
                                rhs = rows_sb[0:rows, j, kt, :]
                            last = pe.matmul(out, probT[0:rows, u % 2, kt * P:(kt + 1) * P], rhs,
                                             start=(kt == 0), stop=(kt == KT - 1))
                        if kts[-1] == KT - 1:
                            last.then_inc(av_done.sem, 1)

                    scores(0)
                    for u in range(U):
                        if u + 1 < U:
                            scores(u + 1)
                        transposes(u, (0, 1))
                        if u > 0:
                            values(u - 1, range(0, KT // 2))
                        transposes(u, (2, 3))
                        if u > 0:
                            values(u - 1, range(KT // 2, KT))
                    values(U - 1, range(KT))

            def take_transposes(eng, i, u, free, groups, copy):
                eng.wait_ge(av_done.sem, i * U + av_done.at(u - 1))
                for g in groups:
                    eng.wait_ge(t_filled.sem, i * (4 * U) + t_filled.at(4 * u + g + 1))
                    n = min(4, KT - 4 * g)
                    rows = key_rows(4 * g)
                    copy(probT[0:rows, u % 2, 4 * g * P:(4 * g + n) * P],
                         k.ps[0:rows, T_BANK + g % 2, 0:n * P]).then_inc(free.sem, 1)

            @block.scalar
            def _(act):
                with act.Fori(0, B // 2) as i:
                    def exps(u):
                        act.wait_ge(max_ready.sem, i * U + (u + 1))
                        act.wait_ge(t_filled.sem, i * (4 * U) + t_filled.at(4 * (u - 1)))
                        src = prob[:, u % 2, :] if heads16 else sflat[:, 0:M]
                        act.activation(prob[:, u % 2, :], src, ACT.Exp, bias=nmx[:, u % 2, :],
                                       accum_out=sums[:, u:u + 1]).then_inc(exp_done.sem, 1)

                    def weighted_rows(u):
                        act.wait_ge(av_done.sem, i * U + av_done.at(u + 1))
                        act.wait_ge(r_ready.sem, i * U + (u + 1))
                        act.activation(q_all.rearrange("p b f n -> p b (f n)")[
                                           :, i * 2 + u // TPB, (u % TPB) * D:(u % TPB + 1) * D],
                                       k.ps[:, O_BANK + u % 2, 0:D], ACT.Copy, scale=rinv[:, u:u + 1]
                                       ).then_inc(o_drained.sem, 1)

                    exps(0)
                    for u in range(U):
                        take_transposes(act, i, u, t_act, (0, 2),
                                        lambda o, s: act.activation(o, s, ACT.Copy))
                        if u + 1 < U:
                            exps(u + 1)
                        if not heads16 and u > 0:
                            weighted_rows(u - 1)
                    if not heads16:
                        weighted_rows(U - 1)

            @block.vector
            def _(dve):
                with dve.Fori(0, B // 2) as i:
                    def maxima(u):
                        j, t = u // TPB, u % TPB
                        if heads16 and t == 0:
                            dve.wait_ge(mask_ready.sem, i * 2 + mask_ready.at(j + 1))
                        dve.wait_ge(t_filled.sem, i * (4 * U) + t_filled.at(4 * (u - 1)))
                        for c, (at, w) in enumerate(CHUNKS):
                            dve.wait_ge(s_filled.sem, i * (U * NCH) + (u * NCH + c + 1))
                            if heads16:
                                dve.sem_inc(k.tick, 1)
                                ins_ = dve.tensor_tensor_reduce(
                                    out=prob[:, u % 2, at:at + w], in0=k.ps[:, S_BANK + c, 0:w],
                                    in1=maskf[:, j, at:at + w], scale=1.0, scalar=-3.0e38, op0=ALU.add,
                                    op1=ALU.max, accum_out=mx[:, u % 2, c:c + 1])
                            else:
                                ins_ = dve.tensor_reduce(mx[:, u % 2, c:c + 1], k.ps[:, S_BANK + c, 0:w], AX.X, ALU.max)
                            ins_.then_inc(s_taken.sem, 1)
                        dve.wait_ge(s_taken.sem, i * (U * NCH) + s_taken.at((u + 1) * NCH))
                        dve.tensor_reduce(nmx[:, u % 2, :], mx[:, u % 2, :], AX.X, ALU.max, negate=True
                                          ).then_inc(max_ready.sem, 1)

                    if heads16:
                        for j in range(2):
                            block_queries(dve, k, q_sb[:, j, :, :], q_all, i * P + j * S, HD ** -0.5
                                          ).then_inc(q_ready.sem, 1)
                    def batch_out(j):
                        dve.wait_ge(exp_done.sem, i * U + exp_done.at((j + 1) * TPB))
                        dve.reciprocal(rinv[:, j * TPB:(j + 1) * TPB], sums[:, j * TPB:(j + 1) * TPB]
                                       ).then_inc(r_ready.sem, 1)
                        dve.wait_ge(r_ready.sem, i * 2 + (j + 1))
                        dve.wait_ge(av_done.sem, i * U + av_done.at((j + 1) * TPB))
                        if j == 0:
                            dve.wait_ge(x_step.sem, i * 3 + x_step.at(0))
                        a4 = att[j * S:(j + 1) * S, :].rearrange("p (t h f) -> p t h f", h=2, f=HD)
                        for h in range(2):
                            o3 = k.ps[h * S:(h + 1) * S, O_BANK + j, 0:TPB * PAIR_F].rearrange(
                                "p (t f) -> p t f", f=PAIR_F)[:, :, h * HD:(h + 1) * HD]
                            r3 = rinv[h * S:(h + 1) * S, j * TPB:(j + 1) * TPB].unsqueeze(2).broadcast_to((S, TPB, HD))
                            ins_ = dve.tensor_tensor(a4[:, :, h, :], o3, r3, ALU.mult)
                            if h == 0:
                                ins_.then_inc(x_step.sem, 1)
                            else:
                                ins_.then_inc(o_drained.sem, 1)

                    maxima(0)
                    for u in range(U):
                        j, t = u // TPB, u % TPB
                        if u + 1 < U:
                            maxima(u + 1)
                        if not heads16:
                            dve.wait_ge(exp_done.sem, i * U + exp_done.at(u + 1))
                            dve.wait_ge(o_drained.sem, i * U + o_drained.at(u - 1))
                            dve.reciprocal(rinv[:, u:u + 1], sums[:, u:u + 1]).then_inc(r_ready.sem, 1)
                        take_transposes(dve, i, u, t_dve, (1, 3), dve.tensor_copy)
                        if heads16 and u > 0 and t == 0:
                            batch_out(u // TPB - 1)
                    if heads16:
                        batch_out(1)
                    if heads16:
                        dve.wait_ge(x_step.sem, i * 3 + x_step.at(2))
                        dve.wait_ge(o_drained.sem, i * 2 + o_drained.at(2))
                        xt = k.x[:, i, :]
                        dve.tensor_tensor(xt, xt, att[:], ALU.add).then_inc(x_step.sem, 1)


def silu_cross_attention(nc, k, name, ins):
    with ExitStack() as ctx:
        def sb(n, shape, dt=F32):
            return ctx.enter_context(nc.sbuf_tensor(f"{name}_{n}", shape, dt))

        def signal(n, credit=0):
            return Signal(nc, ctx, f"{name}_{n}", credit)

        U = 2 * KT
        rows_sb = sb("rows", [P, 2, KT, D])
        keysT = sb("keysT", [P, 2, DC, M])
        q_sb = sb("q", [P, 2, H16, S])
        w_sb = sb("w", [P, 2, H16, S])
        att = sb("att", [P, D])
        zeros = sb("zeros", [P, D], BF16)
        loaded = [signal(f"loaded{j}") for j in range(2)]
        q_ready = signal("q_ready")
        zeros_ready = signal("zeros_ready")
        s_filled = signal("s_filled")
        s_taken = signal("s_taken", 2)
        av_done = signal("av_done", U)
        o_taken = signal("o_taken", 4)
        x_done = signal("x_done", 1)
        give_credits(nc, [s_taken, av_done, o_taken, x_done])
        O_BANK = 6

        with nc.Block() as block:

            @block.sync
            def _(sp):
                with sp.Fori(0, B // 2) as i:
                    for j in range(2):
                        b = i * 2 + j
                        sp.wait_ge(av_done.sem, i * U + av_done.at((j + 1) * KT - U))
                        sp.dma_start(keysT[:, j, :, :], ins["ctxT"][b].rearrange("c p n -> p c n")
                                     ).then_inc(loaded[j].sem, 16)
                        sp.dma_start(rows_sb[:, j, 0:KFULL, :],
                                     ins["ctx"][b, 0:KFULL * P, :].rearrange("(t p) d -> p t d", p=P)
                                     ).then_inc(loaded[j].sem, 16)
                        sp.dma_start(rows_sb[0:KREST, j, KFULL, :], ins["ctx"][b, KFULL * P:M, :]
                                     ).then_inc(loaded[j].sem, 16)

            @block.tensor
            def _(pe):
                pe.wait_ge(zeros_ready.sem, 1)
                with pe.Fori(0, B // 2) as i:
                    def scores(u):
                        j, t = u // KT, u % KT
                        rows = key_rows(t)
                        if t == 0:
                            pe.wait_ge(loaded[j].sem, i * 48 + 48)
                            pe.wait_ge(q_ready.sem, i * 2 + (j + 1))
                        pe.wait_ge(s_taken.sem, i * U + s_taken.at(u - 1))
                        for g in range(DC):
                            last = pe.matmul(k.ps[0:rows, 2 * (u % 2) + g, :], keysT[:, j, g, t * P:t * P + rows],
                                             q_sb[:, j, g * 8:(g + 1) * 8, :], start=True, stop=True)
                        last.then_inc(s_filled.sem, 1)

                    def values(u):
                        j, t = u // KT, u % KT
                        rows = key_rows(t)
                        pe.wait_ge(s_taken.sem, i * U + s_taken.at(u + 1))
                        if t == 0:
                            pe.wait_ge(o_taken.sem, i * 4 + o_taken.at(2 * (j - 1)))
                            pe.matmul(k.ps[:, O_BANK + j, 0:D], zeros[:, 0:P], zeros[:], start=True, stop=False)
                        for pair in range(PAIRS):
                            f = slice(pair * PAIR_F, (pair + 1) * PAIR_F)
                            last = pe.matmul(k.ps[:, O_BANK + j, f], w_sb[0:rows, u % 2, 2 * pair:2 * pair + 2, :],
                                             rows_sb[0:rows, j, t, f], start=False, stop=(t == KT - 1 and pair == PAIRS - 1))
                        last.then_inc(av_done.sem, 1)

                    scores(0)
                    for u in range(U):
                        if u + 1 < U:
                            scores(u + 1)
                        values(u)

            @block.gpsimd
            def _(pool):
                pool.memset(zeros[:], 0.0).then_inc(zeros_ready.sem, 1)

            @block.scalar
            def _(act):
                with act.Fori(0, B // 2) as i:
                    for u in range(U):
                        rows = key_rows(u % KT)
                        act.wait_ge(s_filled.sem, i * U + (u + 1))
                        act.wait_ge(av_done.sem, i * U + av_done.at(u - 1))
                        act.activation(w_sb[0:rows, u % 2, :, :].rearrange("p h q -> p (h q)"),
                                       k.ps[0:rows, 2 * (u % 2):2 * (u % 2) + 2, :].rearrange("p a b -> p (a b)"),
                                       ACT.Silu).then_inc(s_taken.sem, 1)

            @block.vector
            def _(dve):
                with dve.Fori(0, B // 2) as i:
                    for j in range(2):
                        dve.wait_ge(av_done.sem, i * U + av_done.at((j + 1) * KT - U))
                        block_queries(dve, k, q_sb[:, j, :, :], k.xnT, i * P + j * S, 1.0).then_inc(q_ready.sem, 1)
                    for j in range(2):
                        dve.wait_ge(av_done.sem, i * U + av_done.at((j + 1) * KT))
                        if j == 0:
                            dve.wait_ge(x_done.sem, i + x_done.at(0))
                        for h in range(2):
                            own = k.ps[h * S:(h + 1) * S, O_BANK + j, 0:D].rearrange(
                                "p (t f) -> p t f", f=PAIR_F)[:, :, h * HD:(h + 1) * HD]
                            dve.tensor_copy(att[j * S:(j + 1) * S, :].rearrange(
                                "p (t h f) -> p t h f", h=2, f=HD)[:, :, h, :], own).then_inc(o_taken.sem, 1)
                    dve.wait_ge(o_taken.sem, i * 4 + o_taken.at(4))
                    dve.tensor_tensor(k.x[:, i, :], k.x[:, i, :], att[:], ALU.add).then_inc(x_done.sem, 1)


def block_queries(dve, k, out, xT, at, scale):
    for g in range(DC):
        last = dve.scalar_tensor_tensor(out[:, g * 8:(g + 1) * 8, :],
                                        xT[:, g:g + 1, bass.ds(at, S)].broadcast_to((P, 8, S)), scale,
                                        k.blocks8[:].unsqueeze(2).broadcast_to((P, 8, S)), ALU.mult, ALU.mult)
    return last


def take_own_blocks(dve, k, products, own, taken, done, nth, out):
    dve.wait_ge(done.sem, nth * 1 + done.at(0))
    for g in range(DC):
        ins_ = dve.tensor_tensor(own[:, g, :, :], products[:, g, :].rearrange("p (h q) -> p h q", q=S),
                                 k.blocks8[:].unsqueeze(2).broadcast_to((P, H16 // DC, S)), ALU.mult)
    ins_.then_inc(taken.sem, 1)
    dve.wait_ge(taken.sem, nth + taken.at(1))
    dve.tensor_reduce(out, own[:].rearrange("p g h q -> p g q h"), AX.X, ALU.add).then_inc(done.sem, 1)


def relu_cross_attention(nc, k, name, ins, wk_sb, wv_sb, qT, maskT, loaded_weights):
    with ExitStack() as ctx:
        def sb(n, shape, dt=F32):
            return ctx.enter_context(nc.sbuf_tensor(f"{name}_{n}", shape, dt))

        def signal(n, credit=0):
            return Signal(nc, ctx, f"{name}_{n}", credit)

        ctxT = sb("ctxT", [P, 2, DC, M])
        kT = sb("kT", [P, DC, M])
        v = sb("v", [P, KT, D])
        q_sb = sb("q", [P, 2, DC, S])
        lg = sb("lg", [P, KT, S])
        att = sb("att", [P, D])
        bk = k.col("L2x_bk")
        loaded = [signal(f"loaded{j}") for j in range(2)]
        q_ready = signal("q_ready", 2)
        p_filled = signal("p_filled")
        p_taken = signal("p_taken", 8)
        l_filled = signal("l_filled", 1)
        l_relu = signal("l_relu", 2)
        l_ready = signal("l_ready", 2)
        av_done = signal("av_done", 2)
        att_done = signal("att_done", 2)
        x_done = signal("x_done", 1)
        give_credits(nc, [q_ready, p_taken, l_filled, l_relu, l_ready, av_done, att_done, x_done])
        kjobs = [(m, c) for m in range(DC) for c in range(NCH)]
        vjobs = [list(range(t, min(t + 2, KT))) for t in range(0, KT, 2)]
        NJ = len(kjobs) + len(vjobs)
        PB = 4

        with nc.Block() as block:

            @block.sync
            def _(sp):
                with sp.Fori(0, B // 2) as i:
                    for j in range(2):
                        sp.wait_ge(av_done.sem, i * 2 + av_done.at(j - 1))
                        sp.dma_start(ctxT[:, j, :, :], ins["ctxT"][i * 2 + j].rearrange("c p n -> p c n")
                                     ).then_inc(loaded[j].sem, 16)

            @block.gpsimd
            def _(pool):
                with pool.Fori(0, B // 2) as i:
                    for j in range(2):
                        pool.wait_ge(av_done.sem, i * 2 + av_done.at(j - 1))
                        pool.tensor_copy(q_sb[:, j, :, :], qT[:, :, bass.ds(i * P + j * S, S)]
                                         ).then_inc(q_ready.sem, 1)

            @block.tensor
            def _(pe):
                pe.wait_ge(*loaded_weights)
                with pe.Fori(0, B // 2) as i:
                    for j in range(2):
                        pe.wait_ge(loaded[j].sem, i * 16 + 16)

                        def project(ns):
                            for n in ns:
                                pe.wait_ge(p_taken.sem, i * (2 * NJ) + p_taken.at(max(j * NJ + n - PB + 1, 0)))
                                bank = k.ps[:, (j * NJ + n) % PB, :]
                                if n < len(kjobs):
                                    m, c = kjobs[n]
                                    at, w = CHUNKS[c]
                                    for f in range(DC):
                                        last = pe.matmul(bank[:, 0:w], wk_sb[:, f, m * P:(m + 1) * P],
                                                         ctxT[:, j, f, at:at + w], start=(f == 0), stop=(f == DC - 1))
                                else:
                                    for s, t in enumerate(vjobs[n - len(kjobs)]):
                                        rows = key_rows(t)
                                        for f in range(DC):
                                            pe.matmul(bank[0:rows, s * D:(s + 1) * D],
                                                      ctxT[:, j, f, t * P:t * P + rows], wv_sb[:, f, :],
                                                      start=(f == 0), stop=False)
                                        last = pe.matmul(bank[0:rows, s * D:(s + 1) * D], k.ones3[:, 0:rows],
                                                         k.row("L2x_bv"), start=False, stop=True)
                                last.then_inc(p_filled.sem, 1)

                        def scores(ts):
                            if ts[0] == 0:
                                pe.wait_ge(q_ready.sem, i * 2 + q_ready.at(j + 1))
                                pe.wait_ge(p_taken.sem, i * (2 * NJ) + p_taken.at(j * NJ + len(kjobs)))
                                pe.wait_ge(l_relu.sem, i * 4 + l_relu.at(j * 2))
                            for t in ts:
                                rows = key_rows(t)
                                for f in range(DC):
                                    last = pe.matmul(k.ps[0:rows, 4 + t // 8, (t % 8) * S:(t % 8 + 1) * S],
                                                     kT[:, f, t * P:t * P + rows], q_sb[:, j, f, :],
                                                     start=(f == 0), stop=(f == DC - 1))
                            last.then_inc(l_filled.sem, 1)

                        NK = len(kjobs)
                        project(range(0, NK + 2))
                        scores(range(0, 8))
                        project(range(NK + 2, NK + 4))
                        scores(range(8, KT))
                        project(range(NK + 4, NJ))
                        for t in range(KT):
                            rows = key_rows(t)
                            if t == 0:
                                pe.wait_ge(l_ready.sem, i * 6 + l_ready.at(j * 3 + 1))
                                pe.wait_ge(att_done.sem, i * 2 + att_done.at(j - 1))
                            if t == 8:
                                pe.wait_ge(l_ready.sem, i * 6 + l_ready.at(j * 3 + 3))
                            if t % 2 == 0:
                                pe.wait_ge(p_taken.sem, i * (2 * NJ) + p_taken.at(j * NJ + NK + t // 2 + 1))
                            last = pe.matmul(k.ps[0:S, 6 + j, 0:D], lg[0:rows, t, :], v[0:rows, t, :],
                                             start=(t == 0), stop=(t == KT - 1))
                        last.then_inc(av_done.sem, 1)

            @block.scalar
            def _(act):
                with act.Fori(0, B // 2) as i:
                    for j in range(2):
                        act.wait_ge(l_filled.sem, i * 4 + l_filled.at(2 * j))
                        for n in range(NJ):
                            if n == len(kjobs):
                                act.wait_ge(av_done.sem, i * 2 + av_done.at(j))
                            act.wait_ge(p_filled.sem, i * (2 * NJ) + (j * NJ + n + 1))
                            bank = k.ps[:, (j * NJ + n) % PB, :]
                            if n < len(kjobs):
                                m, c = kjobs[n]
                                at, w = CHUNKS[c]
                                ins_ = act.activation(kT[:, m, at:at + w], bank[:, 0:w], ACT.Relu, bias=bk[:, m:m + 1])
                            else:
                                ts = vjobs[n - len(kjobs)]
                                rows = key_rows(ts[-1])
                                ins_ = act.activation(v[0:rows, ts[0]:ts[-1] + 1, :],
                                                      bank[0:rows, 0:len(ts) * D].rearrange("p (t d) -> p t d", d=D),
                                                      ACT.Relu)
                            ins_.then_inc(p_taken.sem, 1)

            @block.vector
            def _(dve):
                dve.wait_ge(*loaded_weights)
                with dve.Fori(0, B // 2) as i:
                    for j in range(2):
                        dve.wait_ge(av_done.sem, i * 2 + av_done.at(j))
                        spans = [(P, 0, 8), (P, 8, KFULL), (KREST, KFULL, KT)]
                        for n, (rows, t0, t1) in enumerate(spans):
                            dve.wait_ge(l_filled.sem, i * 4 + l_filled.at(2 * j + min(n, 1) + 1))
                            src = k.ps[0:rows, 4 + t0 // 8, (t0 % 8) * S:(t0 % 8 + t1 - t0) * S].rearrange(
                                "p (t q) -> p t q", q=S)
                            ins_ = dve.tensor_scalar(lg[0:rows, t0:t1, :], src, 0.0, D ** -0.5, ALU.max, ALU.mult)
                            if n != 1:
                                ins_.then_inc(l_relu.sem, 1)
                        dve.wait_ge(l_relu.sem, i * 4 + l_relu.at(2 * j + 2))
                        for rows, t0, t1 in spans:
                            dve.tensor_tensor(lg[0:rows, t0:t1, :], lg[0:rows, t0:t1, :], maskT[0:rows, t0:t1, :],
                                              ALU.add).then_inc(l_ready.sem, 1)
                        dve.wait_ge(av_done.sem, i * 2 + av_done.at(j + 1))
                        if j == 0:
                            dve.wait_ge(x_done.sem, i + x_done.at(0))
                        dve.tensor_scalar(att[j * S:(j + 1) * S, :], k.ps[0:S, 6 + j, 0:D], 0.0, None, ALU.max
                                          ).then_inc(att_done.sem, 1)
                    dve.wait_ge(att_done.sem, i * 2 + att_done.at(2))
                    xt = k.x[:, i, :]
                    dve.tensor_tensor(xt, xt, att[:], ALU.add).then_inc(x_done.sem, 1)


def self_attention(nc, k, name, qT, kT, v_all, out, softmax, eps=0.0):
    with ExitStack() as ctx:
        def sb(n, shape, dt=F32):
            return ctx.enter_context(nc.sbuf_tensor(f"{name}_{n}", shape, dt))

        def signal(n, credit=0):
            return Signal(nc, ctx, f"{name}_{n}", credit)

        NB = 4
        VW = PAIR_F + 1
        kb = sb("kb", [P, NB, DC, S])
        vb = sb("vb", [S, NB, PAIRS, VW])
        qb = sb("qb", [P, 2, H16, S])
        wT = sb("wT", [S, 2, PAIRS * P])
        rinv = sb("rinv", [P, PAIRS, 1])
        kv_ready = signal("kv_ready")
        q_ready = signal("q_ready")
        s_filled = signal("s_filled", 2)
        wT_ready = signal("wT_ready", 2)
        av_done = signal("av_done", NB)
        out_done = signal("out_done", 2)
        step = signal("step")
        credited = [s_filled, wT_ready, av_done, out_done]
        if softmax:
            w = sb("w", [P, 2, PAIRS, S])
            mxs = sb("mxs", [P, 2, PAIRS])
            s_taken = signal("s_taken", 2)
            shifted = signal("shifted")
            exp_done = signal("exp_done")
            t_filled = signal("t_filled", 2)
            credited += [s_taken, t_filled]
        give_credits(nc, credited)
        T_BANK, O_BANK = 4, 6
        with nc.Block() as block:

            @block.gpsimd
            def _(pool):
                with pool.Fori(0, B // NB) as i:
                    for b in range(NB):
                        pool.wait_ge(av_done.sem, i * NB + av_done.at(b + 1 - NB))
                        pool.tensor_copy(kb[:, b, :, :], kT[:, :, bass.ds(i * (NB * S) + b * S, S)]
                                         ).then_inc(kv_ready.sem, 1)
                        pool.tensor_copy(vb[:, b, :, :], v_all[:, i * NB + b, :, :]).then_inc(kv_ready.sem, 1)

            @block.tensor
            def _(pe):
                with pe.Fori(0, B // NB) as i:
                    def scores(b):
                        pe.wait_ge(kv_ready.sem, i * (2 * NB) + (2 * b + 2))
                        pe.wait_ge(q_ready.sem, i * NB + (b + 1))
                        free = s_taken if softmax else wT_ready
                        pe.wait_ge(free.sem, i * NB + free.at(b - 1))
                        pe.sem_inc(k.tick, 1)
                        if softmax:
                            for pair in range(PAIRS):
                                last = pe.matmul(k.ps[:, b % 2, pair * S:(pair + 1) * S],
                                                 qb[:, b % 2, 2 * pair:2 * pair + 2, :],
                                                 kb[:, b, pair // 4, :], start=True, stop=True)
                        else:
                            for g in range(DC):
                                last = pe.matmul(k.ps[0:S, 2 * (b % 2) + g, :], kb[:, b, g, :],
                                                 qb[:, b % 2, g * 8:(g + 1) * 8, :], start=True, stop=True)
                        last.then_inc(s_filled.sem, 1)

                    def transposes(b):
                        pe.wait_ge(exp_done.sem, i * NB + (b + 1))
                        pe.wait_ge(wT_ready.sem, i * NB + wT_ready.at(b))
                        pe.sem_inc(k.tick, 1)
                        for pair in range(PAIRS):
                            last = pe.transpose(k.ps[0:S, T_BANK + pair // 4, (pair % 4) * P:(pair % 4 + 1) * P],
                                                w[:, b % 2, pair, :], k.ident[:])
                        last.then_inc(t_filled.sem, 1)

                    def values(b):
                        pe.wait_ge(wT_ready.sem, i * NB + wT_ready.at(b + 1))
                        pe.wait_ge(out_done.sem, i * NB + out_done.at(b - 1))
                        for pair in range(PAIRS):
                            last = pe.matmul(k.ps[:, O_BANK + b % 2, pair * VW:(pair + 1) * VW],
                                             wT[:, b % 2, pair * P:(pair + 1) * P], vb[:, b, pair, :],
                                             start=True, stop=True)
                        last.then_inc(av_done.sem, 1)

                    scores(0)
                    for b in range(NB):
                        if b + 1 < NB:
                            scores(b + 1)
                        if softmax:
                            transposes(b)
                            if b > 0:
                                values(b - 1)
                        else:
                            values(b)
                    if softmax:
                        values(NB - 1)

            @block.scalar
            def _(act):
                if softmax:
                    with act.Fori(0, B // NB) as i:
                        def exps(b):
                            act.wait_ge(shifted.sem, i * NB + (b + 1))
                            act.activation(w[:, b % 2, :, :], w[:, b % 2, :, :], ACT.Exp).then_inc(exp_done.sem, 1)

                        exps(0)
                        for b in range(NB):
                            if b + 1 < NB:
                                exps(b + 1)
                            act.wait_ge(t_filled.sem, i * NB + t_filled.at(b + 1))
                            act.wait_ge(av_done.sem, i * NB + av_done.at(b - 1))
                            act.activation(wT[:, b % 2, :], k.ps[0:S, T_BANK:T_BANK + 2, :].rearrange(
                                "p a b -> p (a b)"), ACT.Copy).then_inc(wT_ready.sem, 1)

            @block.vector
            def _(dve):
                with dve.Fori(0, B // NB) as i:
                    per_body = NB * 3
                    count = [0]

                    def link(ins_):
                        count[0] += 1
                        ins_.then_inc(step.sem, 1)
                        dve.wait_ge(step.sem, i * per_body + count[0])

                    def queries(b):
                        dve.wait_ge(s_filled.sem, i * NB + s_filled.at(b - 1))
                        block_queries(dve, k, qb[:, b % 2, :, :], qT, i * (NB * S) + b * S,
                                      HD ** -0.5 if softmax else 1.0).then_inc(q_ready.sem, 1)

                    def weights(b):
                        dve.wait_ge(s_filled.sem, i * NB + s_filled.at(b + 1))
                        if softmax:
                            dve.wait_ge(t_filled.sem, i * NB + t_filled.at(b - 1))
                            ins_ = dve.tensor_tensor(
                                w[:, b % 2, :, :], k.ps[:, b % 2, :].rearrange("p (a s) -> p a s", s=S),
                                k.causal_rows[:].unsqueeze(1).broadcast_to((P, PAIRS, S)), ALU.add)
                            ins_.then_inc(s_taken.sem, 1)
                            dve.wait_ge(s_taken.sem, i * NB + s_taken.at(b + 1))
                            link(dve.tensor_reduce(mxs[:, b % 2, :], w[:, b % 2, :, :], AX.X, ALU.max))
                            dve.tensor_tensor(w[:, b % 2, :, :], w[:, b % 2, :, :], mxs[:, b % 2, :].unsqueeze(
                                2).broadcast_to((P, PAIRS, S)), ALU.subtract).then_inc(shifted.sem, 1)
                        else:
                            dve.wait_ge(av_done.sem, i * NB + av_done.at(b - 1))
                            dve.tensor_tensor(
                                wT[:, b % 2, :].rearrange("p (h q) -> p h q", q=S),
                                k.ps[0:S, 2 * (b % 2):2 * (b % 2) + 2, :].rearrange("p g (h q) -> p (g h) q", q=S),
                                k.causal_keys[0:S, :].unsqueeze(1).broadcast_to((S, H16, S)),
                                ALU.mult).then_inc(wT_ready.sem, 1)

                    def divided(b):
                        dve.wait_ge(av_done.sem, i * NB + av_done.at(b + 1))
                        got = k.ps[:, O_BANK + b % 2, 0:PAIRS * VW].rearrange("p (a f) -> p a f", f=VW)
                        total = got[:, :, PAIR_F:VW]
                        if not softmax:
                            link(dve.tensor_scalar(rinv[:], total, eps, None, ALU.add))
                            total = rinv[:]
                        link(dve.reciprocal(rinv[:], total))
                        for h in range(2):
                            rows, place = slice(h * S, (h + 1) * S), slice(b % 2 * S, (b % 2 + 1) * S)
                            ins_ = dve.tensor_tensor(
                                out[place, i * (NB // 2) + b // 2, :].rearrange(
                                    "p (a h f) -> p a h f", h=2, f=HD)[:, :, h, :],
                                got[rows, :, h * HD:(h + 1) * HD], rinv[rows, :, :].broadcast_to((S, PAIRS, HD)),
                                ALU.mult)
                            if h == 0:
                                link(ins_)
                        ins_.then_inc(out_done.sem, 1)
                        dve.wait_ge(out_done.sem, i * NB + out_done.at(b + 1))

                    queries(0)
                    queries(1)
                    for b in range(NB):
                        weights(b)
                        if b + 2 < NB:
                            queries(b + 2)
                        if b > 1:
                            divided(b - 2)
                    divided(NB - 2)
                    divided(NB - 1)
                    assert count[0] == per_body


def expert_tiles(choices):
    return (TOK * choices + E8 * (P - 1)) // P


def place_tokens(nc, k, st, hot, choices, kept=None):
    W = choices * E8
    tiles = expert_tiles(choices)
    count = st.sb("count", [P, NT + 1, W])
    row, row_u = st.sb("row", [P, NT, choices]), st.sb("row_u", [P, NT, choices], U32)
    total, used = st.sb("total", [P, E8]), st.sb("used", [P, E8])
    pairwise, before = st.sb("pairwise", [P, E8, E8]), st.sb("before", [P, E8])
    shift = st.sb("shift", [P, W])
    past, owner = st.sb("past", [P, tiles, E8]), st.sb("owner", [P, tiles])
    owner_u = st.sb("owner_u", [P, tiles], U32)
    earlier = st.sb("earlier", [P, NT, W])
    matmul_pass(nc, k, [
        Job([(lambda bank: bank[:, 0:NT * W], [(k.upto[:], hot)])], "dve", lambda e, bank: e.tensor_copy(
            count[:, 0:NT, :].rearrange("p t w -> p (t w)"), bank[:, 0:NT * W])),
        Job([(lambda bank: bank[:, 0:NT * W], [(k.ones64[:], hot)])], "act", lambda e, bank: e.activation(
            earlier[:].rearrange("p t w -> p (t w)"), bank[:, 0:NT * W], ACT.Copy))])

    def over_e(ap, n):
        return ap.unsqueeze(2).broadcast_to((P, n, E8))

    def along(ap, n):
        return ap.unsqueeze(1).broadcast_to((P, n, E8))

    def steps(dve, link):
        for t in range(1, NT):
            link(dve.tensor_tensor(earlier[:, t, :], earlier[:, t, :], earlier[:, t - 1, :], ALU.add))
        link(dve.tensor_tensor(count[:, 1:NT, :], count[:, 1:NT, :], earlier[:, 0:NT - 1, :], ALU.add))
        link(dve.tensor_copy(count[:, NT, :], earlier[:, NT - 1, :]))
        link(dve.tensor_reduce(total[:], count[:, NT, :].rearrange("p (r e) -> p e r", e=E8), AX.X, ALU.add))
        link(dve.tensor_scalar(before[:], k.iota[:, 0:E8], float(P), None, ALU.mult))
        link(dve.tensor_tensor(pairwise[:], over_e(total[:], E8), along(before[:], E8), ALU.is_gt))
        link(dve.tensor_reduce(used[:], pairwise[:], AX.X, ALU.add))
        link(dve.tensor_tensor(pairwise[:], over_e(k.iota[:, 0:E8], E8), along(k.iota[:, 0:E8], E8), ALU.is_gt))
        link(dve.tensor_tensor(pairwise[:], pairwise[:], along(used[:], E8), ALU.mult))
        link(dve.tensor_reduce(before[:], pairwise[:], AX.X, ALU.add))
        link(dve.tensor_tensor(used[:], used[:], before[:], ALU.add))
        link(dve.tensor_tensor(past[:], along(used[:], tiles), over_e(k.iota[:, 0:tiles], tiles), ALU.is_le))
        link(dve.tensor_reduce(owner[:], past[:], AX.X, ALU.add))
        link(dve.tensor_scalar(owner[:], owner[:], float(E8 - 1), None, ALU.min))
        link(dve.tensor_copy(owner_u[:], owner[:]))
        for r in range(choices):
            link(dve.tensor_scalar(shift[:, r * E8:(r + 1) * E8], before[:], float(P), -1.0, ALU.mult, ALU.add))
        if choices > 1:
            link(dve.tensor_tensor(shift[:, E8:W], shift[:, E8:W], count[:, NT, 0:E8], ALU.add))
        if kept is not None:
            within = st.sb("within", [P, NT, W])
            link(dve.tensor_scalar(within[:], count[:, 0:NT, :], float(CAPACITY), None, ALU.is_le))
            link(dve.tensor_tensor(within[:], within[:], hot, ALU.mult))
            link(dve.tensor_reduce(kept, within[:].rearrange("p t (r e) -> p t r e", e=E8), AX.X, ALU.add))
        link(dve.tensor_tensor(count[:, 0:NT, :], count[:, 0:NT, :],
                               shift[:].unsqueeze(1).broadcast_to((P, NT, W)), ALU.add))
        link(dve.tensor_tensor(count[:, 0:NT, :], count[:, 0:NT, :], hot, ALU.mult))
        link(dve.tensor_reduce(row[:], count[:, 0:NT, :].rearrange("p t (r e) -> p t r e", e=E8), AX.X, ALU.add))
        link(dve.tensor_copy(row_u[:], row[:]))

    vector_block(nc, k, steps)
    return row_u, owner_u


def experts(nc, k, name, w_in, w_gate, w_out, hidden, rows, owner, gates, choices, b_in=None, b_out=None):
    gated = w_gate is not None
    MT = (hidden + P - 1) // P
    HW = [min(P, hidden - m * P) for m in range(MT)]
    full_w2 = hidden % P == 0
    tiles = expert_tiles(choices)
    whole = hidden // P
    sorted_out = nc.dram_tensor(f"{name}_sorted_out", (tiles * P, D), F32).ap()

    with ExitStack() as ctx:
        def sb(n, shape, dt=F32):
            return ctx.enter_context(nc.sbuf_tensor(f"{name}_{n}", shape, dt))

        def signal(n, credit=0):
            return Signal(nc, ctx, f"{name}_{n}", credit)

        w1 = sb("w1", [P, 2, DC, hidden])
        wg = sb("wg", [P, 2, DC, hidden]) if gated else None
        w2 = sb("w2", [P, 2, MT, D])
        b1 = sb("b1", [P, 2, MT]) if b_in is not None else None
        b2 = sb("b2", [1, 2, D]) if b_out is not None else None
        tokens = sb("tokens", [P, 2, D])
        tokT = sb("tokT", [P, 2, DC, P])
        sig = sb("sig", [P, 2, P]) if gated else None
        hid = sb("hid", [P, 2, MT, P])
        y = sb("y", [P, 2, D])
        in_loads, out_loads = 1 + gated + (b_in is not None), 1 + (not full_w2) + (b_out is not None)
        RING = 2 if gated else 4

        tok_loaded = [signal(f"tok_loaded{j}") for j in range(2)]
        in_loaded = [signal(f"in_loaded{j}") for j in range(2)]
        out_loaded = [signal(f"out_loaded{j}") for j in range(2)]
        t_filled = signal("t_filled", 1)
        t_taken = signal("t_taken")
        h_filled = signal("h_filled")
        sig_done = signal("sig_done") if gated else None
        h_taken = signal("h_taken", 2 * MT)
        o_filled = signal("o_filled", 2)
        o_taken = signal("o_taken", 2)
        y_stored = signal("y_stored")
        y_free = signal("y_free", 2)
        scattered = signal("scattered")
        give_credits(nc, [t_filled, h_taken, o_filled, o_taken, y_free])

        with nc.Block() as block:

            @block.gpsimd
            def _(pool):
                pool.wait_ge(k.zeroed, 16 * ZERO_PARTS)
                for t in range(NT):
                    for r in range(choices):
                        pool.indirect_dma_start(k.sorted_in, bass.IndirectOffsetOnAxis(rows[:, t, r:r + 1], 0),
                                                k.xn[:, t, :], None).then_inc(scattered.sem, 16)
                pool.wait_ge(scattered.sem, 16 * NT * choices)

        def over_tiles(engine, body):
            with engine.Fori(0, tiles // 2) as i:
                for j in range(2):
                    body(i, j)
            if tiles % 2:
                body(tiles // 2, 0)

        with nc.Block() as block:

            @block.sync
            def _(sp):
                def body(i, j):
                    n = i * 2 + j
                    e = nc.values_load(owner[0:1, bass.ds(n, 1)], [mybir.EngineType.SP], min_val=0, max_val=E8 - 1,
                                       skip_runtime_bounds_check_because="place_tokens clamps it to 0..7")
                    sp.wait_ge(h_taken.sem, i * (2 * MT) + h_taken.at((j - 1) * MT))
                    sp.sem_inc(k.tick, 1)
                    sp.dma_start(tokens[:, j, :], k.sorted_in[bass.ds(n * P, P), :]
                                 ).then_inc(tok_loaded[j].sem, 16)
                    done = in_loaded[j].sem
                    sp.dma_start(w1[:, j, :, :], w_in[e].rearrange("(c p) n -> p c n", p=P)).then_inc(done, 16)
                    if gated:
                        sp.dma_start(wg[:, j, :, :], w_gate[e].rearrange("(c p) n -> p c n", p=P)).then_inc(done, 16)
                    if b_in is not None:
                        sp.dma_start(b1[:, j, :], b_in[e]).then_inc(done, 16)
                    sp.wait_ge(o_filled.sem, i * 2 + o_filled.at(j - 1))
                    sp.sem_inc(k.tick, 1)
                    done = out_loaded[j].sem
                    if b_out is not None:
                        sp.dma_start(b2[:, j, :], b_out[e]).then_inc(done, 16)
                    sp.dma_start(w2[:, j, 0:whole, :],
                                 w_out[e][0:whole * P, :].rearrange("(c p) n -> p c n", p=P)).then_inc(done, 16)
                    if not full_w2:
                        sp.dma_start(w2[0:HW[-1], j, whole, :], w_out[e][whole * P:hidden, :]).then_inc(done, 16)

                over_tiles(sp, body)

            @block.tensor
            def _(pe):
                def transposes(i, j):
                    pe.wait_ge(tok_loaded[j].sem, i * 16 + 16)
                    pe.sem_inc(k.tick, 1)
                    for c in range(DC):
                        last = pe.transpose(k.ps[:, 4 + j, c * P:(c + 1) * P], tokens[:, j, c * P:(c + 1) * P],
                                            k.ident[:])
                    last.then_inc(t_filled.sem, 1)

                def body(i, j, more=True):
                    pe.wait_ge(t_taken.sem, i * 2 + (j + 1))
                    pe.wait_ge(in_loaded[j].sem, i * (16 * in_loads) + 16 * in_loads)
                    for m in range(MT):
                        job = j * MT + m
                        pe.wait_ge(h_taken.sem, i * (2 * MT) + h_taken.at(job - RING + 1))
                        for x, w in enumerate((w1, wg) if gated else (w1,)):
                            bank = (2 * (job % 2) + x) if gated else job % 4
                            for c in range(DC):
                                last = pe.matmul(k.ps[0:HW[m], bank, 0:P], w[:, j, c, m * P:m * P + HW[m]],
                                                 tokT[:, j, c, :], start=(c == 0), stop=(c == DC - 1))
                        last.then_inc(h_filled.sem, 1)
                    if more:
                        transposes(i + (j == 1), 1 - j)
                    pe.wait_ge(out_loaded[j].sem, i * (16 * out_loads) + 16 * out_loads)
                    pe.wait_ge(o_taken.sem, i * 2 + o_taken.at(j - 1))
                    for m in range(MT):
                        pe.wait_ge(h_taken.sem, i * (2 * MT) + h_taken.at(j * MT + m + 1))
                        last = pe.matmul(k.ps[:, 6 + j, 0:D], hid[0:HW[m], j, m, :], w2[0:HW[m], j, m, :],
                                         start=(m == 0), stop=(m == MT - 1 and b2 is None))
                    if b2 is not None:
                        last = pe.matmul(k.ps[:, 6 + j, 0:D], k.ones_row[0:1, :], b2[0:1, j, :],
                                         start=False, stop=True)
                    last.then_inc(o_filled.sem, 1)

                transposes(0, 0)
                with pe.Fori(0, tiles // 2) as i:
                    for j in range(2):
                        body(i, j)
                body(tiles // 2, 0, False)

            @block.scalar
            def _(act):
                def body(i, j):
                    act.wait_ge(o_filled.sem, i * 2 + o_filled.at(j - 1))
                    act.sem_inc(k.tick, 1)
                    for m in range(MT):
                        job = j * MT + m
                        act.wait_ge(h_filled.sem, i * (2 * MT) + (job + 1))
                        if gated:
                            act.wait_ge(h_taken.sem, i * (2 * MT) + h_taken.at(job - 1))
                            act.activation(sig[0:HW[m], job % 2, :], k.ps[0:HW[m], 2 * (job % 2), 0:P],
                                           ACT.Silu).then_inc(sig_done.sem, 1)
                        else:
                            bias = b1[:, j, m:m + 1] if b1 is not None else 0.0
                            act.activation(hid[:, j, m, :], k.ps[:, job % 4, 0:P], ACT.Gelu, bias=bias
                                           ).then_inc(h_taken.sem, 1)

                over_tiles(act, body)

            @block.vector
            def _(dve):
                def take_transposed(i, j):
                    dve.wait_ge(t_filled.sem, i * 2 + t_filled.at(j + 1))
                    dve.tensor_copy(tokT[:, j, :, :].rearrange("p c n -> p (c n)"), k.ps[:, 4 + j, 0:D]
                                    ).then_inc(t_taken.sem, 1)

                def body(i, j, more=True):
                    if gated:
                        dve.wait_ge(o_filled.sem, i * 2 + o_filled.at(j - 1))
                        dve.sem_inc(k.tick, 1)
                        for m in range(MT):
                            job = j * MT + m
                            dve.wait_ge(sig_done.sem, i * (2 * MT) + (job + 1))
                            dve.tensor_tensor(hid[0:HW[m], j, m, :], sig[0:HW[m], job % 2, :],
                                              k.ps[0:HW[m], 2 * (job % 2) + 1, 0:P], ALU.mult
                                              ).then_inc(h_taken.sem, 1)
                    if more:
                        take_transposed(i + (j == 1), 1 - j)
                    dve.wait_ge(y_free.sem, i * 2 + y_free.at(j - 1))
                    dve.wait_ge(o_filled.sem, i * 2 + o_filled.at(j + 1))
                    dve.tensor_copy(y[:, j, :], k.ps[:, 6 + j, 0:D]).then_inc(o_taken.sem, 1)

                take_transposed(0, 0)
                with dve.Fori(0, tiles // 2) as i:
                    for j in range(2):
                        body(i, j)
                body(tiles // 2, 0, False)

            @block.gpsimd
            def _(pool):
                def body(i, j):
                    pool.wait_ge(o_taken.sem, i * 2 + o_taken.at(j + 1))
                    pool.sem_inc(k.tick, 1)
                    pool.dma_start(sorted_out[bass.ds((i * 2 + j) * P, P), :], y[:, j, :]
                                   ).then_inc(y_stored.sem, 16)
                    pool.wait_ge(y_stored.sem, i * 32 + (16 * j + 16))
                    pool.sem_inc(y_free.sem, 1)

                over_tiles(pool, body)

    with ExitStack() as ctx:
        back = ctx.enter_context(nc.sbuf_tensor(f"{name}_back", [P, NT, choices, D], F32))
        fetched = Signal(nc, ctx, f"{name}_fetched")
        with nc.Block() as block:

            @block.gpsimd
            def _(pool):
                for t in range(NT):
                    for r in range(choices):
                        pool.indirect_dma_start(back[:, t, r, :], None, sorted_out,
                                                bass.IndirectOffsetOnAxis(rows[:, t, r:r + 1], 0)
                                                ).then_inc(fetched.sem, 16)

            @block.vector
            def _(dve):
                for r in range(choices):
                    for t in range(NT):
                        dve.wait_ge(fetched.sem, 16 * NT * choices)
                        if r:
                            dve.wait_ge(k.dve_link, k.n_dve_link + t + 1)
                        dve.scalar_tensor_tensor(k.x[:, t, :], back[:, t, r, :], gates[:, t, r:r + 1],
                                                 k.x[:, t, :], ALU.mult, ALU.add).then_inc(k.dve_link, 1)
        k.n_dve_link += NT * choices


def vector_block(nc, k, steps):
    with nc.Block() as block:

        @block.vector
        def _(dve):
            def link(ins_):
                k.n_dve_link += 1
                ins_.then_inc(k.dve_link, 1)
                dve.wait_ge(k.dve_link, k.n_dve_link)

            steps(dve, link)


def scalar_block(nc, k, steps):
    with nc.Block() as block:

        @block.scalar
        def _(act):
            def link(ins_):
                k.n_act_link += 1
                ins_.then_inc(k.act_link, 1)
                act.wait_ge(k.act_link, k.n_act_link)

            steps(act, link)


def add_bias(col, func):
    return lambda out: lambda e, bank, m, n: e.activation(
        out[0:bank.shape[0], m, n * BANK:(n + 1) * BANK], bank, func, bias=col[0:bank.shape[0], m:m + 1])


def top2_gates(nc, k, st, logits, top, kept=None):
    idx, idxf = st.sb("idx", [P, NT, 8], U32), st.sb("idxf", [P, NT, 8])
    hot = st.sb("hot", [P, NT, 2, E8])
    gap, g2 = st.sb("gap", [P, NT]), st.sb("g2", [P, NT, 2])

    def first(dve, link):
        for t in range(NT):
            link(dve.max(top[:, t, :], logits[:, t, :]))
            link(dve.max_index(idx[:, t, :], top[:, t, :], logits[:, t, :]))
        link(dve.tensor_copy(idxf[:], idx[:]))
        for r in range(2):
            link(dve.tensor_tensor(hot[:, :, r, :], k.iota8[:].unsqueeze(1).broadcast_to((P, NT, E8)),
                                   idxf[:, :, r:r + 1].broadcast_to((P, NT, E8)), ALU.is_equal))
        link(dve.tensor_tensor(gap[:], top[:, :, 1], top[:, :, 0], ALU.subtract))

    vector_block(nc, k, first)
    scalar_block(nc, k, lambda act, link: link(act.activation(g2[:, :, 1], gap[:], ACT.Exp)))
    rows, owner = place_tokens(nc, k, st, hot[:].rearrange("p t r e -> p t (r e)"), 2, kept)

    def second(dve, link):
        link(dve.tensor_scalar(gap[:], g2[:, :, 1], 1.0, None, ALU.add))
        link(dve.reciprocal(g2[:, :, 0], gap[:]))
        link(dve.tensor_tensor(g2[:, :, 1], g2[:, :, 1], g2[:, :, 0], ALU.mult))
        if kept is not None:
            link(dve.tensor_tensor(g2[:], g2[:], kept, ALU.mult))

    vector_block(nc, k, second)
    return rows, owner, g2


def router_logits(nc, k, wgT, logits, loaded):
    groups = [(lambda bank, t=t: bank[:, t * E8:(t + 1) * E8],
               [(k.xnT[:, c, t * P:(t + 1) * P], wgT[:, c, :]) for c in range(DC)]) for t in range(NT)]
    matmul_pass(nc, k, [Job(groups, "dve", lambda e, bank: e.tensor_copy(
        logits[:].rearrange("p t e -> p (t e)"), bank[:, 0:NT * E8]))], [loaded])


def values_job(groups, v_all, pair):
    return Job(groups, "dve", lambda e, bank: e.tensor_copy(
        v_all[:, 2 * pair:2 * pair + 2, :, 0:PAIR_F],
        bank[0:S, :].rearrange("p (b a f) -> p b a f", b=2, f=PAIR_F)))


def conv3(dve, link, out, src, w, bias, batches=B):
    o = out.rearrange("p (b s) -> p b s", s=S)
    x = src.rearrange("p (b s) -> p b s", s=S)
    link(dve.tensor_scalar(o, x, w[:, 1:2], bias, ALU.mult, ALU.add))
    link(dve.scalar_tensor_tensor(o[:, :, 1:S], x[:, :, 0:S - 1], w[:, 0:1], o[:, :, 1:S], ALU.mult, ALU.add))
    link(dve.scalar_tensor_tensor(o[:, :, 0:S - 1], x[:, :, 1:S], w[:, 2:3], o[:, :, 0:S - 1], ALU.mult, ALU.add))


class Stage:
    def __init__(self, nc, name):
        self.nc, self.name, self.ctx = nc, name, ExitStack()

    def __enter__(self):
        self.ctx.__enter__()
        return self

    def __exit__(self, *a):
        return self.ctx.__exit__(*a)

    def sb(self, n, shape, dt=F32):
        return self.ctx.enter_context(self.nc.sbuf_tensor(f"{self.name}_{n}", shape, dt))


def normed(nc, k):
    layer_norm(nc, k, k.x, k.xn, 1e-5)
    to_features(nc, k, k.xn, k.xnT)


def stage_L0_cross(nc, k, ins):
    normed(nc, k)
    softmax_cross_attention(nc, k, "L0x", ins, True, k.xnT)


def stage_L0_attn(nc, k, ins):
    normed(nc, k)
    with Stage(nc, "L0a") as st:
        w = {}
        copies = []
        for n, dout in (("wq", 64), ("wkv", 64), ("wqr", 128), ("wqr_sw", 128), ("wkr", 128), ("wkr_sw", 128),
                        ("wo", 256)):
            w[n] = st.sb(n, [P, DC, dout])
            copies.append((w[n][:], wk(ins["L0_" + n])))
        for n, dout in (("wqc", 128), ("wkc", 128), ("wv", 256)):
            w[n] = st.sb(n, [64, 1, dout])
            copies.append((w[n][:, 0, :], ins["L0_" + n]))
        loaded = load_block(nc, k, copies)
        cT = {n: st.sb("c" + n, [64, 1, TOK]) for n in ("q", "kv")}
        rot = {n: st.sb("rot" + n, [P, 2, TOK]) for n in "qk"}
        heads = {n: st.sb("heads" + n, [P, DC, TOK]) for n in "qk"}
        v_all = st.sb("v", [S, B, PAIRS, PAIR_F + 1])
        att, attT = st.sb("att", [P, NT, D]), st.sb("attT", [P, DC, TOK])
        jobs = []
        for n, bias in (("q", "L0_bq"), ("kv", "L0_bkv")):
            jobs += linear_jobs(w["w" + n], k.xnT, DC, 64, add_bias(k.col(bias), ACT.Gelu)(cT[n]))
        for n in "qk":
            for x, (suffix, table) in enumerate((("", k.rope_cos), ("_sw", k.rope_sin))):
                def drain(e, bank, m, n_, n=n, x=x, suffix=suffix, table=table):
                    return e.scalar_tensor_tensor(
                        rot[n][:, x, n_ * BANK:(n_ + 1) * BANK].rearrange("p (b s) -> p b s", s=S),
                        bank.rearrange("p (b s) -> p b s", s=S), k.col(f"L0_b{n}r{suffix}"),
                        table[:].unsqueeze(1).broadcast_to((P, BANK // S, S)), ALU.add, ALU.mult)
                jobs += linear_jobs(w[f"w{n}r{suffix}"], k.xnT, DC, 128, drain, by="dve")
        matmul_pass(nc, k, jobs, [loaded])

        def rope(dve, link):
            for n in "qk":
                link(dve.tensor_tensor(rot[n][:, 0, :], rot[n][:, 0, :], rot[n][:, 1, :], ALU.add))
            link(dve.memset(v_all[:, :, :, PAIR_F:PAIR_F + 1], 1.0))

        vector_block(nc, k, rope)
        jobs = []
        for n, c in (("q", "q"), ("k", "kv")):
            jobs += linear_jobs(w[f"w{n}c"], cT[c], 1, 128, add_bias(k.col(f"L0_b{n}c"), ACT.Gelu)(heads[n]), krows=64)
        for pair in range(B // 2):
            groups = [(lambda bank, h=h: bank[0:S, h * D:(h + 1) * D],
                       [(cT["kv"][:, 0, (2 * pair + h) * S:(2 * pair + h + 1) * S], w["wv"][:, 0, :]),
                        (k.ones3[:, 0:S], k.row("L0_bv"))]) for h in range(2)]
            jobs.append(values_job(groups, v_all, pair))
        matmul_pass(nc, k, jobs)

        def gelus(act, link):
            for n in "qk":
                link(act.activation(heads[n][:, 1, :], rot[n][:, 0, :], ACT.Gelu))

        scalar_block(nc, k, gelus)
        self_attention(nc, k, "L0s", heads["q"], heads["k"], v_all, att, True)
        to_features(nc, k, att, attT)
        residual_linear(nc, k, attT, w["wo"], DC, "L0_bo", k.x)


def stage_L0_ffn(nc, k, ins):
    normed(nc, k)
    with Stage(nc, "L0f") as st:
        wgT = st.sb("wgT", [P, DC, E8])
        loaded = load_block(nc, k, [(wgT[:], wk(ins["L0_Wg"]))])
        logits, top = st.sb("logits", [P, NT, E8]), st.sb("top", [P, NT, E8])
        router_logits(nc, k, wgT, logits, loaded)
        rows, owner, gates = top2_gates(nc, k, st, logits, top)
        experts(nc, k, "L0e", ins["L0_W1"], ins["L0_W2"], ins["L0_W3"], 682, rows, owner, gates, 2)


def stage_L1_cross(nc, k, ins):
    normed(nc, k)
    with Stage(nc, "L1x") as st:
        INNER, HDIM = 512, 64
        IC = INNER // P
        q_ctx = st.sb("q_ctx", [P, B, 2, BANK])
        with Stage(nc, "L1q") as s2:
            wq, wkT = s2.sb("wq", [P, DC, INNER]), s2.sb("wkT", [P, IC, D])
            qT = s2.sb("qT", [P, IC, TOK])
            loaded = load_block(nc, k, [(wq[:], wk(ins["L1x_Wq"])), (wkT[:], wk(ins["L1x_WkT"]))])
            matmul_pass(nc, k, linear_jobs(wq, k.xnT, DC, INNER, lambda e, bank, m, n: e.activation(
                qT[:, m, n * BANK:(n + 1) * BANK], bank, ACT.Copy, scale=HDIM ** -0.5)), [loaded])
            jobs = []
            for h in range(8):
                r = HDIM * (h % 2)
                for f in range(DC):
                    for n in range(NHALF):
                        products = [(wkT[r:r + HDIM, h // 2, f * P:(f + 1) * P],
                                     qT[r:r + HDIM, h // 2, n * BANK:(n + 1) * BANK])]
                        out = q_ctx[:, n * 8:(n + 1) * 8, f, h * S:(h + 1) * S]
                        by = ("act", "dve")[n]
                        jobs.append(Job([(full, products)], by, lambda e, bank, out=out, by=by: (
                            e.activation(out, bank.rearrange("p (b s) -> p b s", s=S), ACT.Copy) if by == "act"
                            else e.tensor_copy(out, bank.rearrange("p (b s) -> p b s", s=S)))))
            matmul_pass(nc, k, jobs)
        softmax_cross_attention(nc, k, "L1c", ins, False, q_ctx)
        wv, wo = st.sb("wv", [P, DC, INNER]), st.sb("wo", [P, IC, D])
        loaded = load_block(nc, k, [(wv[:], wk(ins["L1x_Wv"])), (wo[:], wk(ins["L1x_Wo"]))])
        accT = st.sb("accT", [P, DC, 8, TOK])
        oT = st.sb("oT", [P, IC, TOK])
        rows = q_ctx[:].rearrange("p b f n -> p b (f n)")
        jobs = []
        for b in range(B):
            for f in range(DC):
                groups = [(lambda bank, t=t: bank[:, t * P:(t + 1) * P],
                           [(rows[:, b, t * D + f * P:t * D + (f + 1) * P], None)]) for t in range(4)]
                out = accT[:, f, :, b * S:(b + 1) * S]
                by = ("act", "dve")[f]
                jobs.append(Job(groups, by, lambda e, bank, out=out, by=by: (
                    e.activation(out, bank.rearrange("p (h s) -> p h s", s=S), ACT.Copy) if by == "act"
                    else e.tensor_copy(out, bank.rearrange("p (h s) -> p h s", s=S)))))
        matmul_pass(nc, k, jobs, [loaded])
        jobs = []
        for c in range(IC):
            for n in range(NHALF):
                groups = [(lambda bank, h=h: bank[h * HDIM:(h + 1) * HDIM, :],
                           [(wv[:, f, (2 * c + h) * HDIM:(2 * c + h + 1) * HDIM],
                             accT[:, f, 2 * c + h, n * BANK:(n + 1) * BANK]) for f in range(DC)]) for h in range(2)]
                jobs.append(Job(groups, "act", lambda e, bank, c=c, n=n: e.activation(
                    oT[:, c, n * BANK:(n + 1) * BANK], bank, ACT.Copy)))
        matmul_pass(nc, k, jobs)
        residual_linear(nc, k, oT, wo, IC, "L1x_bo", k.x)


def stage_L1_attn(nc, k, ins):
    normed(nc, k)
    with Stage(nc, "L1a") as st:
        wqkv, wo = st.sb("wqkv", [P, DC, 3 * D]), st.sb("wo", [P, DC, D])
        loaded = load_block(nc, k, [(wqkv[:], wk(ins["L1a_wqkv"])), (wo[:], wk(ins["L1a_wo"]))])
        qk = st.sb("qk", [P, 2 * DC, TOK])
        pos = st.sb("pos", [P, 2 * DC, TOK])
        v_all = st.sb("v", [S, B, PAIRS, PAIR_F + 1])
        att, attT = st.sb("att", [P, NT, D]), st.sb("attT", [P, DC, TOK])
        bias = k.col("L1a_bqk")
        jobs = linear_jobs(wqkv, k.xnT, DC, 2 * D, lambda e, bank, m, n: e.activation(
            pos[:, m, n * BANK:(n + 1) * BANK], bank, ACT.Identity, bias=bias[:, m:m + 1]))
        for pair in range(B // 2):
            groups = [(lambda bank, h=h: bank[0:S, h * D:(h + 1) * D],
                       [(k.xnT[:, c, (2 * pair + h) * S:(2 * pair + h + 1) * S], wqkv[:, c, 2 * D:3 * D])
                        for c in range(DC)] + [(k.ones3[:, 0:S], k.row("L1a_bv"))]) for h in range(2)]
            jobs.append(values_job(groups, v_all, pair))
        matmul_pass(nc, k, jobs, [loaded])
        elu_plus_one(nc, k, qk, pos)
        vector_block(nc, k, lambda dve, link: link(dve.memset(v_all[:, :, :, PAIR_F:PAIR_F + 1], 1.0)))
        self_attention(nc, k, "L1s", qk[:, 0:DC, :], qk[:, DC:2 * DC, :], v_all, att, False, 1e-6)
        to_features(nc, k, att, attT)
        residual_linear(nc, k, attT, wo, DC, "L1a_bo", k.x)


def elu_plus_one(nc, k, out, src):
    vector_block(nc, k, lambda dve, link: link(dve.tensor_scalar(out[:], src[:], 0.0, None, ALU.min)))
    scalar_block(nc, k, lambda act, link: link(act.activation(out[:], out[:], ACT.Exp)))
    vector_block(nc, k, lambda dve, link: link(
        dve.scalar_tensor_tensor(out[:], src[:], 0.0, out[:], ALU.max, ALU.add)))


ROUND = 1.5 * 2.0 ** 23


def round_clip(dve, link, t, lo, hi):
    link(dve.tensor_scalar(t, t, ROUND, None, ALU.add))
    link(dve.tensor_scalar(t, t, ROUND, None, ALU.subtract))
    link(dve.tensor_scalar(t, t, lo, hi, ALU.max, ALU.min))


def quantise_rows(nc, k, st, name, src, width):
    amax, sc, inv = (st.sb(name + n, [P, NT]) for n in ("amax", "scale", "inv"))

    def steps(dve, link):
        link(dve.tensor_reduce(amax[:], src[:], AX.X, ALU.max, apply_absolute_value=True))
        link(dve.tensor_scalar(amax[:], amax[:], 1e-5, None, ALU.max))
        link(dve.reciprocal(inv[:], amax[:]))
        link(dve.tensor_scalar(sc[:], inv[:], 127.0, None, ALU.mult))
        link(dve.reciprocal(inv[:], sc[:]))
        link(dve.tensor_tensor(src[:], src[:], sc[:].unsqueeze(2).broadcast_to((P, NT, width)), ALU.mult))
        round_clip(dve, link, src[:], -128.0, 127.0)
        link(dve.tensor_tensor(src[:], src[:], inv[:].unsqueeze(2).broadcast_to((P, NT, width)), ALU.mult))

    vector_block(nc, k, steps)


def quantise_weight(nc, k, st, name, w, chunks, width):
    part, mean, sc = (st.sb(name + n, [P, 1]) for n in ("part", "mean", "scale"))
    vector_block(nc, k, lambda dve, link: link(
        dve.tensor_reduce(part[:], w[:].rearrange("p c n -> p (c n)"), AX.X, ALU.add, apply_absolute_value=True)))
    matmul_pass(nc, k, [Job([(lambda bank: bank[:, 0:1], [(k.ones64[:], part[:])])], "dve",
                            lambda e, bank: e.tensor_scalar(mean[:], bank[:, 0:1], 1.0 / (P * chunks * width), 1e-5,
                                                            ALU.mult, ALU.max))])

    def steps(dve, link):
        link(dve.reciprocal(sc[:], mean[:]))
        link(dve.tensor_scalar(w[:], w[:], sc[:, 0:1], None, ALU.mult))
        round_clip(dve, link, w[:], -1.0, 1.0)

    vector_block(nc, k, steps)
    return mean


def stage_L1_ffn(nc, k, ins):
    HID = 1024
    HC = HID // P
    layer_norm(nc, k, k.x, k.xn, 1e-5)
    with Stage(nc, "L1f") as st:
        w1, w2 = st.sb("w1", [P, DC, HID]), st.sb("w2", [P, HC, D])
        loaded = load_block(nc, k, [(w1[:], wk(ins["L1f_w1"])), (w2[:], wk(ins["L1f_w2"]))])
        vector_wait(nc, k, loaded)
        m1 = quantise_weight(nc, k, st, "q1", w1, DC, HID)
        m2 = quantise_weight(nc, k, st, "q2", w2, HC, D)
        quantise_rows(nc, k, st, "x", k.xn, D)
        to_features(nc, k, k.xn, k.xnT)
        hT = st.sb("hT", [P, HC, TOK])
        cT = st.sb("cT", [P, HC, TOK])
        h_tok = st.sb("h", [P, NT, HID])
        matmul_pass(nc, k, linear_jobs(w1, k.xnT, DC, HID, lambda e, bank, m, n: e.activation(
            hT[:, m, n * BANK:(n + 1) * BANK], bank, ACT.Copy, scale=m1[:, 0:1])))
        cw, cb = k.col("L1f_cw"), k.col("L1f_cb")

        def conv(dve, link):
            for c in range(HC):
                conv3(dve, link, cT[:, c, :], hT[:, c, :], cw[:, 3 * c:3 * c + 3], cb[:, c:c + 1])

        vector_block(nc, k, conv)
        scalar_block(nc, k, lambda act, link: link(act.activation(cT[:], cT[:], ACT.Silu)))
        jobs = []
        for t in range(NT):
            for half in range(2):
                groups = [(lambda bank, c=c: bank[:, c * P:(c + 1) * P],
                           [(cT[:, 4 * half + c, t * P:(t + 1) * P], None)]) for c in range(4)]
                out = h_tok[:, t, half * BANK:(half + 1) * BANK]
                jobs.append(Job(groups, "act", lambda e, bank, out=out: e.activation(out, bank, ACT.Copy)))
        matmul_pass(nc, k, jobs)
        quantise_rows(nc, k, st, "h", h_tok, HID)
        to_features(nc, k, h_tok, hT, chunks=HC)
        jobs = []
        for t in range(NT):
            products = [(hT[:, c, t * P:(t + 1) * P], w2[:, c, :]) for c in range(HC)]
            jobs.append(Job([(lambda bank: bank[:, 0:D], products)], "dve", lambda e, bank, t=t:
                            e.scalar_tensor_tensor(k.x[:, t, :], bank[:, 0:D], m2[:, 0:1], k.x[:, t, :],
                                                   ALU.mult, ALU.add)))
        matmul_pass(nc, k, jobs)


def vector_wait(nc, k, loaded):
    with nc.Block() as block:

        @block.vector
        def _(dve):
            dve.wait_ge(*loaded)


def stage_L2_cross(nc, k, ins):
    normed(nc, k)
    with Stage(nc, "L2x") as st:
        wq, wkk, wv = (st.sb(n, [P, DC, D]) for n in ("wq", "wk", "wv"))
        maskT = st.sb("maskT", [P, KT, S])
        qT = st.sb("qT", [P, DC, TOK])
        loaded = load_block(nc, k, [
            (wq[:], wk(ins["L2x_wq"])), (wkk[:], wk(ins["L2x_wk"])), (wv[:], wk(ins["L2x_wv"])),
            (maskT[:, 0:KFULL, :], ins["maskT"][0:KFULL * P, :].rearrange("(t p) q -> p t q", p=P)),
            (maskT[0:KREST, KFULL, :], ins["maskT"][KFULL * P:M, :])])
        matmul_pass(nc, k, linear_jobs(wq, k.xnT, DC, D, add_bias(k.col("L2x_bq"), ACT.Relu)(qT)), [loaded])
        relu_cross_attention(nc, k, "L2c", ins, wkk, wv, qT, maskT, loaded)


def stage_L2_attn(nc, k, ins):
    normed(nc, k)
    with Stage(nc, "L2a") as st:
        w = {n: st.sb(n, [P, DC, D]) for n in ("wq", "wk", "wv", "wfc")}
        loaded = load_block(nc, k, [(w[n][:], wk(ins["L2a_" + n])) for n in w])
        qT, kT = st.sb("qT", [P, DC, TOK]), st.sb("kT", [P, DC, TOK])
        v = st.sb("v", [P, NT, D])
        s, sT = st.sb("s", [P, NT, P]), st.sb("sT", [P, NT, P])
        mxs = st.sb("mxs", [P, NT])
        jobs = linear_jobs(w["wq"], k.xnT, DC, D, lambda e, bank, m, n: e.activation(
            qT[:, m, n * BANK:(n + 1) * BANK], bank, ACT.Copy, scale=D ** -0.5))
        jobs += linear_jobs(w["wk"], k.xnT, DC, D, lambda e, bank, m, n: e.activation(
            kT[:, m, n * BANK:(n + 1) * BANK], bank, ACT.Copy))
        matmul_pass(nc, k, jobs, [loaded])
        residual_linear(nc, k, k.xnT, w["wv"], DC, None, v, add=False)
        jobs = []
        for t in range(NT):
            products = [(qT[:, c, t * P:(t + 1) * P], kT[:, c, t * P:(t + 1) * P]) for c in range(DC)]
            jobs.append(Job([(lambda bank: bank[:, 0:P], products)], "dve", lambda e, bank, t=t: e.tensor_tensor(
                s[:, t, :], bank[:, 0:P], k.causal_tile[:], ALU.add)))
        matmul_pass(nc, k, jobs)

        def shift(dve, link):
            link(dve.tensor_reduce(mxs[:], s[:], AX.X, ALU.max))
            link(dve.tensor_tensor(s[:], s[:], mxs[:].unsqueeze(2).broadcast_to((P, NT, P)), ALU.subtract))

        vector_block(nc, k, shift)
        scalar_block(nc, k, lambda act, link: link(act.activation(s[:], s[:], ACT.Exp)))

        def divide(dve, link):
            link(dve.tensor_reduce(mxs[:], s[:], AX.X, ALU.add))
            link(dve.reciprocal(mxs[:], mxs[:]))
            link(dve.tensor_tensor(s[:], s[:], mxs[:].unsqueeze(2).broadcast_to((P, NT, P)), ALU.mult))

        vector_block(nc, k, divide)
        jobs = []
        for n in range(2):
            groups = [(lambda bank, t=t: bank[:, t * P:(t + 1) * P], [(s[:, 4 * n + t, :], None)]) for t in range(4)]
            jobs.append(Job(groups, "act", lambda e, bank, n=n: e.activation(
                sT[:, 4 * n:4 * n + 4, :].rearrange("p t q -> p (t q)"), bank, ACT.Copy)))
        matmul_pass(nc, k, jobs)
        jobs = []
        for t in range(NT):
            jobs.append(Job([(lambda bank: bank[:, 0:D], [(sT[:, t, :], v[:, t, :])])], "dve",
                            lambda e, bank, t=t: e.tensor_tensor(k.xn[:, t, :], bank[:, 0:D], v[:, t, :], ALU.add)))
        matmul_pass(nc, k, jobs)
        layer_norm(nc, k, k.xn, k.xn, 1e-5)
        to_features(nc, k, k.xn, k.xnT, scale=k.col("L2a_gamma"), bias=k.col("L2a_beta"))
        residual_linear(nc, k, k.xnT, w["wfc"], DC, "L2a_bfc", k.x)


def stage_L2_ffn(nc, k, ins):
    normed(nc, k)
    with Stage(nc, "L2f") as st:
        GD = 16
        redT, wg = st.sb("redT", [P, DC, GD]), st.sb("wg", [E8, GD])
        wgT = st.sb("wgT", [GD, E8])
        loaded = load_block(nc, k, [(redT[:], wk(ins["L2f_redT"])), (wg[:], ins["L2f_wg"])])
        sq, norm = st.sb("sq", [E8, GD]), st.sb("norm", [E8, 1])
        xr = st.sb("xr", [GD, TOK])
        logits, top = st.sb("logits", [P, NT, E8]), st.sb("top", [P, NT, 8])
        idx, idxf = st.sb("idx", [P, NT, 8], U32), st.sb("idxf", [P, NT, 8])
        ex, score = st.sb("ex", [P, NT, E8]), st.sb("score", [P, NT, 1])
        vector_wait(nc, k, loaded)

        def squares(dve, link):
            link(dve.tensor_tensor(sq[:], wg[:], wg[:], ALU.mult))
            link(dve.tensor_reduce(norm[:], sq[:], AX.X, ALU.add))

        vector_block(nc, k, squares)
        scalar_block(nc, k, lambda act, link: link(act.activation(norm[:], norm[:], ACT.Sqrt)))

        def unit(dve, link):
            link(dve.tensor_scalar(norm[:], norm[:], 1e-4, None, ALU.max))
            link(dve.reciprocal(norm[:], norm[:]))
            link(dve.tensor_scalar(wg[:], wg[:], norm[:, 0:1], None, ALU.mult))

        vector_block(nc, k, unit)
        jobs = [Job([(lambda bank: bank[0:GD, 0:E8], [(wg[:], None)])], "dve",
                    lambda e, bank: e.tensor_copy(wgT[:], bank[0:GD, 0:E8]))]
        for n in range(NHALF):
            jobs.append(Job([(lambda bank: bank[0:GD, :], [
                (redT[:, c, :], k.xnT[:, c, n * BANK:(n + 1) * BANK]) for c in range(DC)])], "act",
                lambda e, bank, n=n: e.activation(xr[:, n * BANK:(n + 1) * BANK], bank[0:GD, :], ACT.Copy)))
        matmul_pass(nc, k, jobs)
        groups = [(lambda bank, t=t: bank[:, t * E8:(t + 1) * E8], [(xr[:, t * P:(t + 1) * P], wgT[:])])
                  for t in range(NT)]
        matmul_pass(nc, k, [Job(groups, "dve", lambda e, bank: e.tensor_copy(
            logits[:].rearrange("p t e -> p (t e)"), bank[:, 0:NT * E8]))])

        def pick(dve, link):
            for t in range(NT):
                link(dve.max(top[:, t, :], logits[:, t, :]))
                link(dve.max_index(idx[:, t, :], top[:, t, :], logits[:, t, :]))
            link(dve.tensor_copy(idxf[:], idx[:]))
            link(dve.tensor_tensor(ex[:], logits[:], top[:, :, 0:1].broadcast_to((P, NT, E8)), ALU.subtract))

        vector_block(nc, k, pick)
        scalar_block(nc, k, lambda act, link: link(act.activation(ex[:], ex[:], ACT.Exp)))

        def score_gates(dve, link):
            link(dve.tensor_reduce(score[:, :, 0], ex[:], AX.X, ALU.add))
            link(dve.reciprocal(score[:, :, 0], score[:, :, 0]))
            link(dve.tensor_tensor(ex[:], k.iota8[:].unsqueeze(1).broadcast_to((P, NT, E8)),
                                   idxf[:, :, 0:1].broadcast_to((P, NT, E8)), ALU.is_equal))

        vector_block(nc, k, score_gates)
        rows, owner = place_tokens(nc, k, st, ex[:], 1)
        experts(nc, k, "L2e", ins["L2f_w1"], None, ins["L2f_w2"], 1024, rows, owner, score, 1,
                ins["L2f_b1"], ins["L2f_b2"])


def stage_L3_cross(nc, k, ins):
    normed(nc, k)
    silu_cross_attention(nc, k, "L3c", ins)


def stage_L3_attn(nc, k, ins):
    normed(nc, k)
    HID = 1024
    with Stage(nc, "L3a") as st:
        shapes = {"in_w": D, "actp_w": D, "qk_w": 2 * D, "out_w": D, "fc1_w": HID}
        w = {n: st.sb(n, [P, DC, dout]) for n, dout in shapes.items()}
        w["fc2_w"] = st.sb("fc2_w", [P, HID // P, D])
        loaded = load_block(nc, k, [(w[n][:], wk(ins["L3a_" + n])) for n in w])
        u = st.sb("u", [P, DC, TOK])
        u2 = st.sb("u2", [P, DC, TOK])
        gate = st.sb("gate", [P, DC, TOK])
        xi = st.sb("xi", [P, DC, TOK])
        qk = st.sb("qk", [P, 2 * DC, TOK])
        tok = st.sb("tok", [P, NT, D])

        def cpe1(dve, link):
            for c in range(DC):
                conv3(dve, link, u[:, c, :], k.xnT[:, c, :], k.col("L3_cpe1_w")[:, 3 * c:3 * c + 3],
                      k.col("L3_cpe1_b")[:, c:c + 1])
            link(dve.tensor_tensor(u[:], u[:], k.xnT[:], ALU.add))

        vector_block(nc, k, cpe1)
        add_transposed(nc, k, u, tok, add=False)
        layer_norm(nc, k, tok, tok, 1e-5)
        to_features(nc, k, tok, k.xnT, scale=k.col("L3_n1g"), bias=k.col("L3_n1b"))
        jobs = linear_jobs(w["actp_w"], k.xnT, DC, D, add_bias(k.col("L3_actp_b"), ACT.Silu)(gate))
        jobs += linear_jobs(w["in_w"], k.xnT, DC, D, lambda e, bank, m, n: e.tensor_scalar(
            u2[:, m, n * BANK:(n + 1) * BANK], bank, k.col("L3_in_b")[:, m:m + 1], None, ALU.add), by="dve")
        matmul_pass(nc, k, jobs, [loaded])

        def dwc(dve, link):
            for c in range(DC):
                conv3(dve, link, xi[:, c, :], u2[:, c, :], k.col("L3_dwc_w")[:, 3 * c:3 * c + 3],
                      k.col("L3_dwc_b")[:, c:c + 1])

        vector_block(nc, k, dwc)
        scalar_block(nc, k, lambda act, link: link(act.activation(xi[:], xi[:], ACT.Silu)))
        with Stage(nc, "L3q") as s2:
            pos = s2.sb("pos", [P, 2 * DC, TOK])
            rope = s2.sb("rope", [P, 2 * DC, TOK])
            k_tok, v_tok = s2.sb("k_tok", [S, B, D]), s2.sb("v_tok", [S, B, D])
            kmean = s2.sb("kmean", [P, DC, B])
            zd = s2.sb("zd", [P, DC, TOK])
            kv = s2.sb("kv", [P, B, DC, P])
            matmul_pass(nc, k, linear_jobs(w["qk_w"], xi, DC, 2 * D, lambda e, bank, m, n: e.activation(
                pos[:, m, n * BANK:(n + 1) * BANK], bank, ACT.Identity, bias=k.col("L3_qk_b")[:, m:m + 1])))
            elu_plus_one(nc, k, qk, pos)
            jobs = []
            for m in range(2 * DC):
                for n in range(NHALF):
                    jobs.append(Job([(full, [(k.rotation[:, m % DC, :], qk[:, m, n * BANK:(n + 1) * BANK])])], "act",
                                    lambda e, bank, m=m, n=n: e.activation(rope[:, m, n * BANK:(n + 1) * BANK],
                                                                           bank, ACT.Copy)))
            matmul_pass(nc, k, jobs)

            def means(dve, link):
                link(dve.tensor_reduce(kmean[:], qk[:, DC:2 * DC, :].rearrange("p c (b s) -> p c b s", s=S),
                                       AX.X, ALU.add))
                link(dve.tensor_scalar(kmean[:], kmean[:], 1.0 / S, None, ALU.mult))
                for c in range(DC):
                    link(dve.tensor_tensor(zd[:, c, :].rearrange("p (b s) -> p b s", s=S),
                                           qk[:, c, :].rearrange("p (b s) -> p b s", s=S),
                                           kmean[:, c, :].unsqueeze(2).broadcast_to((P, B, S)), ALU.mult))

            vector_block(nc, k, means)
            jobs = []
            for c in range(DC):
                for n in range(NHALF):
                    jobs.append(Job([(full, [(k.same_head[:], zd[:, c, n * BANK:(n + 1) * BANK])])], "dve",
                                    lambda e, bank, c=c, n=n: e.tensor_scalar(u2[:, c, n * BANK:(n + 1) * BANK],
                                                                              bank, 1e-6, None, ALU.add)))
            for src, dst in ((rope[:, DC:2 * DC, :], k_tok), (xi, v_tok)):
                for pair in range(B // 2):
                    groups = [(lambda bank, h=h, c=c: bank[0:S, h * D + c * P:h * D + (c + 1) * P],
                               [(src[:, c, (2 * pair + h) * S:(2 * pair + h + 1) * S], None)])
                              for h in range(2) for c in range(DC)]
                    out = dst[:, 2 * pair:2 * pair + 2, :].rearrange("p b d -> p (b d)")
                    jobs.append(Job(groups, "act", lambda e, bank, out=out: e.activation(out, bank[0:S, :], ACT.Copy)))
            matmul_pass(nc, k, jobs)
            vector_block(nc, k, lambda dve, link: link(dve.reciprocal(u2[:], u2[:])))
            jobs = []
            for pair in range(B // 2):
                groups = [(lambda bank, h=h, c=c: bank[:, (h * DC + c) * P:(h * DC + c + 1) * P],
                           [(k_tok[:, 2 * pair + h, c * P:(c + 1) * P], v_tok[:, 2 * pair + h, c * P:(c + 1) * P])])
                          for h in range(2) for c in range(DC)]
                out = kv[:, 2 * pair:2 * pair + 2, :, :].rearrange("p b c n -> p (b c) n")
                jobs.append(Job(groups, "dve", lambda e, bank, out=out: e.scalar_tensor_tensor(
                    out, bank.rearrange("p (a n) -> p a n", n=P), 1.0 / S,
                    k.same_head[:].unsqueeze(1).broadcast_to((P, 2 * DC, P)), ALU.mult, ALU.mult)))
            matmul_pass(nc, k, jobs)
            jobs = []
            for c in range(DC):
                for n in range(NHALF):
                    groups = [(lambda bank, b=b: bank[:, b * S:(b + 1) * S],
                               [(kv[:, 8 * n + b, c, :], rope[:, c, (8 * n + b) * S:(8 * n + b + 1) * S])])
                              for b in range(8)]
                    sl = slice(n * BANK, (n + 1) * BANK)
                    jobs.append(Job(groups, "dve", lambda e, bank, c=c, sl=sl: e.tensor_tensor(
                        zd[:, c, sl], bank, u2[:, c, sl], ALU.mult)))
            matmul_pass(nc, k, jobs)

            def lepe(dve, link):
                for c in range(DC):
                    conv3(dve, link, u2[:, c, :], xi[:, c, :], k.col("L3_lepe_w")[:, 3 * c:3 * c + 3],
                          k.col("L3_lepe_b")[:, c:c + 1])
                link(dve.tensor_tensor(zd[:], zd[:], u2[:], ALU.add))
                link(dve.tensor_tensor(xi[:], zd[:], gate[:], ALU.mult))

            vector_block(nc, k, lepe)
        jobs = linear_jobs(w["out_w"], xi, DC, D, lambda e, bank, m, n: e.scalar_tensor_tensor(
            u[:, m, n * BANK:(n + 1) * BANK], bank, k.col("L3_out_b")[:, m:m + 1],
            u[:, m, n * BANK:(n + 1) * BANK], ALU.add, ALU.add), by="dve")
        matmul_pass(nc, k, jobs)

        def cpe2(dve, link):
            for c in range(DC):
                conv3(dve, link, u2[:, c, :], u[:, c, :], k.col("L3_cpe2_w")[:, 3 * c:3 * c + 3],
                      k.col("L3_cpe2_b")[:, c:c + 1])
            link(dve.tensor_tensor(u[:], u[:], u2[:], ALU.add))

        vector_block(nc, k, cpe2)
        add_transposed(nc, k, u, tok, add=False)
        vector_block(nc, k, lambda dve, link: link(dve.tensor_tensor(k.x[:], k.x[:], tok[:], ALU.add)))
        layer_norm(nc, k, tok, tok, 1e-5)
        to_features(nc, k, tok, k.xnT, scale=k.col("L3_n2g"), bias=k.col("L3_n2b"))
        h1 = st.sb("h1", [P, HID // P, TOK])
        matmul_pass(nc, k, linear_jobs(w["fc1_w"], k.xnT, DC, HID, add_bias(k.col("L3_fc1_b"), ACT.Gelu)(h1)))
        residual_linear(nc, k, h1, w["fc2_w"], HID // P, "L3_fc2_b", k.x)


CAPACITY = int(1.25 * TOK / E8 * 2)


def stage_L3_ffn(nc, k, ins):
    normed(nc, k)
    with Stage(nc, "L3f") as st:
        wgT = st.sb("wgT", [P, DC, E8])
        loaded = load_block(nc, k, [(wgT[:], wk(ins["L3f_router"]))])
        logits, top = st.sb("logits", [P, NT, E8]), st.sb("top", [P, NT, E8])
        kept = st.sb("kept", [P, NT, 2])
        router_logits(nc, k, wgT, logits, loaded)
        rows, owner, gates = top2_gates(nc, k, st, logits, top, kept[:])
        experts(nc, k, "L3e", ins["L3f_w1"], None, ins["L3f_w2"], 1024, rows, owner, gates, 2)


STAGES = [stage_L0_cross, stage_L0_attn, stage_L0_ffn, stage_L1_cross, stage_L1_attn, stage_L1_ffn,
          stage_L2_cross, stage_L2_attn, stage_L2_ffn, stage_L3_cross, stage_L3_attn, stage_L3_ffn]

CONSTS = [("ident", P), ("ones64", P), ("parity", 2), ("blocks8", 8), ("same_head", P), ("causal_rows", S),
          ("causal_keys", S), ("causal_tile", P), ("upto", P), ("iota", 24),
          ("rope_cos", S), ("rope_sin", S), ("rotation", DC * P)]
N_CONST = sum(w for _, w in CONSTS)


def constants():
    p = np.arange(P)
    t = {}
    t["ident"] = np.eye(P)
    t["ones64"] = np.ones((P, P))
    t["parity"] = (p[:, None] // HD % 2 == np.arange(2)[None])
    t["blocks8"] = (p[:, None] // HD == np.arange(8)[None])
    t["same_head"] = (p[:, None] // HD == p[None] // HD)
    t["causal_rows"] = np.where(np.arange(S)[None] > p[:, None] % S, NEG, 0.0)
    t["causal_keys"] = (p[:, None] % S <= np.arange(S)[None])
    t["causal_tile"] = np.where((p[:, None] // S == p[None] // S) & (p[None] <= p[:, None]), 0.0, NEG)
    t["upto"] = (p[:, None] <= p[None])
    t["iota"] = np.broadcast_to(np.arange(24)[None], (P, 24))
    half = P // 2
    inv = (np.float32(1.0) / np.float32(10000.0) ** (np.arange(0, P, 2, dtype=np.float32) / np.float32(P)))
    ang = (np.arange(S, dtype=np.float32)[None] * inv[p % half][:, None]).astype(np.float32)
    t["rope_cos"] = np.cos(ang)
    t["rope_sin"] = np.where(p[:, None] < half, -1.0, 1.0) * np.sin(ang)
    kmax = D // 2
    theta = (np.float32(1.0) / np.float32(10000.0) ** (np.arange(kmax, dtype=np.float32) / np.float32(kmax)))
    rot = np.zeros((P, DC, P))
    for c in range(DC):
        for m in range(P // 2):
            cos, sin = np.cos(theta[c * half + m]), np.sin(theta[c * half + m])
            rot[2 * m, c, 2 * m], rot[2 * m + 1, c, 2 * m] = cos, -sin
            rot[2 * m, c, 2 * m + 1], rot[2 * m + 1, c, 2 * m + 1] = sin, cos
    t["rotation"] = rot.reshape(P, DC * P)
    return np.concatenate([np.asarray(t[n], np.float32).reshape(P, w) for n, w in CONSTS], axis=1)


def build(nc, ins, out, stages=STAGES):
    with ExitStack() as ctx:
        k = Kit()

        def sb(name, shape, dt=F32):
            return ctx.enter_context(nc.sbuf_tensor(name, shape, dt))

        def sem(name):
            return ctx.enter_context(nc.semaphore(name))

        k.ps = ctx.enter_context(nc.psum_tensor("ps", [P, 8, BANK], F32))
        k.x, k.xn, k.xnT = sb("x", [P, NT, D]), sb("xn", [P, NT, D]), sb("xnT", [P, DC, TOK])
        k.stats, k.mv, k.rstd = sb("stats", [P, NT, 6]), sb("mv", [P, NT, 2]), sb("rstd", [P, 3, NT])
        consts = sb("consts_sb", [P, N_CONST])

        def table(name):
            names = [n for n, _ in CONSTS]
            at = sum(w for _, w in CONSTS[:names.index(name)])
            return consts[:, at:at + CONSTS[names.index(name)][1]]

        k.ident, k.ones64, k.parity, k.blocks8 = table("ident"), table("ones64"), table("parity"), table("blocks8")
        k.same_head, k.upto, k.iota = table("same_head"), table("upto"), table("iota")
        k.iota8 = k.iota[:, 0:E8]
        k.causal_rows, k.causal_keys, k.causal_tile = table("causal_rows"), table("causal_keys"), table("causal_tile")
        k.rope_cos, k.rope_sin = table("rope_cos"), table("rope_sin")
        k.rotation = table("rotation").rearrange("p (c n) -> p c n", n=P)
        k.ones_row = k.ones64
        cols = sb("cols_sb", [P, NCOLS])
        k.col = lambda n: cols[:, COL_AT[n][0]:COL_AT[n][0] + COL_AT[n][1]]
        parts = sb("row_parts", [2 * THIRD + 1, len(ROWS), D], BF16)
        k.ones3 = sb("ones3", [2 * THIRD + 1, P], BF16)
        k.row = lambda n: parts[:, ROWS.index(n), :]
        k.filled, k.act_drained, k.dve_drained = sem("filled"), sem("act_drained"), sem("dve_drained")
        k.weights, k.ln_step, k.ln_root = sem("weights"), sem("ln_step"), sem("ln_root")
        k.dve_link, k.act_link, k.start, k.stored = sem("dve_link"), sem("act_link"), sem("start"), sem("stored")
        k.tick = sem("tick")
        k.sorted_in = nc.dram_tensor("sorted_in", (expert_tiles(2) * P, D), F32).ap()
        k.zeroed, k.zeros_made = sem("zeroed"), sem("zeros_made")
        k.n_filled = k.n_act = k.n_dve = k.n_weights = k.n_ln = k.n_root = k.n_dve_link = k.n_act_link = 0

        with Stage(nc, "first") as st:
            rows, rest = st.sb("rows", [1, len(ROWS), D]), st.sb("rest", [1, len(ROWS), D])
            with nc.Block() as block:

                @block.sync
                def _(sp):
                    sp.dma_start(k.x[:], ins["x"].rearrange("(t p) d -> p t d", p=P)).then_inc(k.start, 16)
                    sp.dma_start(consts[:], ins["consts"]).then_inc(k.start, 16)
                    sp.dma_start(cols[:], ins["cols"]).then_inc(k.start, 16)
                    sp.dma_start(rows[:], ins["rows"]).then_inc(k.start, 16)
                    sp.wait_ge(k.zeros_made, 1)
                    for part in range(ZERO_PARTS):
                        n = min(NT, expert_tiles(2) - part * NT)
                        sp.dma_start(k.sorted_in.rearrange("(t p) d -> p t d", p=P)[:, part * NT:part * NT + n, :],
                                     k.xn[:, 0:n, :]).then_inc(k.zeroed, 16)
                    sp.wait_ge(k.start, START)
                    sp.wait_ge(k.zeroed, 16 * ZERO_PARTS)

                @block.vector
                def _(dve):
                    dve.memset(k.xn[:], 0.0).then_inc(k.zeros_made, 1)

            def split_rows(dve, link):
                link(dve.memset(k.ones3[:], 1.0))
                link(dve.memset(parts[:], 0.0))
                for n in range(3):
                    part = parts[n * THIRD:n * THIRD + 1, :, :]
                    link(dve.tensor_copy(part, rows[:]))
                    if n < 2:
                        link(dve.tensor_copy(rest[:], part))
                        link(dve.tensor_tensor(rows[:], rows[:], rest[:], ALU.subtract))

            vector_block(nc, k, split_rows)
        for stage in stages:
            stage(nc, k, ins)

        with nc.Block() as block:

            @block.sync
            def _(sp):
                sp.dma_start(out.rearrange("(t p) d -> p t d", p=P), k.x[:]).then_inc(k.stored, 16)
                sp.wait_ge(k.stored, 16)


def laid_out(v):
    a = {n: np.asarray(x) for n, x in v.items()}
    o = {"x": a["x"].reshape(TOK, D), "ctx": a["ctx_1024"],
         "ctxT": a["ctx_1024"].transpose(0, 2, 1).reshape(B, DC, P, M),
         "mask": a["mask_BxSxS2_bk1"], "maskT": a["mask_1xSxS2_ff0"][0].T}
    half = P // 2

    def swap(w):
        return np.concatenate([w[..., half:], w[..., :half]], axis=-1)

    for n in ("wq", "wqc", "wqr", "wkv", "wkr", "wkc", "wv", "wo"):
        o["L0_" + n] = a["L0_attn_" + n]
    o["L0_wqr_sw"], o["L0_wkr_sw"] = swap(a["L0_attn_wqr"]), swap(a["L0_attn_wkr"])
    o["L0_Wg"] = a["L0_ffn_Wg"].T
    o["L0_W1"], o["L0_W2"] = (a["L0_ffn_" + n].transpose(0, 2, 1) for n in ("W1", "W2"))
    o["L0_W3"] = a["L0_ffn_W3"].transpose(0, 2, 1)
    o["L1x_Wq"], o["L1x_WkT"] = a["L1_xattn_Wq"], a["L1_xattn_Wk"].T
    o["L1x_Wv"], o["L1x_Wo"] = a["L1_xattn_Wv"], a["L1_xattn_Wo"]
    o["L1a_wqkv"], o["L1a_wo"] = a["L1_attn_w_qkv"].T, a["L1_attn_w_out"].T
    o["L1f_w1"], o["L1f_w2"] = a["L1_ffn_w1"].T, a["L1_ffn_w2"].T
    for n in "qkv":
        o["L2x_w" + n] = a["L2_xattn_kernel_" + n][0, 0]
    for n, m in (("wq", "Wq"), ("wk", "Wk"), ("wv", "Wv"), ("wfc", "Wfc")):
        o["L2a_" + n] = a["L2_attn_" + m]
    o["L2f_redT"], o["L2f_wg"] = a["L2_ffn_wg_red"].T, a["L2_ffn_wg"]
    o["L2f_w1"], o["L2f_w2"] = a["L2_ffn_w1"], a["L2_ffn_w2"]
    o["L2f_b1"] = a["L2_ffn_b1"].reshape(E8, 8, P).transpose(0, 2, 1)
    o["L2f_b2"] = a["L2_ffn_b2"].reshape(E8, 1, D)
    for n in ("in_w", "actp_w", "qk_w", "out_w", "fc1_w", "fc2_w"):
        o["L3a_" + n] = a["L3_attn_" + n]
    o["L3f_router"] = a["L3_ffn_router_w"].T
    o["L3f_w1"], o["L3f_w2"] = a["L3_ffn_w1"], a["L3_ffn_w2"]

    def taps(w):
        return w[:, 0, :].reshape(-1, P, 3).transpose(1, 0, 2).reshape(P, -1)

    def col(b):
        if b.size < P:
            b = np.concatenate([b, np.zeros(P - b.size, np.float32)])
        return b.reshape(-1, P).T

    c = {"L0_bq": a["L0_attn_bq"], "L0_bkv": a["L0_attn_bkv"], "L0_bqc": a["L0_attn_bqc"],
         "L0_bkc": a["L0_attn_bkc"], "L0_bqr": a["L0_attn_bqr"], "L0_bkr": a["L0_attn_bkr"],
         "L0_bqr_sw": swap(a["L0_attn_bqr"]), "L0_bkr_sw": swap(a["L0_attn_bkr"]),
         "L1a_bqk": a["L1_attn_b_qkv"][:2 * D], "L1f_cb": a["L1_ffn_conv_b"],
         "L2x_bq": a["L2_xattn_bias_q"], "L2x_bk": a["L2_xattn_bias_k"],
         "L2a_gamma": a["L2_attn_gamma"], "L2a_beta": a["L2_attn_beta"]}
    for n, m in (("cpe1_b", "cpe1_b"), ("n1g", "norm1_g"), ("n1b", "norm1_b"), ("in_b", "in_b"),
                 ("actp_b", "actp_b"), ("dwc_b", "dwc_b"), ("qk_b", "qk_b"), ("lepe_b", "lepe_b"),
                 ("out_b", "out_b"), ("cpe2_b", "cpe2_b"), ("n2g", "norm2_g"), ("n2b", "norm2_b"),
                 ("fc1_b", "fc1_b")):
        c["L3_" + n] = a["L3_attn_" + m]
    c = {n: col(x) for n, x in c.items()}
    c["L1f_cw"] = taps(a["L1_ffn_conv_w"])
    for n in ("cpe1_w", "dwc_w", "lepe_w", "cpe2_w"):
        c["L3_" + n] = taps(a["L3_attn_" + n])
    o["cols"] = np.concatenate([c[n] for n, _ in COLS], axis=1)
    r = {"L0_bv": a["L0_attn_bv"], "L0_bo": a["L0_attn_bo"], "L1x_bo": a["L1_xattn_bo"],
         "L1a_bv": a["L1_attn_b_qkv"][2 * D:], "L1a_bo": a["L1_attn_b_out"], "L2x_bv": a["L2_xattn_bias_v"],
         "L2a_bfc": a["L2_attn_bfc"], "L3_fc2_b": a["L3_attn_fc2_b"]}
    o["rows"] = np.stack([r[n] for n in ROWS])[None]
    o["consts"] = constants()
    return {n: np.ascontiguousarray(x) for n, x in o.items()}


def kernel(**inputs):
    import concourse.bacc as _bacc
    from concourse.bass_utils import run_bass_kernel_spmd as _run

    arrays = {f"in_{n}": x for n, x in laid_out(inputs).items()}
    nc = _bacc.Bacc("TRN2", target_bir_lowering=False, num_devices=1)
    ins = {n[3:]: nc.dram_tensor(n, x.shape, mybir.dt.from_np(x.dtype), kind="ExternalInput").ap()
           for n, x in arrays.items()}
    out = nc.dram_tensor("out_x", (TOK, D), F32, kind="ExternalOutput").ap()
    build(nc, ins, out)
    r = _run(nc, [arrays], core_ids=[0])
    return r.results[0]["out_x"].reshape(B, S, D)
```

```python
from contextlib import ExitStack

import numpy as np

import concourse.bass as bass
from concourse import mybir

F32 = mybir.dt.float32
U32 = mybir.dt.uint32
U8 = mybir.dt.uint8
BF16 = mybir.dt.bfloat16
F32R = mybir.dt.float32r
ALU = mybir.AluOpType
ACT = mybir.ActivationFunctionType
AX = mybir.AxisListType

P = 128
B, S, D = 16, 64, 256
M = 1601
TOK = B * S
NT = TOK // P
DC = D // P
KT = (M + P - 1) // P
KFULL = M // P
KREST = M - KFULL * P
BANK = 512
NHALF = TOK // BANK
H16 = 16
HD = D // H16
E8 = 8
PAIRS = H16 // 2
PAIR_F = 2 * HD
NEG = -1.0e30
START = 64

CHUNKS = [(c, min(BANK, M - c)) for c in range(0, M, BANK)]
NCH = len(CHUNKS)
MP = M + M % 2
ZERO_PARTS = 3
THIRD = 32


def key_rows(t):
    return P if t < KFULL else KREST


COLS = [
    ("L0_bq", 1), ("L0_bkv", 1), ("L0_bqc", 1), ("L0_bkc", 1), ("L0_bqr", 1), ("L0_bkr", 1),
    ("L0_bqr_sw", 1), ("L0_bkr_sw", 1), ("L1a_bqk", 4), ("L1f_cw", 24), ("L1f_cb", 8),
    ("L2x_bq", 2), ("L2x_bk", 2), ("L2a_gamma", 2), ("L2a_beta", 2),
    ("L3_cpe1_w", 6), ("L3_cpe1_b", 2), ("L3_n1g", 2), ("L3_n1b", 2), ("L3_in_b", 2), ("L3_actp_b", 2),
    ("L3_dwc_w", 6), ("L3_dwc_b", 2), ("L3_qk_b", 4), ("L3_lepe_w", 6), ("L3_lepe_b", 2),
    ("L3_out_b", 2), ("L3_cpe2_w", 6), ("L3_cpe2_b", 2), ("L3_n2g", 2), ("L3_n2b", 2), ("L3_fc1_b", 8),
]
ROWS = ["L0_bv", "L0_bo", "L1x_bo", "L1a_bv", "L1a_bo", "L2x_bv", "L2a_bfc", "L3_fc2_b"]
COL_AT, _n = {}, 0
for _name, _w in COLS:
    COL_AT[_name] = (_n, _w)
    _n += _w
NCOLS = _n


class Signal:

    def __init__(self, nc, ctx, name, credit=0):
        self.sem = ctx.enter_context(nc.semaphore(name))
        self.credit = credit

    def at(self, count):
        return count + self.credit


class Kit:
    pass


def give_credits(nc, signals):
    with nc.Block() as block:

        @block.sync
        def _(sp):
            for s in signals:
                if s.credit:
                    sp.sem_inc(s.sem, s.credit)


class Job:

    def __init__(self, groups, by, drain):
        self.groups, self.by, self.drain = groups, by, drain


def matmul_pass(nc, k, jobs, loaded=()):
    base_f, base_a, base_v = k.n_filled, k.n_act, k.n_dve
    nth = []
    na = nv = 0
    for job in jobs:
        if job.by == "act":
            na += 1
            nth.append((k.act_drained, base_a + na))
        else:
            nv += 1
            nth.append((k.dve_drained, base_v + nv))
    with nc.Block() as block:

        @block.tensor
        def _(pe):
            for sem, value in loaded:
                pe.wait_ge(sem, value)
            for j, job in enumerate(jobs):
                bank = k.ps[:, j % 8, :]
                if j >= 8:
                    pe.wait_ge(*nth[j - 8])
                for where, products in job.groups:
                    out = where(bank)
                    for n, (lhsT, rhs) in enumerate(products):
                        if rhs is None:
                            rows = lhsT.shape[0]
                            last = pe.transpose(out, lhsT, k.ident[0:rows, 0:rows])
                        else:
                            last = pe.matmul(out, lhsT, rhs, start=(n == 0), stop=(n == len(products) - 1))
                last.then_inc(k.filled, 1)

        @block.scalar
        def _(act):
            for j, job in enumerate(jobs):
                if job.by == "act":
                    act.wait_ge(k.filled, base_f + j + 1)
                    job.drain(act, k.ps[:, j % 8, :]).then_inc(k.act_drained, 1)

        @block.vector
        def _(dve):
            for j, job in enumerate(jobs):
                if job.by == "dve":
                    dve.wait_ge(k.filled, base_f + j + 1)
                    job.drain(dve, k.ps[:, j % 8, :]).then_inc(k.dve_drained, 1)

    k.n_filled += len(jobs)
    k.n_act += na
    k.n_dve += nv


def full(bank):
    return bank


def load_block(nc, k, copies):
    with nc.Block() as block:

        @block.sync
        def _(sp):
            for dst, src in copies:
                sp.dma_start(dst, src).then_inc(k.weights, 16)

    k.n_weights += 16 * len(copies)
    return (k.weights, k.n_weights)


def wk(w):
    return w.rearrange("(c p) n -> p c n", p=P)


def layer_norm(nc, k, src, out, eps, outT=None):
    banks = [(n, c) for n in range(NHALF) for c in range(DC)] if outT is not None else []
    drained_by = ["act"] * (len(banks) - 1) + ["dve"] * min(1, len(banks))
    halves = [outT[:, c, n * BANK:(n + 1) * BANK] for n, c in banks]
    base_f = k.n_filled
    with nc.Block() as block:
        base = k.n_ln

        @block.tensor
        def _(pe):
            for x, (n, c) in enumerate(banks):
                for t in range(4):
                    pe.wait_ge(k.ln_step, base + 2 * NT + 2 + 4 * n + t + 1)
                    last = pe.transpose(k.ps[:, x, t * P:(t + 1) * P], out[:, 4 * n + t, c * P:(c + 1) * P], k.ident[:])
                last.then_inc(k.filled, 1)

        @block.vector
        def _(dve):
            for t in range(NT):
                dve.bn_stats(k.stats[:, t, :], src[:, t, :]).then_inc(k.ln_step, 1)
            for t in range(NT):
                dve.wait_ge(k.ln_step, base + t + 1)
                dve.bn_aggr(k.mv[:, t, :], k.stats[:, t, :]).then_inc(k.ln_step, 1)
            dve.wait_ge(k.ln_step, base + 2 * NT)
            dve.tensor_scalar(k.rstd[:, 0, :], k.mv[:, :, 1], eps, None, ALU.add).then_inc(k.ln_step, 1)
            dve.wait_ge(k.ln_root, k.n_root + 1)
            dve.reciprocal(k.rstd[:, 2, :], k.rstd[:, 1, :]).then_inc(k.ln_step, 1)
            dve.wait_ge(k.ln_step, base + 2 * NT + 2)
            for t in range(NT):
                dve.tensor_scalar(out[:, t, :], src[:, t, :], k.mv[:, t, 0:1], k.rstd[:, 2, t:t + 1],
                                  ALU.subtract, ALU.mult).then_inc(k.ln_step, 1)
            for x, by in enumerate(drained_by):
                if by == "dve":
                    dve.wait_ge(k.filled, base_f + x + 1)
                    dve.tensor_copy(halves[x], k.ps[:, x, :]).then_inc(k.dve_drained, 1)

        @block.scalar
        def _(act):
            act.wait_ge(k.ln_step, base + 2 * NT + 1)
            act.activation(k.rstd[:, 1, :], k.rstd[:, 0, :], ACT.Sqrt).then_inc(k.ln_root, 1)
            for x, by in enumerate(drained_by):
                if by == "act":
                    act.wait_ge(k.filled, base_f + x + 1)
                    act.activation(halves[x], k.ps[:, x, :], ACT.Copy).then_inc(k.act_drained, 1)

    k.n_filled += len(banks)
    k.n_act += drained_by.count("act")
    k.n_dve += drained_by.count("dve")
    k.n_ln += 3 * NT + 2
    k.n_root += 1


def to_features(nc, k, src, dst, chunks=DC, scale=None, bias=None):
    jobs = []
    for c in range(chunks):
        for n in range(NHALF):
            groups = [(lambda bank, t=t: bank[:, t * P:(t + 1) * P],
                       [(src[:, n * 4 + t, c * P:(c + 1) * P], None)]) for t in range(4)]
            out = dst[:, c, n * BANK:(n + 1) * BANK]
            if scale is not None:
                jobs.append(Job(groups, "dve", lambda e, bank, out=out, c=c: e.tensor_scalar(
                    out, bank, scale[:, c:c + 1], bias[:, c:c + 1], ALU.mult, ALU.add)))
            elif (c + n) % 2:
                jobs.append(Job(groups, "dve", lambda e, bank, out=out: e.tensor_copy(out, bank)))
            else:
                jobs.append(Job(groups, "act", lambda e, bank, out=out: e.activation(out, bank, ACT.Copy)))
    matmul_pass(nc, k, jobs)


def add_transposed(nc, k, srcT, dst, add=True):
    jobs = []
    for t in range(NT):
        groups = [(lambda bank, c=c: bank[:, c * P:(c + 1) * P], [(srcT[:, c, t * P:(t + 1) * P], None)])
                  for c in range(DC)]
        if add:
            jobs.append(Job(groups, "dve", lambda e, bank, t=t: e.tensor_tensor(
                dst[:, t, :], dst[:, t, :], bank[:, 0:D], ALU.add)))
        else:
            jobs.append(Job(groups, "act", lambda e, bank, t=t: e.activation(
                dst[:, t, :], bank[:, 0:D], ACT.Copy)))
    matmul_pass(nc, k, jobs)


def linear_jobs(wt, xT, kchunks, width, drain, by="act", krows=P):
    jobs = []
    for m0 in range(0, width, P):
        mw = min(P, width - m0)
        for n in range(NHALF):
            products = [(wt[0:krows, c, m0:m0 + mw], xT[0:krows, c, n * BANK:(n + 1) * BANK])
                        for c in range(kchunks)]
            jobs.append(Job([(lambda bank, mw=mw: bank[0:mw, :], products)], by,
                            lambda e, bank, m=m0 // P, n=n, mw=mw: drain(e, bank[0:mw, :], m, n)))
    return jobs


def residual_linear(nc, k, xT, w, kchunks, bias_row, dst, loaded=(), add=True):
    jobs = []
    for t in range(NT):
        products = [(xT[:, c, t * P:(t + 1) * P], w[:, c, :]) for c in range(kchunks)]
        if bias_row is not None:
            products.append((k.ones3[:, :], k.row(bias_row)))
        if add:
            jobs.append(Job([(lambda bank: bank[:, 0:D], products)], "dve", lambda e, bank, t=t: e.tensor_tensor(
                dst[:, t, :], dst[:, t, :], bank[:, 0:D], ALU.add)))
        else:
            jobs.append(Job([(lambda bank: bank[:, 0:D], products)], "act", lambda e, bank, t=t: e.activation(
                dst[:, t, :], bank[:, 0:D], ACT.Copy)))
    matmul_pass(nc, k, jobs, loaded)


def keep_high(engine, hi, x):
    return engine.tensor_copy(hi.bitcast(F32R), x)


def keep_low(engine, lo, x, hi):
    return engine.tensor_tensor(lo.bitcast(F32R), x, hi, ALU.subtract)


def matmul_split(pe, out, lhsT, rhs, start, stop):
    (ah, al), (bh, bl) = [(hi.bitcast(F32R), lo.bitcast(F32R)) for hi, lo in (lhsT, rhs)]
    pe.matmul(out, ah, bh, start=start, stop=False)
    pe.matmul(out, ah, bl, start=False, stop=False)
    return pe.matmul(out, al, bh, start=False, stop=stop)


class SplitKeys:

    def __init__(self, k, ctx, signal, name, ins, staging):
        self.k, self.ins, self.staging = k, ins, staging
        self.low = ctx.enter_context(k.nc.sbuf_tensor(f"{name}_keys_lo", [P, 2, DC, MP], F32))
        self.high = ctx.enter_context(k.nc.sbuf_tensor(f"{name}_keys_hi", [P, 2, DC, MP], F32))
        self.n = len(staging)
        self.staged = [signal(f"staged{x}") for x in range(self.n)]
        self.high_done, self.ready = signal("keys_high"), signal("keys_split", self.n)

    def pad(self, dve):
        for part in (self.high, self.low):
            dve.memset(part[:, :, :, M:MP], 0.0)

    def first(self, dve):
        self.pad(dve)
        self.split(dve, 0, 0)

    def others(self, pool, body):
        pool.wait_ge(self.ready.sem, self.ready.at(DC))
        body(0, 0, False)
        body(0, 1, True)
        with pool.Fori(1, B // 2) as i:
            for j in range(2):
                body(i, j, True)

    def load(self, sp, i, j):
        for f in range(DC):
            chunk = j * DC + f
            sp.wait_ge(self.ready.sem, i * (2 * DC) + self.ready.at(chunk + 1 - self.n))
            sp.sem_inc(self.k.tick, 1)
            sp.dma_start(self.staging[chunk % self.n], self.ins["ctxT"][i * 2 + j, f]
                         ).then_inc(self.staged[chunk % self.n].sem, 16)

    def split(self, pool, i, j):
        each = 2 * DC // self.n
        for f in range(DC):
            chunk = j * DC + f
            src = self.staging[chunk % self.n]
            pool.wait_ge(self.staged[chunk % self.n].sem, i * (16 * each) + 16 * (chunk // self.n + 1))
            pool.sem_inc(self.k.tick, 1)
            keep_high(pool, self.high[:, j, f, 0:M], src).then_inc(self.high_done.sem, 1)
            pool.wait_ge(self.high_done.sem, i * (2 * DC) + (chunk + 1))
            pool.sem_inc(self.k.tick, 1)
            keep_low(pool, self.low[:, j, f, 0:M], src, self.high[:, j, f, 0:M]).then_inc(self.ready.sem, 1)

    def wait_ready(self, pe, i, j):
        pe.wait_ge(self.ready.sem, i * (2 * DC) + self.ready.at((j + 1) * DC))

    def columns(self, j, f, at, n):
        return self.high[:, j, f, at:at + n], self.low[:, j, f, at:at + n]


def softmax_cross_attention(nc, k, name, ins, heads16, q_all):
    TPB = PAIRS if heads16 else 4
    U = 2 * TPB
    with ExitStack() as ctx:
        def sb(n, shape, dt=F32):
            return ctx.enter_context(nc.sbuf_tensor(f"{name}_{n}", shape, dt))

        def signal(n, credit=0):
            return Signal(nc, ctx, f"{name}_{n}", credit)

        rows_sb = sb("rows", [P, 2, KT, D])
        prob = sb("prob", [P, 2, M])
        mx = sb("mx", [P, 2, NCH])
        nmx = sb("nmx", [P, 2, 1])
        sums = sb("sums", [P, U])
        rinv = sb("rinv", [P, U])
        if heads16:
            mask8 = sb("mask8", [P, 2, M], U8)
            maskf = sb("maskf", [P, 2, M])
            probT = [sb(f"probT{x}", [P, KT * P]) for x in range(2)]
            q_raw = sb("q_raw", [P, H16, S])
            q_sb, q_hi = sb("q", [P, 2, H16, S]), sb("q_hi", [P, 2, H16, S])
            stage = sb("stage", [P, 2, M])
            staging = [stage[:, x, :] for x in range(2)]
            att = sb("att", [P, D])
        else:
            q_sb = sb("q", [P, 2, DC, BANK])
            q_hi = sb("q_hi", [P, 2, DC, BANK])
            probT = [k.xn[:].rearrange("p t d -> p (t d)")[:, 0:KT * P], sb("probT", [P, KT * P])]
            staging = [k.xnT[:].rearrange("p c n -> p (c n)")[:, 0:M]]

        keys = SplitKeys(k, ctx, signal, name, ins, staging)
        loaded = [signal(f"loaded{j}") for j in range(2)]
        mask_ready = signal("mask_ready", 2)
        q_ready, q_step = signal("q_ready"), signal("q_step")
        s_filled = signal("s_filled", U * NCH)
        s_taken = signal("s_taken", (U + 1) * NCH)
        max_ready = signal("max_ready")
        exp_done = signal("exp_done", 1)
        t_filled = signal("t_filled", 8)
        t_act = signal("t_act", 1)
        t_dve = signal("t_dve", 1)
        av_done = signal("av_done", U + 2)
        r_ready = signal("r_ready")
        o_drained = signal("o_drained", 2)
        x_step = signal("x_step", 1)
        give_credits(nc, [keys.ready, mask_ready, s_filled, s_taken, exp_done, t_filled, t_act, t_dve, av_done, o_drained, x_step])
        S_BANK, T_BANK, O_BANK = 0, 4, 6
        n_loads = 4 if heads16 else 2
        sflat = k.ps[:, S_BANK:S_BANK + NCH, :].rearrange("p a b -> p (a b)")

        with nc.Block() as block:

            @block.sync
            def _(sp):
                with sp.Fori(0, B // 2) as i:
                    for j in range(2):
                        b = i * 2 + j
                        keys.load(sp, i, j)
                        sp.wait_ge(av_done.sem, i * U + av_done.at(-U + (j + 1) * TPB))
                        sp.dma_start(rows_sb[:, j, 0:KFULL, :],
                                     ins["ctx"][b, 0:KFULL * P, :].rearrange("(t p) d -> p t d", p=P)
                                     ).then_inc(loaded[j].sem, 16)
                        sp.dma_start(rows_sb[0:KREST, j, KFULL, :], ins["ctx"][b, KFULL * P:M, :]
                                     ).then_inc(loaded[j].sem, 16)
                        if heads16:
                            sp.wait_ge(mask_ready.sem, i * 2 + mask_ready.at(j - 1))
                            sp.sem_inc(k.tick, 1)
                            for h in range(2):
                                sp.dma_start(mask8[h * S:(h + 1) * S, j, :], ins["mask"][b]
                                             ).then_inc(loaded[j].sem, 16)

            @block.gpsimd
            def _(pool):
                def body(i, j, split):
                    if split:
                        pool.wait_ge(s_filled.sem, i * (U * NCH) + s_filled.at(((j + 1) * TPB - U) * NCH))
                        pool.sem_inc(k.tick, 1)
                        keys.split(pool, i, j)
                    if heads16:
                        pool.wait_ge(loaded[j].sem, i * 16 * n_loads + 16 * n_loads)
                        pool.wait_ge(s_taken.sem, i * (U * NCH) + s_taken.at(((j + 1) * TPB - U) * NCH))
                        pool.sem_inc(k.tick, 1)
                        pool.tensor_scalar(maskf[:, j, :], mask8[:, j, :], -10000.0, None, ALU.mult
                                           ).then_inc(mask_ready.sem, 1)

                keys.others(pool, body)

            @block.tensor
            def _(pe):
                def body(i, more, first=False):
                    def scores(u):
                        j, t = u // TPB, u % TPB
                        own = j % 2
                        if t == 0:
                            keys.wait_ready(pe, i, j)
                            pe.wait_ge(q_ready.sem, i * 2 + (j + 1))
                        for c, (at, w) in enumerate(CHUNKS):
                            if heads16:
                                pe.wait_ge(s_taken.sem, i * (U * NCH) + s_taken.at(NCH * (u - 1) + c + 1))
                                pair = slice(2 * t, 2 * t + 2)
                                last = matmul_split(pe, k.ps[:, S_BANK + c, 0:w + w % 2],
                                                    (q_hi[:, own, pair, :], q_sb[:, own, pair, :]),
                                                    keys.columns(own, t // 4, at, w + w % 2), True, True)
                            else:
                                if c == 0:
                                    pe.wait_ge(exp_done.sem, i * U + exp_done.at(u))
                                for f in range(DC):
                                    rows = slice(t * P, (t + 1) * P)
                                    last = matmul_split(pe, k.ps[:, S_BANK + c, 0:w + w % 2],
                                                        (q_hi[:, own, f, rows], q_sb[:, own, f, rows]),
                                                        keys.columns(own, f, at, w + w % 2), f == 0, f == DC - 1)
                            last.then_inc(s_filled.sem, 1)

                    def transposes(u, groups):
                        if groups[0] == 0:
                            pe.wait_ge(exp_done.sem, i * U + exp_done.at(u + 1))
                        for g in groups:
                            free = (t_act, t_dve)[g % 2]
                            pe.wait_ge(free.sem, i * (2 * U) + free.at(2 * u + g // 2))
                            for kt in range(4 * g, min(4 * g + 4, KT)):
                                rows = key_rows(kt)
                                last = pe.transpose(k.ps[0:rows, T_BANK + g % 2, (kt % 4) * P:(kt % 4 + 1) * P],
                                                    prob[:, u % 2, kt * P:kt * P + rows], k.ident[:])
                            last.then_inc(t_filled.sem, 1)

                    def values(u, kts):
                        j, t = u // TPB, u % TPB
                        if kts[0] == 0:
                            if t == 0:
                                pe.wait_ge(loaded[j].sem, i * 16 * n_loads + 16 * n_loads)
                            pe.wait_ge(t_act.sem, i * (2 * U) + t_act.at(2 * u + 2))
                            pe.wait_ge(t_dve.sem, i * (2 * U) + t_dve.at(2 * u + 2))
                            if not heads16:
                                pe.wait_ge(o_drained.sem, i * U + o_drained.at(u - 1))
                            elif t == 0:
                                pe.wait_ge(o_drained.sem, i * 2 + o_drained.at(j - 1))
                        for kt in kts:
                            rows = key_rows(kt)
                            if heads16:
                                out = k.ps[:, O_BANK + j, t * PAIR_F:(t + 1) * PAIR_F]
                                rhs = rows_sb[0:rows, j, kt, t * PAIR_F:(t + 1) * PAIR_F]
                            else:
                                out = k.ps[:, O_BANK + u % 2, 0:D]
                                rhs = rows_sb[0:rows, j, kt, :]
                            last = pe.matmul(out, probT[u % 2][0:rows, kt * P:(kt + 1) * P], rhs,
                                             start=(kt == 0), stop=(kt == KT - 1))
                        if kts[-1] == KT - 1:
                            last.then_inc(av_done.sem, 1)

                    if first:
                        scores(0)
                        return
                    for u in range(U):
                        if u + 1 < U or more:
                            scores(u + 1)
                        transposes(u, (0, 1))
                        if u > 0:
                            values(u - 1, range(0, KT // 2))
                        transposes(u, (2, 3))
                        if u > 0:
                            values(u - 1, range(KT // 2, KT))
                    values(U - 1, range(KT))

                body(0, True, first=True)
                with pe.Fori(0, B // 2 - 1) as i:
                    body(i, True)
                body(B // 2 - 1, False)

            def take_transposes(eng, i, u, free, groups, copy):
                eng.wait_ge(av_done.sem, i * U + av_done.at(u - 1))
                for g in groups:
                    eng.wait_ge(t_filled.sem, i * (4 * U) + t_filled.at(4 * u + g + 1))
                    n = min(4, KT - 4 * g)
                    rows = key_rows(4 * g)
                    copy(probT[u % 2][0:rows, 4 * g * P:(4 * g + n) * P],
                         k.ps[0:rows, T_BANK + g % 2, 0:n * P]).then_inc(free.sem, 1)

            @block.scalar
            def _(act):
                def body(i, more, first=False):
                    def exps(u):
                        act.wait_ge(max_ready.sem, i * U + (u + 1))
                        act.wait_ge(t_filled.sem, i * (4 * U) + t_filled.at(4 * (u - 1)))
                        src = prob[:, u % 2, :] if heads16 else sflat[:, 0:M]
                        act.activation(prob[:, u % 2, :], src, ACT.Exp, bias=nmx[:, u % 2, :],
                                       accum_out=sums[:, u % U:u % U + 1]).then_inc(exp_done.sem, 1)

                    def weighted_rows(u):
                        act.wait_ge(av_done.sem, i * U + av_done.at(u + 1))
                        act.wait_ge(r_ready.sem, i * U + (u + 1))
                        act.activation(q_all.rearrange("p b f n -> p b (f n)")[
                                           :, i * 2 + u // TPB, (u % TPB) * D:(u % TPB + 1) * D],
                                       k.ps[:, O_BANK + u % 2, 0:D], ACT.Copy, scale=rinv[:, u:u + 1]
                                       ).then_inc(o_drained.sem, 1)

                    if first:
                        exps(0)
                        return
                    for u in range(U):
                        take_transposes(act, i, u, t_act, (0, 2),
                                        lambda o, s: act.activation(o, s, ACT.Copy))
                        if u + 1 < U or more:
                            exps(u + 1)
                        if not heads16 and u > 0:
                            weighted_rows(u - 1)
                    if not heads16:
                        weighted_rows(U - 1)

                body(0, True, first=True)
                with act.Fori(0, B // 2 - 1) as i:
                    body(i, True)
                body(B // 2 - 1, False)

            @block.vector
            def _(dve):
                def queries(i, j):
                    if heads16:
                        block_queries(dve, k, q_raw, q_all, i * P + j * S, HD ** -0.5).then_inc(q_step.sem, 1)
                        dve.wait_ge(q_step.sem, i * 4 + (2 * j + 1))
                        keep_high(dve, q_hi[:, j, :, :], q_raw[:]).then_inc(q_step.sem, 1)
                        dve.wait_ge(q_step.sem, i * 4 + (2 * j + 2))
                        keep_low(dve, q_sb[:, j, :, :], q_raw[:], q_hi[:, j, :, :]).then_inc(q_ready.sem, 1)
                    else:
                        keep_high(dve, q_hi[:, j, :, :], q_all[:, i * 2 + j, :, :]).then_inc(q_step.sem, 1)
                        dve.wait_ge(q_step.sem, i * 2 + (j + 1))
                        keep_low(dve, q_sb[:, j, :, :], q_all[:, i * 2 + j, :, :], q_hi[:, j, :, :]
                                 ).then_inc(q_ready.sem, 1)

                def body(i, more, first=False):
                    def maxima(u):
                        j, t = u // TPB, u % TPB
                        if heads16 and t == 0:
                            dve.wait_ge(mask_ready.sem, i * 2 + mask_ready.at(j + 1))
                        dve.wait_ge(t_filled.sem, i * (4 * U) + t_filled.at(4 * (u - 1)))
                        for c, (at, w) in enumerate(CHUNKS):
                            dve.wait_ge(s_filled.sem, i * (U * NCH) + s_filled.at(u * NCH + c + 1))
                            if heads16:
                                dve.sem_inc(k.tick, 1)
                                ins_ = dve.tensor_tensor_reduce(
                                    out=prob[:, u % 2, at:at + w], in0=k.ps[:, S_BANK + c, 0:w],
                                    in1=maskf[:, j % 2, at:at + w], scale=1.0, scalar=-3.0e38, op0=ALU.add,
                                    op1=ALU.max, accum_out=mx[:, u % 2, c:c + 1])
                            else:
                                ins_ = dve.tensor_reduce(mx[:, u % 2, c:c + 1], k.ps[:, S_BANK + c, 0:w], AX.X, ALU.max)
                            ins_.then_inc(s_taken.sem, 1)
                        dve.wait_ge(s_taken.sem, i * (U * NCH) + s_taken.at((u + 1) * NCH))
                        dve.tensor_reduce(nmx[:, u % 2, :], mx[:, u % 2, :], AX.X, ALU.max, negate=True
                                          ).then_inc(max_ready.sem, 1)

                    def batch_out(j):
                        dve.wait_ge(exp_done.sem, i * U + exp_done.at((j + 1) * TPB))
                        dve.reciprocal(rinv[:, j * TPB:(j + 1) * TPB], sums[:, j * TPB:(j + 1) * TPB]
                                       ).then_inc(r_ready.sem, 1)
                        dve.wait_ge(r_ready.sem, i * 2 + (j + 1))
                        dve.wait_ge(av_done.sem, i * U + av_done.at((j + 1) * TPB))
                        if j == 0:
                            dve.wait_ge(x_step.sem, i * 3 + x_step.at(0))
                        a4 = att[j * S:(j + 1) * S, :].rearrange("p (t h f) -> p t h f", h=2, f=HD)
                        for h in range(2):
                            o3 = k.ps[h * S:(h + 1) * S, O_BANK + j, 0:TPB * PAIR_F].rearrange(
                                "p (t f) -> p t f", f=PAIR_F)[:, :, h * HD:(h + 1) * HD]
                            r3 = rinv[h * S:(h + 1) * S, j * TPB:(j + 1) * TPB].unsqueeze(2).broadcast_to((S, TPB, HD))
                            ins_ = dve.tensor_tensor(a4[:, :, h, :], o3, r3, ALU.mult)
                            if h == 0:
                                ins_.then_inc(x_step.sem, 1)
                            else:
                                ins_.then_inc(o_drained.sem, 1)

                    if first:
                        maxima(0)
                        return
                    for u in range(U):
                        j, t = u // TPB, u % TPB
                        if u == TPB - 2:
                            queries(i, 1)
                        if u == U - 2 and more:
                            queries(i + 1, 0)
                        if u + 1 < U or more:
                            maxima(u + 1)
                        if not heads16:
                            dve.wait_ge(exp_done.sem, i * U + exp_done.at(u + 1))
                            dve.wait_ge(o_drained.sem, i * U + o_drained.at(u - 1))
                            dve.reciprocal(rinv[:, u:u + 1], sums[:, u:u + 1]).then_inc(r_ready.sem, 1)
                        take_transposes(dve, i, u, t_dve, (1, 3), dve.tensor_copy)
                        if heads16 and u > 0 and t == 0:
                            batch_out(u // TPB - 1)
                    if heads16:
                        batch_out(1)
                    if heads16:
                        dve.wait_ge(x_step.sem, i * 3 + x_step.at(2))
                        dve.wait_ge(o_drained.sem, i * 2 + o_drained.at(2))
                        xt = k.x[:, i, :]
                        dve.tensor_tensor(xt, xt, att[:], ALU.add).then_inc(x_step.sem, 1)

                queries(0, 0)
                keys.first(dve)
                body(0, True, first=True)
                with dve.Fori(0, B // 2 - 1) as i:
                    body(i, True)
                body(B // 2 - 1, False)


def silu_cross_attention(nc, k, name, ins, attT):
    with ExitStack() as ctx:
        def sb(n, shape, dt=F32):
            return ctx.enter_context(nc.sbuf_tensor(f"{name}_{n}", shape, dt))

        def signal(n, credit=0):
            return Signal(nc, ctx, f"{name}_{n}", credit)

        U = 2 * KT
        rows_sb = sb("rows", [P, 2, KT, D])
        stage, q_raw = sb("stage", [P, 2, M]), sb("q_raw", [P, H16, S])
        q_sb, q_hi = sb("q", [P, 2, H16, S]), sb("q_hi", [P, 2, H16, S])
        w_sb = sb("w", [P, 2, H16 * S])
        own = sb("own", [P, DC, H16 // DC, S])
        loaded = [signal(f"loaded{j}") for j in range(2)]
        keys = SplitKeys(k, ctx, signal, name, ins, [stage[:, x, :] for x in range(2)])
        q_ready = signal("q_ready", 1)
        q_step = signal("q_step")
        s_filled = signal("s_filled")
        s_taken = signal("s_taken", 2)
        av_done = signal("av_done", U)
        o_taken = signal("o_taken", 2)
        own_done = signal("own_done", 1)
        give_credits(nc, [keys.ready, q_ready, s_taken, av_done, o_taken, own_done])
        O_BANK = 4

        with nc.Block() as block:

            @block.sync
            def _(sp):
                with sp.Fori(0, B // 2) as i:
                    for j in range(2):
                        b = i * 2 + j
                        keys.load(sp, i, j)
                        sp.wait_ge(av_done.sem, i * U + av_done.at((j + 1) * KT - U))
                        sp.dma_start(rows_sb[:, j, 0:KFULL, :],
                                     ins["ctx"][b, 0:KFULL * P, :].rearrange("(t p) d -> p t d", p=P)
                                     ).then_inc(loaded[j].sem, 16)
                        sp.dma_start(rows_sb[0:KREST, j, KFULL, :], ins["ctx"][b, KFULL * P:M, :]
                                     ).then_inc(loaded[j].sem, 16)

            @block.gpsimd
            def _(pool):
                def body(i, j, split):
                    if split:
                        pool.wait_ge(av_done.sem, i * U + av_done.at((j + 1) * KT - U))
                        keys.split(pool, i, j)

                keys.others(pool, body)

            @block.tensor
            def _(pe):
                def body(i, more, first=False):
                    def scores(u):
                        j, t = u // KT, u % KT
                        own = j % 2
                        rows = key_rows(t)
                        if t == 0:
                            keys.wait_ready(pe, i, j)
                            pe.wait_ge(q_ready.sem, i * 2 + q_ready.at(j + 1))
                        pe.wait_ge(s_taken.sem, i * U + s_taken.at(u - 1))
                        for g in range(DC):
                            heads = slice(g * 8, (g + 1) * 8)
                            last = matmul_split(pe, k.ps[0:rows, 2 * (u % 2) + g, :],
                                                keys.columns(own, g, t * P, rows),
                                                (q_hi[:, own, heads, :], q_sb[:, own, heads, :]), True, True)
                        last.then_inc(s_filled.sem, 1)

                    def values(u):
                        j, t = u // KT, u % KT
                        rows = key_rows(t)
                        pe.wait_ge(s_taken.sem, i * U + s_taken.at(u + 1))
                        if t == 0:
                            pe.wait_ge(loaded[j].sem, i * 32 + 32)
                        if t == 0:
                            pe.wait_ge(o_taken.sem, i * 2 + o_taken.at(j - 1))
                        for g in range(DC):
                            last = pe.matmul(k.ps[:, O_BANK + 2 * j + g, :], rows_sb[0:rows, j, t, g * P:(g + 1) * P],
                                             w_sb[0:rows, u % 2, g * BANK:(g + 1) * BANK],
                                             start=(t == 0), stop=(t == KT - 1))
                        last.then_inc(av_done.sem, 1)

                    if first:
                        scores(0)
                        return
                    for u in range(U):
                        if u + 1 < U or more:
                            scores(u + 1)
                        values(u)

                body(0, True, first=True)
                with pe.Fori(0, B // 2 - 1) as i:
                    body(i, True)
                body(B // 2 - 1, False)

            @block.scalar
            def _(act):
                with act.Fori(0, B // 2) as i:
                    for u in range(U):
                        rows = key_rows(u % KT)
                        act.wait_ge(s_filled.sem, i * U + (u + 1))
                        act.wait_ge(av_done.sem, i * U + av_done.at(u - 1))
                        act.activation(w_sb[0:rows, u % 2, :],
                                       k.ps[0:rows, 2 * (u % 2):2 * (u % 2) + 2, :].rearrange("p a b -> p (a b)"),
                                       ACT.Silu).then_inc(s_taken.sem, 1)

            @block.vector
            def _(dve):
                def queries(i, j):
                    dve.wait_ge(av_done.sem, i * U + av_done.at((j + 1) * KT - U))
                    dve.wait_ge(q_ready.sem, i * 2 + q_ready.at(j))
                    block_queries(dve, k, q_raw, k.xnT, i * P + j * S, 1.0).then_inc(q_step.sem, 1)
                    dve.wait_ge(q_step.sem, i * 4 + (2 * j + 1))
                    keep_high(dve, q_hi[:, j, :, :], q_raw[:]).then_inc(q_step.sem, 1)
                    dve.wait_ge(q_step.sem, i * 4 + (2 * j + 2))
                    keep_low(dve, q_sb[:, j, :, :], q_raw[:], q_hi[:, j, :, :]).then_inc(q_ready.sem, 1)

                def batch_out(i, j):
                    dve.wait_ge(av_done.sem, i * U + av_done.at((j + 1) * KT))
                    take_own_blocks(dve, k, k.ps[:, O_BANK + 2 * j:O_BANK + 2 * j + 2, :], own, o_taken,
                                    own_done, i * 2 + j, attT[:, :, bass.ds(i * P + j * S, S)])

                def body(i, more):
                    queries(i, 1)
                    batch_out(i, 0)
                    if more:
                        queries(i + 1, 0)
                    batch_out(i, 1)

                queries(0, 0)
                keys.first(dve)
                with dve.Fori(0, B // 2 - 1) as i:
                    body(i, True)
                body(B // 2 - 1, False)


def block_queries(dve, k, out, xT, at, scale):
    for g in range(DC):
        last = dve.scalar_tensor_tensor(out[:, g * 8:(g + 1) * 8, :],
                                        xT[:, g:g + 1, bass.ds(at, S)].broadcast_to((P, 8, S)), scale,
                                        k.blocks8[:].unsqueeze(2).broadcast_to((P, 8, S)), ALU.mult, ALU.mult)
    return last


def take_own_blocks(dve, k, products, own, taken, done, nth, out):
    dve.wait_ge(done.sem, nth * 1 + done.at(0))
    for g in range(DC):
        ins_ = dve.tensor_tensor(own[:, g, :, :], products[:, g, :].rearrange("p (h q) -> p h q", q=S),
                                 k.blocks8[:].unsqueeze(2).broadcast_to((P, H16 // DC, S)), ALU.mult)
    ins_.then_inc(taken.sem, 1)
    dve.wait_ge(taken.sem, nth + taken.at(1))
    dve.tensor_reduce(out, own[:].rearrange("p g h q -> p g q h"), AX.X, ALU.add).then_inc(done.sem, 1)


def relu_cross_attention(nc, k, name, ins, wk_sb, wv_sb, qT, maskT, loaded_weights):
    with ExitStack() as ctx:
        def sb(n, shape, dt=F32):
            return ctx.enter_context(nc.sbuf_tensor(f"{name}_{n}", shape, dt))

        def signal(n, credit=0):
            return Signal(nc, ctx, f"{name}_{n}", credit)

        kT = sb("kT", [P, DC, M])
        v = sb("v", [P, KT, D])
        q_sb = sb("q", [P, 2, DC, S])
        lg = sb("lg", [P, KT, S])
        att = sb("att", [P, D])
        bk = k.col("L2x_bk")
        stage = sb("stage", [P, 2, M])
        keys = SplitKeys(k, ctx, signal, name, ins, [stage[:, x, :] for x in range(2)])
        weights_hi = [sb("wk_hi", [P, DC, D]), sb("wv_hi", [P, DC, D])]
        weights_lo = [sb("wk_lo", [P, DC, D]), sb("wv_lo", [P, DC, D])]
        w_step, w_split = signal("w_step"), signal("w_split")
        q_ready = signal("q_ready", 2)
        p_filled = signal("p_filled")
        p_taken = signal("p_taken", 8)
        l_filled = signal("l_filled", 1)
        l_relu = signal("l_relu", 2)
        l_ready = signal("l_ready", 2)
        av_done = signal("av_done", 2)
        att_done = signal("att_done", 2)
        x_done = signal("x_done", 1)
        give_credits(nc, [keys.ready, q_ready, p_taken, l_filled, l_relu, l_ready, av_done, att_done, x_done])
        kjobs = [(m, c) for m in range(DC) for c in range(NCH)]
        vjobs = [list(range(t, min(t + 2, KT))) for t in range(0, KT, 2)]
        NJ = len(kjobs) + len(vjobs)
        PB = 4

        with nc.Block() as block:

            @block.sync
            def _(sp):
                with sp.Fori(0, B // 2) as i:
                    for j in range(2):
                        keys.load(sp, i, j)

            @block.gpsimd
            def _(pool):
                def body(i, j, split):
                    pool.wait_ge(av_done.sem, i * 2 + av_done.at(j - 1))
                    pool.sem_inc(k.tick, 1)
                    if split:
                        keys.split(pool, i, j)
                    pool.tensor_copy(q_sb[:, j, :, :], qT[:, :, bass.ds(i * P + j * S, S)]
                                     ).then_inc(q_ready.sem, 1)

                keys.others(pool, body)

            @block.tensor
            def _(pe):
                pe.wait_ge(w_split.sem, 2)
                with pe.Fori(0, B // 2) as i:
                    for j in range(2):
                        keys.wait_ready(pe, i, j)

                        def project(ns):
                            for n in ns:
                                pe.wait_ge(p_taken.sem, i * (2 * NJ) + p_taken.at(max(j * NJ + n - PB + 1, 0)))
                                bank = k.ps[:, (j * NJ + n) % PB, :]
                                if n < len(kjobs):
                                    m, c = kjobs[n]
                                    at, w = CHUNKS[c]
                                    for f in range(DC):
                                        out = slice(m * P, (m + 1) * P)
                                        last = matmul_split(pe, bank[:, 0:w + w % 2],
                                                            (weights_hi[0][:, f, out], weights_lo[0][:, f, out]),
                                                            keys.columns(j, f, at, w + w % 2), f == 0, f == DC - 1)
                                else:
                                    for s, t in enumerate(vjobs[n - len(kjobs)]):
                                        rows = key_rows(t)
                                        for f in range(DC):
                                            matmul_split(pe, bank[0:rows, s * D:(s + 1) * D],
                                                         keys.columns(j, f, t * P, rows),
                                                         (weights_hi[1][:, f, :], weights_lo[1][:, f, :]), f == 0, False)
                                        last = pe.matmul(bank[0:rows, s * D:(s + 1) * D], k.ones3[:, 0:rows],
                                                         k.row("L2x_bv"), start=False, stop=True)
                                last.then_inc(p_filled.sem, 1)

                        def scores(ts):
                            if ts[0] == 0:
                                pe.wait_ge(q_ready.sem, i * 2 + q_ready.at(j + 1))
                                pe.wait_ge(p_taken.sem, i * (2 * NJ) + p_taken.at(j * NJ + len(kjobs)))
                                pe.wait_ge(l_relu.sem, i * 4 + l_relu.at(j * 2))
                            for t in ts:
                                rows = key_rows(t)
                                for f in range(DC):
                                    last = pe.matmul(k.ps[0:rows, 4 + t // 8, (t % 8) * S:(t % 8 + 1) * S],
                                                     kT[:, f, t * P:t * P + rows], q_sb[:, j, f, :],
                                                     start=(f == 0), stop=(f == DC - 1))
                            last.then_inc(l_filled.sem, 1)

                        NK = len(kjobs)
                        project(range(0, NK + 2))
                        scores(range(0, 8))
                        project(range(NK + 2, NK + 4))
                        scores(range(8, KT))
                        project(range(NK + 4, NJ))
                        for t in range(KT):
                            rows = key_rows(t)
                            if t == 0:
                                pe.wait_ge(l_ready.sem, i * 6 + l_ready.at(j * 3 + 1))
                                pe.wait_ge(att_done.sem, i * 2 + att_done.at(j - 1))
                            if t == 8:
                                pe.wait_ge(l_ready.sem, i * 6 + l_ready.at(j * 3 + 3))
                            if t % 2 == 0:
                                pe.wait_ge(p_taken.sem, i * (2 * NJ) + p_taken.at(j * NJ + NK + t // 2 + 1))
                            last = pe.matmul(k.ps[0:S, 6 + j, 0:D], lg[0:rows, t, :], v[0:rows, t, :],
                                             start=(t == 0), stop=(t == KT - 1))
                        last.then_inc(av_done.sem, 1)

            @block.scalar
            def _(act):
                with act.Fori(0, B // 2) as i:
                    for j in range(2):
                        act.wait_ge(l_filled.sem, i * 4 + l_filled.at(2 * j))
                        for n in range(NJ):
                            if n == len(kjobs):
                                act.wait_ge(av_done.sem, i * 2 + av_done.at(j))
                            act.wait_ge(p_filled.sem, i * (2 * NJ) + (j * NJ + n + 1))
                            bank = k.ps[:, (j * NJ + n) % PB, :]
                            if n < len(kjobs):
                                m, c = kjobs[n]
                                at, w = CHUNKS[c]
                                ins_ = act.activation(kT[:, m, at:at + w], bank[:, 0:w], ACT.Relu, bias=bk[:, m:m + 1])
                            else:
                                ts = vjobs[n - len(kjobs)]
                                rows = key_rows(ts[-1])
                                ins_ = act.activation(v[0:rows, ts[0]:ts[-1] + 1, :],
                                                      bank[0:rows, 0:len(ts) * D].rearrange("p (t d) -> p t d", d=D),
                                                      ACT.Relu)
                            ins_.then_inc(p_taken.sem, 1)

            @block.vector
            def _(dve):
                dve.wait_ge(*loaded_weights)
                for n, x in enumerate((wk_sb, wv_sb)):
                    keep_high(dve, weights_hi[n][:], x[:]).then_inc(w_step.sem, 1)
                    dve.wait_ge(w_step.sem, n + 1)
                    keep_low(dve, weights_lo[n][:], x[:], weights_hi[n][:]).then_inc(w_split.sem, 1)

                keys.first(dve)
                with dve.Fori(0, B // 2) as i:
                    for j in range(2):
                        dve.wait_ge(av_done.sem, i * 2 + av_done.at(j))
                        spans = [(P, 0, 8), (P, 8, KFULL), (KREST, KFULL, KT)]
                        for n, (rows, t0, t1) in enumerate(spans):
                            dve.wait_ge(l_filled.sem, i * 4 + l_filled.at(2 * j + min(n, 1) + 1))
                            src = k.ps[0:rows, 4 + t0 // 8, (t0 % 8) * S:(t0 % 8 + t1 - t0) * S].rearrange(
                                "p (t q) -> p t q", q=S)
                            ins_ = dve.tensor_scalar(lg[0:rows, t0:t1, :], src, 0.0, D ** -0.5, ALU.max, ALU.mult)
                            if n != 1:
                                ins_.then_inc(l_relu.sem, 1)
                        dve.wait_ge(l_relu.sem, i * 4 + l_relu.at(2 * j + 2))
                        for rows, t0, t1 in spans:
                            dve.tensor_tensor(lg[0:rows, t0:t1, :], lg[0:rows, t0:t1, :], maskT[0:rows, t0:t1, :],
                                              ALU.add).then_inc(l_ready.sem, 1)
                        dve.wait_ge(av_done.sem, i * 2 + av_done.at(j + 1))
                        if j == 0:
                            dve.wait_ge(x_done.sem, i + x_done.at(0))
                        dve.tensor_scalar(att[j * S:(j + 1) * S, :], k.ps[0:S, 6 + j, 0:D], 0.0, None, ALU.max
                                          ).then_inc(att_done.sem, 1)
                    dve.wait_ge(att_done.sem, i * 2 + att_done.at(2))
                    xt = k.x[:, i, :]
                    dve.tensor_tensor(xt, xt, att[:], ALU.add).then_inc(x_done.sem, 1)


def self_attention(nc, k, name, qT, kT, v_all, out, softmax, eps=0.0):
    with ExitStack() as ctx:
        def sb(n, shape, dt=F32):
            return ctx.enter_context(nc.sbuf_tensor(f"{name}_{n}", shape, dt))

        def signal(n, credit=0):
            return Signal(nc, ctx, f"{name}_{n}", credit)

        NB = 4
        VW = PAIR_F + 1
        kb = sb("kb", [P, NB, DC, S])
        vb = sb("vb", [S, NB, PAIRS, VW])
        qb = sb("qb", [P, 2, H16, S])
        wT = sb("wT", [S, 2, PAIRS * P])
        rinv = sb("rinv", [P, PAIRS, 1])
        kv_ready = signal("kv_ready")
        q_ready = signal("q_ready")
        s_filled = signal("s_filled", 2)
        wT_ready = signal("wT_ready", 2)
        av_done = signal("av_done", NB)
        out_done = signal("out_done", 2)
        step = signal("step")
        credited = [s_filled, wT_ready, av_done, out_done]
        if softmax:
            w = sb("w", [P, 2, PAIRS, S])
            mxs = sb("mxs", [P, 2, PAIRS])
            s_taken = signal("s_taken", 2)
            shifted = signal("shifted")
            exp_done = signal("exp_done")
            t_filled = signal("t_filled", 2)
            credited += [s_taken, t_filled]
        give_credits(nc, credited)
        T_BANK, O_BANK = 4, 6
        with nc.Block() as block:

            @block.gpsimd
            def _(pool):
                with pool.Fori(0, B // NB) as i:
                    for b in range(NB):
                        pool.wait_ge(av_done.sem, i * NB + av_done.at(b + 1 - NB))
                        pool.tensor_copy(kb[:, b, :, :], kT[:, :, bass.ds(i * (NB * S) + b * S, S)]
                                         ).then_inc(kv_ready.sem, 1)
                        pool.tensor_copy(vb[:, b, :, :], v_all[:, i * NB + b, :, :]).then_inc(kv_ready.sem, 1)

            @block.tensor
            def _(pe):
                with pe.Fori(0, B // NB) as i:
                    def scores(b):
                        pe.wait_ge(kv_ready.sem, i * (2 * NB) + (2 * b + 2))
                        pe.wait_ge(q_ready.sem, i * NB + (b + 1))
                        free = s_taken if softmax else wT_ready
                        pe.wait_ge(free.sem, i * NB + free.at(b - 1))
                        pe.sem_inc(k.tick, 1)
                        if softmax:
                            for pair in range(PAIRS):
                                last = pe.matmul(k.ps[:, b % 2, pair * S:(pair + 1) * S],
                                                 qb[:, b % 2, 2 * pair:2 * pair + 2, :],
                                                 kb[:, b, pair // 4, :], start=True, stop=True)
                        else:
                            for g in range(DC):
                                last = pe.matmul(k.ps[0:S, 2 * (b % 2) + g, :], kb[:, b, g, :],
                                                 qb[:, b % 2, g * 8:(g + 1) * 8, :], start=True, stop=True)
                        last.then_inc(s_filled.sem, 1)

                    def transposes(b):
                        pe.wait_ge(exp_done.sem, i * NB + (b + 1))
                        pe.wait_ge(wT_ready.sem, i * NB + wT_ready.at(b))
                        pe.sem_inc(k.tick, 1)
                        for pair in range(PAIRS):
                            last = pe.transpose(k.ps[0:S, T_BANK + pair // 4, (pair % 4) * P:(pair % 4 + 1) * P],
                                                w[:, b % 2, pair, :], k.ident[:])
                        last.then_inc(t_filled.sem, 1)

                    def values(b):
                        pe.wait_ge(wT_ready.sem, i * NB + wT_ready.at(b + 1))
                        pe.wait_ge(out_done.sem, i * NB + out_done.at(b - 1))
                        for pair in range(PAIRS):
                            last = pe.matmul(k.ps[:, O_BANK + b % 2, pair * VW:(pair + 1) * VW],
                                             wT[:, b % 2, pair * P:(pair + 1) * P], vb[:, b, pair, :],
                                             start=True, stop=True)
                        last.then_inc(av_done.sem, 1)

                    scores(0)
                    for b in range(NB):
                        if b + 1 < NB:
                            scores(b + 1)
                        if softmax:
                            transposes(b)
                            if b > 0:
                                values(b - 1)
                        else:
                            values(b)
                    if softmax:
                        values(NB - 1)

            @block.scalar
            def _(act):
                if softmax:
                    with act.Fori(0, B // NB) as i:
                        def exps(b):
                            act.wait_ge(shifted.sem, i * NB + (b + 1))
                            act.activation(w[:, b % 2, :, :], w[:, b % 2, :, :], ACT.Exp).then_inc(exp_done.sem, 1)

                        exps(0)
                        for b in range(NB):
                            if b + 1 < NB:
                                exps(b + 1)
                            act.wait_ge(t_filled.sem, i * NB + t_filled.at(b + 1))
                            act.wait_ge(av_done.sem, i * NB + av_done.at(b - 1))
                            act.activation(wT[:, b % 2, :], k.ps[0:S, T_BANK:T_BANK + 2, :].rearrange(
                                "p a b -> p (a b)"), ACT.Copy).then_inc(wT_ready.sem, 1)

            @block.vector
            def _(dve):
                with dve.Fori(0, B // NB) as i:
                    per_body = NB * 3
                    count = [0]

                    def link(ins_):
                        count[0] += 1
                        ins_.then_inc(step.sem, 1)
                        dve.wait_ge(step.sem, i * per_body + count[0])

                    def queries(b):
                        dve.wait_ge(s_filled.sem, i * NB + s_filled.at(b - 1))
                        block_queries(dve, k, qb[:, b % 2, :, :], qT, i * (NB * S) + b * S,
                                      HD ** -0.5 if softmax else 1.0).then_inc(q_ready.sem, 1)

                    def weights(b):
                        dve.wait_ge(s_filled.sem, i * NB + s_filled.at(b + 1))
                        if softmax:
                            dve.wait_ge(t_filled.sem, i * NB + t_filled.at(b - 1))
                            ins_ = dve.tensor_tensor(
                                w[:, b % 2, :, :], k.ps[:, b % 2, :].rearrange("p (a s) -> p a s", s=S),
                                k.causal_rows[:].unsqueeze(1).broadcast_to((P, PAIRS, S)), ALU.add)
                            ins_.then_inc(s_taken.sem, 1)
                            dve.wait_ge(s_taken.sem, i * NB + s_taken.at(b + 1))
                            link(dve.tensor_reduce(mxs[:, b % 2, :], w[:, b % 2, :, :], AX.X, ALU.max))
                            dve.tensor_tensor(w[:, b % 2, :, :], w[:, b % 2, :, :], mxs[:, b % 2, :].unsqueeze(
                                2).broadcast_to((P, PAIRS, S)), ALU.subtract).then_inc(shifted.sem, 1)
                        else:
                            dve.wait_ge(av_done.sem, i * NB + av_done.at(b - 1))
                            dve.tensor_tensor(
                                wT[:, b % 2, :].rearrange("p (h q) -> p h q", q=S),
                                k.ps[0:S, 2 * (b % 2):2 * (b % 2) + 2, :].rearrange("p g (h q) -> p (g h) q", q=S),
                                k.causal_keys[0:S, :].unsqueeze(1).broadcast_to((S, H16, S)),
                                ALU.mult).then_inc(wT_ready.sem, 1)

                    def divided(b):
                        dve.wait_ge(av_done.sem, i * NB + av_done.at(b + 1))
                        got = k.ps[:, O_BANK + b % 2, 0:PAIRS * VW].rearrange("p (a f) -> p a f", f=VW)
                        total = got[:, :, PAIR_F:VW]
                        if not softmax:
                            link(dve.tensor_scalar(rinv[:], total, eps, None, ALU.add))
                            total = rinv[:]
                        link(dve.reciprocal(rinv[:], total))
                        for h in range(2):
                            rows, place = slice(h * S, (h + 1) * S), slice(b % 2 * S, (b % 2 + 1) * S)
                            ins_ = dve.tensor_tensor(
                                out[place, i * (NB // 2) + b // 2, :].rearrange(
                                    "p (a h f) -> p a h f", h=2, f=HD)[:, :, h, :],
                                got[rows, :, h * HD:(h + 1) * HD], rinv[rows, :, :].broadcast_to((S, PAIRS, HD)),
                                ALU.mult)
                            if h == 0:
                                link(ins_)
                        ins_.then_inc(out_done.sem, 1)
                        dve.wait_ge(out_done.sem, i * NB + out_done.at(b + 1))

                    queries(0)
                    queries(1)
                    for b in range(NB):
                        weights(b)
                        if b + 2 < NB:
                            queries(b + 2)
                        if b > 1:
                            divided(b - 2)
                    divided(NB - 2)
                    divided(NB - 1)
                    assert count[0] == per_body


def expert_tiles(choices):
    return (TOK * choices + E8 * (P - 1)) // P


def place_tokens(nc, k, st, hot, choices, kept=None):
    W = choices * E8
    tiles = expert_tiles(choices)
    count = st.sb("count", [P, NT + 1, W])
    row, row_u = st.sb("row", [P, NT, choices]), st.sb("row_u", [P, NT, choices], U32)
    total, used = st.sb("total", [P, E8]), st.sb("used", [P, E8])
    pairwise, before = st.sb("pairwise", [P, E8, E8]), st.sb("before", [P, E8])
    shift = st.sb("shift", [P, W])
    past, owner = st.sb("past", [P, tiles, E8]), st.sb("owner", [P, tiles])
    owner_u = st.sb("owner_u", [P, tiles], U32)
    earlier = st.sb("earlier", [P, NT, W])
    matmul_pass(nc, k, [
        Job([(lambda bank: bank[:, 0:NT * W], [(k.upto[:], hot)])], "dve", lambda e, bank: e.tensor_copy(
            count[:, 0:NT, :].rearrange("p t w -> p (t w)"), bank[:, 0:NT * W])),
        Job([(lambda bank: bank[:, 0:NT * W], [(k.ones64[:], hot)])], "act", lambda e, bank: e.activation(
            earlier[:].rearrange("p t w -> p (t w)"), bank[:, 0:NT * W], ACT.Copy))])

    def over_e(ap, n):
        return ap.unsqueeze(2).broadcast_to((P, n, E8))

    def along(ap, n):
        return ap.unsqueeze(1).broadcast_to((P, n, E8))

    def steps(dve, link):
        for t in range(1, NT):
            link(dve.tensor_tensor(earlier[:, t, :], earlier[:, t, :], earlier[:, t - 1, :], ALU.add))
        link(dve.tensor_tensor(count[:, 1:NT, :], count[:, 1:NT, :], earlier[:, 0:NT - 1, :], ALU.add))
        link(dve.tensor_copy(count[:, NT, :], earlier[:, NT - 1, :]))
        link(dve.tensor_reduce(total[:], count[:, NT, :].rearrange("p (r e) -> p e r", e=E8), AX.X, ALU.add))
        link(dve.tensor_scalar(before[:], k.iota[:, 0:E8], float(P), None, ALU.mult))
        link(dve.tensor_tensor(pairwise[:], over_e(total[:], E8), along(before[:], E8), ALU.is_gt))
        link(dve.tensor_reduce(used[:], pairwise[:], AX.X, ALU.add))
        link(dve.tensor_tensor(pairwise[:], over_e(k.iota[:, 0:E8], E8), along(k.iota[:, 0:E8], E8), ALU.is_gt))
        link(dve.tensor_tensor(pairwise[:], pairwise[:], along(used[:], E8), ALU.mult))
        link(dve.tensor_reduce(before[:], pairwise[:], AX.X, ALU.add))
        link(dve.tensor_tensor(used[:], used[:], before[:], ALU.add))
        link(dve.tensor_tensor(past[:], along(used[:], tiles), over_e(k.iota[:, 0:tiles], tiles), ALU.is_le))
        link(dve.tensor_reduce(owner[:], past[:], AX.X, ALU.add))
        link(dve.tensor_scalar(owner[:], owner[:], float(E8 - 1), None, ALU.min))
        link(dve.tensor_copy(owner_u[:], owner[:]))
        for r in range(choices):
            link(dve.tensor_scalar(shift[:, r * E8:(r + 1) * E8], before[:], float(P), -1.0, ALU.mult, ALU.add))
        if choices > 1:
            link(dve.tensor_tensor(shift[:, E8:W], shift[:, E8:W], count[:, NT, 0:E8], ALU.add))
        if kept is not None:
            within = st.sb("within", [P, NT, W])
            link(dve.tensor_scalar(within[:], count[:, 0:NT, :], float(CAPACITY), None, ALU.is_le))
            link(dve.tensor_tensor(within[:], within[:], hot, ALU.mult))
            link(dve.tensor_reduce(kept, within[:].rearrange("p t (r e) -> p t r e", e=E8), AX.X, ALU.add))
        link(dve.tensor_tensor(count[:, 0:NT, :], count[:, 0:NT, :],
                               shift[:].unsqueeze(1).broadcast_to((P, NT, W)), ALU.add))
        link(dve.tensor_tensor(count[:, 0:NT, :], count[:, 0:NT, :], hot, ALU.mult))
        link(dve.tensor_reduce(row[:], count[:, 0:NT, :].rearrange("p t (r e) -> p t r e", e=E8), AX.X, ALU.add))
        link(dve.tensor_copy(row_u[:], row[:]))

    vector_block(nc, k, steps)
    return row_u, owner_u


def experts(nc, k, name, w_in, w_gate, w_out, hidden, rows, owner, gates, choices, b_in=None, b_out=None):
    gated = w_gate is not None
    MT = (hidden + P - 1) // P
    HW = [min(P, hidden - m * P) for m in range(MT)]
    full_w2 = hidden % P == 0
    tiles = expert_tiles(choices)
    whole = hidden // P
    sorted_out = nc.dram_tensor(f"{name}_sorted_out", (tiles * P, D), F32).ap()

    with ExitStack() as ctx:
        def sb(n, shape, dt=F32):
            return ctx.enter_context(nc.sbuf_tensor(f"{name}_{n}", shape, dt))

        def signal(n, credit=0):
            return Signal(nc, ctx, f"{name}_{n}", credit)

        w1 = sb("w1", [P, 2, DC, hidden])
        wg = sb("wg", [P, 2, DC, hidden]) if gated else None
        w2 = sb("w2", [P, 2, MT, D])
        b1 = sb("b1", [P, 2, MT]) if b_in is not None else None
        b2 = sb("b2", [1, 2, D]) if b_out is not None else None
        tokens = sb("tokens", [P, 2, D])
        tokT = sb("tokT", [P, 2, DC, P])
        sig = sb("sig", [P, 2, P]) if gated else None
        hid = sb("hid", [P, 2, MT, P])
        y = sb("y", [P, 2, D])
        in_loads, out_loads = 1 + gated + (b_in is not None), 1 + (not full_w2) + (b_out is not None)
        RING = 2 if gated else 4

        tok_loaded = [signal(f"tok_loaded{j}") for j in range(2)]
        in_loaded = [signal(f"in_loaded{j}") for j in range(2)]
        out_loaded = [signal(f"out_loaded{j}") for j in range(2)]
        t_filled = signal("t_filled", 1)
        t_taken = signal("t_taken")
        h_filled = signal("h_filled")
        sig_done = signal("sig_done") if gated else None
        h_taken = signal("h_taken", 2 * MT)
        o_filled = signal("o_filled", 2)
        o_taken = signal("o_taken", 2)
        y_stored = signal("y_stored")
        y_free = signal("y_free", 2)
        scattered = signal("scattered")
        give_credits(nc, [t_filled, h_taken, o_filled, o_taken, y_free])

        def over_tiles(engine, body):
            with engine.Fori(0, tiles // 2) as i:
                for j in range(2):
                    body(i, j)
            if tiles % 2:
                body(tiles // 2, 0)

        with nc.Block() as block:

            @block.sync
            def _(sp):
                def body(i, j):
                    n = i * 2 + j
                    e = nc.values_load(owner[0:1, bass.ds(n, 1)], [mybir.EngineType.SP], min_val=0, max_val=E8 - 1,
                                       skip_runtime_bounds_check_because="place_tokens clamps it to 0..7")
                    sp.wait_ge(h_taken.sem, i * (2 * MT) + h_taken.at((j - 1) * MT))
                    sp.sem_inc(k.tick, 1)
                    done = in_loaded[j].sem
                    sp.dma_start(w1[:, j, :, :], w_in[e].rearrange("(c p) n -> p c n", p=P)).then_inc(done, 16)
                    if gated:
                        sp.dma_start(wg[:, j, :, :], w_gate[e].rearrange("(c p) n -> p c n", p=P)).then_inc(done, 16)
                    if b_in is not None:
                        sp.dma_start(b1[:, j, :], b_in[e]).then_inc(done, 16)
                    sp.wait_ge(scattered.sem, 16 * NT * choices)
                    sp.dma_start(tokens[:, j, :], k.sorted_in[bass.ds(n * P, P), :]
                                 ).then_inc(tok_loaded[j].sem, 16)
                    sp.wait_ge(o_filled.sem, i * 2 + o_filled.at(j - 1))
                    sp.sem_inc(k.tick, 1)
                    done = out_loaded[j].sem
                    if b_out is not None:
                        sp.dma_start(b2[:, j, :], b_out[e]).then_inc(done, 16)
                    sp.dma_start(w2[:, j, 0:whole, :],
                                 w_out[e][0:whole * P, :].rearrange("(c p) n -> p c n", p=P)).then_inc(done, 16)
                    if not full_w2:
                        sp.dma_start(w2[0:HW[-1], j, whole, :], w_out[e][whole * P:hidden, :]).then_inc(done, 16)

                over_tiles(sp, body)

            @block.tensor
            def _(pe):
                def transposes(i, j):
                    pe.wait_ge(tok_loaded[j].sem, i * 16 + 16)
                    pe.sem_inc(k.tick, 1)
                    for c in range(DC):
                        last = pe.transpose(k.ps[:, 4 + j, c * P:(c + 1) * P], tokens[:, j, c * P:(c + 1) * P],
                                            k.ident[:])
                    last.then_inc(t_filled.sem, 1)

                def body(i, j, more=True):
                    pe.wait_ge(t_taken.sem, i * 2 + (j + 1))
                    pe.wait_ge(in_loaded[j].sem, i * (16 * in_loads) + 16 * in_loads)
                    for m in range(MT):
                        job = j * MT + m
                        pe.wait_ge(h_taken.sem, i * (2 * MT) + h_taken.at(job - RING + 1))
                        for x, w in enumerate((w1, wg) if gated else (w1,)):
                            bank = (2 * (job % 2) + x) if gated else job % 4
                            for c in range(DC):
                                last = pe.matmul(k.ps[0:HW[m], bank, 0:P], w[:, j, c, m * P:m * P + HW[m]],
                                                 tokT[:, j, c, :], start=(c == 0), stop=(c == DC - 1))
                        last.then_inc(h_filled.sem, 1)
                    if more:
                        transposes(i + (j == 1), 1 - j)
                    pe.wait_ge(out_loaded[j].sem, i * (16 * out_loads) + 16 * out_loads)
                    pe.wait_ge(o_taken.sem, i * 2 + o_taken.at(j - 1))
                    for m in range(MT):
                        pe.wait_ge(h_taken.sem, i * (2 * MT) + h_taken.at(j * MT + m + 1))
                        last = pe.matmul(k.ps[:, 6 + j, 0:D], hid[0:HW[m], j, m, :], w2[0:HW[m], j, m, :],
                                         start=(m == 0), stop=(m == MT - 1 and b2 is None))
                    if b2 is not None:
                        last = pe.matmul(k.ps[:, 6 + j, 0:D], k.ones_row[0:1, :], b2[0:1, j, :],
                                         start=False, stop=True)
                    last.then_inc(o_filled.sem, 1)

                transposes(0, 0)
                with pe.Fori(0, tiles // 2) as i:
                    for j in range(2):
                        body(i, j)
                body(tiles // 2, 0, False)

            @block.scalar
            def _(act):
                def body(i, j):
                    act.wait_ge(o_filled.sem, i * 2 + o_filled.at(j - 1))
                    act.sem_inc(k.tick, 1)
                    for m in range(MT):
                        job = j * MT + m
                        act.wait_ge(h_filled.sem, i * (2 * MT) + (job + 1))
                        if gated:
                            act.wait_ge(h_taken.sem, i * (2 * MT) + h_taken.at(job - 1))
                            act.activation(sig[0:HW[m], job % 2, :], k.ps[0:HW[m], 2 * (job % 2), 0:P],
                                           ACT.Silu).then_inc(sig_done.sem, 1)
                        else:
                            bias = b1[:, j, m:m + 1] if b1 is not None else 0.0
                            act.activation(hid[:, j, m, :], k.ps[:, job % 4, 0:P], ACT.Gelu, bias=bias
                                           ).then_inc(h_taken.sem, 1)

                over_tiles(act, body)

            @block.vector
            def _(dve):
                def take_transposed(i, j):
                    dve.wait_ge(t_filled.sem, i * 2 + t_filled.at(j + 1))
                    dve.tensor_copy(tokT[:, j, :, :].rearrange("p c n -> p (c n)"), k.ps[:, 4 + j, 0:D]
                                    ).then_inc(t_taken.sem, 1)

                def body(i, j, more=True):
                    if gated:
                        dve.wait_ge(o_filled.sem, i * 2 + o_filled.at(j - 1))
                        dve.sem_inc(k.tick, 1)
                        for m in range(MT):
                            job = j * MT + m
                            dve.wait_ge(sig_done.sem, i * (2 * MT) + (job + 1))
                            dve.tensor_tensor(hid[0:HW[m], j, m, :], sig[0:HW[m], job % 2, :],
                                              k.ps[0:HW[m], 2 * (job % 2) + 1, 0:P], ALU.mult
                                              ).then_inc(h_taken.sem, 1)
                    if more:
                        take_transposed(i + (j == 1), 1 - j)
                    dve.wait_ge(y_free.sem, i * 2 + y_free.at(j - 1))
                    dve.wait_ge(o_filled.sem, i * 2 + o_filled.at(j + 1))
                    dve.tensor_copy(y[:, j, :], k.ps[:, 6 + j, 0:D]).then_inc(o_taken.sem, 1)

                take_transposed(0, 0)
                with dve.Fori(0, tiles // 2) as i:
                    for j in range(2):
                        body(i, j)
                body(tiles // 2, 0, False)

            @block.gpsimd
            def _(pool):
                for t in range(NT):
                    for r in range(choices):
                        pool.indirect_dma_start(k.sorted_in, bass.IndirectOffsetOnAxis(rows[:, t, r:r + 1], 0),
                                                k.xn[:, t, :], None).then_inc(scattered.sem, 16)

                def body(i, j):
                    pool.wait_ge(o_taken.sem, i * 2 + o_taken.at(j + 1))
                    pool.sem_inc(k.tick, 1)
                    pool.dma_start(sorted_out[bass.ds((i * 2 + j) * P, P), :], y[:, j, :]
                                   ).then_inc(y_stored.sem, 16)
                    pool.wait_ge(y_stored.sem, i * 32 + (16 * j + 16))
                    pool.sem_inc(y_free.sem, 1)

                over_tiles(pool, body)

    with ExitStack() as ctx:
        back = ctx.enter_context(nc.sbuf_tensor(f"{name}_back", [P, NT, choices, D], F32))
        fetched = Signal(nc, ctx, f"{name}_fetched")
        with nc.Block() as block:

            @block.gpsimd
            def _(pool):
                for t in range(NT):
                    for r in range(choices):
                        pool.indirect_dma_start(back[:, t, r, :], None, sorted_out,
                                                bass.IndirectOffsetOnAxis(rows[:, t, r:r + 1], 0)
                                                ).then_inc(fetched.sem, 16)

            @block.vector
            def _(dve):
                for r in range(choices):
                    for t in range(NT):
                        dve.wait_ge(fetched.sem, 16 * NT * choices)
                        if r:
                            dve.wait_ge(k.dve_link, k.n_dve_link + t + 1)
                        dve.scalar_tensor_tensor(k.x[:, t, :], back[:, t, r, :], gates[:, t, r:r + 1],
                                                 k.x[:, t, :], ALU.mult, ALU.add).then_inc(k.dve_link, 1)
        k.n_dve_link += NT * choices


def vector_block(nc, k, steps, sync_steps=None):
    with nc.Block() as block:
        if sync_steps:

            @block.sync
            def _(sp):
                sync_steps(sp)

        @block.vector
        def _(dve):
            def link(ins_):
                k.n_dve_link += 1
                ins_.then_inc(k.dve_link, 1)
                dve.wait_ge(k.dve_link, k.n_dve_link)

            steps(dve, link)


def scalar_block(nc, k, steps):
    with nc.Block() as block:

        @block.scalar
        def _(act):
            def link(ins_):
                k.n_act_link += 1
                ins_.then_inc(k.act_link, 1)
                act.wait_ge(k.act_link, k.n_act_link)

            steps(act, link)


def add_bias(col, func):
    return lambda out: lambda e, bank, m, n: e.activation(
        out[0:bank.shape[0], m, n * BANK:(n + 1) * BANK], bank, func, bias=col[0:bank.shape[0], m:m + 1])


def top2_gates(nc, k, st, logits, top, kept=None):
    idx, idxf = st.sb("idx", [P, NT, 8], U32), st.sb("idxf", [P, NT, 8])
    hot = st.sb("hot", [P, NT, 2, E8])
    gap, g2 = st.sb("gap", [P, NT]), st.sb("g2", [P, NT, 2])

    def first(dve, link):
        for t in range(NT):
            link(dve.max(top[:, t, :], logits[:, t, :]))
            link(dve.max_index(idx[:, t, :], top[:, t, :], logits[:, t, :]))
        link(dve.tensor_copy(idxf[:], idx[:]))
        for r in range(2):
            link(dve.tensor_tensor(hot[:, :, r, :], k.iota8[:].unsqueeze(1).broadcast_to((P, NT, E8)),
                                   idxf[:, :, r:r + 1].broadcast_to((P, NT, E8)), ALU.is_equal))
        link(dve.tensor_tensor(gap[:], top[:, :, 1], top[:, :, 0], ALU.subtract))

    vector_block(nc, k, first)
    scalar_block(nc, k, lambda act, link: link(act.activation(g2[:, :, 1], gap[:], ACT.Exp)))
    rows, owner = place_tokens(nc, k, st, hot[:].rearrange("p t r e -> p t (r e)"), 2, kept)

    def second(dve, link):
        link(dve.tensor_scalar(gap[:], g2[:, :, 1], 1.0, None, ALU.add))
        link(dve.reciprocal(g2[:, :, 0], gap[:]))
        link(dve.tensor_tensor(g2[:, :, 1], g2[:, :, 1], g2[:, :, 0], ALU.mult))
        if kept is not None:
            link(dve.tensor_tensor(g2[:], g2[:], kept, ALU.mult))

    vector_block(nc, k, second)
    return rows, owner, g2


def router_logits(nc, k, wgT, logits, loaded):
    groups = [(lambda bank, t=t: bank[:, t * E8:(t + 1) * E8],
               [(k.xnT[:, c, t * P:(t + 1) * P], wgT[:, c, :]) for c in range(DC)]) for t in range(NT)]
    matmul_pass(nc, k, [Job(groups, "dve", lambda e, bank: e.tensor_copy(
        logits[:].rearrange("p t e -> p (t e)"), bank[:, 0:NT * E8]))], [loaded])


def values_job(groups, v_all, pair):
    return Job(groups, "dve", lambda e, bank: e.tensor_copy(
        v_all[:, 2 * pair:2 * pair + 2, :, 0:PAIR_F],
        bank[0:S, :].rearrange("p (b a f) -> p b a f", b=2, f=PAIR_F)))


def conv3(dve, link, out, src, w, bias, batches=B):
    o = out.rearrange("p (b s) -> p b s", s=S)
    x = src.rearrange("p (b s) -> p b s", s=S)
    link(dve.tensor_scalar(o, x, w[:, 1:2], bias, ALU.mult, ALU.add))
    link(dve.scalar_tensor_tensor(o[:, :, 1:S], x[:, :, 0:S - 1], w[:, 0:1], o[:, :, 1:S], ALU.mult, ALU.add))
    link(dve.scalar_tensor_tensor(o[:, :, 0:S - 1], x[:, :, 1:S], w[:, 2:3], o[:, :, 0:S - 1], ALU.mult, ALU.add))


class Stage:
    def __init__(self, nc, name):
        self.nc, self.name, self.ctx = nc, name, ExitStack()

    def __enter__(self):
        self.ctx.__enter__()
        return self

    def __exit__(self, *a):
        return self.ctx.__exit__(*a)

    def sb(self, n, shape, dt=F32):
        return self.ctx.enter_context(self.nc.sbuf_tensor(f"{self.name}_{n}", shape, dt))


def normed(nc, k):
    layer_norm(nc, k, k.x, k.xn, 1e-5, k.xnT)


def stage_L0_cross(nc, k, ins):
    normed(nc, k)
    softmax_cross_attention(nc, k, "L0x", ins, True, k.xnT)


def stage_L0_attn(nc, k, ins):
    normed(nc, k)
    with Stage(nc, "L0a") as st:
        w = {}
        copies = []
        for n, dout in (("wq", 64), ("wkv", 64), ("wqr", 128), ("wqr_sw", 128), ("wkr", 128), ("wkr_sw", 128),
                        ("wo", 256)):
            w[n] = st.sb(n, [P, DC, dout])
            copies.append((w[n][:], wk(ins["L0_" + n])))
        for n, dout in (("wqc", 128), ("wkc", 128), ("wv", 256)):
            w[n] = st.sb(n, [64, 1, dout])
            copies.append((w[n][:, 0, :], ins["L0_" + n]))
        loaded = load_block(nc, k, copies)
        cT = {n: st.sb("c" + n, [64, 1, TOK]) for n in ("q", "kv")}
        rot = {n: st.sb("rot" + n, [P, 2, TOK]) for n in "qk"}
        heads = {n: st.sb("heads" + n, [P, DC, TOK]) for n in "qk"}
        v_all = st.sb("v", [S, B, PAIRS, PAIR_F + 1])
        att, attT = st.sb("att", [P, NT, D]), st.sb("attT", [P, DC, TOK])
        jobs = []
        for n, bias in (("q", "L0_bq"), ("kv", "L0_bkv")):
            jobs += linear_jobs(w["w" + n], k.xnT, DC, 64, add_bias(k.col(bias), ACT.Gelu)(cT[n]))
        for n in "qk":
            for x, (suffix, table) in enumerate((("", k.rope_cos), ("_sw", k.rope_sin))):
                def drain(e, bank, m, n_, n=n, x=x, suffix=suffix, table=table):
                    return e.scalar_tensor_tensor(
                        rot[n][:, x, n_ * BANK:(n_ + 1) * BANK].rearrange("p (b s) -> p b s", s=S),
                        bank.rearrange("p (b s) -> p b s", s=S), k.col(f"L0_b{n}r{suffix}"),
                        table[:].unsqueeze(1).broadcast_to((P, BANK // S, S)), ALU.add, ALU.mult)
                jobs += linear_jobs(w[f"w{n}r{suffix}"], k.xnT, DC, 128, drain, by="dve")
        matmul_pass(nc, k, jobs, [loaded])

        def rope(dve, link):
            for n in "qk":
                link(dve.tensor_tensor(rot[n][:, 0, :], rot[n][:, 0, :], rot[n][:, 1, :], ALU.add))
            link(dve.memset(v_all[:, :, :, PAIR_F:PAIR_F + 1], 1.0))

        vector_block(nc, k, rope)
        jobs = []
        for n, c in (("q", "q"), ("k", "kv")):
            jobs += linear_jobs(w[f"w{n}c"], cT[c], 1, 128, add_bias(k.col(f"L0_b{n}c"), ACT.Gelu)(heads[n]), krows=64)
        for pair in range(B // 2):
            groups = [(lambda bank, h=h: bank[0:S, h * D:(h + 1) * D],
                       [(cT["kv"][:, 0, (2 * pair + h) * S:(2 * pair + h + 1) * S], w["wv"][:, 0, :]),
                        (k.ones3[:, 0:S], k.row("L0_bv"))]) for h in range(2)]
            jobs.append(values_job(groups, v_all, pair))
        matmul_pass(nc, k, jobs)

        def gelus(act, link):
            for n in "qk":
                link(act.activation(heads[n][:, 1, :], rot[n][:, 0, :], ACT.Gelu))

        scalar_block(nc, k, gelus)
        self_attention(nc, k, "L0s", heads["q"], heads["k"], v_all, att, True)
        to_features(nc, k, att, attT)
        residual_linear(nc, k, attT, w["wo"], DC, "L0_bo", k.x)


def stage_L0_ffn(nc, k, ins):
    normed(nc, k)
    with Stage(nc, "L0f") as st:
        wgT = st.sb("wgT", [P, DC, E8])
        loaded = load_block(nc, k, [(wgT[:], wk(ins["L0_Wg"]))])
        logits, top = st.sb("logits", [P, NT, E8]), st.sb("top", [P, NT, E8])
        router_logits(nc, k, wgT, logits, loaded)
        rows, owner, gates = top2_gates(nc, k, st, logits, top)
        experts(nc, k, "L0e", ins["L0_W1"], ins["L0_W2"], ins["L0_W3"], 682, rows, owner, gates, 2)


def stage_L1_cross(nc, k, ins):
    normed(nc, k)
    with Stage(nc, "L1x") as st:
        INNER, HDIM = 512, 64
        IC = INNER // P
        q_ctx = st.sb("q_ctx", [P, B, 2, BANK])
        with Stage(nc, "L1q") as s2:
            wq, wkT = s2.sb("wq", [P, DC, INNER]), s2.sb("wkT", [P, IC, 2, D])
            qT = s2.sb("qT", [P, IC, TOK])
            vector_block(nc, k, lambda dve, link: link(dve.memset(wkT[:], 0.0)))
            halves = [slice(h * HDIM, (h + 1) * HDIM) for h in range(2)]
            loaded = load_block(nc, k, [(wq[:], wk(ins["L1x_Wq"]))] + [
                (wkT[rows, :, h, :], wk(ins["L1x_WkT"])[rows, :, :]) for h, rows in enumerate(halves)])
            matmul_pass(nc, k, linear_jobs(wq, k.xnT, DC, INNER, lambda e, bank, m, n: e.activation(
                qT[:, m, n * BANK:(n + 1) * BANK], bank, ACT.Copy, scale=HDIM ** -0.5)), [loaded])
            jobs = []
            for h in range(8):
                for f in range(DC):
                    for n in range(NHALF):
                        products = [(wkT[:, h // 2, h % 2, f * P:(f + 1) * P],
                                     qT[:, h // 2, n * BANK:(n + 1) * BANK])]
                        out = q_ctx[:, n * 8:(n + 1) * 8, f, h * S:(h + 1) * S]
                        by = ("act", "dve")[n]
                        jobs.append(Job([(full, products)], by, lambda e, bank, out=out, by=by: (
                            e.activation(out, bank.rearrange("p (b s) -> p b s", s=S), ACT.Copy) if by == "act"
                            else e.tensor_copy(out, bank.rearrange("p (b s) -> p b s", s=S)))))
            matmul_pass(nc, k, jobs)
        softmax_cross_attention(nc, k, "L1c", ins, False, q_ctx)
        wv, wo = st.sb("wv", [P, DC, INNER]), st.sb("wo", [P, IC, D])
        loaded = load_block(nc, k, [(wv[:], wk(ins["L1x_Wv"])), (wo[:], wk(ins["L1x_Wo"]))])
        accT = st.sb("accT", [P, DC, 8, TOK])
        oT = st.sb("oT", [P, IC, TOK])
        rows = q_ctx[:].rearrange("p b f n -> p b (f n)")
        jobs = []
        for b in range(B):
            for f in range(DC):
                groups = [(lambda bank, t=t: bank[:, t * P:(t + 1) * P],
                           [(rows[:, b, t * D + f * P:t * D + (f + 1) * P], None)]) for t in range(4)]
                out = accT[:, f, :, b * S:(b + 1) * S]
                by = ("act", "dve")[f]
                jobs.append(Job(groups, by, lambda e, bank, out=out, by=by: (
                    e.activation(out, bank.rearrange("p (h s) -> p h s", s=S), ACT.Copy) if by == "act"
                    else e.tensor_copy(out, bank.rearrange("p (h s) -> p h s", s=S)))))
        matmul_pass(nc, k, jobs, [loaded])
        jobs = []
        for c in range(IC):
            for n in range(NHALF):
                groups = [(lambda bank, h=h: bank[h * HDIM:(h + 1) * HDIM, :],
                           [(wv[:, f, (2 * c + h) * HDIM:(2 * c + h + 1) * HDIM],
                             accT[:, f, 2 * c + h, n * BANK:(n + 1) * BANK]) for f in range(DC)]) for h in range(2)]
                jobs.append(Job(groups, "act", lambda e, bank, c=c, n=n: e.activation(
                    oT[:, c, n * BANK:(n + 1) * BANK], bank, ACT.Copy)))
        matmul_pass(nc, k, jobs)
        residual_linear(nc, k, oT, wo, IC, "L1x_bo", k.x)


def stage_L1_attn(nc, k, ins):
    normed(nc, k)
    with Stage(nc, "L1a") as st:
        wqkv, wo = st.sb("wqkv", [P, DC, 3 * D]), st.sb("wo", [P, DC, D])
        loaded = load_block(nc, k, [(wqkv[:], wk(ins["L1a_wqkv"])), (wo[:], wk(ins["L1a_wo"]))])
        qk = st.sb("qk", [P, 2 * DC, TOK])
        pos = st.sb("pos", [P, 2 * DC, TOK])
        v_all = st.sb("v", [S, B, PAIRS, PAIR_F + 1])
        att, attT = st.sb("att", [P, NT, D]), st.sb("attT", [P, DC, TOK])
        bias = k.col("L1a_bqk")
        jobs = linear_jobs(wqkv, k.xnT, DC, 2 * D, lambda e, bank, m, n: e.activation(
            pos[:, m, n * BANK:(n + 1) * BANK], bank, ACT.Identity, bias=bias[:, m:m + 1]))
        for pair in range(B // 2):
            groups = [(lambda bank, h=h: bank[0:S, h * D:(h + 1) * D],
                       [(k.xnT[:, c, (2 * pair + h) * S:(2 * pair + h + 1) * S], wqkv[:, c, 2 * D:3 * D])
                        for c in range(DC)] + [(k.ones3[:, 0:S], k.row("L1a_bv"))]) for h in range(2)]
            jobs.append(values_job(groups, v_all, pair))
        matmul_pass(nc, k, jobs, [loaded])
        elu_plus_one(nc, k, qk, pos)
        vector_block(nc, k, lambda dve, link: link(dve.memset(v_all[:, :, :, PAIR_F:PAIR_F + 1], 1.0)))
        self_attention(nc, k, "L1s", qk[:, 0:DC, :], qk[:, DC:2 * DC, :], v_all, att, False, 1e-6)
        to_features(nc, k, att, attT)
        residual_linear(nc, k, attT, wo, DC, "L1a_bo", k.x)


def elu_plus_one(nc, k, out, src):
    vector_block(nc, k, lambda dve, link: link(dve.tensor_scalar(out[:], src[:], 0.0, None, ALU.min)))
    scalar_block(nc, k, lambda act, link: link(act.activation(out[:], out[:], ACT.Exp)))
    vector_block(nc, k, lambda dve, link: link(
        dve.scalar_tensor_tensor(out[:], src[:], 0.0, out[:], ALU.max, ALU.add)))


ROUND = 1.5 * 2.0 ** 23


def round_clip(dve, link, t, lo, hi):
    link(dve.tensor_scalar(t, t, ROUND, None, ALU.add))
    link(dve.tensor_scalar(t, t, ROUND, None, ALU.subtract))
    link(dve.tensor_scalar(t, t, lo, hi, ALU.max, ALU.min))


def quantise_rows(nc, k, st, name, src, width, scaled=True):
    amax, sc, inv = (st.sb(name + n, [P, NT]) for n in ("amax", "scale", "inv"))

    def steps(dve, link):
        link(dve.tensor_reduce(amax[:], src[:], AX.X, ALU.max, apply_absolute_value=True))
        link(dve.tensor_scalar(amax[:], amax[:], 1e-5, None, ALU.max))
        link(dve.reciprocal(inv[:], amax[:]))
        link(dve.tensor_scalar(sc[:], inv[:], 127.0, None, ALU.mult))
        link(dve.reciprocal(inv[:], sc[:]))
        first = [k.n_dve_link]
        tiles = [(src[:, t, :], sc[:, t:t + 1], inv[:, t:t + 1]) for t in range(NT)]
        for x, s, r in tiles:
            dve.tensor_scalar(x, x, s, ROUND, ALU.mult, ALU.add).then_inc(k.dve_link, 1)
        for x, s, r in tiles:
            first[0] += 1
            dve.wait_ge(k.dve_link, first[0])
            dve.tensor_scalar(x, x, ROUND, -128.0, ALU.subtract, ALU.max).then_inc(k.dve_link, 1)
        for x, s, r in tiles:
            first[0] += 1
            dve.wait_ge(k.dve_link, first[0])
            dve.tensor_scalar(x, x, 127.0, r if scaled else 1.0, ALU.min, ALU.mult).then_inc(k.dve_link, 1)
        dve.wait_ge(k.dve_link, first[0] + NT)
        k.n_dve_link = first[0] + NT

    vector_block(nc, k, steps)
    return inv


def quantise_weight(nc, k, st, name, w, chunks, width):
    part, mean, sc = (st.sb(name + n, [P, 1]) for n in ("part", "mean", "scale"))
    vector_block(nc, k, lambda dve, link: link(
        dve.tensor_reduce(part[:], w[:].rearrange("p c n -> p (c n)"), AX.X, ALU.add, apply_absolute_value=True)))
    matmul_pass(nc, k, [Job([(lambda bank: bank[:, 0:1], [(k.ones64[:], part[:])])], "dve",
                            lambda e, bank: e.tensor_scalar(mean[:], bank[:, 0:1], 1.0 / (P * chunks * width), 1e-5,
                                                            ALU.mult, ALU.max))])

    def steps(dve, link):
        link(dve.reciprocal(sc[:], mean[:]))
        link(dve.tensor_scalar(w[:], w[:], sc[:, 0:1], None, ALU.mult))
        round_clip(dve, link, w[:], -1.0, 1.0)

    vector_block(nc, k, steps)
    return mean


def stage_L1_ffn(nc, k, ins):
    HID = 1024
    HC = HID // P
    layer_norm(nc, k, k.x, k.xn, 1e-5)
    with Stage(nc, "L1f") as st:
        w1, w2 = st.sb("w1", [P, DC, HID]), st.sb("w2", [P, HC, D])
        loaded = load_block(nc, k, [(w1[:], wk(ins["L1f_w1"])), (w2[:], wk(ins["L1f_w2"]))])
        vector_wait(nc, k, loaded)
        m1 = quantise_weight(nc, k, st, "q1", w1, DC, HID)
        m2 = quantise_weight(nc, k, st, "q2", w2, HC, D)
        quantise_rows(nc, k, st, "x", k.xn, D)
        to_features(nc, k, k.xn, k.xnT)
        hT = st.sb("hT", [P, HC, TOK])
        cT = st.sb("cT", [P, HC, TOK])
        h_tok = st.sb("h", [P, NT, HID])
        matmul_pass(nc, k, linear_jobs(w1, k.xnT, DC, HID, lambda e, bank, m, n: e.activation(
            hT[:, m, n * BANK:(n + 1) * BANK], bank, ACT.Copy, scale=m1[:, 0:1])))
        cw, cb = k.col("L1f_cw"), k.col("L1f_cb")

        def conv(dve, link):
            for c in range(HC):
                conv3(dve, link, cT[:, c, :], hT[:, c, :], cw[:, 3 * c:3 * c + 3], cb[:, c:c + 1])

        vector_block(nc, k, conv)
        scalar_block(nc, k, lambda act, link: link(act.activation(cT[:], cT[:], ACT.Silu)))
        jobs = []
        for t in range(NT):
            for half in range(2):
                groups = [(lambda bank, c=c: bank[:, c * P:(c + 1) * P],
                           [(cT[:, 4 * half + c, t * P:(t + 1) * P], None)]) for c in range(4)]
                out = h_tok[:, t, half * BANK:(half + 1) * BANK]
                jobs.append(Job(groups, "act", lambda e, bank, out=out: e.activation(out, bank, ACT.Copy)))
        matmul_pass(nc, k, jobs)
        row_scale = quantise_rows(nc, k, st, "h", h_tok, HID, scaled=False)
        hq, w2q = st.sb("hq", [P, HC, TOK], BF16), st.sb("w2q", [P, HC, D], BF16)
        to_features(nc, k, h_tok, hq, chunks=HC)
        scale = st.sb("out_scale", [P, NT])

        def integer_weights(dve, link):
            link(dve.tensor_copy(w2q[:], w2[:]))
            link(dve.tensor_scalar(scale[:], row_scale[:], m2[:, 0:1], None, ALU.mult))

        vector_block(nc, k, integer_weights)
        jobs = []
        for t in range(NT):
            products = [(hq[:, c, t * P:(t + 1) * P], w2q[:, c, :]) for c in range(HC)]
            jobs.append(Job([(lambda bank: bank[:, 0:D], products)], "dve", lambda e, bank, t=t:
                            e.scalar_tensor_tensor(k.x[:, t, :], bank[:, 0:D], scale[:, t:t + 1], k.x[:, t, :],
                                                   ALU.mult, ALU.add)))
        matmul_pass(nc, k, jobs)


def vector_wait(nc, k, loaded):
    with nc.Block() as block:

        @block.vector
        def _(dve):
            dve.wait_ge(*loaded)


def stage_L2_cross(nc, k, ins):
    normed(nc, k)
    with Stage(nc, "L2x") as st:
        wq, wkk, wv = (st.sb(n, [P, DC, D]) for n in ("wq", "wk", "wv"))
        maskT = st.sb("maskT", [P, KT, S])
        qT = st.sb("qT", [P, DC, TOK])
        loaded = load_block(nc, k, [
            (wq[:], wk(ins["L2x_wq"])), (wkk[:], wk(ins["L2x_wk"])), (wv[:], wk(ins["L2x_wv"])),
            (maskT[:, 0:KFULL, :], ins["maskT"][0:KFULL * P, :].rearrange("(t p) q -> p t q", p=P)),
            (maskT[0:KREST, KFULL, :], ins["maskT"][KFULL * P:M, :])])
        matmul_pass(nc, k, linear_jobs(wq, k.xnT, DC, D, add_bias(k.col("L2x_bq"), ACT.Relu)(qT)), [loaded])
        relu_cross_attention(nc, k, "L2c", ins, wkk, wv, qT, maskT, loaded)


def stage_L2_attn(nc, k, ins):
    normed(nc, k)
    with Stage(nc, "L2a") as st:
        w = {n: st.sb(n, [P, DC, D]) for n in ("wq", "wk", "wv", "wfc")}
        causal_tile = st.sb("causal_tile", [P, P])
        loaded = load_block(nc, k, [(w[n][:], wk(ins["L2a_" + n])) for n in w] + [(causal_tile[:], ins["causal_tile"])])
        qT, kT = st.sb("qT", [P, DC, TOK]), st.sb("kT", [P, DC, TOK])
        v = st.sb("v", [P, NT, D])
        s, sT = st.sb("s", [P, NT, P]), st.sb("sT", [P, NT, P])
        mxs = st.sb("mxs", [P, NT])
        jobs = linear_jobs(w["wq"], k.xnT, DC, D, lambda e, bank, m, n: e.activation(
            qT[:, m, n * BANK:(n + 1) * BANK], bank, ACT.Copy, scale=D ** -0.5))
        jobs += linear_jobs(w["wk"], k.xnT, DC, D, lambda e, bank, m, n: e.activation(
            kT[:, m, n * BANK:(n + 1) * BANK], bank, ACT.Copy))
        matmul_pass(nc, k, jobs, [loaded])
        residual_linear(nc, k, k.xnT, w["wv"], DC, None, v, add=False)
        jobs = []
        for t in range(NT):
            products = [(qT[:, c, t * P:(t + 1) * P], kT[:, c, t * P:(t + 1) * P]) for c in range(DC)]
            jobs.append(Job([(lambda bank: bank[:, 0:P], products)], "dve", lambda e, bank, t=t: e.tensor_tensor(
                s[:, t, :], bank[:, 0:P], causal_tile[:], ALU.add)))
        matmul_pass(nc, k, jobs)

        def shift(dve, link):
            link(dve.tensor_reduce(mxs[:], s[:], AX.X, ALU.max))
            link(dve.tensor_tensor(s[:], s[:], mxs[:].unsqueeze(2).broadcast_to((P, NT, P)), ALU.subtract))

        vector_block(nc, k, shift)
        scalar_block(nc, k, lambda act, link: link(act.activation(s[:], s[:], ACT.Exp)))

        def divide(dve, link):
            link(dve.tensor_reduce(mxs[:], s[:], AX.X, ALU.add))
            link(dve.reciprocal(mxs[:], mxs[:]))
            link(dve.tensor_tensor(s[:], s[:], mxs[:].unsqueeze(2).broadcast_to((P, NT, P)), ALU.mult))

        vector_block(nc, k, divide)
        jobs = []
        for n in range(2):
            groups = [(lambda bank, t=t: bank[:, t * P:(t + 1) * P], [(s[:, 4 * n + t, :], None)]) for t in range(4)]
            jobs.append(Job(groups, "act", lambda e, bank, n=n: e.activation(
                sT[:, 4 * n:4 * n + 4, :].rearrange("p t q -> p (t q)"), bank, ACT.Copy)))
        matmul_pass(nc, k, jobs)
        jobs = []
        for t in range(NT):
            jobs.append(Job([(lambda bank: bank[:, 0:D], [(sT[:, t, :], v[:, t, :])])], "dve",
                            lambda e, bank, t=t: e.tensor_tensor(k.xn[:, t, :], bank[:, 0:D], v[:, t, :], ALU.add)))
        matmul_pass(nc, k, jobs)
        layer_norm(nc, k, k.xn, k.xn, 1e-5)
        to_features(nc, k, k.xn, k.xnT, scale=k.col("L2a_gamma"), bias=k.col("L2a_beta"))
        residual_linear(nc, k, k.xnT, w["wfc"], DC, "L2a_bfc", k.x)


def stage_L2_ffn(nc, k, ins):
    normed(nc, k)
    with Stage(nc, "L2f") as st:
        GD = 16
        redT, wg = st.sb("redT", [P, DC, GD]), st.sb("wg", [E8, GD])
        wgT = st.sb("wgT", [GD, E8])
        loaded = load_block(nc, k, [(redT[:], wk(ins["L2f_redT"])), (wg[:], ins["L2f_wg"])])
        sq, norm = st.sb("sq", [E8, GD]), st.sb("norm", [E8, 1])
        xr = st.sb("xr", [GD, TOK])
        logits, top = st.sb("logits", [P, NT, E8]), st.sb("top", [P, NT, 8])
        idx, idxf = st.sb("idx", [P, NT, 8], U32), st.sb("idxf", [P, NT, 8])
        ex, score = st.sb("ex", [P, NT, E8]), st.sb("score", [P, NT, 1])
        vector_wait(nc, k, loaded)

        def squares(dve, link):
            link(dve.tensor_tensor(sq[:], wg[:], wg[:], ALU.mult))
            link(dve.tensor_reduce(norm[:], sq[:], AX.X, ALU.add))

        vector_block(nc, k, squares)
        scalar_block(nc, k, lambda act, link: link(act.activation(norm[:], norm[:], ACT.Sqrt)))

        def unit(dve, link):
            link(dve.tensor_scalar(norm[:], norm[:], 1e-4, None, ALU.max))
            link(dve.reciprocal(norm[:], norm[:]))
            link(dve.tensor_scalar(wg[:], wg[:], norm[:, 0:1], None, ALU.mult))

        vector_block(nc, k, unit)
        jobs = [Job([(lambda bank: bank[0:GD, 0:E8], [(wg[:], None)])], "dve",
                    lambda e, bank: e.tensor_copy(wgT[:], bank[0:GD, 0:E8]))]
        for n in range(NHALF):
            jobs.append(Job([(lambda bank: bank[0:GD, :], [
                (redT[:, c, :], k.xnT[:, c, n * BANK:(n + 1) * BANK]) for c in range(DC)])], "act",
                lambda e, bank, n=n: e.activation(xr[:, n * BANK:(n + 1) * BANK], bank[0:GD, :], ACT.Copy)))
        matmul_pass(nc, k, jobs)
        groups = [(lambda bank, t=t: bank[:, t * E8:(t + 1) * E8], [(xr[:, t * P:(t + 1) * P], wgT[:])])
                  for t in range(NT)]
        matmul_pass(nc, k, [Job(groups, "dve", lambda e, bank: e.tensor_copy(
            logits[:].rearrange("p t e -> p (t e)"), bank[:, 0:NT * E8]))])

        def pick(dve, link):
            for t in range(NT):
                link(dve.max(top[:, t, :], logits[:, t, :]))
                link(dve.max_index(idx[:, t, :], top[:, t, :], logits[:, t, :]))
            link(dve.tensor_copy(idxf[:], idx[:]))
            link(dve.tensor_tensor(ex[:], logits[:], top[:, :, 0:1].broadcast_to((P, NT, E8)), ALU.subtract))

        vector_block(nc, k, pick)
        scalar_block(nc, k, lambda act, link: link(act.activation(ex[:], ex[:], ACT.Exp)))

        def score_gates(dve, link):
            link(dve.tensor_reduce(score[:, :, 0], ex[:], AX.X, ALU.add))
            link(dve.reciprocal(score[:, :, 0], score[:, :, 0]))
            link(dve.tensor_tensor(ex[:], k.iota8[:].unsqueeze(1).broadcast_to((P, NT, E8)),
                                   idxf[:, :, 0:1].broadcast_to((P, NT, E8)), ALU.is_equal))

        vector_block(nc, k, score_gates)
        rows, owner = place_tokens(nc, k, st, ex[:], 1)
        experts(nc, k, "L2e", ins["L2f_w1"], None, ins["L2f_w2"], 1024, rows, owner, score, 1,
                ins["L2f_b1"], ins["L2f_b2"])


def stage_L3_cross(nc, k, ins):
    normed(nc, k)
    with Stage(nc, "L3x") as st:
        attT = st.sb("attT", [P, DC, TOK])
        silu_cross_attention(nc, k, "L3c", ins, attT)
        add_transposed(nc, k, attT, k.x)


def stage_L3_attn(nc, k, ins):
    normed(nc, k)
    HID = 1024
    with Stage(nc, "L3a") as st:
        shapes = {"in_w": D, "actp_w": D, "qk_w": 2 * D, "out_w": D, "fc1_w": HID}
        w = {n: st.sb(n, [P, DC, dout]) for n, dout in shapes.items()}
        w["fc2_w"] = st.sb("fc2_w", [P, HID // P, D])
        rotation = st.sb("rotation", [P, DC, P])
        loaded = load_block(nc, k, [(w[n][:], wk(ins["L3a_" + n])) for n in w] + [(rotation[:], ins["rotation"])])
        u = st.sb("u", [P, DC, TOK])
        u2 = st.sb("u2", [P, DC, TOK])
        gate = st.sb("gate", [P, DC, TOK])
        xi = st.sb("xi", [P, DC, TOK])
        qk = st.sb("qk", [P, 2 * DC, TOK])
        tok = st.sb("tok", [P, NT, D])

        def cpe1(dve, link):
            for c in range(DC):
                conv3(dve, link, u[:, c, :], k.xnT[:, c, :], k.col("L3_cpe1_w")[:, 3 * c:3 * c + 3],
                      k.col("L3_cpe1_b")[:, c:c + 1])
            link(dve.tensor_tensor(u[:], u[:], k.xnT[:], ALU.add))

        vector_block(nc, k, cpe1)
        add_transposed(nc, k, u, tok, add=False)
        layer_norm(nc, k, tok, tok, 1e-5)
        to_features(nc, k, tok, k.xnT, scale=k.col("L3_n1g"), bias=k.col("L3_n1b"))
        jobs = linear_jobs(w["actp_w"], k.xnT, DC, D, add_bias(k.col("L3_actp_b"), ACT.Silu)(gate))
        jobs += linear_jobs(w["in_w"], k.xnT, DC, D, lambda e, bank, m, n: e.tensor_scalar(
            u2[:, m, n * BANK:(n + 1) * BANK], bank, k.col("L3_in_b")[:, m:m + 1], None, ALU.add), by="dve")
        matmul_pass(nc, k, jobs, [loaded])

        def dwc(dve, link):
            for c in range(DC):
                conv3(dve, link, xi[:, c, :], u2[:, c, :], k.col("L3_dwc_w")[:, 3 * c:3 * c + 3],
                      k.col("L3_dwc_b")[:, c:c + 1])

        vector_block(nc, k, dwc)
        scalar_block(nc, k, lambda act, link: link(act.activation(xi[:], xi[:], ACT.Silu)))
        with Stage(nc, "L3q") as s2:
            pos = s2.sb("pos", [P, 2 * DC, TOK])
            rope = s2.sb("rope", [P, 2 * DC, TOK])
            k_tok, v_tok = s2.sb("k_tok", [S, B, D]), s2.sb("v_tok", [S, B, D])
            kmean = s2.sb("kmean", [P, DC, B])
            zd = s2.sb("zd", [P, DC, TOK])
            kv = s2.sb("kv", [P, B, DC, P])
            matmul_pass(nc, k, linear_jobs(w["qk_w"], xi, DC, 2 * D, lambda e, bank, m, n: e.activation(
                pos[:, m, n * BANK:(n + 1) * BANK], bank, ACT.Identity, bias=k.col("L3_qk_b")[:, m:m + 1])))
            elu_plus_one(nc, k, qk, pos)
            jobs = []
            for m in range(2 * DC):
                for n in range(NHALF):
                    jobs.append(Job([(full, [(rotation[:, m % DC, :], qk[:, m, n * BANK:(n + 1) * BANK])])], "act",
                                    lambda e, bank, m=m, n=n: e.activation(rope[:, m, n * BANK:(n + 1) * BANK],
                                                                           bank, ACT.Copy)))
            matmul_pass(nc, k, jobs)

            def means(dve, link):
                link(dve.tensor_reduce(kmean[:], qk[:, DC:2 * DC, :].rearrange("p c (b s) -> p c b s", s=S),
                                       AX.X, ALU.add))
                link(dve.tensor_scalar(kmean[:], kmean[:], 1.0 / S, None, ALU.mult))
                for c in range(DC):
                    link(dve.tensor_tensor(zd[:, c, :].rearrange("p (b s) -> p b s", s=S),
                                           qk[:, c, :].rearrange("p (b s) -> p b s", s=S),
                                           kmean[:, c, :].unsqueeze(2).broadcast_to((P, B, S)), ALU.mult))

            vector_block(nc, k, means)
            jobs = []
            for c in range(DC):
                for n in range(NHALF):
                    jobs.append(Job([(full, [(k.same_head[:], zd[:, c, n * BANK:(n + 1) * BANK])])], "dve",
                                    lambda e, bank, c=c, n=n: e.tensor_scalar(u2[:, c, n * BANK:(n + 1) * BANK],
                                                                              bank, 1e-6, None, ALU.add)))
            for src, dst in ((rope[:, DC:2 * DC, :], k_tok), (xi, v_tok)):
                for pair in range(B // 2):
                    groups = [(lambda bank, h=h, c=c: bank[0:S, h * D + c * P:h * D + (c + 1) * P],
                               [(src[:, c, (2 * pair + h) * S:(2 * pair + h + 1) * S], None)])
                              for h in range(2) for c in range(DC)]
                    out = dst[:, 2 * pair:2 * pair + 2, :].rearrange("p b d -> p (b d)")
                    jobs.append(Job(groups, "act", lambda e, bank, out=out: e.activation(out, bank[0:S, :], ACT.Copy)))
            matmul_pass(nc, k, jobs)
            vector_block(nc, k, lambda dve, link: link(dve.reciprocal(u2[:], u2[:])))
            jobs = []
            for pair in range(B // 2):
                groups = [(lambda bank, h=h, c=c: bank[:, (h * DC + c) * P:(h * DC + c + 1) * P],
                           [(k_tok[:, 2 * pair + h, c * P:(c + 1) * P], v_tok[:, 2 * pair + h, c * P:(c + 1) * P])])
                          for h in range(2) for c in range(DC)]
                out = kv[:, 2 * pair:2 * pair + 2, :, :].rearrange("p b c n -> p (b c) n")
                jobs.append(Job(groups, "dve", lambda e, bank, out=out: e.scalar_tensor_tensor(
                    out, bank.rearrange("p (a n) -> p a n", n=P), 1.0 / S,
                    k.same_head[:].unsqueeze(1).broadcast_to((P, 2 * DC, P)), ALU.mult, ALU.mult)))
            matmul_pass(nc, k, jobs)
            jobs = []
            for c in range(DC):
                for n in range(NHALF):
                    groups = [(lambda bank, b=b: bank[:, b * S:(b + 1) * S],
                               [(kv[:, 8 * n + b, c, :], rope[:, c, (8 * n + b) * S:(8 * n + b + 1) * S])])
                              for b in range(8)]
                    sl = slice(n * BANK, (n + 1) * BANK)
                    jobs.append(Job(groups, "dve", lambda e, bank, c=c, sl=sl: e.tensor_tensor(
                        zd[:, c, sl], bank, u2[:, c, sl], ALU.mult)))
            matmul_pass(nc, k, jobs)

            def lepe(dve, link):
                for c in range(DC):
                    conv3(dve, link, u2[:, c, :], xi[:, c, :], k.col("L3_lepe_w")[:, 3 * c:3 * c + 3],
                          k.col("L3_lepe_b")[:, c:c + 1])
                link(dve.tensor_tensor(zd[:], zd[:], u2[:], ALU.add))
                link(dve.tensor_tensor(xi[:], zd[:], gate[:], ALU.mult))

            vector_block(nc, k, lepe)
        jobs = linear_jobs(w["out_w"], xi, DC, D, lambda e, bank, m, n: e.scalar_tensor_tensor(
            u[:, m, n * BANK:(n + 1) * BANK], bank, k.col("L3_out_b")[:, m:m + 1],
            u[:, m, n * BANK:(n + 1) * BANK], ALU.add, ALU.add), by="dve")
        matmul_pass(nc, k, jobs)

        def cpe2(dve, link):
            for c in range(DC):
                conv3(dve, link, u2[:, c, :], u[:, c, :], k.col("L3_cpe2_w")[:, 3 * c:3 * c + 3],
                      k.col("L3_cpe2_b")[:, c:c + 1])
            link(dve.tensor_tensor(u[:], u[:], u2[:], ALU.add))

        vector_block(nc, k, cpe2)
        add_transposed(nc, k, u, tok, add=False)
        vector_block(nc, k, lambda dve, link: link(dve.tensor_tensor(k.x[:], k.x[:], tok[:], ALU.add)))
        layer_norm(nc, k, tok, tok, 1e-5)
        to_features(nc, k, tok, k.xnT, scale=k.col("L3_n2g"), bias=k.col("L3_n2b"))
        h1 = st.sb("h1", [P, HID // P, TOK])
        matmul_pass(nc, k, linear_jobs(w["fc1_w"], k.xnT, DC, HID, add_bias(k.col("L3_fc1_b"), ACT.Gelu)(h1)))
        residual_linear(nc, k, h1, w["fc2_w"], HID // P, "L3_fc2_b", k.x)


CAPACITY = int(1.25 * TOK / E8 * 2)


def stage_L3_ffn(nc, k, ins):
    normed(nc, k)
    with Stage(nc, "L3f") as st:
        wgT = st.sb("wgT", [P, DC, E8])
        loaded = load_block(nc, k, [(wgT[:], wk(ins["L3f_router"]))])
        logits, top = st.sb("logits", [P, NT, E8]), st.sb("top", [P, NT, E8])
        kept = st.sb("kept", [P, NT, 2])
        router_logits(nc, k, wgT, logits, loaded)
        rows, owner, gates = top2_gates(nc, k, st, logits, top, kept[:])
        experts(nc, k, "L3e", ins["L3f_w1"], None, ins["L3f_w2"], 1024, rows, owner, gates, 2)


STAGES = [stage_L0_cross, stage_L0_attn, stage_L0_ffn, stage_L1_cross, stage_L1_attn, stage_L1_ffn,
          stage_L2_cross, stage_L2_attn, stage_L2_ffn, stage_L3_cross, stage_L3_attn, stage_L3_ffn]

CONSTS = [("ident", P), ("ones64", P), ("blocks8", 8), ("same_head", P), ("causal_rows", S),
          ("causal_keys", S), ("upto", P), ("iota", 24),
          ("rope_cos", S), ("rope_sin", S)]
N_CONST = sum(w for _, w in CONSTS)


def constants():
    p = np.arange(P)
    t = {}
    t["ident"] = np.eye(P)
    t["ones64"] = np.ones((P, P))
    t["blocks8"] = (p[:, None] // HD == np.arange(8)[None])
    t["same_head"] = (p[:, None] // HD == p[None] // HD)
    t["causal_rows"] = np.where(np.arange(S)[None] > p[:, None] % S, NEG, 0.0)
    t["causal_keys"] = (p[:, None] % S <= np.arange(S)[None])
    t["causal_tile"] = np.where((p[:, None] // S == p[None] // S) & (p[None] <= p[:, None]), 0.0, NEG)
    t["upto"] = (p[:, None] <= p[None])
    t["iota"] = np.broadcast_to(np.arange(24)[None], (P, 24))
    half = P // 2
    inv = (np.float32(1.0) / np.float32(10000.0) ** (np.arange(0, P, 2, dtype=np.float32) / np.float32(P)))
    ang = (np.arange(S, dtype=np.float32)[None] * inv[p % half][:, None]).astype(np.float32)
    t["rope_cos"] = np.cos(ang)
    t["rope_sin"] = np.where(p[:, None] < half, -1.0, 1.0) * np.sin(ang)
    kmax = D // 2
    theta = (np.float32(1.0) / np.float32(10000.0) ** (np.arange(kmax, dtype=np.float32) / np.float32(kmax)))
    rot = np.zeros((P, DC, P))
    for c in range(DC):
        for m in range(P // 2):
            cos, sin = np.cos(theta[c * half + m]), np.sin(theta[c * half + m])
            rot[2 * m, c, 2 * m], rot[2 * m + 1, c, 2 * m] = cos, -sin
            rot[2 * m, c, 2 * m + 1], rot[2 * m + 1, c, 2 * m + 1] = sin, cos
    late = {"causal_tile": np.asarray(t.pop("causal_tile"), np.float32), "rotation": np.asarray(rot, np.float32)}
    return late, np.concatenate([np.asarray(t[n], np.float32).reshape(P, w) for n, w in CONSTS], axis=1)


def build(nc, ins, out, stages=STAGES):
    with ExitStack() as ctx:
        k = Kit()
        k.nc = nc

        def sb(name, shape, dt=F32):
            return ctx.enter_context(nc.sbuf_tensor(name, shape, dt))

        def sem(name):
            return ctx.enter_context(nc.semaphore(name))

        k.ps = ctx.enter_context(nc.psum_tensor("ps", [P, 8, BANK], F32))
        k.x, k.xn, k.xnT = sb("x", [P, NT, D]), sb("xn", [P, NT, D]), sb("xnT", [P, DC, TOK])
        k.stats, k.mv, k.rstd = sb("stats", [P, NT, 6]), sb("mv", [P, NT, 2]), sb("rstd", [P, 3, NT])
        consts = sb("consts_sb", [P, N_CONST])

        def table(name):
            names = [n for n, _ in CONSTS]
            at = sum(w for _, w in CONSTS[:names.index(name)])
            return consts[:, at:at + CONSTS[names.index(name)][1]]

        k.ident, k.ones64, k.blocks8 = table("ident"), table("ones64"), table("blocks8")
        k.same_head, k.upto, k.iota = table("same_head"), table("upto"), table("iota")
        k.iota8 = k.iota[:, 0:E8]
        k.causal_rows, k.causal_keys = table("causal_rows"), table("causal_keys")
        k.rope_cos, k.rope_sin = table("rope_cos"), table("rope_sin")
        k.ones_row = k.ones64
        cols = sb("cols_sb", [P, NCOLS])
        k.col = lambda n: cols[:, COL_AT[n][0]:COL_AT[n][0] + COL_AT[n][1]]
        parts = sb("row_parts", [2 * THIRD + 1, len(ROWS), D], BF16)
        k.ones3 = sb("ones3", [2 * THIRD + 1, P], BF16)
        k.row = lambda n: parts[:, ROWS.index(n), :]
        k.filled, k.act_drained, k.dve_drained = sem("filled"), sem("act_drained"), sem("dve_drained")
        k.weights, k.ln_step, k.ln_root = sem("weights"), sem("ln_step"), sem("ln_root")
        k.dve_link, k.act_link, k.start, k.stored = sem("dve_link"), sem("act_link"), sem("start"), sem("stored")
        k.tick = sem("tick")
        k.sorted_in = nc.dram_tensor("sorted_in", (expert_tiles(2) * P, D), F32).ap()
        k.zeroed, k.zeros_made = sem("zeroed"), sem("zeros_made")
        k.n_filled = k.n_act = k.n_dve = k.n_weights = k.n_ln = k.n_root = k.n_dve_link = k.n_act_link = 0

        with Stage(nc, "first") as st:
            rows, rest = st.sb("rows", [1, len(ROWS), D]), st.sb("rest", [1, len(ROWS), D])
            with nc.Block() as block:

                @block.sync
                def _(sp):
                    sp.dma_start(k.x[:], ins["x"].rearrange("(t p) d -> p t d", p=P)).then_inc(k.start, 16)
                    sp.dma_start(consts[:], ins["consts"]).then_inc(k.start, 16)
                    sp.dma_start(cols[:], ins["cols"]).then_inc(k.start, 16)
                    sp.dma_start(rows[:], ins["rows"]).then_inc(k.start, 16)
                    sp.wait_ge(k.zeros_made, 1)
                    for part in range(ZERO_PARTS):
                        n = min(NT, expert_tiles(2) - part * NT)
                        sp.dma_start(k.sorted_in.rearrange("(t p) d -> p t d", p=P)[:, part * NT:part * NT + n, :],
                                     k.xn[:, 0:n, :]).then_inc(k.zeroed, 16)
                    sp.wait_ge(k.start, START)

                @block.vector
                def _(dve):
                    dve.memset(k.xn[:], 0.0).then_inc(k.zeros_made, 1)

            def split_rows(dve, link):
                link(dve.memset(k.ones3[:], 1.0))
                link(dve.memset(parts[:], 0.0))
                for n in range(3):
                    part = parts[n * THIRD:n * THIRD + 1, :, :]
                    link(dve.tensor_copy(part, rows[:]))
                    if n < 2:
                        link(dve.tensor_copy(rest[:], part))
                        link(dve.tensor_tensor(rows[:], rows[:], rest[:], ALU.subtract))

            vector_block(nc, k, split_rows, lambda sp: sp.wait_ge(k.zeroed, 16 * ZERO_PARTS))
        for stage in stages:
            stage(nc, k, ins)

        with nc.Block() as block:

            @block.sync
            def _(sp):
                sp.dma_start(out.rearrange("(t p) d -> p t d", p=P), k.x[:]).then_inc(k.stored, 16)
                sp.wait_ge(k.stored, 16)


def laid_out(v):
    a = {n: np.asarray(x) for n, x in v.items()}
    o = {"x": a["x"].reshape(TOK, D), "ctx": a["ctx_1024"],
         "ctxT": a["ctx_1024"].transpose(0, 2, 1).reshape(B, DC, P, M),
         "mask": a["mask_BxSxS2_bk1"], "maskT": a["mask_1xSxS2_ff0"][0].T}
    half = P // 2

    def swap(w):
        return np.concatenate([w[..., half:], w[..., :half]], axis=-1)

    for n in ("wq", "wqc", "wqr", "wkv", "wkr", "wkc", "wv", "wo"):
        o["L0_" + n] = a["L0_attn_" + n]
    o["L0_wqr_sw"], o["L0_wkr_sw"] = swap(a["L0_attn_wqr"]), swap(a["L0_attn_wkr"])
    o["L0_Wg"] = a["L0_ffn_Wg"].T
    o["L0_W1"], o["L0_W2"] = (a["L0_ffn_" + n].transpose(0, 2, 1) for n in ("W1", "W2"))
    o["L0_W3"] = a["L0_ffn_W3"].transpose(0, 2, 1)
    o["L1x_Wq"], o["L1x_WkT"] = a["L1_xattn_Wq"], a["L1_xattn_Wk"].T
    o["L1x_Wv"], o["L1x_Wo"] = a["L1_xattn_Wv"], a["L1_xattn_Wo"]
    o["L1a_wqkv"], o["L1a_wo"] = a["L1_attn_w_qkv"].T, a["L1_attn_w_out"].T
    o["L1f_w1"], o["L1f_w2"] = a["L1_ffn_w1"].T, a["L1_ffn_w2"].T
    for n in "qkv":
        o["L2x_w" + n] = a["L2_xattn_kernel_" + n][0, 0]
    for n, m in (("wq", "Wq"), ("wk", "Wk"), ("wv", "Wv"), ("wfc", "Wfc")):
        o["L2a_" + n] = a["L2_attn_" + m]
    o["L2f_redT"], o["L2f_wg"] = a["L2_ffn_wg_red"].T, a["L2_ffn_wg"]
    o["L2f_w1"], o["L2f_w2"] = a["L2_ffn_w1"], a["L2_ffn_w2"]
    o["L2f_b1"] = a["L2_ffn_b1"].reshape(E8, 8, P).transpose(0, 2, 1)
    o["L2f_b2"] = a["L2_ffn_b2"].reshape(E8, 1, D)
    for n in ("in_w", "actp_w", "qk_w", "out_w", "fc1_w", "fc2_w"):
        o["L3a_" + n] = a["L3_attn_" + n]
    o["L3f_router"] = a["L3_ffn_router_w"].T
    o["L3f_w1"], o["L3f_w2"] = a["L3_ffn_w1"], a["L3_ffn_w2"]

    def taps(w):
        return w[:, 0, :].reshape(-1, P, 3).transpose(1, 0, 2).reshape(P, -1)

    def col(b):
        if b.size < P:
            b = np.concatenate([b, np.zeros(P - b.size, np.float32)])
        return b.reshape(-1, P).T

    c = {"L0_bq": a["L0_attn_bq"], "L0_bkv": a["L0_attn_bkv"], "L0_bqc": a["L0_attn_bqc"],
         "L0_bkc": a["L0_attn_bkc"], "L0_bqr": a["L0_attn_bqr"], "L0_bkr": a["L0_attn_bkr"],
         "L0_bqr_sw": swap(a["L0_attn_bqr"]), "L0_bkr_sw": swap(a["L0_attn_bkr"]),
         "L1a_bqk": a["L1_attn_b_qkv"][:2 * D], "L1f_cb": a["L1_ffn_conv_b"],
         "L2x_bq": a["L2_xattn_bias_q"], "L2x_bk": a["L2_xattn_bias_k"],
         "L2a_gamma": a["L2_attn_gamma"], "L2a_beta": a["L2_attn_beta"]}
    for n, m in (("cpe1_b", "cpe1_b"), ("n1g", "norm1_g"), ("n1b", "norm1_b"), ("in_b", "in_b"),
                 ("actp_b", "actp_b"), ("dwc_b", "dwc_b"), ("qk_b", "qk_b"), ("lepe_b", "lepe_b"),
                 ("out_b", "out_b"), ("cpe2_b", "cpe2_b"), ("n2g", "norm2_g"), ("n2b", "norm2_b"),
                 ("fc1_b", "fc1_b")):
        c["L3_" + n] = a["L3_attn_" + m]
    c = {n: col(x) for n, x in c.items()}
    c["L1f_cw"] = taps(a["L1_ffn_conv_w"])
    for n in ("cpe1_w", "dwc_w", "lepe_w", "cpe2_w"):
        c["L3_" + n] = taps(a["L3_attn_" + n])
    o["cols"] = np.concatenate([c[n] for n, _ in COLS], axis=1)
    r = {"L0_bv": a["L0_attn_bv"], "L0_bo": a["L0_attn_bo"], "L1x_bo": a["L1_xattn_bo"],
         "L1a_bv": a["L1_attn_b_qkv"][2 * D:], "L1a_bo": a["L1_attn_b_out"], "L2x_bv": a["L2_xattn_bias_v"],
         "L2a_bfc": a["L2_attn_bfc"], "L3_fc2_b": a["L3_attn_fc2_b"]}
    o["rows"] = np.stack([r[n] for n in ROWS])[None]
    late, o["consts"] = constants()
    o.update(late)
    return {n: np.ascontiguousarray(x) for n, x in o.items()}


def kernel(**inputs):
    import concourse.bacc as _bacc
    from concourse.bass_utils import run_bass_kernel_spmd as _run

    arrays = {f"in_{n}": x for n, x in laid_out(inputs).items()}
    nc = _bacc.Bacc("TRN2", target_bir_lowering=False, num_devices=1)
    ins = {n[3:]: nc.dram_tensor(n, x.shape, mybir.dt.from_np(x.dtype), kind="ExternalInput").ap()
           for n, x in arrays.items()}
    out = nc.dram_tensor("out_x", (TOK, D), F32, kind="ExternalOutput").ap()
    build(nc, ins, out)
    r = _run(nc, [arrays], core_ids=[0])
    return r.results[0]["out_x"].reshape(B, S, D)
```
